# Optimizing a Trainium2 kernel written in Bass

```python
import numpy as np
import jax
import jax.numpy as jnp

def _softmax(x, axis=-1):
    return jax.nn.softmax(x, axis=axis)

def _gelu(x):
    return jax.nn.gelu(x, approximate=True)

def _silu(x):
    return jax.nn.silu(x)

def _sigmoid(x):
    return jax.nn.sigmoid(x)

def _layernorm(x, axis=-1, eps=1e-05):
    m = jnp.mean(x, axis=axis, keepdims=True)
    v = jnp.var(x, axis=axis, keepdims=True)
    return (x - m) / jnp.sqrt(v + eps)

def _scatter_add(tgt, idx, src, axis=0):
    return tgt.at[idx].add(src)

def _segment_sum(src, seg, n):
    return jax.ops.segment_sum(src, seg, n)
kernel_name = 'mk_prb_d4_jaxref_r8_bc4863'

def setup_inputs(seed: int=0):
    np.random.seed(seed)
    _w = jnp.asarray

    def _L0_attn_setup():
        import jax, jax.numpy as jnp
        import numpy as np
        N_HIDDEN = 128
        N_HEADS = 16
        HEAD_DIM = N_HIDDEN // N_HEADS
        KERNEL = 4
        GN_EPS = 1e-05

        def _short_conv_1d(x, weight):
            F, K = weight.shape
            xp = jnp.pad(x, ((0, 0), (K - 1, 0), (0, 0)))
            shifts = jnp.stack([xp[:, i:i + x.shape[1], :] for i in range(K)], axis=-1)
            return jnp.sum(shifts * weight[None, None, :, :], axis=-1)
        key = jax.random.key(seed)
        ks = jax.random.split(key, 16)
        B, S = (4, 512)
        H, Hd = (N_HEADS, N_HIDDEN)
        sc = 0.02
        inp = {'x': jax.random.normal(ks[0], (B, S, Hd), dtype=jnp.float32), 'Wq': jax.random.normal(ks[1], (Hd, Hd), dtype=jnp.float32) * sc, 'bq': jnp.zeros((Hd,), jnp.float32), 'Wk': jax.random.normal(ks[2], (Hd, Hd), dtype=jnp.float32) * sc, 'bk': jnp.zeros((Hd,), jnp.float32), 'Wv': jax.random.normal(ks[3], (Hd, Hd), dtype=jnp.float32) * sc, 'bv': jnp.zeros((Hd,), jnp.float32), 'q_conv': jax.random.normal(ks[4], (Hd, KERNEL), dtype=jnp.float32) * sc, 'k_conv': jax.random.normal(ks[5], (Hd, KERNEL), dtype=jnp.float32) * sc, 'v_conv': jax.random.normal(ks[6], (Hd, KERNEL), dtype=jnp.float32) * sc, 'Wa': jax.random.normal(ks[7], (Hd, H), dtype=jnp.float32) * sc, 'ba': jnp.zeros((H,), jnp.float32), 'Wb': jax.random.normal(ks[8], (Hd, H), dtype=jnp.float32) * sc, 'bb': jnp.zeros((H,), jnp.float32), 'Wg': jax.random.normal(ks[9], (Hd, Hd), dtype=jnp.float32) * sc, 'bg': jnp.zeros((Hd,), jnp.float32), 'gn_scale': jnp.ones((Hd,), jnp.float32), 'gn_bias': jnp.zeros((Hd,), jnp.float32), 'Wo': jax.random.normal(ks[10], (Hd, Hd), dtype=jnp.float32) * sc, 'bo': jnp.zeros((Hd,), jnp.float32)}
        return inp
    _L0_attn_in = _L0_attn_setup()

    def _L0_ffn_setup():
        import jax, jax.numpy as jnp
        import numpy as np
        SQRT_2_PI = 0.7978845608028654
        GELU_COEF = 0.044715
        LN_EPS = 1e-06
        TOP_K = 2

        def gelu_kernel(x):
            inner = SQRT_2_PI * (x + GELU_COEF * x ** 3)
            return 0.5 * x * (1.0 + jnp.tanh(inner))
        key = jax.random.key(seed)
        ks = jax.random.split(key, 8)
        B, S, D, F, E = (2, 256, 128, 512, 8)
        s = lambda d: 1.0 / np.sqrt(d)
        return {'x': jax.random.normal(ks[0], (B, S, D), jnp.float32), 'Wr1': jax.random.normal(ks[1], (D, D // 2), jnp.float32) * s(D), 'br1': jnp.zeros((D // 2,), jnp.float32), 'ln_scale': jnp.ones((D // 2,), jnp.float32), 'ln_bias': jnp.zeros((D // 2,), jnp.float32), 'Wr2': jax.random.normal(ks[2], (D // 2, E), jnp.float32) * s(D // 2), 'br2': jnp.zeros((E,), jnp.float32), 'W1': jax.random.normal(ks[3], (E, D, 2 * F), jnp.float32) * s(D), 'b1': jnp.zeros((E, 2 * F), jnp.float32), 'W2': jax.random.normal(ks[4], (E, F, D), jnp.float32) * s(F), 'b2': jnp.zeros((E, D), jnp.float32)}
    _L0_ffn_in = _L0_ffn_setup()

    def _L1_attn_setup():
        import jax, jax.numpy as jnp
        import numpy as np
        B, S, D, H, MLP = (4, 512, 128, 16, 512)
        HD = D // H
        KEPS = 0.001
        LNEPS = 1e-06

        def _ln(x, scale, bias):
            mu = jnp.mean(x, axis=-1, keepdims=True)
            var = jnp.var(x, axis=-1, keepdims=True)
            return (x - mu) * jax.lax.rsqrt(var + LNEPS) * scale + bias
        key = jax.random.key(seed)
        ks = jax.random.split(key, 8)
        s = 0.02
        f32 = jnp.float32
        return {'inputs': jax.random.normal(ks[0], (B, S, D), f32), 'ln1_scale': jnp.ones((D,), f32), 'ln1_bias': jnp.zeros((D,), f32), 'Wq': jax.random.normal(ks[1], (D, H, HD), f32) * s, 'bq': jnp.zeros((H, HD), f32), 'Wk': jax.random.normal(ks[2], (D, H, HD), f32) * s, 'bk': jnp.zeros((H, HD), f32), 'Wv': jax.random.normal(ks[3], (D, H, HD), f32) * s, 'bv': jnp.zeros((H, HD), f32), 'Wo': jax.random.normal(ks[4], (H, HD, D), f32) * s, 'bo': jnp.zeros((D,), f32), 'ln2_scale': jnp.ones((D,), f32), 'ln2_bias': jnp.zeros((D,), f32), 'W1': jax.random.normal(ks[5], (D, MLP), f32) * s, 'b1': jnp.zeros((MLP,), f32), 'W2': jax.random.normal(ks[6], (MLP, D), f32) * s, 'b2': jnp.zeros((D,), f32)}
    _L1_attn_in = _L1_attn_setup()

    def _L1_ffn_setup():
        import jax, jax.numpy as jnp
        import numpy as np
        D_MODEL = 128
        M = 64
        INNER = 16
        key = jax.random.key(seed)
        ks = jax.random.split(key, 9)

        def init(k, shape, fan_in):
            bound = 1.0 / np.sqrt(fan_in)
            return jax.random.uniform(k, shape, jnp.float32, -bound, bound)
        x = jax.random.normal(ks[0], (16, 512, D_MODEL), dtype=jnp.float32)
        Win = init(ks[1], (D_MODEL, M), D_MODEL)
        bin_ = init(ks[2], (M,), D_MODEL)
        W1 = init(ks[3], (M, INNER), 1)
        b1 = init(ks[4], (M, INNER), 1)
        W2 = init(ks[5], (M, INNER), INNER)
        b2 = init(ks[6], (M,), INNER)
        Wout = init(ks[7], (M, D_MODEL), M)
        bout = init(ks[8], (D_MODEL,), M)
        return {'x': x, 'Win': Win, 'bin_': bin_, 'W1': W1, 'b1': b1, 'W2': W2, 'b2': b2, 'Wout': Wout, 'bout': bout}
    _L1_ffn_in = _L1_ffn_setup()

    def _L2_attn_setup():
        import jax, jax.numpy as jnp
        import numpy as np
        D_MODEL = 128
        N_HEADS = 16
        LATENT_HEADS = 8
        LATENT_DIM = 64
        N_LATENTS = 64
        WINDOW = 32
        HEAD_DIM = D_MODEL // N_HEADS
        LAT_HD = LATENT_DIM // LATENT_HEADS
        B, S = (2, 512)

        def _pool_to_latents(x):
            Bx, Sx, C = x.shape
            chunk = max(1, Sx // N_LATENTS)
            return x.reshape(Bx, N_LATENTS, chunk, C).mean(axis=2)

        def _local_window_attn(Q, K, V):
            Bx, H, Sx, D = Q.shape
            W = WINDOW
            nb = Sx // W
            Qb = Q.reshape(Bx, H, nb, W, D)
            Kp = jnp.pad(K, ((0, 0), (0, 0), (W, 0), (0, 0))).reshape(Bx, H, nb + 1, W, D)
            Vp = jnp.pad(V, ((0, 0), (0, 0), (W, 0), (0, 0))).reshape(Bx, H, nb + 1, W, D)
            Kw = jnp.concatenate([Kp[:, :, :-1], Kp[:, :, 1:]], axis=3)
            Vw = jnp.concatenate([Vp[:, :, :-1], Vp[:, :, 1:]], axis=3)
            i = jnp.arange(W)[:, None]
            j = jnp.arange(2 * W)[None, :]
            base = (j > i) & (j <= i + W)
            blk0 = (jnp.arange(nb) > 0)[:, None, None] | (j >= W)[None, :, :]
            mask = base[None, :, :] & blk0
            sc = jnp.einsum('bhnid,bhnjd->bhnij', Qb, Kw) / np.sqrt(D).astype(np.float32)
            sc = jnp.where(mask[None, None], sc, -jnp.inf)
            p = jax.nn.softmax(sc, axis=-1)
            out = jnp.einsum('bhnij,bhnjd->bhnid', p, Vw)
            return out.reshape(Bx, H, Sx, D)
        key = jax.random.key(seed)
        ks = jax.random.split(key, 11)
        std = 0.02
        w = lambda k, shp: jax.random.normal(k, shp, jnp.float32) * std
        return {'x': jax.random.normal(ks[0], (B, S, D_MODEL), jnp.float32), 'wq': w(ks[1], (D_MODEL, D_MODEL)), 'wk': w(ks[2], (D_MODEL, D_MODEL)), 'wv': w(ks[3], (D_MODEL, D_MODEL)), 'wgq': w(ks[4], (D_MODEL, LATENT_DIM)), 'wgk': w(ks[5], (D_MODEL, LATENT_DIM)), 'wgv': w(ks[6], (D_MODEL, LATENT_DIM)), 'r_out_w': w(ks[7], (LATENT_DIM, D_MODEL)), 'gate_local_w': w(ks[8], (N_HEADS, HEAD_DIM)), 'gate_remote_w': w(ks[9], (N_HEADS, HEAD_DIM)), 'w_out': w(ks[10], (D_MODEL, D_MODEL))}
    _L2_attn_in = _L2_attn_setup()

    def _L2_ffn_setup():
        import jax, jax.numpy as jnp
        import numpy as np
        DIM = 128

        def _reference_tuple_inner(x, W_r, W_k, W_v, mu_r, mu_k):
            B, T, C = x.shape
            x_prev = jnp.concatenate([jnp.zeros((B, 1, C), x.dtype), x[:, :-1, :]], axis=1)
            xr = mu_r * x + (1.0 - mu_r) * x_prev
            xk = mu_k * x + (1.0 - mu_k) * x_prev
            r = jax.nn.sigmoid(jnp.einsum('btc,dc->btd', xr, W_r))
            k = jnp.einsum('btc,dc->btd', xk, W_k)
            k_act = jnp.square(jax.nn.relu(k))
            out = r * jnp.einsum('btc,dc->btd', k_act, W_v)
            new_state = x[:, -1, :]
            return (out, new_state)
        key = jax.random.key(seed)
        ks = jax.random.split(key, 6)
        B, T, C = (8, 256, DIM)
        x = jax.random.normal(ks[0], (B, T, C), dtype=jnp.float32)
        s = 1.0 / np.sqrt(C)
        W_r = jax.random.uniform(ks[1], (C, C), jnp.float32, -s, s)
        W_k = jax.random.uniform(ks[2], (C, C), jnp.float32, -s, s)
        W_v = jax.random.uniform(ks[3], (C, C), jnp.float32, -s, s)
        mu_r = jax.random.uniform(ks[4], (C,), jnp.float32)
        mu_k = jax.random.uniform(ks[5], (C,), jnp.float32)
        return {'x': x, 'W_r': W_r, 'W_k': W_k, 'W_v': W_v, 'mu_r': mu_r, 'mu_k': mu_k}
    _L2_ffn_in = _L2_ffn_setup()

    def _L3_attn_setup():
        import jax, jax.numpy as jnp
        import numpy as np
        HEADS = 16
        DIM_HEAD = 64
        EPS = 1e-08
        key = jax.random.key(seed)
        ks = jax.random.split(key, 5)
        B, N, D = (2, 256, 128)
        inner = HEADS * DIM_HEAD
        return {'x': jax.random.normal(ks[0], (B, N, D), jnp.float32), 'Wq': jax.random.normal(ks[1], (D, inner), jnp.float32) * D ** (-0.5), 'Wkv': jax.random.normal(ks[2], (D, 2 * inner), jnp.float32) * D ** (-0.5), 'Wo': jax.random.normal(ks[3], (inner, D), jnp.float32) * inner ** (-0.5), 'bo': jax.random.normal(ks[4], (D,), jnp.float32) * 0.02}
    _L3_attn_in = _L3_attn_setup()

    def _L3_ffn_setup():
        import math
        import jax, jax.numpy as jnp
        import numpy as np
        HIDDEN = 128
        INTER = 512
        EXPERTS = 8
        B, T = (4, 256)
        EPS = 1e-12
        CAP_FACTOR = 1.0
        MIN_CAP = 4

        def layer_norm(x, g, b, eps=EPS):
            m = jnp.mean(x, axis=-1, keepdims=True)
            v = jnp.var(x, axis=-1, keepdims=True)
            return (x - m) * jax.lax.rsqrt(v + eps) * g + b

        def top1_gate(x, wg, capacity):
            logits = x @ wg
            gates = jax.nn.softmax(logits, axis=-1)
            E = wg.shape[-1]
            idx = jnp.argmax(gates, axis=-1)
            mask1 = jax.nn.one_hot(idx, E, dtype=gates.dtype)
            locations = jnp.cumsum(mask1, axis=0) - mask1
            mask1 = mask1 * (locations < capacity).astype(gates.dtype)
            gates1_s = jnp.sum(gates * mask1, axis=-1)
            loc_s = jnp.sum(locations * mask1, axis=-1).astype(jnp.int32)
            loc_oh = jax.nn.one_hot(loc_s, capacity, dtype=gates.dtype)
            combine = gates1_s[:, None, None] * mask1[:, :, None] * loc_oh[:, None, :]
            dispatch = jax.lax.stop_gradient((combine > 0).astype(x.dtype))
            return (combine, dispatch)
        key = jax.random.key(seed)
        ks = jax.random.split(key, 8)
        s = 0.02
        return {'x': jax.random.normal(ks[0], (B, T, HIDDEN), jnp.float32), 'attn_nw': jnp.ones((HIDDEN,), jnp.float32), 'attn_nb': jnp.zeros((HIDDEN,), jnp.float32), 'wg': jax.random.normal(ks[1], (HIDDEN, EXPERTS), jnp.float32) * s, 'inter_w': jax.random.normal(ks[2], (EXPERTS, HIDDEN, INTER), jnp.float32) * s, 'inter_b': jnp.zeros((EXPERTS, INTER), jnp.float32), 'output_w': jax.random.normal(ks[3], (EXPERTS, INTER, HIDDEN), jnp.float32) * s, 'output_b': jnp.zeros((EXPERTS, HIDDEN), jnp.float32), 'res_inter_w': jax.random.normal(ks[4], (HIDDEN, INTER), jnp.float32) * s, 'res_inter_b': jnp.zeros((INTER,), jnp.float32), 'res_output_w': jax.random.normal(ks[5], (INTER, HIDDEN), jnp.float32) * s, 'res_output_b': jnp.zeros((HIDDEN,), jnp.float32), 'res_coef': jax.random.normal(ks[6], (HIDDEN, 2), jnp.float32) * s}
    _L3_ffn_in = _L3_ffn_setup()
    _d = {'L0_attn_x': _L0_attn_in['x'], 'L0_attn_Wq': _L0_attn_in['Wq'], 'L0_attn_bq': _L0_attn_in['bq'], 'L0_attn_Wk': _L0_attn_in['Wk'], 'L0_attn_bk': _L0_attn_in['bk'], 'L0_attn_Wv': _L0_attn_in['Wv'], 'L0_attn_bv': _L0_attn_in['bv'], 'L0_attn_q_conv': _L0_attn_in['q_conv'], 'L0_attn_k_conv': _L0_attn_in['k_conv'], 'L0_attn_v_conv': _L0_attn_in['v_conv'], 'L0_attn_Wa': _L0_attn_in['Wa'], 'L0_attn_ba': _L0_attn_in['ba'], 'L0_attn_Wb': _L0_attn_in['Wb'], 'L0_attn_bb': _L0_attn_in['bb'], 'L0_attn_Wg': _L0_attn_in['Wg'], 'L0_attn_bg': _L0_attn_in['bg'], 'L0_attn_gn_scale': _L0_attn_in['gn_scale'], 'L0_attn_gn_bias': _L0_attn_in['gn_bias'], 'L0_attn_Wo': _L0_attn_in['Wo'], 'L0_attn_bo': _L0_attn_in['bo'], 'L0_ffn_Wr1': _L0_ffn_in['Wr1'], 'L0_ffn_br1': _L0_ffn_in['br1'], 'L0_ffn_ln_scale': _L0_ffn_in['ln_scale'], 'L0_ffn_ln_bias': _L0_ffn_in['ln_bias'], 'L0_ffn_Wr2': _L0_ffn_in['Wr2'], 'L0_ffn_br2': _L0_ffn_in['br2'], 'L0_ffn_W1': _L0_ffn_in['W1'], 'L0_ffn_b1': _L0_ffn_in['b1'], 'L0_ffn_W2': _L0_ffn_in['W2'], 'L0_ffn_b2': _L0_ffn_in['b2'], 'L1_attn_ln1_scale': _L1_attn_in['ln1_scale'], 'L1_attn_ln1_bias': _L1_attn_in['ln1_bias'], 'L1_attn_Wq': _L1_attn_in['Wq'], 'L1_attn_bq': _L1_attn_in['bq'], 'L1_attn_Wk': _L1_attn_in['Wk'], 'L1_attn_bk': _L1_attn_in['bk'], 'L1_attn_Wv': _L1_attn_in['Wv'], 'L1_attn_bv': _L1_attn_in['bv'], 'L1_attn_Wo': _L1_attn_in['Wo'], 'L1_attn_bo': _L1_attn_in['bo'], 'L1_attn_ln2_scale': _L1_attn_in['ln2_scale'], 'L1_attn_ln2_bias': _L1_attn_in['ln2_bias'], 'L1_attn_W1': _L1_attn_in['W1'], 'L1_attn_b1': _L1_attn_in['b1'], 'L1_attn_W2': _L1_attn_in['W2'], 'L1_attn_b2': _L1_attn_in['b2'], 'L1_ffn_Win': _L1_ffn_in['Win'], 'L1_ffn_bin_': _L1_ffn_in['bin_'], 'L1_ffn_W1': _L1_ffn_in['W1'], 'L1_ffn_b1': _L1_ffn_in['b1'], 'L1_ffn_W2': _L1_ffn_in['W2'], 'L1_ffn_b2': _L1_ffn_in['b2'], 'L1_ffn_Wout': _L1_ffn_in['Wout'], 'L1_ffn_bout': _L1_ffn_in['bout'], 'L2_attn_wq': _L2_attn_in['wq'], 'L2_attn_wk': _L2_attn_in['wk'], 'L2_attn_wv': _L2_attn_in['wv'], 'L2_attn_wgq': _L2_attn_in['wgq'], 'L2_attn_wgk': _L2_attn_in['wgk'], 'L2_attn_wgv': _L2_attn_in['wgv'], 'L2_attn_r_out_w': _L2_attn_in['r_out_w'], 'L2_attn_gate_local_w': _L2_attn_in['gate_local_w'], 'L2_attn_gate_remote_w': _L2_attn_in['gate_remote_w'], 'L2_attn_w_out': _L2_attn_in['w_out'], 'L2_ffn_W_r': _L2_ffn_in['W_r'], 'L2_ffn_W_k': _L2_ffn_in['W_k'], 'L2_ffn_W_v': _L2_ffn_in['W_v'], 'L2_ffn_mu_r': _L2_ffn_in['mu_r'], 'L2_ffn_mu_k': _L2_ffn_in['mu_k'], 'L3_attn_Wq': _L3_attn_in['Wq'], 'L3_attn_Wkv': _L3_attn_in['Wkv'], 'L3_attn_Wo': _L3_attn_in['Wo'], 'L3_attn_bo': _L3_attn_in['bo'], 'L3_ffn_attn_nw': _L3_ffn_in['attn_nw'], 'L3_ffn_attn_nb': _L3_ffn_in['attn_nb'], 'L3_ffn_wg': _L3_ffn_in['wg'], 'L3_ffn_inter_w': _L3_ffn_in['inter_w'], 'L3_ffn_inter_b': _L3_ffn_in['inter_b'], 'L3_ffn_output_w': _L3_ffn_in['output_w'], 'L3_ffn_output_b': _L3_ffn_in['output_b'], 'L3_ffn_res_inter_w': _L3_ffn_in['res_inter_w'], 'L3_ffn_res_inter_b': _L3_ffn_in['res_inter_b'], 'L3_ffn_res_output_w': _L3_ffn_in['res_output_w'], 'L3_ffn_res_output_b': _L3_ffn_in['res_output_b'], 'L3_ffn_res_coef': _L3_ffn_in['res_coef']}
    _x0 = _d['L0_attn_x']
    _d['L0_attn_x'] = jax.random.normal(jax.random.fold_in(jax.random.key(seed), 1), (1, 2048, 128), dtype=_x0.dtype)
    del _x0
    return _d

def reference(L0_attn_x, L0_attn_Wq, L0_attn_bq, L0_attn_Wk, L0_attn_bk, L0_attn_Wv, L0_attn_bv, L0_attn_q_conv, L0_attn_k_conv, L0_attn_v_conv, L0_attn_Wa, L0_attn_ba, L0_attn_Wb, L0_attn_bb, L0_attn_Wg, L0_attn_bg, L0_attn_gn_scale, L0_attn_gn_bias, L0_attn_Wo, L0_attn_bo, L0_ffn_Wr1, L0_ffn_br1, L0_ffn_ln_scale, L0_ffn_ln_bias, L0_ffn_Wr2, L0_ffn_br2, L0_ffn_W1, L0_ffn_b1, L0_ffn_W2, L0_ffn_b2, L1_attn_ln1_scale, L1_attn_ln1_bias, L1_attn_Wq, L1_attn_bq, L1_attn_Wk, L1_attn_bk, L1_attn_Wv, L1_attn_bv, L1_attn_Wo, L1_attn_bo, L1_attn_ln2_scale, L1_attn_ln2_bias, L1_attn_W1, L1_attn_b1, L1_attn_W2, L1_attn_b2, L1_ffn_Win, L1_ffn_bin_, L1_ffn_W1, L1_ffn_b1, L1_ffn_W2, L1_ffn_b2, L1_ffn_Wout, L1_ffn_bout, L2_attn_wq, L2_attn_wk, L2_attn_wv, L2_attn_wgq, L2_attn_wgk, L2_attn_wgv, L2_attn_r_out_w, L2_attn_gate_local_w, L2_attn_gate_remote_w, L2_attn_w_out, L2_ffn_W_r, L2_ffn_W_k, L2_ffn_W_v, L2_ffn_mu_r, L2_ffn_mu_k, L3_attn_Wq, L3_attn_Wkv, L3_attn_Wo, L3_attn_bo, L3_ffn_attn_nw, L3_ffn_attn_nb, L3_ffn_wg, L3_ffn_inter_w, L3_ffn_inter_b, L3_ffn_output_w, L3_ffn_output_b, L3_ffn_res_inter_w, L3_ffn_res_inter_b, L3_ffn_res_output_w, L3_ffn_res_output_b, L3_ffn_res_coef):

    def _L0_attn_ref(x, Wq, bq, Wk, bk, Wv, bv, q_conv, k_conv, v_conv, Wa, ba, Wb, bb, Wg, bg, gn_scale, gn_bias, Wo, bo):
        import jax, jax.numpy as jnp
        import numpy as np
        N_HIDDEN = 128
        N_HEADS = 16
        HEAD_DIM = N_HIDDEN // N_HEADS
        KERNEL = 4
        GN_EPS = 1e-05

        def _short_conv_1d(x, weight):
            F, K = weight.shape
            xp = jnp.pad(x, ((0, 0), (K - 1, 0), (0, 0)))
            shifts = jnp.stack([xp[:, i:i + x.shape[1], :] for i in range(K)], axis=-1)
            return jnp.sum(shifts * weight[None, None, :, :], axis=-1)
        B, S, _ = x.shape
        h, d = (N_HEADS, HEAD_DIM)
        q = jax.nn.silu(_short_conv_1d(x @ Wq + bq, q_conv)).reshape(B, S, h, d)
        q = q / (jnp.linalg.norm(q, axis=-1, keepdims=True) + 1e-06)
        k = jax.nn.silu(_short_conv_1d(x @ Wk + bk, k_conv)).reshape(B, S, h, d)
        k = k / (jnp.linalg.norm(k, axis=-1, keepdims=True) + 1e-06)
        v = jax.nn.silu(_short_conv_1d(x @ Wv + bv, v_conv)).reshape(B, S, h, d)
        alpha = jax.nn.sigmoid(x @ Wa + ba)
        beta = jax.nn.sigmoid(x @ Wb + bb)
        out_gate = jax.nn.silu(x @ Wg + bg)
        qT = jnp.transpose(q, (1, 0, 2, 3))
        kT = jnp.transpose(k, (1, 0, 2, 3))
        vT = jnp.transpose(v, (1, 0, 2, 3))
        aT = jnp.transpose(alpha, (1, 0, 2))
        bT = jnp.transpose(beta, (1, 0, 2))

        def _step(Sst, inputs):
            q_t, k_t, v_t, a_t, b_t = inputs
            a = a_t[:, :, None, None]
            b = b_t[:, :, None, None]
            Sk = jnp.einsum('bhde,bhe->bhd', Sst, k_t)
            delta_gated = v_t - a_t[:, :, None] * Sk
            update = b * jnp.einsum('bhd,bhe->bhde', delta_gated, k_t)
            Sst = a * Sst + update
            o_t = jnp.einsum('bhde,bhe->bhd', Sst, q_t)
            return (Sst, o_t)
        S0 = jnp.zeros((B, h, d, d), dtype=x.dtype)
        _, outs = jax.lax.scan(_step, S0, (qT, kT, vT, aT, bT))
        outs = jnp.transpose(outs, (1, 0, 2, 3)).reshape(B, S, N_HIDDEN)
        g = outs.reshape(B, S, h, d)
        mu = jnp.mean(g, axis=(1, 3), keepdims=True)
        var = jnp.mean(jnp.square(g), axis=(1, 3), keepdims=True) - jnp.square(mu)
        g = (g - mu) * jax.lax.rsqrt(var + GN_EPS)
        y = g.reshape(B, S, N_HIDDEN) * gn_scale + gn_bias
        return out_gate * y @ Wo + bo

    def _L0_ffn_ref(x, Wr1, br1, ln_scale, ln_bias, Wr2, br2, W1, b1, W2, b2):
        import jax, jax.numpy as jnp
        import numpy as np
        SQRT_2_PI = 0.7978845608028654
        GELU_COEF = 0.044715
        LN_EPS = 1e-06
        TOP_K = 2

        def gelu_kernel(x):
            inner = SQRT_2_PI * (x + GELU_COEF * x ** 3)
            return 0.5 * x * (1.0 + jnp.tanh(inner))
        E = W1.shape[0]
        h = jnp.einsum('bsd,dk->bsk', x, Wr1) + br1
        mu = jnp.mean(h, axis=-1, keepdims=True)
        var = jnp.mean((h - mu) ** 2, axis=-1, keepdims=True)
        h = (h - mu) * jax.lax.rsqrt(var + LN_EPS) * ln_scale + ln_bias
        h = gelu_kernel(h)
        router_logits = jnp.einsum('bsk,ke->bse', h, Wr2) + br2
        routing_probs = jax.nn.softmax(router_logits, axis=-1)
        top_k_probs, top_k_indices = jax.lax.top_k(routing_probs, TOP_K)
        top_k_probs = top_k_probs / jnp.sum(top_k_probs, axis=-1, keepdims=True)
        expert_mask = jnp.sum(jax.nn.one_hot(top_k_indices, E, dtype=x.dtype) * top_k_probs[..., None], axis=-2)
        output = jnp.zeros_like(x)
        for e in range(E):
            x12 = jnp.einsum('bsd,df->bsf', x, W1[e]) + b1[e]
            x1, x2 = jnp.split(x12, 2, axis=-1)
            g = x1 * gelu_kernel(x2)
            y = jnp.einsum('bsf,fd->bsd', g, W2[e]) + b2[e]
            output = output + y * expert_mask[:, :, e][:, :, None]
        return output

    def _L1_attn_ref(inputs, ln1_scale, ln1_bias, Wq, bq, Wk, bk, Wv, bv, Wo, bo, ln2_scale, ln2_bias, W1, b1, W2, b2):
        import jax, jax.numpy as jnp
        import numpy as np
        B, S, D, H, MLP = (4, 512, 128, 16, 512)
        HD = D // H
        KEPS = 0.001
        LNEPS = 1e-06

        def _ln(x, scale, bias):
            mu = jnp.mean(x, axis=-1, keepdims=True)
            var = jnp.var(x, axis=-1, keepdims=True)
            return (x - mu) * jax.lax.rsqrt(var + LNEPS) * scale + bias
        x = _ln(inputs, ln1_scale, ln1_bias)
        q = jnp.einsum('bsd,dhm->bshm', x, Wq) + bq
        k = jnp.einsum('bsd,dhm->bshm', x, Wk) + bk
        v = jnp.einsum('bsd,dhm->bshm', x, Wv) + bv
        phi_q = jax.nn.relu(q) + KEPS
        phi_k = jax.nn.relu(k) + KEPS
        kv = jnp.einsum('bshm,bshd->bhmd', phi_k, v)
        num = jnp.einsum('bshm,bhmd->bshd', phi_q, kv)
        ksum = jnp.sum(phi_k, axis=1)
        den = jnp.einsum('bshm,bhm->bsh', phi_q, ksum)
        attn = num / den[..., None]
        x_res = inputs + (jnp.einsum('bshm,hmd->bsd', attn, Wo) + bo)
        y = _ln(x_res, ln2_scale, ln2_bias)
        y = jax.nn.gelu(jnp.einsum('bsd,df->bsf', y, W1) + b1)
        y = jnp.einsum('bsf,fd->bsd', y, W2) + b2
        return x_res + y

    def _L1_ffn_ref(x, Win, bin_, W1, b1, W2, b2, Wout, bout):
        import jax, jax.numpy as jnp
        import numpy as np
        D_MODEL = 128
        M = 64
        INNER = 16
        s = jnp.einsum('btd,dm->btm', x, Win) + bin_
        h = jax.nn.relu(s[..., None] * W1 + b1)
        g = jnp.einsum('btmh,mh->btm', h, W2) + b2
        out = jnp.einsum('btm,md->btd', g, Wout) + bout
        return out

    def _L2_attn_ref(x, wq, wk, wv, wgq, wgk, wgv, r_out_w, gate_local_w, gate_remote_w, w_out):
        import jax, jax.numpy as jnp
        import numpy as np
        D_MODEL = 128
        N_HEADS = 16
        LATENT_HEADS = 8
        LATENT_DIM = 64
        N_LATENTS = 64
        WINDOW = 32
        HEAD_DIM = D_MODEL // N_HEADS
        LAT_HD = LATENT_DIM // LATENT_HEADS
        B, S = (2, 512)

        def _pool_to_latents(x):
            Bx, Sx, C = x.shape
            chunk = max(1, Sx // N_LATENTS)
            return x.reshape(Bx, N_LATENTS, chunk, C).mean(axis=2)

        def _local_window_attn(Q, K, V):
            Bx, H, Sx, D = Q.shape
            W = WINDOW
            nb = Sx // W
            Qb = Q.reshape(Bx, H, nb, W, D)
            Kp = jnp.pad(K, ((0, 0), (0, 0), (W, 0), (0, 0))).reshape(Bx, H, nb + 1, W, D)
            Vp = jnp.pad(V, ((0, 0), (0, 0), (W, 0), (0, 0))).reshape(Bx, H, nb + 1, W, D)
            Kw = jnp.concatenate([Kp[:, :, :-1], Kp[:, :, 1:]], axis=3)
            Vw = jnp.concatenate([Vp[:, :, :-1], Vp[:, :, 1:]], axis=3)
            i = jnp.arange(W)[:, None]
            j = jnp.arange(2 * W)[None, :]
            base = (j > i) & (j <= i + W)
            blk0 = (jnp.arange(nb) > 0)[:, None, None] | (j >= W)[None, :, :]
            mask = base[None, :, :] & blk0
            sc = jnp.einsum('bhnid,bhnjd->bhnij', Qb, Kw) / np.sqrt(D).astype(np.float32)
            sc = jnp.where(mask[None, None], sc, -jnp.inf)
            p = jax.nn.softmax(sc, axis=-1)
            out = jnp.einsum('bhnij,bhnjd->bhnid', p, Vw)
            return out.reshape(Bx, H, Sx, D)
        Bx, Sx, _ = x.shape
        chunk = max(1, Sx // N_LATENTS)
        Q = (x @ wq).reshape(Bx, Sx, N_HEADS, HEAD_DIM).transpose(0, 2, 1, 3)
        K = (x @ wk).reshape(Bx, Sx, N_HEADS, HEAD_DIM).transpose(0, 2, 1, 3)
        V = (x @ wv).reshape(Bx, Sx, N_HEADS, HEAD_DIM).transpose(0, 2, 1, 3)
        local = _local_window_attn(Q, K, V)
        GQ = (x @ wgq).reshape(Bx, Sx, LATENT_HEADS, LAT_HD).transpose(0, 2, 1, 3)
        GK = _pool_to_latents(x @ wgk).reshape(Bx, N_LATENTS, LATENT_HEADS, LAT_HD).transpose(0, 2, 1, 3)
        GV = _pool_to_latents(x @ wgv).reshape(Bx, N_LATENTS, LATENT_HEADS, LAT_HD).transpose(0, 2, 1, 3)
        lsc = jnp.einsum('bhsd,bhnd->bhsn', GQ, GK) / np.sqrt(LAT_HD).astype(np.float32)
        lmask = jnp.arange(N_LATENTS)[None, :] <= (jnp.arange(Sx) // chunk)[:, None]
        lsc = jnp.where(lmask[None, None], lsc, -jnp.inf)
        lp = jax.nn.softmax(lsc, axis=-1)
        rem = jnp.einsum('bhsn,bhnd->bhsd', lp, GV)
        rem = rem.transpose(0, 2, 1, 3).reshape(Bx, Sx, LATENT_DIM) @ r_out_w
        rem = rem.reshape(Bx, Sx, N_HEADS, HEAD_DIM).transpose(0, 2, 1, 3)
        gl = jax.nn.sigmoid(jnp.einsum('bhsd,hd->bhs', Q, gate_local_w))[..., None]
        gr = jax.nn.sigmoid(jnp.einsum('bhsd,hd->bhs', Q, gate_remote_w))[..., None]
        out = gl * local + gr * rem
        out = out.transpose(0, 2, 1, 3).reshape(Bx, Sx, D_MODEL)
        return out @ w_out

    def _L2_ffn_ref(x, W_r, W_k, W_v, mu_r, mu_k):
        import jax, jax.numpy as jnp
        import numpy as np
        DIM = 128

        def _reference_tuple_inner(x, W_r, W_k, W_v, mu_r, mu_k):
            B, T, C = x.shape
            x_prev = jnp.concatenate([jnp.zeros((B, 1, C), x.dtype), x[:, :-1, :]], axis=1)
            xr = mu_r * x + (1.0 - mu_r) * x_prev
            xk = mu_k * x + (1.0 - mu_k) * x_prev
            r = jax.nn.sigmoid(jnp.einsum('btc,dc->btd', xr, W_r))
            k = jnp.einsum('btc,dc->btd', xk, W_k)
            k_act = jnp.square(jax.nn.relu(k))
            out = r * jnp.einsum('btc,dc->btd', k_act, W_v)
            new_state = x[:, -1, :]
            return (out, new_state)
        return _reference_tuple_inner(x, W_r, W_k, W_v, mu_r, mu_k)[0]

    def _L3_attn_ref(x, Wq, Wkv, Wo, bo):
        import jax, jax.numpy as jnp
        import numpy as np
        HEADS = 16
        DIM_HEAD = 64
        EPS = 1e-08
        B, N, D = x.shape
        H, Dh = (HEADS, DIM_HEAD)
        scale = Dh ** (-0.5)
        q = (x @ Wq).reshape(B, N, H, Dh).transpose(0, 2, 1, 3)
        kv = x @ Wkv
        k = kv[..., :H * Dh].reshape(B, N, H, Dh).transpose(0, 2, 1, 3)
        v = kv[..., H * Dh:].reshape(B, N, H, Dh).transpose(0, 2, 1, 3)
        s = jnp.einsum('bhid,bhjd->bhij', q * scale, k)
        gm = jax.lax.stop_gradient(jnp.max(s, axis=-1, keepdims=True))
        causal_mask = jnp.triu(jnp.ones((N, N), bool), 1)
        p = jnp.where(causal_mask, 0.0, jnp.exp(s - gm))
        num = jnp.einsum('bhij,bhjd->bhid', p, v)
        out = num / (jnp.sum(p, axis=-1, keepdims=True) + EPS)
        out = out.transpose(0, 2, 1, 3).reshape(B, N, H * Dh)
        return out @ Wo + bo

    def _L3_ffn_ref(x, attn_nw, attn_nb, wg, inter_w, inter_b, output_w, output_b, res_inter_w, res_inter_b, res_output_w, res_output_b, res_coef):
        import math
        import jax, jax.numpy as jnp
        import numpy as np
        HIDDEN = 128
        INTER = 512
        EXPERTS = 8
        B, T = (4, 256)
        EPS = 1e-12
        CAP_FACTOR = 1.0
        MIN_CAP = 4

        def layer_norm(x, g, b, eps=EPS):
            m = jnp.mean(x, axis=-1, keepdims=True)
            v = jnp.var(x, axis=-1, keepdims=True)
            return (x - m) * jax.lax.rsqrt(v + eps) * g + b

        def top1_gate(x, wg, capacity):
            logits = x @ wg
            gates = jax.nn.softmax(logits, axis=-1)
            E = wg.shape[-1]
            idx = jnp.argmax(gates, axis=-1)
            mask1 = jax.nn.one_hot(idx, E, dtype=gates.dtype)
            locations = jnp.cumsum(mask1, axis=0) - mask1
            mask1 = mask1 * (locations < capacity).astype(gates.dtype)
            gates1_s = jnp.sum(gates * mask1, axis=-1)
            loc_s = jnp.sum(locations * mask1, axis=-1).astype(jnp.int32)
            loc_oh = jax.nn.one_hot(loc_s, capacity, dtype=gates.dtype)
            combine = gates1_s[:, None, None] * mask1[:, :, None] * loc_oh[:, None, :]
            dispatch = jax.lax.stop_gradient((combine > 0).astype(x.dtype))
            return (combine, dispatch)
        Bx, Tx, M = x.shape
        S = Bx * Tx
        E = wg.shape[-1]
        capacity = max(MIN_CAP, math.ceil(S / E * CAP_FACTOR))
        residual = x.reshape(S, M)
        attn_out = layer_norm(residual, attn_nw, attn_nb)
        combine, dispatch = top1_gate(attn_out, wg, capacity)
        dispatched = jnp.einsum('sec,sm->ecm', dispatch, attn_out)
        h = jax.nn.gelu(jnp.einsum('ecm,emi->eci', dispatched, inter_w) + inter_b[:, None, :], approximate=True)
        expert_out = jnp.einsum('eci,eim->ecm', h, output_w) + output_b[:, None, :]
        moe_out = jnp.einsum('sec,ecm->sm', combine, expert_out)
        rh = jax.nn.gelu(attn_out @ res_inter_w + res_inter_b, approximate=True)
        res_mlp_out = rh @ res_output_w + res_output_b
        coef = jax.nn.softmax(attn_out @ res_coef, axis=-1)
        out = res_mlp_out * coef[:, :1] + moe_out * coef[:, 1:]
        out = out + residual
        return out.reshape(Bx, Tx, M)
    x = L0_attn_x
    xn = _layernorm(x, axis=-1)
    x = x + _L0_attn_ref(xn, L0_attn_Wq, L0_attn_bq, L0_attn_Wk, L0_attn_bk, L0_attn_Wv, L0_attn_bv, L0_attn_q_conv, L0_attn_k_conv, L0_attn_v_conv, L0_attn_Wa, L0_attn_ba, L0_attn_Wb, L0_attn_bb, L0_attn_Wg, L0_attn_bg, L0_attn_gn_scale, L0_attn_gn_bias, L0_attn_Wo, L0_attn_bo) + _L0_ffn_ref(xn, L0_ffn_Wr1, L0_ffn_br1, L0_ffn_ln_scale, L0_ffn_ln_bias, L0_ffn_Wr2, L0_ffn_br2, L0_ffn_W1, L0_ffn_b1, L0_ffn_W2, L0_ffn_b2)
    xn = _layernorm(x, axis=-1)
    x = x + _L1_attn_ref(xn, L1_attn_ln1_scale, L1_attn_ln1_bias, L1_attn_Wq, L1_attn_bq, L1_attn_Wk, L1_attn_bk, L1_attn_Wv, L1_attn_bv, L1_attn_Wo, L1_attn_bo, L1_attn_ln2_scale, L1_attn_ln2_bias, L1_attn_W1, L1_attn_b1, L1_attn_W2, L1_attn_b2) + _L1_ffn_ref(xn, L1_ffn_Win, L1_ffn_bin_, L1_ffn_W1, L1_ffn_b1, L1_ffn_W2, L1_ffn_b2, L1_ffn_Wout, L1_ffn_bout)
    xn = _layernorm(x, axis=-1)
    x = x + _L2_attn_ref(xn, L2_attn_wq, L2_attn_wk, L2_attn_wv, L2_attn_wgq, L2_attn_wgk, L2_attn_wgv, L2_attn_r_out_w, L2_attn_gate_local_w, L2_attn_gate_remote_w, L2_attn_w_out) + _L2_ffn_ref(xn, L2_ffn_W_r, L2_ffn_W_k, L2_ffn_W_v, L2_ffn_mu_r, L2_ffn_mu_k)
    xn = _layernorm(x, axis=-1)
    x = x + _L3_attn_ref(xn, L3_attn_Wq, L3_attn_Wkv, L3_attn_Wo, L3_attn_bo) + _L3_ffn_ref(xn, L3_ffn_attn_nw, L3_ffn_attn_nb, L3_ffn_wg, L3_ffn_inter_w, L3_ffn_inter_b, L3_ffn_output_w, L3_ffn_output_b, L3_ffn_res_inter_w, L3_ffn_res_inter_b, L3_ffn_res_output_w, L3_ffn_res_output_b, L3_ffn_res_coef)
    return x

_drawn_inputs = setup_inputs


def setup_inputs(seed=0):
    import zlib

    import numpy as np

    out = dict(_drawn_inputs(seed))
    spreads = {'L0_attn_bq': (0.0, 0.8),
     'L0_attn_bk': (0.0, 0.8),
     'L0_attn_bv': (0.0, 0.8),
     'L0_attn_ba': (0.0, 0.8),
     'L0_attn_bb': (0.0, 0.8),
     'L0_attn_bg': (0.0, 0.8),
     'L0_attn_gn_scale': (1.0, 0.6),
     'L0_attn_gn_bias': (0.0, 0.8),
     'L0_attn_bo': (0.0, 0.1),
     'L0_ffn_br1': (0.0, 0.1),
     'L0_ffn_ln_scale': (1.0, 0.2),
     'L0_ffn_ln_bias': (0.0, 0.1),
     'L0_ffn_br2': (0.0, 0.1),
     'L0_ffn_b1': (0.0, 0.1),
     'L0_ffn_b2': (0.0, 0.1),
     'L1_attn_ln1_scale': (1.0, 0.6),
     'L1_attn_ln1_bias': (0.0, 0.8),
     'L1_attn_bq': (0.0, 0.8),
     'L1_attn_bk': (0.0, 0.8),
     'L1_attn_bv': (0.0, 0.668),
     'L1_attn_bo': (0.0, 0.1),
     'L1_attn_ln2_scale': (1.0, 0.6),
     'L1_attn_ln2_bias': (0.0, 0.8),
     'L1_attn_b1': (0.0, 0.611),
     'L1_attn_b2': (0.0, 0.1),
     'L3_ffn_attn_nw': (1.0, 0.6),
     'L3_ffn_attn_nb': (0.0, 0.8),
     'L3_ffn_inter_b': (0.0, 0.8),
     'L3_ffn_output_b': (0.0, 0.8),
     'L3_ffn_res_inter_b': (0.0, 0.8),
     'L3_ffn_res_output_b': (0.0, 2.0)}
    factors = {'L0_attn_Wq': 7.988,
     'L0_attn_Wk': 8.0,
     'L0_attn_Wv': 8.0,
     'L0_attn_q_conv': 7.085,
     'L0_attn_k_conv': 6.949,
     'L0_attn_v_conv': 7.059,
     'L0_attn_Wa': 8.0,
     'L0_attn_Wb': 8.0,
     'L0_attn_Wg': 7.626,
     'L0_attn_Wo': 7.129,
     'L1_attn_Wq': 8.0,
     'L1_attn_Wk': 8.0,
     'L1_attn_Wv': 8.0,
     'L1_attn_Wo': 4.348,
     'L1_ffn_bin_': 8.0,
     'L2_attn_wq': 8.0,
     'L2_attn_wk': 8.0,
     'L2_attn_wv': 8.0,
     'L2_attn_wgq': 8.0,
     'L2_attn_wgk': 8.0,
     'L2_attn_wgv': 8.0,
     'L2_attn_r_out_w': 8.0,
     'L2_attn_gate_local_w': 8.0,
     'L2_attn_gate_remote_w': 8.0,
     'L2_attn_w_out': 8.0,
     'L2_ffn_W_r': 6.801,
     'L2_ffn_mu_r': 8.0,
     'L3_attn_bo': 8.0,
     'L3_ffn_wg': 8.0,
     'L3_ffn_inter_w': 8.0,
     'L3_ffn_output_w': 8.0,
     'L3_ffn_res_inter_w': 6.021,
     'L3_ffn_res_output_w': 5.417,
     'L3_ffn_res_coef': 8.0,
     'L3_attn_Wq': 3.891}
    for name, (base, spread) in spreads.items():
        noise = np.random.default_rng([zlib.crc32(name.encode()), seed]).standard_normal(out[name].shape)
        drawn = base * np.exp(spread * noise) if base else spread * noise
        out[name] = jnp.asarray(drawn.astype(out[name].dtype))
    for name, factor in factors.items():
        out[name] = (out[name] * factor).astype(out[name].dtype)
    return out
```

```python
from contextlib import ExitStack, contextmanager

import concourse.bass as bass
from concourse import mybir

F32 = mybir.dt.float32
ALU = mybir.AluOpType
ACT = mybir.ActivationFunctionType
AX = mybir.AxisListType
ds = bass.ds

P = 128
TOK = 2048
CH = 512
NCH = TOK // CH
NT = TOK // P
HEADS, HD = 16, 8
LN_EPS = 1e-5


class Named:
    pass


def sbuf(nc, name, shape):
    return nc.sbuf_tensor(f"{name}_{nc.next_id()}", shape, F32)


def psum(nc, name, shape):
    return nc.psum_tensor(f"{name}_{nc.next_id()}", shape, F32)


def cs(c):
    return slice(c * CH, (c + 1) * CH)


@contextmanager
def stage(nc, *signals):
    sems = [nc.alloc_semaphore(f"{name}_{nc.next_id()}") for name in signals]
    with nc.Block() as block:
        yield (block, *sems)
    nc.clear_and_free_semaphores(sems)
    nc.all_engine_barrier()


VECTORS = {
    "L0_attn_bq": 1, "L0_attn_bk": 1, "L0_attn_bv": 1, "L0_attn_bg": 1, "L0_attn_gn_scale": 1,
    "L0_attn_gn_bias": 1, "L0_attn_bo": 1, "L0_ffn_b1": 64, "L0_ffn_b2": 8,
    "L1_attn_ln1_scale": 1, "L1_attn_ln1_bias": 1, "L1_attn_bq": 1, "L1_attn_bo": 1,
    "L1_attn_ln2_scale": 1, "L1_attn_ln2_bias": 1, "L1_attn_b1": 4, "L1_attn_b2": 1,
    "L1_ffn_b1": 8, "L1_ffn_W1": 8, "L1_ffn_W2": 8, "L1_ffn_bout": 1,
    "L2_ffn_mu_r": 1, "L2_ffn_mu_k": 1, "L2_attn_gate_local_w": 1, "L2_attn_gate_remote_w": 1,
    "L3_attn_bo": 1, "L3_ffn_attn_nw": 1, "L3_ffn_attn_nb": 1, "L3_ffn_inter_b": 32, "L3_ffn_output_b": 8,
    "L3_ffn_res_inter_b": 4, "L3_ffn_res_output_b": 1,
    "L0_ffn_br1": 1, "L0_ffn_ln_scale": 1, "L0_ffn_ln_bias": 1, "L1_ffn_bin_": 1, "L1_ffn_b2": 1,
}
SHORT = {"L0_ffn_br1": 64, "L0_ffn_ln_scale": 64, "L0_ffn_ln_bias": 64, "L1_ffn_bin_": 64, "L1_ffn_b2": 64}


def row_of_vectors():
    at, n = {}, 0
    for name, rows in VECTORS.items():
        if n % P + rows > P:
            n = (n // P + 1) * P
        at[name] = n
        n += rows
    return at, -(-n // P)


def constants(nc, m, inp, alloc):
    at, tiles = row_of_vectors()
    m.at = at
    m.ident = alloc("ident", [P, P])
    m.mean_w = alloc("mean_w", [P, P])
    m.head_ones = alloc("head_ones", [P, P])
    m.pick = alloc("pick", [P, HD, P])
    m.hmod = alloc("hmod", [P, 4])
    m.eye8 = alloc("eye8", [P, HD])
    m.hdiv = alloc("hdiv", [P, 4])
    m.ones = alloc("ones", [P, P])
    m.cols = alloc("cols", [P, tiles * P])
    m.col = lambda name, i=0, n=P: m.cols[0:n, at[name] + i:at[name] + i + 1]
    with ExitStack() as own:
        rows = own.enter_context(sbuf(nc, "vector_rows", [P, tiles, P]))
        turned = own.enter_context(psum(nc, "vectors_turned", [P, tiles, CH]))
        with stage(nc, "rows_zeroed", "ones_set", "shaped", "rows_loaded", "vectors_turned", "cols_ready") as (
                block, rows_zeroed, ones_set, shaped, rows_loaded, vectors_turned, cols_ready):

            @block.gpsimd
            def _(pool):
                for t in (m.ident, m.head_ones, m.pick, m.ones):
                    pool.memset(t[:], 1.0).then_inc(ones_set, 1)
                pool.memset(m.mean_w[:], 1.0 / P).then_inc(ones_set, 1)
                pool.memset(m.hdiv[:], 1.0).then_inc(ones_set, 1)
                pool.wait_ge(ones_set, 6)
                pool.affine_select(out=m.ident[:], in_=m.ident[:], compare_op=ALU.is_equal, fill=0.0, base=0,
                                   pattern=[[-1, P]], channel_multiplier=1).then_inc(shaped, 1)
                pool.affine_select(out=m.pick[:].rearrange("p e (h d) -> p e h d", d=HD),
                                   in_=m.pick[:].rearrange("p e (h d) -> p e h d", d=HD),
                                   compare_op=ALU.is_equal, fill=0.0, base=0,
                                   pattern=[[-1, HD], [-HD, HEADS], [0, HD]], channel_multiplier=1).then_inc(shaped, 1)
                blocks = m.head_ones[:].rearrange("p (h d) -> p h d", d=HD)
                pool.affine_select(out=blocks, in_=blocks, compare_op=ALU.is_ge, fill=0.0, base=0,
                                   pattern=[[-HD, HEADS], [0, HD]], channel_multiplier=1).then_inc(shaped, 1)
                pool.wait_ge(shaped, 3)
                pool.affine_select(out=blocks, in_=blocks, compare_op=ALU.is_ge, fill=0.0, base=HD - 1,
                                   pattern=[[HD, HEADS], [0, HD]], channel_multiplier=-1).then_inc(shaped, 1)
                pool.affine_select(out=m.hdiv[:], in_=m.hdiv[:], compare_op=ALU.is_ge, fill=0.0, base=0,
                                   pattern=[[-32, 4]], channel_multiplier=1).then_inc(shaped, 1)
                pool.wait_ge(shaped, 5)
                pool.affine_select(out=m.hdiv[:], in_=m.hdiv[:], compare_op=ALU.is_ge, fill=0.0, base=31,
                                   pattern=[[32, 4]], channel_multiplier=-1).then_inc(shaped, 1)

            @block.sync
            def _(sp):
                sp.wait_ge(rows_zeroed, 1)
                n = 0
                for name, k in VECTORS.items():
                    tile, r = divmod(at[name], P)
                    src = inp[name]
                    if len(src.shape) == 2:
                        src = src.rearrange("a b -> (a b)")
                    w = SHORT.get(name, P)
                    sp.dma_start(rows[r:r + k, tile, 0:w], src.rearrange("(r c) -> r c", c=w)).then_inc(rows_loaded, 16)
                    n += 1
                m.n_vector_loads = n

            @block.vector
            def _(dve):
                dve.memset(rows[:], 0.0).then_inc(rows_zeroed, 1)
                for t in range(tiles):
                    dve.wait_ge(vectors_turned, t + 1)
                    dve.tensor_copy(m.cols[:, t * P:(t + 1) * P], turned[:, t, 0:P]).then_inc(cols_ready, 1)
                dve.wait_ge(shaped, 6)
                dve.tensor_reduce(m.hmod[:], m.head_ones[:].rearrange("p (g i d) -> p i g d", g=4, i=4)[:, :, :, 0],
                                  AX.X, ALU.max).then_inc(cols_ready, 1)
                dve.tensor_reduce(m.eye8[:], m.ident[:].rearrange("p (h e) -> p e h", e=HD),
                                  AX.X, ALU.max).then_inc(cols_ready, 1)

            @block.tensor
            def _(pe):
                pe.wait_ge(shaped, 6)
                pe.wait_ge(rows_loaded, 16 * m.n_vector_loads)
                for t in range(tiles):
                    pe.transpose(turned[:, t, 0:P], rows[:, t, :], m.ident[:]).then_inc(vectors_turned, 1)


def turn_in(nc, m, x_dram):
    with ExitStack() as own:
        xtm = own.enter_context(sbuf(nc, "x_token_major", [P, NT, P]))
        ps = own.enter_context(psum(nc, "x_turned", [P, NCH, CH]))
        with stage(nc, "x_loaded", "x_turned", "xT_ready") as (block, x_loaded, x_turned, xT_ready):
            @block.sync
            def _(sp):
                sp.dma_start(xtm[:], x_dram.rearrange("b (n p) f -> p (b n) f", p=P)).then_inc(x_loaded, 16)

            @block.tensor
            def _(pe):
                pe.wait_ge(x_loaded, 16)
                for n in range(NT):
                    c, k = divmod(n, CH // P)
                    pe.transpose(ps[:, c, k * P:(k + 1) * P], xtm[:, n, :], m.ident[:]).then_inc(x_turned, 1)

            @block.vector
            def _(dve):
                for c in range(NCH):
                    dve.wait_ge(x_turned, (c + 1) * (CH // P))
                    dve.tensor_copy(m.x[:, cs(c)], ps[:, c, :]).then_inc(xT_ready, 1)


def turn_out(nc, m, out_dram):
    with ExitStack() as own:
        xtm = own.enter_context(sbuf(nc, "y_token_major", [P, NT, P]))
        ps = own.enter_context(psum(nc, "y_turned", [P, NCH, CH]))
        with stage(nc, "y_turned", "y_copied", "y_stored") as (block, y_turned, y_copied, y_stored):
            @block.tensor
            def _(pe):
                for n in range(NT):
                    c, k = divmod(n, CH // P)
                    pe.transpose(ps[:, c, k * P:(k + 1) * P], m.x[:, n * P:(n + 1) * P], m.ident[:]).then_inc(y_turned, 1)

            @block.vector
            def _(dve):
                for c in range(NCH):
                    dve.wait_ge(y_turned, (c + 1) * (CH // P))
                    dve.tensor_copy(xtm[:, 4 * c:4 * c + 4, :], ps[:, c, :].rearrange("p (n f) -> p n f", f=P))\
                       .then_inc(y_copied, 1)

            @block.sync
            def _(sp):
                out = out_dram.rearrange("b (n p) f -> p (b n) f", p=P)
                for c in range(NCH):
                    sp.wait_ge(y_copied, c + 1)
                    sp.dma_start(out[:, 4 * c:4 * c + 4, :], xtm[:, 4 * c:4 * c + 4, :]).then_inc(y_stored, 16)
                sp.wait_ge(y_stored, 16 * NCH)


def layernorm(nc, m, src, dst, eps, width=P, scale=None, bias=None, after=None):
    w = slice(0, width)
    with ExitStack() as own:
        mean = own.enter_context(psum(nc, "ln_mean", [P, NCH, CH]))
        var = own.enter_context(psum(nc, "ln_var", [P, NCH, CH]))
        cen = own.enter_context(sbuf(nc, "ln_centered", [P, TOK]))
        work = own.enter_context(sbuf(nc, "ln_work", [P, TOK]))
        epst = own.enter_context(sbuf(nc, "ln_eps", [P, 1]))
        with stage(nc, "eps_set", "mean_ready", "centered", "squared", "var_ready", "std_ready", "inverted", "normed",
                   "scaled", "activated") as (
                block, eps_set, mean_ready, centered, squared, var_ready, std_ready, inverted, normed, scaled, activated):
            @block.tensor
            def _(pe):
                for c in range(NCH):
                    pe.matmul(mean[w, c, :], m.mean_w[w, w], src[w, cs(c)], start=True, stop=True).then_inc(mean_ready, 1)
                for c in range(NCH):
                    pe.wait_ge(squared, c + 1)
                    pe.matmul(var[w, c, :], m.mean_w[w, w], work[w, cs(c)], start=True, stop=True).then_inc(var_ready, 1)

            @block.scalar
            def _(act):
                act.wait_ge(eps_set, 1)
                for c in range(NCH):
                    act.wait_ge(centered, c + 1)
                    act.activation(work[w, cs(c)], cen[w, cs(c)], ACT.Square).then_inc(squared, 1)
                for c in range(NCH):
                    act.wait_ge(var_ready, c + 1)
                    act.activation(work[w, cs(c)], var[w, c, :], ACT.Sqrt, bias=epst[w, :], scale=float(P // width))\
                       .then_inc(std_ready, 1)
                if after is not None:
                    for c in range(NCH):
                        act.wait_ge(scaled, c + 1)
                        act.activation(dst[w, cs(c)], dst[w, cs(c)], after).then_inc(activated, 1)

            @block.vector
            def _(dve):
                dve.memset(epst[:], eps).then_inc(eps_set, 1)
                for c in range(NCH):
                    dve.wait_ge(mean_ready, c + 1)
                    dve.scalar_tensor_tensor(out=cen[w, cs(c)], in0=mean[w, c, :], scalar=-float(P // width),
                                             in1=src[w, cs(c)], op0=ALU.mult, op1=ALU.add).then_inc(centered, 1)
                for c in range(NCH):
                    dve.wait_ge(std_ready, c + 1)
                    dve.reciprocal(work[w, cs(c)], work[w, cs(c)]).then_inc(inverted, 1)
                    dve.wait_ge(inverted, c + 1)
                    dve.tensor_tensor(dst[w, cs(c)], cen[w, cs(c)], work[w, cs(c)], ALU.mult).then_inc(normed, 1)
                    if scale is not None:
                        dve.wait_ge(normed, c + 1)
                        dve.tensor_scalar(dst[w, cs(c)], dst[w, cs(c)], scale, bias, ALU.mult, ALU.add)\
                           .then_inc(scaled, 1)


def load_all(nc, loads):
    with stage(nc, "loaded") as (block, loaded):
        @block.sync
        def _(sp):
            for dst, src in loads[0::2]:
                sp.dma_start(dst, src).then_inc(loaded, 16)
            sp.wait_ge(loaded, 16 * len(loads))

        @block.scalar
        def _(act):
            for dst, src in loads[1::2]:
                act.dma_start(dst, src).then_inc(loaded, 16)



SEG = 32
NSEG = TOK // SEG


def l0_project(nc, m, inp, r):
    with ExitStack() as own:
        sb = lambda name, shape: own.enter_context(sbuf(nc, name, shape))
        wqkvg = sb("w_qkvg", [P, 4, P])
        wab = sb("w_ab", [P, 2, HEADS])
        wab_wide = sb("w_ab_wide", [P, 2, P])
        bab, bab_wide, bab_col = sb("b_ab", [1, 2, HEADS]), sb("b_ab_wide", [1, 2, P]), sb("b_ab_col", [P, 2])
        conv = sb("conv_w", [P, 3, 4])
        raw = sb("raw", [P, 2, 3 + TOK])
        load_all(nc, [(wqkvg[:, 0, :], inp["L0_attn_Wq"]), (wqkvg[:, 1, :], inp["L0_attn_Wk"]),
                      (wqkvg[:, 2, :], inp["L0_attn_Wv"]), (wqkvg[:, 3, :], inp["L0_attn_Wg"]),
                      (wab[:, 0, :], inp["L0_attn_Wa"]), (wab[:, 1, :], inp["L0_attn_Wb"]),
                      (bab[:, 0, :], inp["L0_attn_ba"].rearrange("(a h) -> a h", a=1)),
                      (bab[:, 1, :], inp["L0_attn_bb"].rearrange("(a h) -> a h", a=1)),
                      (conv[:, 0, :], inp["L0_attn_q_conv"]), (conv[:, 1, :], inp["L0_attn_k_conv"]),
                      (conv[:, 2, :], inp["L0_attn_v_conv"])])
        ps = own.enter_context(psum(nc, "proj", [P, 2, 4, CH]))
        tmp = sb("tmp", [P, TOK])
        sq = sb("sq", [P, TOK])
        for i, (dst, b) in enumerate(((r.q, "L0_attn_bq"), (r.k, "L0_attn_bk"), (r.bv, "L0_attn_bv"))):
            with stage(nc, "padded", "projected", "biased", "tap", "silued", "squared", "summed", "rooted", "shifted",
                       "inverted", "done") as (
                    block, padded, projected, biased, tap, silued, squared, summed, rooted, shifted, inverted, done):
                x = raw[:, i % 2, :]

                @block.tensor
                def _(pe):
                    for c in range(NCH):
                        pe.matmul(ps[:, 0, c, :], wqkvg[:, i, :], m.xn[:, cs(c)], start=True, stop=True)\
                          .then_inc(projected, 1)
                    if i < 2:
                        for c in range(NCH):
                            pe.wait_ge(squared, c + 1)
                            pe.matmul(ps[:, 1, c, :], m.head_ones[:], sq[:, cs(c)], start=True, stop=True)\
                              .then_inc(summed, 1)

                @block.vector
                def _(dve):
                    dve.memset(x[:, 0:3], 0.0).then_inc(padded, 1)
                    dve.wait_ge(padded, 1)
                    dve.wait_ge(biased, NCH)
                    dve.tensor_scalar(tmp[:], x[:, 0:TOK], conv[:, i, 0:1], None, ALU.mult).then_inc(tap, 1)
                    for j in range(1, 4):
                        dve.wait_ge(tap, j)
                        dve.scalar_tensor_tensor(out=tmp[:], in0=x[:, j:j + TOK], scalar=conv[:, i, j:j + 1], in1=tmp[:],
                                                 op0=ALU.mult, op1=ALU.add).then_inc(tap, 1)
                    if i < 2:
                        for c in range(NCH):
                            dve.wait_ge(rooted, c + 1)
                            dve.tensor_scalar(sq[:, cs(c)], sq[:, cs(c)], 1e-6, None, ALU.add).then_inc(shifted, 1)
                            dve.wait_ge(shifted, c + 1)
                            dve.reciprocal(sq[:, cs(c)], sq[:, cs(c)]).then_inc(inverted, 1)
                            dve.wait_ge(inverted, c + 1)
                            dve.tensor_tensor(dst[:, cs(c)], dst[:, cs(c)], sq[:, cs(c)], ALU.mult).then_inc(done, 1)

                @block.scalar
                def _(act):
                    for c in range(NCH):
                        act.wait_ge(projected, c + 1)
                        act.activation(x[:, 3 + c * CH:3 + (c + 1) * CH], ps[:, 0, c, :], ACT.Identity,
                                       bias=m.col(b)).then_inc(biased, 1)
                    act.wait_ge(tap, 4)
                    for c in range(NCH):
                        act.activation(dst[:, cs(c)], tmp[:, cs(c)], ACT.Silu).then_inc(silued, 1)
                    if i < 2:
                        for c in range(NCH):
                            act.wait_ge(silued, c + 1)
                            act.activation(sq[:, cs(c)], dst[:, cs(c)], ACT.Square).then_inc(squared, 1)
                        for c in range(NCH):
                            act.wait_ge(summed, c + 1)
                            act.activation(sq[:, cs(c)], ps[:, 1, c, :], ACT.Sqrt).then_inc(rooted, 1)
        with stage(nc, "widened", "bias_turned", "bias_ready", "a_logits", "b_logits", "g_logits", "a_ready", "b_ready", "g_ready", "used") as (
                block, widened, bias_turned, bias_ready, a_logits, b_logits, g_logits, a_ready, b_ready, g_ready, used):
            @block.tensor
            def _(pe):
                pe.wait_ge(widened, 4)
                for i in range(2):
                    mm = pe.matmul(ps[:, 0, 0, i:i + 1], bab_wide[:, i, :], m.ones[0:1, 0:1], start=True, stop=True)
                mm.then_inc(bias_turned, 1)
                pe.wait_ge(bias_ready, 1)
                for c in range(NCH):
                    pe.matmul(ps[:, 0, c, :], wab_wide[:, 0, :], m.xn[:, cs(c)], start=True, stop=True).then_inc(a_logits, 1)
                for c in range(NCH):
                    pe.matmul(ps[:, 1, c, :], wab_wide[:, 1, :], m.xn[:, cs(c)], start=True, stop=True).then_inc(b_logits, 1)
                for c in range(NCH):
                    pe.wait_ge(a_ready, c + 1)
                    pe.matmul(ps[:, 0, c, :], wqkvg[:, 3, :], m.xn[:, cs(c)], start=True, stop=True).then_inc(g_logits, 1)

            @block.scalar
            def _(act):
                for c in range(NCH):
                    act.wait_ge(a_logits, c + 1)
                    act.activation(r.a[:, cs(c)], ps[:, 0, c, :], ACT.Sigmoid, bias=bab_col[:, 0:1]).then_inc(a_ready, 1)
                for c in range(NCH):
                    act.wait_ge(b_logits, c + 1)
                    act.activation(tmp[:, cs(c)], ps[:, 1, c, :], ACT.Sigmoid, bias=bab_col[:, 1:2]).then_inc(b_ready, 1)
                for c in range(NCH):
                    act.wait_ge(g_logits, c + 1)
                    act.activation(r.gate[:, cs(c)], ps[:, 0, c, :], ACT.Silu, bias=m.col("L0_attn_bg")).then_inc(g_ready, 1)

            @block.vector
            def _(dve):
                for i in range(2):
                    dve.tensor_copy(wab_wide[:, i, :].rearrange("p (h d) -> p h d", d=HD),
                                    wab[:, i, :].unsqueeze(2).to_broadcast([P, HEADS, HD])).then_inc(widened, 1)
                    dve.tensor_copy(bab_wide[:, i, :].rearrange("p (h d) -> p h d", d=HD),
                                    bab[:, i, :].unsqueeze(2).to_broadcast([1, HEADS, HD])).then_inc(widened, 1)
                dve.wait_ge(bias_turned, 1)
                dve.tensor_copy(bab_col[:], ps[:, 0, 0, 0:2]).then_inc(bias_ready, 1)
                for c in range(NCH):
                    dve.wait_ge(b_ready, c + 1)
                    dve.tensor_tensor(r.bv[:, cs(c)], r.bv[:, cs(c)], tmp[:, cs(c)], ALU.mult).then_inc(used, 1)
                    dve.scalar_tensor_tensor(out=r.nab[:, cs(c)], in0=r.a[:, cs(c)], scalar=-1.0, in1=tmp[:, cs(c)],
                                             op0=ALU.mult, op1=ALU.mult).then_inc(used, 1)


def l0_scan(nc, m, r):
    kT = r.k[:].rearrange("p (j t) -> p t j", t=SEG)
    qT = r.q[:].rearrange("p (j t) -> p t j", t=SEG)
    aT = r.a[:].rearrange("p (j t) -> p t j", t=SEG)
    nabT = r.nab[:].rearrange("p (j t) -> p t j", t=SEG)
    bvT = r.bv[:].rearrange("p (j t) -> p t j", t=SEG)
    woT = r.wo[:].rearrange("p k (j t) -> p k t j", t=SEG)
    FULL = [P, 2, HD, NSEG]
    with ExitStack() as own:
        sb = lambda name, shape: own.enter_context(sbuf(nc, name, shape))
        Zk, Zq, aZ, outer = (sb(n, [P, 2, HD * NSEG]) for n in ("Z_k", "Z_q", "a_Z", "u_k"))
        u = sb("u", [P, 2, NSEG])
        kps = own.enter_context(psum(nc, "k_spread", [P, 2, CH]))
        qps = own.enter_context(psum(nc, "q_spread", [P, 2, CH]))
        Z = r.Z
        ejk = lambda t: t.rearrange("p k (e j) -> p k j e", e=HD)
        with stage(nc, "z_set", "k_spread", "q_spread", "zk_ready", "r_ready", "nabr_ready", "u_ready", "uk_ready",
                   "az_ready", "z_ready", "zq_ready", "wo_ready") as (
                block, z_set, k_spread, q_spread, zk_ready, r_ready, nabr_ready, u_ready, uk_ready, az_ready, z_ready,
                zq_ready, wo_ready):
            @block.tensor
            def _(pe):
                with pe.Fori(0, SEG // 2) as pair:
                    for par in range(2):
                        t = pair * 2 + par
                        pe.wait_ge(uk_ready, t)
                        for e in range(HD):
                            mm = pe.matmul(kps[:, par, e * NSEG:(e + 1) * NSEG], m.pick[:, e, :], kT[:, ds(t, 1), :],
                                           start=True, stop=True)
                        mm.then_inc(k_spread, 1)
                        pe.wait_ge(wo_ready, t)
                        for e in range(HD):
                            mm = pe.matmul(qps[:, par, e * NSEG:(e + 1) * NSEG], m.pick[:, e, :], qT[:, ds(t, 1), :],
                                           start=True, stop=True)
                        mm.then_inc(q_spread, 1)

            @block.gpsimd
            def _(pool):
                pool.wait_ge(z_set, 2)
                with pool.Fori(0, SEG) as t:
                    pool.wait_ge(z_ready, t)
                    pool.tensor_tensor(aZ[:].rearrange("p k (e j) -> p (k e) j", e=HD),
                                       Z[:].rearrange("p k (e j) -> p (k e) j", e=HD),
                                       aT[:, ds(t, 1), :].to_broadcast([P, 2 * HD, NSEG]), ALU.mult).then_inc(az_ready, 1)

            @block.vector
            def _(dve):
                dve.memset(Z[:, 0, :], 0.0).then_inc(z_set, 1)
                dve.tensor_copy(Z[:, 1, :].rearrange("p (e j) -> p e j", e=HD),
                                m.eye8[:].unsqueeze(2).to_broadcast([P, HD, NSEG])).then_inc(z_set, 1)
                dve.wait_ge(z_set, 2)
                with dve.Fori(0, SEG // 2) as pair:
                    for par in range(2):
                        t = pair * 2 + par
                        kb = kps[:, par, :].unsqueeze(1).to_broadcast([P, 2, HD * NSEG])
                        qb = qps[:, par, :].unsqueeze(1).to_broadcast([P, 2, HD * NSEG])
                        dve.wait_ge(k_spread, t + 1)
                        dve.wait_ge(z_ready, t)
                        dve.tensor_tensor(Zk[:], Z[:], kb, ALU.mult).then_inc(zk_ready, 1)
                        dve.wait_ge(zk_ready, t + 1)
                        dve.tensor_reduce(u[:], ejk(Zk[:]), AX.X, ALU.add).then_inc(r_ready, 1)
                        dve.wait_ge(r_ready, t + 1)
                        dve.tensor_tensor(u[:], u[:], nabT[:, ds(t, 1), :].to_broadcast([P, 2, NSEG]), ALU.mult)\
                           .then_inc(nabr_ready, 1)
                        dve.wait_ge(nabr_ready, t + 1)
                        dve.tensor_tensor(u[:, 0:1, :], u[:, 0:1, :], bvT[:, ds(t, 1), :], ALU.add).then_inc(u_ready, 1)
                        dve.wait_ge(u_ready, t + 1)
                        dve.tensor_tensor(outer[:].rearrange("p k (e j) -> p k e j", e=HD),
                                          kb.rearrange("p k (e j) -> p k e j", e=HD),
                                          u[:].unsqueeze(2).to_broadcast(FULL), ALU.mult).then_inc(uk_ready, 1)
                        dve.wait_ge(uk_ready, t + 1)
                        dve.wait_ge(az_ready, t + 1)
                        dve.tensor_tensor(Z[:], aZ[:], outer[:], ALU.add).then_inc(z_ready, 1)
                        dve.wait_ge(q_spread, t + 1)
                        dve.wait_ge(z_ready, t + 1)
                        dve.tensor_tensor(Zq[:], Z[:], qb, ALU.mult).then_inc(zq_ready, 1)
                        dve.wait_ge(zq_ready, t + 1)
                        dve.tensor_reduce(woT[:, :, ds(t, 1), :], ejk(Zq[:]).unsqueeze(2), AX.X, ALU.add)\
                           .then_inc(wo_ready, 1)


def l0_join(nc, m, r):
    with ExitStack() as own:
        sb = lambda name, shape: own.enter_context(sbuf(nc, name, shape))
        T = sb("T", [P, NSEG + 1, HD])
        Pb, Cb, Sb = (sb(n, [P, 2, P]) for n in ("P_blocks", "C_blocks", "S_blocks"))
        nxt = own.enter_context(psum(nc, "T_next", [P, 2, CH]))
        add = own.enter_context(psum(nc, "o_carried", [P, NCH, CH]))
        Zj = r.Z[:].rearrange("p k (e j) -> p k j e", e=HD)
        hb = m.head_ones[:].rearrange("p (h e) -> p h e", e=HD)
        WIDE = [P, HEADS, HD]
        with stage(nc, "t_zeroed", "p_blocks", "c_blocks", "s_blocks", "t_next", "t_ready", "carried", "o_ready") as (
                block, t_zeroed, p_blocks, c_blocks, s_blocks, t_next, t_ready, carried, o_ready):
            @block.gpsimd
            def _(pool):
                pool.memset(T[:, 0:1, :], 0.0).then_inc(t_zeroed, 1)
                pool.wait_ge(t_zeroed, 1)
                with pool.Fori(0, NSEG // 2) as pair:
                    for par in range(2):
                        j = pair * 2 + par
                        pool.wait_ge(t_ready, j)
                        pool.wait_ge(carried, j)
                        pool.tensor_tensor(Pb[:, par, :].rearrange("p (h e) -> p h e", e=HD),
                                           Zj[:, 1, ds(j, 1), :].to_broadcast(WIDE), hb, ALU.mult).then_inc(p_blocks, 1)
                        pool.tensor_tensor(Cb[:, par, :].rearrange("p (h e) -> p h e", e=HD),
                                           Zj[:, 0, ds(j, 1), :].to_broadcast(WIDE), hb, ALU.mult).then_inc(c_blocks, 1)
                        pool.tensor_tensor(Sb[:, par, :].rearrange("p (h e) -> p h e", e=HD),
                                           T[:, ds(j, 1), :].to_broadcast(WIDE), hb, ALU.mult).then_inc(s_blocks, 1)

            @block.tensor
            def _(pe):
                with pe.Fori(0, NSEG // 2) as pair:
                    for par in range(2):
                        j = pair * 2 + par
                        pe.wait_ge(c_blocks, j + 1)
                        pe.wait_ge(t_ready, j)
                        pe.matmul(nxt[:, par, 0:HD], Cb[:, par, :], m.eye8[:], start=True, stop=False)
                        pe.wait_ge(p_blocks, j + 1)
                        pe.matmul(nxt[:, par, 0:HD], Pb[:, par, :], T[:, ds(j, 1), :], start=False, stop=True)\
                          .then_inc(t_next, 1)
                        pe.wait_ge(s_blocks, j + 1)
                        pe.matmul(add[:].rearrange("p a (b t) -> p (a b) t", t=SEG)[:, ds(j, 1), :], Sb[:, par, :],
                                  r.wo[:, 1, ds(j * SEG, SEG)], start=True, stop=True).then_inc(carried, 1)

            @block.vector
            def _(dve):
                dve.wait_ge(t_zeroed, 1)
                with dve.Fori(0, NSEG // 2) as pair:
                    for par in range(2):
                        j = pair * 2 + par
                        dve.wait_ge(t_next, j + 1)
                        dve.tensor_copy(T[:, ds(j + 1, 1), :], nxt[:, par:par + 1, 0:HD]).then_inc(t_ready, 1)
                dve.wait_ge(carried, NSEG)
                for c in range(NCH):
                    dve.tensor_tensor(r.o[:, cs(c)], add[:, c, :], r.wo[:, 0, cs(c)], ALU.add).then_inc(o_ready, 1)


def l0_output(nc, m, inp, r):
    with ExitStack() as own:
        sb = lambda name, shape: own.enter_context(sbuf(nc, name, shape))
        wo = sb("w_o", [P, P])
        load_all(nc, [(wo[:], inp["L0_attn_Wo"])])
        st = sb("stats", [P, 8])
        sq = sb("o_squared", [P, TOK])
        ps = own.enter_context(psum(nc, "group_sums", [P, CH]))
        po = own.enter_context(psum(nc, "out_proj", [P, NCH, CH]))
        with stage(nc, "summed", "over_heads", "std_ready", "chain", "gated", "projected", "added") as (
                block, summed, over_heads, std_ready, chain, gated, projected, added):
            @block.scalar
            def _(act):
                act.activation(sq[:], r.o[:], ACT.Square, accum_out=st[:, 1:2]).then_inc(summed, 1)
                act.wait_ge(chain, 5)
                act.activation(st[:, 4:5], st[:, 4:5], ACT.Sqrt).then_inc(std_ready, 1)

            @block.tensor
            def _(pe):
                pe.wait_ge(summed, 2)
                pe.matmul(ps[:, 0:2], m.head_ones[:], st[:, 0:2], start=True, stop=True).then_inc(over_heads, 1)
                for c in range(NCH):
                    pe.wait_ge(gated, c + 1)
                    pe.matmul(po[:, c, :], wo[:], r.o[:, cs(c)], start=True, stop=True).then_inc(projected, 1)

            @block.vector
            def _(dve):
                n = [0]

                def link(ins):
                    n[0] += 1
                    ins.then_inc(chain, 1)
                    dve.wait_ge(chain, n[0])

                dve.tensor_reduce(st[:, 0:1], r.o[:], AX.X, ALU.add).then_inc(summed, 1)
                dve.wait_ge(over_heads, 1)
                link(dve.tensor_scalar(st[:, 2:4], ps[:, 0:2], 1.0 / (TOK * HD), None, ALU.mult))
                link(dve.tensor_tensor(st[:, 4:5], st[:, 2:3], st[:, 2:3], ALU.mult))
                link(dve.tensor_tensor(st[:, 4:5], st[:, 3:4], st[:, 4:5], ALU.subtract))
                link(dve.tensor_scalar(st[:, 4:5], st[:, 4:5], 1e-5, None, ALU.add))
                link(dve.tensor_scalar(st[:, 5:6], st[:, 2:3], -1.0, None, ALU.mult))
                dve.wait_ge(std_ready, 1)
                link(dve.reciprocal(st[:, 4:5], st[:, 4:5]))
                link(dve.tensor_tensor(st[:, 6:7], st[:, 4:5], m.col("L0_attn_gn_scale"), ALU.mult))
                link(dve.tensor_scalar(r.o[:], r.o[:], st[:, 5:6], st[:, 6:7], ALU.add, ALU.mult))
                for c in range(NCH):
                    dve.scalar_tensor_tensor(out=r.o[:, cs(c)], in0=r.o[:, cs(c)], scalar=m.col("L0_attn_gn_bias"),
                                             in1=r.gate[:, cs(c)], op0=ALU.add, op1=ALU.mult).then_inc(gated, 1)
                for c in range(NCH):
                    dve.wait_ge(projected, c + 1)
                    dve.scalar_tensor_tensor(out=m.x[:, cs(c)], in0=po[:, c, :], scalar=m.col("L0_attn_bo"),
                                             in1=m.x[:, cs(c)], op0=ALU.add, op1=ALU.add).then_inc(added, 1)


def layer0_attention(nc, m, inp):
    with ExitStack() as own:
        r = Named()
        r.q, r.k, r.bv, r.a, r.nab, r.gate, r.o = (own.enter_context(sbuf(nc, "r_" + name, [P, TOK]))
                                                   for name in ("q", "k", "bv", "a", "nab", "gate", "o"))
        r.Z = own.enter_context(sbuf(nc, "r_Z", [P, 2, HD * NSEG]))
        r.wo = own.enter_context(sbuf(nc, "r_wo", [P, 2, TOK]))
        l0_project(nc, m, inp, r)
        l0_scan(nc, m, r)
        l0_join(nc, m, r)
        l0_output(nc, m, inp, r)



EXPERTS = 8
FF = 512
FT = FF // P


def expert_weights(nc, m, h, width, w, bias, k, renormalize, wT, kept=None, post=None):
    SH = [P, NT, EXPERTS]
    SQ = [P, NT, EXPERTS, EXPERTS]
    with ExitStack() as own:
        sb = lambda name, shape: own.enter_context(sbuf(nc, name, shape))
        p, sel = sb("probs", SH), sb("selected", [P, 2, NT, EXPERTS])
        gt, eq = sb("greater", SQ), sb("equal", SQ)
        lower = sb("lower", [P, EXPERTS, EXPERTS])
        s = sb("s", [P, NT])
        selT = sb("selected_T", [EXPERTS, 3, TOK])
        logits = own.enter_context(psum(nc, "router_logits", [P, NT, EXPERTS]))
        turned = own.enter_context(psum(nc, "weights_turned", [P, NCH, CH]))
        with stage(nc, "lower_set", "lower_shaped", "logits_ready", "less_max", "exp_ready", "chain", "w_ready", "w_turned", "m_turned",
                   "w_copied", "m_copied") as (
                block, lower_set, lower_shaped, logits_ready, less_max, exp_ready, chain, w_ready, w_turned, m_turned,
                w_copied, m_copied):
            @block.gpsimd
            def _(pool):
                pool.memset(lower[:], 1.0).then_inc(lower_set, 1)
                pool.wait_ge(lower_set, 1)
                pool.affine_select(out=lower[:], in_=lower[:], compare_op=ALU.is_gt, fill=0.0, base=0,
                                   pattern=[[1, EXPERTS], [-1, EXPERTS]], channel_multiplier=0).then_inc(lower_shaped, 1)

            @block.tensor
            def _(pe):
                for n in range(NT):
                    mm = pe.matmul(logits[:, n, :], h[0:width, n * P:(n + 1) * P], w, start=True, stop=bias is None)
                    if bias is not None:
                        mm = pe.matmul(logits[:, n, :], m.ones[0:1, :], bias, start=False, stop=True)
                mm.then_inc(logits_ready, 1)
                pe.wait_ge(w_ready, 1)
                for n in range(NT):
                    c, k4 = divmod(n, CH // P)
                    mm = pe.transpose(turned[0:EXPERTS, c, k4 * P:(k4 + 1) * P], p[:, n, :], m.ident[:])
                mm.then_inc(w_turned, 1)
                if kept is not None:
                    pe.wait_ge(w_copied, 1)
                    for n in range(NT):
                        c, k4 = divmod(n, CH // P)
                        mm = pe.transpose(turned[0:EXPERTS, c, k4 * P:(k4 + 1) * P], sel[:, 0, n, :], m.ident[:])
                    mm.then_inc(m_turned, 1)

            @block.scalar
            def _(act):
                act.wait_ge(less_max, 1)
                act.activation(p[:], p[:], ACT.Exp).then_inc(exp_ready, 1)

            @block.vector
            def _(dve):
                n = [0]

                def link(ins):
                    n[0] += 1
                    ins.then_inc(chain, 1)
                    dve.wait_ge(chain, n[0])

                dve.wait_ge(logits_ready, 1)
                link(dve.tensor_reduce(s[:], logits[:], AX.X, ALU.max))
                dve.tensor_tensor(p[:], logits[:], s[:].unsqueeze(2).to_broadcast(SH), ALU.subtract).then_inc(less_max, 1)
                dve.wait_ge(exp_ready, 1)
                link(dve.tensor_reduce(s[:], p[:], AX.X, ALU.add))
                link(dve.reciprocal(s[:], s[:]))
                link(dve.tensor_tensor(p[:], p[:], s[:].unsqueeze(2).to_broadcast(SH), ALU.mult))
                pj, pe_ = p[:].unsqueeze(2).to_broadcast(SQ), p[:].unsqueeze(3).to_broadcast(SQ)
                link(dve.tensor_tensor(gt[:], pj, pe_, ALU.is_gt))
                link(dve.tensor_tensor(eq[:], pj, pe_, ALU.is_equal))
                dve.wait_ge(lower_shaped, 1)
                link(dve.tensor_tensor(eq[:], eq[:], lower[:].unsqueeze(1).to_broadcast(SQ), ALU.mult))
                link(dve.tensor_tensor(gt[:], gt[:], eq[:], ALU.add))
                link(dve.tensor_reduce(sel[:, 1], gt[:], AX.X, ALU.add))
                link(dve.tensor_scalar(sel[:, 0], sel[:, 1], float(k), None, ALU.is_lt))
                link(dve.tensor_tensor(p[:], p[:], sel[:, 0], ALU.mult))
                if renormalize:
                    link(dve.tensor_reduce(s[:], p[:], AX.X, ALU.add))
                    link(dve.reciprocal(s[:], s[:]))
                    link(dve.tensor_tensor(p[:], p[:], s[:].unsqueeze(2).to_broadcast(SH), ALU.mult))
                dve.tensor_copy(eq[:, 0, 0, 0:1], s[:, 0:1]).then_inc(w_ready, 1)
                dve.wait_ge(w_turned, 1)
                dve.tensor_copy(wT, turned[0:EXPERTS, :, :].rearrange("p a b -> p (a b)")).then_inc(w_copied, 1)
                if kept is not None:
                    dve.wait_ge(m_turned, 1)
                    link(dve.tensor_copy(selT[:, 0, :], turned[0:EXPERTS, :, :].rearrange("p a b -> p (a b)")))
                    link(dve.tensor_scalar(selT[:, 1, :], selT[:, 0, :], 0.0, None, ALU.mult))
                    link(dve.tensor_tensor_scan(selT[:, 2, :], selT[:, 0, :], selT[:, 1, :], 0.0, ALU.add, ALU.add))
                    link(dve.tensor_scalar(selT[:, 2, :], selT[:, 2, :], float(kept), None, ALU.is_le))
                    dve.wait_ge(w_copied, 1)
                    dve.tensor_tensor(wT, wT, selT[:, 2, :], ALU.mult).then_inc(m_copied, 1)


def expert_sum(nc, m, src, w1, w2, halves, b1, b2, wT):
    HT = halves * FT
    with ExitStack() as own:
        sb = lambda name, shape: own.enter_context(sbuf(nc, name, shape))
        wa = sb("w_up", [P, 2, halves * FF])
        wb = sb("w_down", [P, 2, FT, P])
        bcol = sb("up_bias", [P, HT])
        gel = sb("gelu_out", [P, 2, CH])
        hid = sb("hidden", [P, 2, FT, CH])
        wrow = sb("expert_row", [EXPERTS, 2, CH])
        wcol = sb("expert_weight", [P, 2, CH])
        part = sb("weighted", [P, 2, CH])
        ups = own.enter_context(psum(nc, "up", [P, 4, CH]))
        yps = own.enter_context(psum(nc, "down", [P, 2, CH]))
        mps = own.enter_context(psum(nc, "weight_spread", [P, 2, CH]))
        with stage(nc, "w_loaded0", "w_loaded1", "bias_ready", "up_ready", "activated", "hid_ready",
                   "row_ready", "spread", "wcol_ready", "down_ready", "y_weighted", "added") as (
                block, w_loaded0, w_loaded1, bias_ready, up_ready, activated, hid_ready,
                row_ready, spread, wcol_ready, down_ready, y_weighted, added):
            loaded = (w_loaded0, w_loaded1)
            w1v = w1.rearrange("e p n -> p e n")
            w2v = w2.rearrange("e (t p) n -> p e t n", p=P)
            UP = 4 // halves

            @block.sync
            def _(sp):
                for par in range(2):
                    sp.dma_start(wa[:, par, :], w1v[:, par, :]).then_inc(loaded[par], 16)
                    sp.dma_start(wb[:, par, :, :], w2v[:, par, :, :]).then_inc(loaded[par], 16)
                with sp.Fori(1, EXPERTS // 2) as pair:
                    for par in range(2):
                        sp.wait_ge(down_ready, (pair * 2 + par - 1) * NCH)
                        sp.dma_start(wa[:, par:par + 1, :], w1v[:, ds(pair * 2 + par, 1), :]).then_inc(loaded[par], 16)
                        sp.dma_start(wb[:, par:par + 1, :, :], w2v[:, ds(pair * 2 + par, 1), :, :]).then_inc(loaded[par], 16)

            @block.gpsimd
            def _(pool):
                with pool.Fori(0, EXPERTS) as e:
                    for c in range(NCH):
                        i = e * NCH + c
                        pool.wait_ge(y_weighted, i + 1)
                        pool.tensor_tensor(m.x[:, cs(c)], m.x[:, cs(c)], part[:, c % 2, :], ALU.add).then_inc(added, 1)

            @block.tensor
            def _(pe):
                with pe.Fori(0, EXPERTS // 2) as pair:
                    for par in range(2):
                        e = pair * 2 + par
                        pe.wait_ge(loaded[par], pair * 32 + 32)
                        for c in range(NCH):
                            i = e * NCH + c
                            for f in range(FT):
                                pe.wait_ge(hid_ready, i * FT + f + 1 - UP if c or f >= UP else e * NCH * FT)
                                for s in reversed(range(halves)):
                                    t = s * FT + f
                                    pe.matmul(ups[:, (f % UP) * halves + s, :], wa[:, par, t * P:(t + 1) * P],
                                              src[:, cs(c)], start=True, stop=True).then_inc(up_ready, 1)
                            pe.wait_ge(row_ready, i + 1)
                            if c >= 2:
                                pe.wait_ge(wcol_ready, i - 1)
                            else:
                                pe.wait_ge(wcol_ready, e * NCH)
                            pe.matmul(mps[:, c % 2, :], m.ones[0:EXPERTS, :], wrow[:, c % 2, :],
                                      start=True, stop=True).then_inc(spread, 1)
                            pe.wait_ge(y_weighted, i - 1 if c >= 2 else e * NCH)
                            for f in range(FT):
                                pe.wait_ge(hid_ready, i * FT + f + 1)
                                mm = pe.matmul(yps[:, c % 2, :], wb[:, par, f, :], hid[:, c % 2, f, :],
                                               start=(f == 0), stop=(f == FT - 1))
                            mm.then_inc(down_ready, 1)

            @block.scalar
            def _(act):
                with act.Fori(0, EXPERTS) as e:
                    act.wait_ge(bias_ready, e + 1)
                    for c in range(NCH):
                        i = e * NCH + c
                        for f in range(FT):
                            bias = bcol[:, (halves - 1) * FT + f:(halves - 1) * FT + f + 1]
                            act.wait_ge(up_ready, (i * FT + f) * halves + 1)
                            if halves == 1:
                                act.wait_ge(down_ready, i - 1 if c >= 2 else e * NCH)
                                act.activation(hid[:, c % 2, f, :], ups[:, f, :], ACT.Gelu_apprx_tanh, bias=bias)\
                                   .then_inc(hid_ready, 1)
                            else:
                                act.wait_ge(hid_ready, i * FT + f - 1 if c or f >= 2 else e * NCH * FT)
                                act.activation(gel[:, f % 2, :], ups[:, (f % UP) * halves + 1, :], ACT.Gelu_apprx_tanh,
                                               bias=bias).then_inc(activated, 1)
                        act.wait_ge(spread, i + 1)
                        act.wait_ge(y_weighted, i - 1 if c >= 2 else e * NCH)
                        act.activation(wcol[:, c % 2, :], mps[:, c % 2, :], ACT.Copy).then_inc(wcol_ready, 1)

            @block.vector
            def _(dve):
                with dve.Fori(0, EXPERTS) as e:
                    dve.wait_ge(hid_ready, e * NCH * FT)
                    dve.tensor_scalar(bcol[:], m.cols[:, ds(m.at[b1] + e * HT, HT)], 1.0, None, ALU.mult)\
                       .then_inc(bias_ready, 1)
                    for c in range(NCH):
                        i = e * NCH + c
                        dve.wait_ge(spread, i - 1 if c >= 2 else e * NCH)
                        dve.tensor_scalar(wrow[:, c % 2, :], wT[:, cs(c)], m.ident[0:EXPERTS, ds(e, 1)], None, ALU.mult)\
                           .then_inc(row_ready, 1)
                        if halves == 2:
                            dve.wait_ge(bias_ready, e + 1)
                            for f in range(FT):
                                dve.wait_ge(activated, i * FT + f + 1)
                                dve.wait_ge(up_ready, (i * FT + f) * halves + 2)
                                dve.wait_ge(down_ready, i - 1 if c >= 2 else e * NCH)
                                dve.scalar_tensor_tensor(out=hid[:, c % 2, f, :], in0=ups[:, (f % UP) * halves, :],
                                                         scalar=bcol[:, f:f + 1],
                                                         in1=gel[:, f % 2, :], op0=ALU.add, op1=ALU.mult)\
                                   .then_inc(hid_ready, 1)
                        dve.wait_ge(down_ready, i + 1)
                        dve.wait_ge(wcol_ready, i + 1)
                        dve.wait_ge(added, i - 1 if c >= 2 else e * NCH)
                        dve.scalar_tensor_tensor(out=part[:, c % 2, :], in0=yps[:, c % 2, :],
                                                 scalar=m.cols[:, ds(m.at[b2] + e, 1)], in1=wcol[:, c % 2, :],
                                                 op0=ALU.add, op1=ALU.mult).then_inc(y_weighted, 1)


def layer0_experts(nc, m, inp):
    with ExitStack() as own:
        sb = lambda name, shape: own.enter_context(sbuf(nc, name, shape))
        R = P // 2
        wr1, wr2, br2 = sb("w_r1", [P, R]), sb("w_r2", [R, EXPERTS]), sb("b_r2", [1, EXPERTS])
        h, wT = sb("router_hidden", [R, TOK]), sb("weights_T", [EXPERTS, TOK])
        load_all(nc, [(wr1[:], inp["L0_ffn_Wr1"]), (wr2[:], inp["L0_ffn_Wr2"]),
                      (br2[:], inp["L0_ffn_br2"].rearrange("(a e) -> a e", a=1))])
        with psum(nc, "router_up", [R, NCH, CH]) as ps, stage(nc, "up", "biased") as (block, up, biased):
            @block.tensor
            def _(pe):
                for c in range(NCH):
                    pe.matmul(ps[:, c, :], wr1[:], m.xn[:, cs(c)], start=True, stop=True).then_inc(up, 1)

            @block.scalar
            def _(act):
                for c in range(NCH):
                    act.wait_ge(up, c + 1)
                    act.activation(h[:, cs(c)], ps[:, c, :], ACT.Identity, bias=m.col("L0_ffn_br1", 0, R)).then_inc(biased, 1)
        layernorm(nc, m, h, h, 1e-6, width=R, scale=m.col("L0_ffn_ln_scale", 0, R), bias=m.col("L0_ffn_ln_bias", 0, R),
                  after=ACT.Gelu_apprx_tanh)
        expert_weights(nc, m, h, R, wr2[:], br2[:], 2, True, wT[:])
        expert_sum(nc, m, m.xn, inp["L0_ffn_W1"], inp["L0_ffn_W2"], 2, "L0_ffn_b1", "L0_ffn_b2", wT)



def layer3_experts(nc, m, inp):
    CAP = max(4, TOK // EXPERTS)
    with ExitStack() as own:
        sb = lambda name, shape: own.enter_context(sbuf(nc, name, shape))
        wg, coef_w = sb("w_gate", [P, EXPERTS]), sb("w_coef", [P, 2])
        w1, w2 = sb("w_res_up", [P, FF]), sb("w_res_down", [P, FT, P])
        y, wT = sb("attn_out", [P, TOK]), sb("weights_T3", [EXPERTS, TOK])
        dif = sb("coef_dif", [P, 2, P])
        cf = sb("coef", [P, 2, TOK])
        hid = sb("res_hidden", [P, 2, FT, CH])
        load_all(nc, [(wg[:], inp["L3_ffn_wg"]), (coef_w[:], inp["L3_ffn_res_coef"]), (w1[:], inp["L3_ffn_res_inter_w"]),
                      (w2[:], inp["L3_ffn_res_output_w"].rearrange("(t p) n -> p t n", p=P))])
        layernorm(nc, m, m.xn, y, 1e-12, scale=m.col("L3_ffn_attn_nw"), bias=m.col("L3_ffn_attn_nb"))
        expert_weights(nc, m, y, P, wg[:], None, 1, False, wT[:], kept=CAP)
        with psum(nc, "coef_logits", [P, 2, CH]) as cps, psum(nc, "res_up", [P, 4, CH]) as ups, \
                psum(nc, "res_down", [P, 2, CH]) as yps, \
                stage(nc, "dif_ready", "logits", "coef_ready", "wT_done", "up", "hidden", "down", "res_weighted", "summed") as (
                block, dif_ready, logits, coef_ready, wT_done, up, hidden, down, res_weighted, summed):
            @block.vector
            def _(dve):
                dve.tensor_scalar(dif[:, 0, 0:1], coef_w[:, 0:1], coef_w[:, 1:2], None, ALU.subtract).then_inc(dif_ready, 1)
                dve.wait_ge(dif_ready, 1)
                dve.tensor_copy(dif[:, 1, :], dif[:, 0, 0:1].to_broadcast([P, P])).then_inc(dif_ready, 1)
                for c in range(NCH):
                    dve.wait_ge(coef_ready, 2 * c + 2)
                    dve.tensor_tensor(wT[:, cs(c)], wT[:, cs(c)], cf[0:EXPERTS, 1, cs(c)], ALU.mult).then_inc(wT_done, 1)
                    dve.tensor_tensor(m.x[:, cs(c)], m.x[:, cs(c)], m.xn[:, cs(c)], ALU.add).then_inc(summed, 1)
                for c in range(NCH):
                    dve.wait_ge(down, c + 1)
                    dve.scalar_tensor_tensor(out=cf[:, 0, cs(c)], in0=yps[:, c % 2, :], scalar=m.col("L3_ffn_res_output_b"),
                                             in1=cf[:, 0, cs(c)], op0=ALU.add, op1=ALU.mult).then_inc(res_weighted, 1)
                    dve.wait_ge(res_weighted, c + 1)
                    dve.wait_ge(summed, NCH)
                    dve.tensor_tensor(m.x[:, cs(c)], m.x[:, cs(c)], cf[:, 0, cs(c)], ALU.add).then_inc(summed, 1)

            @block.tensor
            def _(pe):
                pe.wait_ge(dif_ready, 2)
                for c in range(NCH):
                    if c >= 2:
                        pe.wait_ge(coef_ready, 2 * (c - 1))
                    pe.matmul(cps[:, c % 2, :], dif[:, 1, :], y[:, cs(c)], start=True, stop=True).then_inc(logits, 1)
                for c in range(NCH):
                    for f in range(FT):
                        if c:
                            pe.wait_ge(hidden, (c - 1) * FT + f + 1)
                        pe.matmul(ups[:, f, :], w1[:, f * P:(f + 1) * P], y[:, cs(c)], start=True, stop=True).then_inc(up, 1)
                    if c >= 2:
                        pe.wait_ge(res_weighted, c - 1)
                    for f in range(FT):
                        pe.wait_ge(hidden, c * FT + f + 1)
                        mm = pe.matmul(yps[:, c % 2, :], w2[:, f, :], hid[:, c % 2, f, :], start=(f == 0), stop=(f == FT - 1))
                    mm.then_inc(down, 1)

            @block.scalar
            def _(act):
                for c in range(NCH):
                    act.wait_ge(logits, c + 1)
                    act.activation(cf[:, 0, cs(c)], cps[:, c % 2, :], ACT.Sigmoid).then_inc(coef_ready, 1)
                    act.activation(cf[:, 1, cs(c)], cps[:, c % 2, :], ACT.Sigmoid, scale=-1.0).then_inc(coef_ready, 1)
                for c in range(NCH):
                    if c >= 2:
                        act.wait_ge(down, c - 1)
                    for f in range(FT):
                        act.wait_ge(up, c * FT + f + 1)
                        act.activation(hid[:, c % 2, f, :], ups[:, f, :], ACT.Gelu_apprx_tanh,
                                       bias=m.col("L3_ffn_res_inter_b", f)).then_inc(hidden, 1)
        expert_sum(nc, m, y, inp["L3_ffn_inter_w"], inp["L3_ffn_output_w"], 1, "L3_ffn_inter_b", "L3_ffn_output_b", wT)



def hidden_mlp(nc, m, src, w1, w2, b1, b2, base):
    with ExitStack() as own:
        wa, wb = own.enter_context(sbuf(nc, "w_up", [P, FF])), own.enter_context(sbuf(nc, "w_down", [P, FT, P]))
        hid = own.enter_context(sbuf(nc, "mlp_hidden", [P, 2, FT, CH]))
        ups, yps = own.enter_context(psum(nc, "mlp_up", [P, 4, CH])), own.enter_context(psum(nc, "mlp_down", [P, 2, CH]))
        load_all(nc, [(wa[:], w1), (wb[:], w2.rearrange("(t p) n -> p t n", p=P))])
        with stage(nc, "up", "hidden", "down", "based", "added") as (block, up, hidden, down, based, added):
            @block.tensor
            def _(pe):
                for c in range(NCH):
                    for f in range(FT):
                        if c:
                            pe.wait_ge(hidden, (c - 1) * FT + f + 1)
                        pe.matmul(ups[:, f, :], wa[:, f * P:(f + 1) * P], src[:, cs(c)], start=True, stop=True).then_inc(up, 1)
                    if c >= 2:
                        pe.wait_ge(added, c - 1)
                    for f in range(FT):
                        pe.wait_ge(hidden, c * FT + f + 1)
                        mm = pe.matmul(yps[:, c % 2, :], wb[:, f, :], hid[:, c % 2, f, :], start=(f == 0), stop=(f == FT - 1))
                    mm.then_inc(down, 1)

            @block.scalar
            def _(act):
                for c in range(NCH):
                    if c >= 2:
                        act.wait_ge(down, c - 1)
                    for f in range(FT):
                        act.wait_ge(up, c * FT + f + 1)
                        act.activation(hid[:, c % 2, f, :], ups[:, f, :], ACT.Gelu_apprx_tanh, bias=m.col(b1, f))\
                           .then_inc(hidden, 1)

            @block.gpsimd
            def _(pool):
                for c in range(NCH):
                    pool.tensor_tensor(m.x[:, cs(c)], m.x[:, cs(c)], base[:, cs(c)], ALU.add).then_inc(based, 1)

            @block.vector
            def _(dve):
                for c in range(NCH):
                    dve.wait_ge(down, c + 1)
                    dve.wait_ge(based, c + 1)
                    dve.scalar_tensor_tensor(out=m.x[:, cs(c)], in0=yps[:, c % 2, :], scalar=m.col(b2),
                                             in1=m.x[:, cs(c)], op0=ALU.add, op1=ALU.add).then_inc(added, 1)


def layer1_attention(nc, m, inp):
    KEPS = 1e-3
    with ExitStack() as own:
        sb = lambda name, shape: own.enter_context(sbuf(nc, name, shape))
        y, q, xres = sb("l1_y", [P, TOK]), sb("phi_q", [P, TOK]), sb("x_res", [P, TOK])
        wq, wkv, wo, bkv = sb("w_q", [P, P]), sb("w_kv", [P, 2 * P]), sb("w_o", [P, P]), sb("b_kv", [1, 2 * P])
        load_all(nc, [(wq[:], inp["L1_attn_Wq"].rearrange("i h d -> i (h d)")),
                      (wkv[:, 0:P], inp["L1_attn_Wk"].rearrange("i h d -> i (h d)")),
                      (wkv[:, P:2 * P], inp["L1_attn_Wv"].rearrange("i h d -> i (h d)")),
                      (wo[:], inp["L1_attn_Wo"].rearrange("h d o -> (h d) o")),
                      (bkv[:, 0:P], inp["L1_attn_bk"].rearrange("(o h) d -> o (h d)", o=1)),
                      (bkv[:, P:2 * P], inp["L1_attn_bv"].rearrange("(o h) d -> o (h d)", o=1))])
        layernorm(nc, m, m.xn, y, 1e-6, scale=m.col("L1_attn_ln1_scale"), bias=m.col("L1_attn_ln1_bias"))
        kf, vo = sb("phi_k", [P, 2, P]), sb("v_and_one", [P, 2, P + 1])
        kvb, ksb = sb("kv_blocks", [P, P]), sb("ksum_blocks", [P, P])
        inv = sb("inverse_den", [P, 2, CH])
        with ExitStack() as inner:
            kvps = inner.enter_context(psum(nc, "k_v_tokens", [P, 2, CH]))
            kvsum = inner.enter_context(psum(nc, "kv_sum", [P, CH]))
            qps = inner.enter_context(psum(nc, "q_proj", [P, NCH, CH]))
            with stage(nc, "kv_tokens", "q_logits", "kv_raw", "k_ready", "v_ready", "kv_sum", "ones_set", "blocks", "q_ready",
                       "q_biased") as (
                    block, kv_tokens, q_logits, kv_raw, k_ready, v_ready, kv_sum, ones_set, blocks, q_ready, q_biased):
                @block.tensor
                def _(pe):
                    def sums(n):
                        pe.wait_ge(k_ready, n + 1)
                        pe.wait_ge(v_ready, n + 1)
                        pe.matmul(kvsum[:, 0:P + 1], kf[:, n % 2, :], vo[:, n % 2, :], start=(n == 0), stop=(n == NT - 1))\
                          .then_inc(kv_sum, 1)

                    for n in range(NT):
                        if n >= 2:
                            pe.wait_ge(k_ready, n - 1)
                            pe.wait_ge(v_ready, n - 1)
                        pe.matmul(kvps[:, n % 2, 0:2 * P], y[:, n * P:(n + 1) * P], wkv[:], start=True, stop=False)
                        pe.matmul(kvps[:, n % 2, 0:2 * P], m.ones[0:1, :], bkv[:], start=False, stop=True)\
                          .then_inc(kv_tokens, 1)
                        if n:
                            sums(n - 1)
                    sums(NT - 1)
                    for c in range(NCH):
                        pe.matmul(qps[:, c, :], wq[:], y[:, cs(c)], start=True, stop=True).then_inc(q_logits, 1)

                @block.scalar
                def _(act):
                    act.wait_ge(ones_set, 1)
                    for n in range(NT):
                        act.wait_ge(kv_tokens, n + 1)
                        if n >= 2:
                            act.wait_ge(kv_sum, n - 1)
                        act.activation(vo[:, n % 2, 0:P], kvps[:, n % 2, P:2 * P], ACT.Copy).then_inc(v_ready, 1)
                    for c in range(NCH):
                        act.wait_ge(q_logits, c + 1)
                        act.activation(q[:, cs(c)], qps[:, c, :], ACT.Relu, bias=m.col("L1_attn_bq")).then_inc(q_biased, 1)

                @block.vector
                def _(dve):
                    dve.memset(vo[:, :, P:P + 1], 1.0).then_inc(ones_set, 1)
                    for n in range(NT):
                        dve.wait_ge(v_ready, n + 1)
                        if n >= 2:
                            dve.wait_ge(kv_sum, n - 1)
                        dve.tensor_scalar(kf[:, n % 2, :], kvps[:, n % 2, 0:P], 0.0, KEPS, ALU.max, ALU.add).then_inc(k_ready, 1)
                    dve.wait_ge(kv_sum, NT)
                    dve.tensor_tensor(kvb[:], kvsum[:, 0:P], m.head_ones[:], ALU.mult).then_inc(blocks, 1)
                    dve.tensor_scalar(ksb[:], m.head_ones[:], kvsum[:, P:P + 1], None, ALU.mult).then_inc(blocks, 1)
                    for c in range(NCH):
                        dve.wait_ge(q_biased, c + 1)
                        dve.tensor_scalar(q[:, cs(c)], q[:, cs(c)], KEPS, None, ALU.add).then_inc(q_ready, 1)
        with ExitStack() as inner:
            num = inner.enter_context(psum(nc, "numerator", [P, 2, CH]))
            den = inner.enter_context(psum(nc, "denominator", [P, 2, CH]))
            ops = inner.enter_context(psum(nc, "attn_proj", [P, 2, CH]))
            with stage(nc, "num_ready", "den_ready", "inverted", "attn_ready", "projected", "res_ready", "res_biased") as (
                    block, num_ready, den_ready, inverted, attn_ready, projected, res_ready, res_biased):
                @block.tensor
                def _(pe):
                    def project(c):
                        pe.wait_ge(attn_ready, c + 1)
                        if c >= 2:
                            pe.wait_ge(res_ready, c - 1)
                        pe.matmul(ops[:, c % 2, :], wo[:], q[:, cs(c)], start=True, stop=True).then_inc(projected, 1)

                    for c in range(NCH):
                        if c >= 2:
                            pe.wait_ge(attn_ready, c - 1)
                        pe.matmul(den[:, c % 2, :], ksb[:], q[:, cs(c)], start=True, stop=True).then_inc(den_ready, 1)
                        pe.matmul(num[:, c % 2, :], kvb[:], q[:, cs(c)], start=True, stop=True).then_inc(num_ready, 1)
                        if c:
                            project(c - 1)
                    project(NCH - 1)

                @block.vector
                def _(dve):
                    def residual(c):
                        dve.wait_ge(projected, c + 1)
                        dve.scalar_tensor_tensor(out=xres[:, cs(c)], in0=ops[:, c % 2, :], scalar=m.col("L1_attn_bo"),
                                                 in1=m.xn[:, cs(c)], op0=ALU.add, op1=ALU.add).then_inc(res_ready, 1)

                    for c in range(NCH):
                        dve.wait_ge(den_ready, c + 1)
                        dve.reciprocal(inv[:, c % 2, :], den[:, c % 2, :]).then_inc(inverted, 1)
                        dve.wait_ge(inverted, c + 1)
                        dve.wait_ge(num_ready, c + 1)
                        dve.tensor_tensor(q[:, cs(c)], num[:, c % 2, :], inv[:, c % 2, :], ALU.mult).then_inc(attn_ready, 1)
                        if c:
                            residual(c - 1)
                    residual(NCH - 1)
        layernorm(nc, m, xres, y, 1e-6, scale=m.col("L1_attn_ln2_scale"), bias=m.col("L1_attn_ln2_bias"))
        hidden_mlp(nc, m, y, inp["L1_attn_W1"], inp["L1_attn_W2"], "L1_attn_b1", "L1_attn_b2", xres)


def layer1_ffn(nc, m, inp):
    U, INNER = 64, 16
    UT = U * INNER // P
    PER = P // INNER
    with ExitStack() as own:
        sb = lambda name, shape: own.enter_context(sbuf(nc, name, shape))
        win, wout = sb("w_in", [P, U]), sb("w_out", [U, P])
        unit_rows = sb("unit_rows", [U, UT, P])
        unit_cols = sb("unit_cols", [P, UT, U])
        s, hid, g = sb("units", [U, TOK]), sb("unit_hidden", [P, 2, CH]), sb("unit_out", [U, TOK])
        load_all(nc, [(win[:], inp["L1_ffn_Win"]), (wout[:], inp["L1_ffn_Wout"])])
        sps = own.enter_context(psum(nc, "units_in", [U, 2, CH]))
        hps = own.enter_context(psum(nc, "units_spread", [P, 2, CH]))
        gps = own.enter_context(psum(nc, "units_sum", [U, 2, CH]))
        ops = own.enter_context(psum(nc, "units_out", [P, 2, CH]))
        with stage(nc, "ones_set", "shaped", "scaled", "units_in", "units_ready", "spread", "hidden", "summed", "biased",
                   "out_ready", "added") as (
                block, ones_set, shaped, scaled, units_in, units_ready, spread, hidden, summed, biased, out_ready, added):
            @block.gpsimd
            def _(pool):
                pool.memset(unit_rows[:], 1.0).then_inc(ones_set, 1)
                pool.memset(unit_cols[:], 1.0).then_inc(ones_set, 1)
                pool.wait_ge(ones_set, 2)
                v = unit_rows[:].rearrange("m i (u h) -> m i u h", h=INNER)
                pool.affine_select(out=v, in_=v, compare_op=ALU.is_equal, fill=0.0, base=0,
                                   pattern=[[-PER, UT], [-1, PER], [0, INNER]], channel_multiplier=1).then_inc(shaped, 1)
                pool.affine_select(out=unit_cols[:], in_=unit_cols[:], compare_op=ALU.is_ge, fill=0.0, base=0,
                                   pattern=[[P, UT], [-INNER, U]], channel_multiplier=1).then_inc(shaped, 1)
                pool.wait_ge(shaped, 2)
                pool.affine_select(out=unit_cols[:], in_=unit_cols[:], compare_op=ALU.is_ge, fill=0.0, base=INNER - 1,
                                   pattern=[[-P, UT], [INNER, U]], channel_multiplier=-1).then_inc(shaped, 1)

            @block.tensor
            def _(pe):
                for c in range(NCH):
                    if c >= 2:
                        pe.wait_ge(units_ready, c - 1)
                    pe.matmul(sps[:, c % 2, :], win[:], m.xn[:, cs(c)], start=True, stop=True).then_inc(units_in, 1)
                pe.wait_ge(shaped, 3)
                pe.wait_ge(scaled, UT)

                def add_up(k):
                    c, i = divmod(k, UT)
                    pe.wait_ge(hidden, k + 1)
                    if i == 0 and c >= 2:
                        pe.wait_ge(biased, c - 1)
                    pe.matmul(gps[:, c % 2, :], unit_cols[:, i, :], hid[:, k % 2, :], start=(i == 0), stop=(i == UT - 1))\
                      .then_inc(summed, 1)

                for k in range(NCH * UT):
                    c, i = divmod(k, UT)
                    pe.wait_ge(units_ready, c + 1)
                    if k >= 2:
                        pe.wait_ge(hidden, k - 1)
                    pe.matmul(hps[:, k % 2, :], unit_rows[:, i, :], s[:, cs(c)], start=True, stop=True).then_inc(spread, 1)
                    if k:
                        add_up(k - 1)
                add_up(NCH * UT - 1)
                for c in range(NCH):
                    pe.wait_ge(biased, c + 1)
                    if c >= 2:
                        pe.wait_ge(added, c - 1)
                    pe.matmul(ops[:, c % 2, :], wout[:], g[:, cs(c)], start=True, stop=True).then_inc(out_ready, 1)

            @block.scalar
            def _(act):
                for k in range(NCH * UT):
                    c, i = divmod(k, UT)
                    act.wait_ge(spread, k + 1)
                    if k >= 2:
                        act.wait_ge(summed, k - 1)
                    act.activation(hid[:, k % 2, :], hps[:, k % 2, :], ACT.Relu, bias=m.col("L1_ffn_b1", i),
                                   scale=m.col("L1_ffn_W1", i)).then_inc(hidden, 1)

            @block.vector
            def _(dve):
                dve.wait_ge(shaped, 3)
                for i in range(UT):
                    dve.tensor_scalar(unit_cols[:, i, :], unit_cols[:, i, :], m.col("L1_ffn_W2", i), None, ALU.mult)\
                       .then_inc(scaled, 1)
                for c in range(NCH):
                    dve.wait_ge(units_in, c + 1)
                    dve.tensor_scalar(s[:, cs(c)], sps[:, c % 2, :], m.col("L1_ffn_bin_", 0, U), None, ALU.add)\
                       .then_inc(units_ready, 1)
                for c in range(NCH):
                    dve.wait_ge(summed, (c + 1) * UT)
                    dve.tensor_scalar(g[:, cs(c)], gps[:, c % 2, :], m.col("L1_ffn_b2", 0, U), None, ALU.add).then_inc(biased, 1)
                for c in range(NCH):
                    dve.wait_ge(out_ready, c + 1)
                    dve.scalar_tensor_tensor(out=m.x[:, cs(c)], in0=ops[:, c % 2, :], scalar=m.col("L1_ffn_bout"),
                                             in1=m.x[:, cs(c)], op0=ALU.add, op1=ALU.add).then_inc(added, 1)



def layer2_ffn(nc, m, inp):
    with ExitStack() as own:
        sb = lambda name, shape: own.enter_context(sbuf(nc, name, shape))
        w, wt = sb("w_rkv", [P, 3, P]), sb("w_rkv_T", [P, 3, P])
        om = sb("one_less_mu", [P, 2])
        prev = sb("x_before", [P, TOK])
        mix = sb("mixed", [P, 2, TOK])
        rr, kk = sb("r_gate", [P, TOK]), sb("k_act", [P, TOK])
        load_all(nc, [(w[:, 0, :], inp["L2_ffn_W_r"]), (w[:, 1, :], inp["L2_ffn_W_k"]), (w[:, 2, :], inp["L2_ffn_W_v"])])
        wps = own.enter_context(psum(nc, "w_turned", [P, CH]))
        ps = own.enter_context(psum(nc, "rk", [P, 4, CH]))
        vps = own.enter_context(psum(nc, "v", [P, 2, CH]))
        mus = ("L2_ffn_mu_r", "L2_ffn_mu_k")
        with stage(nc, "w_turned", "w_ready", "om_ready", "zeroed", "prev_ready", "first", "mixed", "r_logits", "k_logits",
                   "r_ready", "k_relu", "k_ready", "v_ready", "gated", "added") as (
                block, w_turned, w_ready, om_ready, zeroed, prev_ready, first, mixed, r_logits, k_logits,
                r_ready, k_relu, k_ready, v_ready, gated, added):
            @block.tensor
            def _(pe):
                for i in range(3):
                    pe.transpose(wps[:, i * P:(i + 1) * P], w[:, i, :], m.ident[:]).then_inc(w_turned, 1)
                pe.wait_ge(w_ready, 1)
                for c in range(NCH):
                    pe.wait_ge(mixed, 2 * c + 2)
                    if c >= 2:
                        pe.wait_ge(r_ready, c - 1)
                        pe.wait_ge(k_relu, c - 1)
                    pe.matmul(ps[:, c % 2, :], wt[:, 0, :], mix[:, 0, cs(c)], start=True, stop=True).then_inc(r_logits, 1)
                    pe.matmul(ps[:, 2 + c % 2, :], wt[:, 1, :], mix[:, 1, cs(c)], start=True, stop=True).then_inc(k_logits, 1)
                for c in range(NCH):
                    pe.wait_ge(k_ready, c + 1)
                    if c >= 2:
                        pe.wait_ge(gated, c - 1)
                    pe.matmul(vps[:, c % 2, :], wt[:, 2, :], kk[:, cs(c)], start=True, stop=True).then_inc(v_ready, 1)

            @block.scalar
            def _(act):
                for c in range(NCH):
                    act.wait_ge(r_logits, c + 1)
                    act.activation(rr[:, cs(c)], ps[:, c % 2, :], ACT.Sigmoid).then_inc(r_ready, 1)
                    act.wait_ge(k_logits, c + 1)
                    act.activation(kk[:, cs(c)], ps[:, 2 + c % 2, :], ACT.Relu).then_inc(k_relu, 1)
                    act.wait_ge(k_relu, c + 1)
                    act.activation(kk[:, cs(c)], kk[:, cs(c)], ACT.Square).then_inc(k_ready, 1)

            @block.gpsimd
            def _(pool):
                pool.memset(prev[:, 0:1], 0.0).then_inc(zeroed, 1)
                pool.tensor_copy(prev[:, 1:TOK], m.xn[:, 0:TOK - 1]).then_inc(prev_ready, 1)
                for c in range(NCH):
                    pool.wait_ge(gated, c + 1)
                    pool.tensor_tensor(m.x[:, cs(c)], m.x[:, cs(c)], rr[:, cs(c)], ALU.add).then_inc(added, 1)

            @block.vector
            def _(dve):
                dve.wait_ge(w_turned, 3)
                dve.tensor_copy(wt[:].rearrange("p i n -> p (i n)"), wps[:, 0:3 * P]).then_inc(w_ready, 1)
                for i in range(2):
                    dve.tensor_scalar(om[:, i:i + 1], m.col(mus[i]), -1.0, 1.0, ALU.mult, ALU.add).then_inc(om_ready, 1)
                dve.wait_ge(om_ready, 2)
                dve.wait_ge(zeroed, 1)
                dve.wait_ge(prev_ready, 1)
                for c in range(NCH):
                    for i in range(2):
                        dve.tensor_scalar(mix[:, i, cs(c)], prev[:, cs(c)], om[:, i:i + 1], None, ALU.mult).then_inc(first, 1)
                        dve.wait_ge(first, 2 * c + i + 1)
                        dve.scalar_tensor_tensor(out=mix[:, i, cs(c)], in0=m.xn[:, cs(c)], scalar=m.col(mus[i]),
                                                 in1=mix[:, i, cs(c)], op0=ALU.mult, op1=ALU.add).then_inc(mixed, 1)
                for c in range(NCH):
                    dve.wait_ge(v_ready, c + 1)
                    dve.wait_ge(r_ready, c + 1)
                    dve.tensor_tensor(rr[:, cs(c)], rr[:, cs(c)], vps[:, c % 2, :], ALU.mult).then_inc(gated, 1)



WIN = 32
LAT, LH = 64, 8
NEG = -1e30


def l2_window(nc, m, inp, r):
    STEPS = TOK // (2 * WIN)
    KW = 2 * WIN
    with ExitStack() as own:
        sb = lambda name, shape: own.enter_context(sbuf(nc, name, shape))
        xpad = sb("x_padded", [P, WIN + TOK])
        kg = sb("k_groups", [P, 4, WIN + TOK])
        mask = sb("window_mask", [P, KW])
        mask0 = sb("first_mask", [P, 2, KW])
        vmask = sb("v_mask", [P, 2, P])
        wv = sb("w_v", [P, P])
        qm = sb("q_masked", [P, 2, 2, 4, WIN])
        xw = sb("x_window", [P, 2, 2, 2, KW])
        x = sb("window_scores", [P, 2, 2 * 4, KW])
        st = sb("window_stats", [P, 2, 2, 8])
        pt = sb("window_pT", [P, 2, 4, P])
        vm = sb("v_masked", [P, 2, 2, 2, P])
        o = sb("window_o", [P, 2, 2, 4, WIN])
        load_all(nc, [(wv[:], inp["L2_attn_wv"])])
        vps = own.enter_context(psum(nc, "v_window", [P, 2, CH]))
        sps = own.enter_context(psum(nc, "window_qk", [P, 2, CH]))
        tps = own.enter_context(psum(nc, "window_turned", [P, 2, CH]))
        ops = own.enter_context(psum(nc, "window_out", [P, 2, CH]))
        with stage(nc, "padded", "k_cut", "masks_set", "vmask_set", "q_masked", "x_copied", "v_raw", "scored",
                      "v_masked", "shifted", "maxed", "less_max", "exped", "totaled", "inverted", "p_ready",
                      "turned", "pt_ready", "out_raw", "out_picked", "local_ready") as (
                block, padded, k_cut, masks_set, vmask_set, q_masked, x_copied, v_raw, scored, v_masked, shifted,
                maxed, less_max, exped, totaled, inverted, p_ready, turned, pt_ready, out_raw, out_picked,
                local_ready):

            def steps(eng, body):
                body(0, 0, True)
                body(1, 1, True)
                with eng.Fori(0, (STEPS - 4) // 2) as i:
                    body(i * 2 + 2, 0, False)
                    body(i * 2 + 3, 1, False)
                body(STEPS - 2, 0, False)
                body(STEPS - 1, 1, False)

            def at(t, s, off):
                return t[:, s * KW + off:s * KW + off + KW] if isinstance(s, int) else t[:, ds(s * KW + off, KW)]

            @block.gpsimd
            def _(pool):
                pool.memset(xpad[:, 0:WIN], 0.0).then_inc(padded, 1)
                pool.tensor_copy(xpad[:, WIN:], m.xn[:]).then_inc(padded, 1)
                pool.memset(kg[:, :, 0:WIN], 0.0).then_inc(padded, 1)
                pool.memset(mask[:], 0.0).then_inc(masks_set, 1)
                pool.wait_ge(masks_set, 1)
                for q in range(4):
                    part = mask[q * WIN:(q + 1) * WIN, :]
                    pool.affine_select(out=part, in_=part, compare_op=ALU.is_gt, fill=NEG, base=0,
                                       pattern=[[1, KW]], channel_multiplier=-1).then_inc(masks_set, 1)
                pool.wait_ge(masks_set, 5)
                for q in range(4):
                    part = mask[q * WIN:(q + 1) * WIN, :]
                    pool.affine_select(out=part, in_=part, compare_op=ALU.is_ge, fill=NEG, base=WIN,
                                       pattern=[[-1, KW]], channel_multiplier=1).then_inc(masks_set, 1)
                pool.wait_ge(masks_set, 9)
                for b in range(2):
                    pool.tensor_copy(mask0[:, b, :], mask[:]).then_inc(masks_set, 1)
                pool.wait_ge(masks_set, 11)
                pool.memset(mask0[:, 0, 0:WIN], NEG).then_inc(masks_set, 1)

                def body(s, par, first):
                    if not first:
                        pool.wait_ge(scored, s - 1)
                        pool.wait_ge(v_raw, s - 1)
                    if first and s == 0:
                        pool.wait_ge(padded, 3)
                    pool.tensor_tensor(qm[:, par], at(r.q, s, 0).rearrange("p (b i) -> p b i", b=2).unsqueeze(2)
                                       .to_broadcast([P, 2, 4, WIN]),
                                       m.hmod[:].unsqueeze(1).unsqueeze(3).to_broadcast([P, 2, 4, WIN]), ALU.mult)\
                        .then_inc(q_masked, 1)
                    for b in range(2):
                        win = at(xpad, s, b * WIN)
                        pool.tensor_copy(xw[:, par, b], win.unsqueeze(1).to_broadcast([P, 2, KW])).then_inc(x_copied, 1)

                steps(pool, body)

            @block.tensor
            def _(pe):
                pe.wait_ge(k_cut, 4)
                pe.wait_ge(padded, 3)

                def front(s, par, first):
                    pe.wait_ge(q_masked, s + 1)
                    pe.wait_ge(x_copied, s * 2 + 2)
                    if not first:
                        pe.wait_ge(shifted, s - 1)
                        pe.wait_ge(v_masked, (s - 1) * 2)
                    for b in range(2):
                        mm = pe.matmul(vps[:, par, b * P:(b + 1) * P], xw[:, par, b].rearrange("p a j -> p (a j)"), wv[:],
                                       start=True, stop=True)
                    mm.then_inc(v_raw, 1)
                    for b in range(2):
                        keys = kg[:, :, (s * 2 + b) * WIN:(s * 2 + b + 2) * WIN] if isinstance(s, int) \
                            else kg[:, :, ds(s * KW + b * WIN, KW)]
                        mm = pe.matmul(sps[:, par, b * 256:(b + 1) * 256], qm[:, par, b].rearrange("p a i -> p (a i)"), keys,
                                       start=True, stop=True)
                    mm.then_inc(scored, 1)

                def back(s, par, first):
                    pe.wait_ge(p_ready, s + 1)
                    if not first:
                        pe.wait_ge(pt_ready, s - 1)
                        pe.wait_ge(out_picked, s - 1)
                    for i in range(4):
                        mm = pe.transpose(tps[:, par, i * P:(i + 1) * P],
                                          x[:, par, 2 * i:2 * i + 2, :].rearrange("p g j -> p (g j)"), m.ident[:])
                    mm.then_inc(turned, 1)
                    pe.wait_ge(pt_ready, s + 1)
                    pe.wait_ge(v_masked, s * 2 + 2)
                    for b in range(2):
                        for i in range(2):
                            mm = pe.matmul(ops[:, par, b * P:(b + 1) * P], vm[:, par, b, i, :], pt[:, par, 2 * b + i, :],
                                           start=(i == 0), stop=(i == 1))
                    mm.then_inc(out_raw, 1)

                def body(s, par, first):
                    if not isinstance(s, int) or s + 1 < STEPS:
                        front(s + 1, 1 - par, first and s == 0)
                    back(s, par, first)

                front(0, 0, True)
                steps(pe, body)

            @block.scalar
            def _(act):
                def body(s, par, first):
                    act.wait_ge(less_max, s + 1)
                    act.activation(x[:, par], x[:, par], ACT.Exp).then_inc(exped, 1)
                    act.wait_ge(turned, s + 1)
                    if not first:
                        act.wait_ge(out_raw, s - 1)
                    act.activation(pt[:, par].rearrange("p a n -> p (a n)"), tps[:, par, :], ACT.Copy).then_inc(pt_ready, 1)

                steps(act, body)

            @block.vector
            def _(dve):
                for g in range(4):
                    dve.tensor_scalar(kg[:, g, WIN:], r.k[:], m.hdiv[:, g:g + 1], None, ALU.mult).then_inc(k_cut, 1)
                for i in range(2):
                    for pair in range(2):
                        g = 2 * pair + i
                        dve.tensor_scalar(vmask[i * 64:(i + 1) * 64, pair, :], m.ones[i * 64:(i + 1) * 64, :], 0.0, None,
                                          ALU.mult).then_inc(vmask_set, 1)
                        dve.wait_ge(vmask_set, 2 * (2 * i + pair) + 1)
                        dve.memset(vmask[i * 64:(i + 1) * 64, pair, 32 * g:32 * g + 32], 1.0).then_inc(vmask_set, 1)
                dve.wait_ge(vmask_set, 8)
                dve.wait_ge(masks_set, 12)
                G8 = [P, 8, KW]

                def front(s, par, first):
                    if not first:
                        dve.wait_ge(out_raw, s - 1)
                        dve.wait_ge(turned, s - 1)
                    dve.wait_ge(v_raw, s + 1)
                    for b in range(2):
                        dve.tensor_tensor(vm[:, par, b], vps[:, par, b * P:(b + 1) * P].unsqueeze(1).to_broadcast([P, 2, P]),
                                          vmask[:], ALU.mult).then_inc(v_masked, 1)
                    dve.wait_ge(scored, s + 1)
                    if first and s == 0:
                        mk = mask0[:].unsqueeze(2).to_broadcast([P, 2, 4, KW])
                        for b in range(2):
                            ins = dve.scalar_tensor_tensor(
                                out=x[:, par, 4 * b:4 * b + 4], in0=sps[:, par, b * 256:(b + 1) * 256].rearrange("p (g j) -> p g j", j=KW),
                                scalar=HD ** -0.5, in1=mk[:, b], op0=ALU.mult, op1=ALU.add)
                        ins.then_inc(shifted, 1)
                    else:
                        dve.scalar_tensor_tensor(out=x[:, par], in0=sps[:, par, :].rearrange("p (g j) -> p g j", j=KW),
                                                 scalar=HD ** -0.5, in1=mask[:].unsqueeze(1).to_broadcast(G8),
                                                 op0=ALU.mult, op1=ALU.add).then_inc(shifted, 1)
                    dve.wait_ge(shifted, s + 1)
                    dve.tensor_reduce(st[:, par, 0, :], x[:, par], AX.X, ALU.max).then_inc(maxed, 1)
                    dve.wait_ge(maxed, s + 1)
                    dve.tensor_tensor(x[:, par], x[:, par], st[:, par, 0, :].unsqueeze(2).to_broadcast(G8), ALU.subtract)\
                       .then_inc(less_max, 1)

                def middle(s, par):
                    dve.wait_ge(exped, s + 1)
                    dve.tensor_reduce(st[:, par, 1, :], x[:, par], AX.X, ALU.add).then_inc(totaled, 1)
                    dve.wait_ge(totaled, s + 1)
                    dve.reciprocal(st[:, par, 1, :], st[:, par, 1, :]).then_inc(inverted, 1)
                    dve.wait_ge(inverted, s + 1)
                    dve.tensor_tensor(x[:, par], x[:, par], st[:, par, 1, :].unsqueeze(2).to_broadcast(G8), ALU.mult)\
                       .then_inc(p_ready, 1)

                def back(s, par):
                    dve.wait_ge(out_raw, s + 1)
                    dve.tensor_tensor(o[:, par], ops[:, par, 0:2 * P].rearrange("p (b a i) -> p b a i", b=2, a=4),
                                      m.hmod[:].unsqueeze(1).unsqueeze(3).to_broadcast([P, 2, 4, WIN]), ALU.mult)\
                       .then_inc(out_picked, 1)
                    dve.wait_ge(out_picked, s + 1)
                    dve.tensor_reduce(at(r.local, s, 0).rearrange("p (b i) -> p b i", b=2),
                                      o[:, par].rearrange("p b a i -> p b i a"), AX.X, ALU.add).then_inc(local_ready, 1)

                def body(s, par, first):
                    middle(s, par)
                    if not isinstance(s, int) or s + 1 < STEPS:
                        front(s + 1, 1 - par, first and s == 0)
                    back(s, par)

                front(0, 0, True)
                steps(dve, body)


def l2_latent(nc, m, inp, r):
    NL = LAT
    W = LH * NL
    LD = 64
    with ExitStack() as own:
        sb = lambda name, shape: own.enter_context(sbuf(nc, name, shape))
        wg = sb("w_latent", [P, 3, LD])
        pool2 = sb("pooled", [P, 2, NL])
        gk = sb("latent_keys", [LD, LH, NL])
        gv = sb("latent_values", [P, 4, LD])
        lmask = sb("latent_mask", [P, NT, NL])
        gq = sb("latent_q", [LD, 2, P])
        x = sb("latent_scores", [P, 2, LH, NL])
        st = sb("latent_stats", [P, 2, 2, LH])
        pt = sb("latent_pT", [P, 2, 4, P])
        pm = sb("pooled_mean", [P, NL])
        load_all(nc, [(wg[:, 0, :], inp["L2_attn_wgq"]), (wg[:, 1, :], inp["L2_attn_wgk"]), (wg[:, 2, :], inp["L2_attn_wgv"])])
        cps = own.enter_context(psum(nc, "latent_const", [P, CH]))
        qps = own.enter_context(psum(nc, "latent_q_raw", [P, CH]))
        sps = own.enter_context(psum(nc, "latent_qk", [P, 2, CH]))
        tps = own.enter_context(psum(nc, "latent_turned", [P, 2, CH]))
        rps = own.enter_context(psum(nc, "latent_out", [LD, 2, CH]))
        with stage(nc, "mask_set", "pooled", "kv_raw", "blocks", "q_raw", "q_ready", "scored", "shifted", "maxed",
                      "less_max", "exped", "totaled", "inverted", "p_ready", "turned", "pt_ready", "out_raw",
                      "rem_ready") as (
                block, mask_set, pooled, kv_raw, blocks, q_raw, q_ready, scored, shifted, maxed, less_max, exped,
                totaled, inverted, p_ready, turned, pt_ready, out_raw, rem_ready):

            def steps(eng, body):
                body(0, 0, True)
                body(1, 1, True)
                with eng.Fori(0, (NT - 4) // 2) as i:
                    body(i * 2 + 2, 0, False)
                    body(i * 2 + 3, 1, False)
                body(NT - 2, 0, False)
                body(NT - 1, 1, False)

            def tile(t, n):
                return t[:, n * P:(n + 1) * P] if isinstance(n, int) else t[:, ds(n * P, P)]

            @block.gpsimd
            def _(pool):
                pool.memset(lmask[:], 0.0).then_inc(mask_set, 1)
                pool.wait_ge(mask_set, 1)
                for q in range(4):
                    part = lmask[q * 32:(q + 1) * 32]
                    pool.affine_select(out=part, in_=part, compare_op=ALU.is_ge, fill=NEG, base=q,
                                       pattern=[[4, NT], [-1, NL]], channel_multiplier=0).then_inc(mask_set, 1)

            @block.tensor
            def _(pe):
                pe.wait_ge(pooled, 3)
                pe.matmul(cps[0:LD, 0:NL], wg[:, 1, :], pm[:], start=True, stop=True)
                pe.matmul(cps[:, NL:NL + LD], pool2[:].rearrange("p a n -> p (a n)"), wg[:, 2, :], start=True, stop=True)\
                  .then_inc(kv_raw, 1)
                pe.wait_ge(blocks, 10)

                def front(n, par, first):
                    if not (isinstance(n, int) and n == 0):
                        pe.wait_ge(q_ready, n)
                    pe.matmul(qps[0:LD, 0:P], wg[:, 0, :], tile(m.xn, n), start=True, stop=True).then_inc(q_raw, 1)
                    pe.wait_ge(q_ready, n + 1)
                    if not first:
                        pe.wait_ge(shifted, n - 1)
                    pe.matmul(sps[:, par, :], gq[:, par, :], gk[:].rearrange("p h n -> p (h n)"), start=True, stop=True)\
                      .then_inc(scored, 1)

                def back(n, par, first):
                    pe.wait_ge(p_ready, n + 1)
                    if not first:
                        pe.wait_ge(pt_ready, n - 1)
                        pe.wait_ge(rem_ready, n - 1)
                    for i in range(4):
                        mm = pe.transpose(tps[:, par, i * P:(i + 1) * P],
                                          x[:, par, 2 * i:2 * i + 2, :].rearrange("p g j -> p (g j)"), m.ident[:])
                    mm.then_inc(turned, 1)
                    pe.wait_ge(pt_ready, n + 1)
                    for i in range(4):
                        mm = pe.matmul(rps[:, par, 0:P], gv[:, i, :], pt[:, par, i, :], start=(i == 0), stop=(i == 3))
                    mm.then_inc(out_raw, 1)

                def body(n, par, first):
                    if not isinstance(n, int) or n + 1 < NT:
                        front(n + 1, 1 - par, first and n == 0)
                    back(n, par, first)

                front(0, 0, True)
                steps(pe, body)

            @block.scalar
            def _(act):
                def copy_q(n, par, first):
                    act.wait_ge(q_raw, n + 1)
                    if not first:
                        act.wait_ge(scored, n - 1)
                    act.activation(gq[:, par, :], qps[0:LD, 0:P], ACT.Copy).then_inc(q_ready, 1)

                def body(n, par, first):
                    act.wait_ge(less_max, n + 1)
                    act.activation(x[:, par], x[:, par], ACT.Exp).then_inc(exped, 1)
                    if not isinstance(n, int) or n + 1 < NT:
                        copy_q(n + 1, 1 - par, first and n == 0)
                    act.wait_ge(turned, n + 1)
                    if not first:
                        act.wait_ge(out_raw, n - 1)
                    act.activation(pt[:, par].rearrange("p a n -> p (a n)"), tps[:, par, :], ACT.Copy).then_inc(pt_ready, 1)

                copy_q(0, 0, True)
                steps(act, body)

            @block.vector
            def _(dve):
                CHUNK = TOK // NL
                dve.tensor_reduce(pm[:], m.xn[:].rearrange("p (n c) -> p n c", c=CHUNK), AX.X, ALU.add).then_inc(pooled, 1)
                dve.wait_ge(pooled, 1)
                dve.tensor_scalar(pm[:], pm[:], 1.0 / CHUNK, None, ALU.mult).then_inc(pooled, 1)
                dve.wait_ge(pooled, 2)
                dve.tensor_copy(pool2[:], pm[:].unsqueeze(1).to_broadcast([P, 2, NL])).then_inc(pooled, 1)
                dve.wait_ge(kv_raw, 1)
                dve.tensor_tensor(gk[:], cps[0:LD, 0:NL].unsqueeze(1).to_broadcast([LD, LH, NL]),
                                  m.head_ones[0:LD, 0:LD].rearrange("p (h e) -> p h e", e=HD)[:, :, 0:1]
                                  .to_broadcast([LD, LH, NL]), ALU.mult).then_inc(blocks, 1)
                dve.tensor_scalar(gv[:], m.ones[:, 0:64].unsqueeze(1).to_broadcast([P, 4, LD]), 0.0, None, ALU.mult)\
                   .then_inc(blocks, 1)
                dve.wait_ge(blocks, 2)
                for i in range(4):
                    for half in range(2):
                        h = 2 * i + half
                        rows = slice(half * 64, half * 64 + 64)
                        dve.tensor_copy(gv[rows, i, HD * h:HD * h + HD], cps[rows, NL + HD * h:NL + HD * h + HD])\
                           .then_inc(blocks, 1)
                dve.wait_ge(mask_set, 5)
                G8 = [P, LH, NL]

                def front(n, par, first):
                    if not first:
                        dve.wait_ge(turned, n - 1)
                    mk = lmask[:, n:n + 1, :] if isinstance(n, int) else lmask[:, ds(n, 1), :]
                    dve.wait_ge(scored, n + 1)
                    dve.scalar_tensor_tensor(out=x[:, par], in0=sps[:, par, :].rearrange("p (g j) -> p g j", j=NL),
                                             scalar=HD ** -0.5, in1=mk.to_broadcast(G8),
                                             op0=ALU.mult, op1=ALU.add).then_inc(shifted, 1)
                    dve.wait_ge(shifted, n + 1)
                    dve.tensor_reduce(st[:, par, 0, :], x[:, par], AX.X, ALU.max).then_inc(maxed, 1)
                    dve.wait_ge(maxed, n + 1)
                    dve.tensor_tensor(x[:, par], x[:, par], st[:, par, 0, :].unsqueeze(2).to_broadcast(G8), ALU.subtract)\
                       .then_inc(less_max, 1)

                def middle(n, par):
                    dve.wait_ge(exped, n + 1)
                    dve.tensor_reduce(st[:, par, 1, :], x[:, par], AX.X, ALU.add).then_inc(totaled, 1)
                    dve.wait_ge(totaled, n + 1)
                    dve.reciprocal(st[:, par, 1, :], st[:, par, 1, :]).then_inc(inverted, 1)
                    dve.wait_ge(inverted, n + 1)
                    dve.tensor_tensor(x[:, par], x[:, par], st[:, par, 1, :].unsqueeze(2).to_broadcast(G8), ALU.mult)\
                       .then_inc(p_ready, 1)

                def body(n, par, first):
                    middle(n, par)
                    if not isinstance(n, int) or n + 1 < NT:
                        front(n + 1, 1 - par, first and n == 0)
                    dve.wait_ge(out_raw, n + 1)
                    dve.tensor_copy(tile(r.rem, n), rps[:, par, 0:P]).then_inc(rem_ready, 1)

                front(0, 0, True)
                steps(dve, body)


def layer2_attention(nc, m, inp):
    with ExitStack() as own:
        sb = lambda name, shape: own.enter_context(sbuf(nc, name, shape))
        r = Named()
        r.q, r.local, r.rem = sb("l2_q", [P, TOK]), sb("l2_local", [P, TOK]), sb("l2_rem", [64, TOK])
        w = sb("w_l2", [P, 3, P])
        wr = sb("w_r_out", [64, P])
        gate_w = sb("gate_blocks", [P, 2, P])
        load_all(nc, [(w[:, 0, :], inp["L2_attn_wq"]), (w[:, 1, :], inp["L2_attn_wk"]), (w[:, 2, :], inp["L2_attn_w_out"]),
                      (wr[:], inp["L2_attn_r_out_w"])])
        with ExitStack() as inner:
            r.k = inner.enter_context(sbuf(nc, "l2_k", [P, TOK]))
            with psum(nc, "qk_proj", [P, 2, NCH, CH]) as ps, stage(nc, "q_raw", "k_raw", "q_ready", "k_ready", "gates") as (
                    block, q_raw, k_raw, q_ready, k_ready, gates):
                @block.tensor
                def _(pe):
                    for c in range(NCH):
                        pe.matmul(ps[:, 0, c, :], w[:, 0, :], m.xn[:, cs(c)], start=True, stop=True).then_inc(q_raw, 1)
                        pe.matmul(ps[:, 1, c, :], w[:, 1, :], m.xn[:, cs(c)], start=True, stop=True).then_inc(k_raw, 1)

                @block.scalar
                def _(act):
                    for c in range(NCH):
                        act.wait_ge(q_raw, c + 1)
                        act.activation(r.q[:, cs(c)], ps[:, 0, c, :], ACT.Copy).then_inc(q_ready, 1)

                @block.vector
                def _(dve):
                    for i, name in enumerate(("L2_attn_gate_local_w", "L2_attn_gate_remote_w")):
                        dve.tensor_scalar(gate_w[:, i, :], m.head_ones[:], m.col(name), None, ALU.mult).then_inc(gates, 1)
                    for c in range(NCH):
                        dve.wait_ge(k_raw, c + 1)
                        dve.tensor_copy(r.k[:, cs(c)], ps[:, 1, c, :]).then_inc(k_ready, 1)
            l2_window(nc, m, inp, r)
        l2_latent(nc, m, inp, r)
        gate = sb("gates", [P, 2, 2, CH])
        gps = own.enter_context(psum(nc, "gate_logits", [P, 2, 2, CH]))
        rps = own.enter_context(psum(nc, "rem_proj", [P, 2, CH]))
        ops = own.enter_context(psum(nc, "l2_out", [P, 2, CH]))
        with stage(nc, "logits", "gated", "rem_raw", "local_scaled", "rem_scaled", "mixed", "projected", "added") as (
                block, logits, gated, rem_raw, local_scaled, rem_scaled, mixed, projected, added):
            @block.tensor
            def _(pe):
                def project(c):
                    pe.wait_ge(mixed, c + 1)
                    if c >= 2:
                        pe.wait_ge(added, c - 1)
                    pe.matmul(ops[:, c % 2, :], w[:, 2, :], r.local[:, cs(c)], start=True, stop=True).then_inc(projected, 1)

                for c in range(NCH):
                    if c >= 2:
                        pe.wait_ge(gated, 2 * c - 2)
                        pe.wait_ge(rem_scaled, c - 1)
                    for i in range(2):
                        pe.matmul(gps[:, i, c % 2, :], gate_w[:, i, :], r.q[:, cs(c)], start=True, stop=True).then_inc(logits, 1)
                    pe.matmul(rps[:, c % 2, :], wr[:], r.rem[:, cs(c)], start=True, stop=True).then_inc(rem_raw, 1)
                    if c:
                        project(c - 1)
                project(NCH - 1)

            @block.scalar
            def _(act):
                for c in range(NCH):
                    if c >= 2:
                        act.wait_ge(mixed, c - 1)
                    for i in range(2):
                        act.wait_ge(logits, 2 * c + i + 1)
                        act.activation(gate[:, i, c % 2, :], gps[:, i, c % 2, :], ACT.Sigmoid).then_inc(gated, 1)

            @block.vector
            def _(dve):
                def add(c):
                    dve.wait_ge(projected, c + 1)
                    dve.tensor_tensor(m.x[:, cs(c)], ops[:, c % 2, :], m.x[:, cs(c)], ALU.add).then_inc(added, 1)

                for c in range(NCH):
                    dve.wait_ge(gated, 2 * c + 1)
                    dve.tensor_tensor(r.local[:, cs(c)], r.local[:, cs(c)], gate[:, 0, c % 2, :], ALU.mult).then_inc(local_scaled, 1)
                    dve.wait_ge(gated, 2 * c + 2)
                    dve.wait_ge(rem_raw, c + 1)
                    dve.tensor_tensor(gate[:, 1, c % 2, :], rps[:, c % 2, :], gate[:, 1, c % 2, :], ALU.mult).then_inc(rem_scaled, 1)
                    dve.wait_ge(rem_scaled, c + 1)
                    dve.wait_ge(local_scaled, c + 1)
                    dve.tensor_tensor(r.local[:, cs(c)], r.local[:, cs(c)], gate[:, 1, c % 2, :], ALU.add).then_inc(mixed, 1)
                    if c:
                        add(c - 1)
                add(NCH - 1)



F16 = mybir.dt.float16


def layer3_attention(nc, m, inp):
    H, DH = 16, 64
    SCALE, EPS = DH ** -0.5, 1e-8
    LIFT = 14
    RB = 5
    VW = 2 * DH + 1
    N_CH = NT * NCH
    bank = lambda t, c: (t * NCH + (NCH - 1 - c)) % RB
    groups = lambda t: t // 4 + 1
    G = sum(groups(t) for t in range(NT))
    g0 = lambda t: sum(groups(x) for x in range(t))
    with ExitStack() as own:
        sb = lambda name, shape, dt=F32: own.enter_context(nc.sbuf_tensor(f"{name}_{nc.next_id()}", shape, dt))
        o_all = sb("o_all", [P, NT, H * DH])
        with ExitStack() as inner:
            sb = lambda name, shape, dt=F32: inner.enter_context(nc.sbuf_tensor(f"{name}_{nc.next_id()}", shape, dt))
            wq, wk, wv = sb("w_q2", [P, 2, DH]), sb("w_k2", [P, 2, DH]), sb("w_v", [P, DH])
            qs, kh, kl = (sb(n, [P, TOK], F16) for n in ("q_pair", "k_high", "k_low"))
            v = sb("v_pair", [P, NT, VW], F16)
            p = sb("p", [P, 2, TOK])
            ph, pl = sb("pT_high", [P, 2, CH], F16), sb("pT_low", [P, 2, CH], F16)
            tri = sb("past", [P, P])
            mx, bias = sb("chunk_max", [P, 2, NCH]), sb("exp_bias", [P, 2, 2])
            olow, osum, den = sb("o_low", [P, DH]), sb("o_sum", [P, DH]), sb("den", [P, 2])
            ps = inner.enter_context(psum(nc, "scores", [P, 8, CH]))
            with stage(nc, "w_loaded", "w_used", "const_set", "q_raw", "k_raw", "v_raw", "q_high", "q_low", "k_highs",
                          "k_lows", "v_high", "v_low", "scored", "chunk_maxed", "tile_maxed", "biased", "exped",
                          "masked", "turned", "pt_high", "pt_low", "summed", "o_lowed", "o_summed", "den_set",
                          "den_inverted", "o_ready") as (
                    block, w_loaded, w_used, const_set, q_raw, k_raw, v_raw, q_high, q_low, k_highs, k_lows, v_high,
                    v_low, scored, chunk_maxed, tile_maxed, biased, exped, masked, turned, pt_high, pt_low,
                    summed, o_lowed, o_summed, den_set, den_inverted, o_ready):

                @block.sync
                def _(sp):
                    with sp.Fori(0, H) as h:
                        sp.wait_ge(w_used, h)
                        for dst, src in ((wq, inp["L3_attn_Wq"]), (wk, inp["L3_attn_Wkv"])):
                            for r in range(2):
                                sp.dma_start(dst[:, r, :], src[:, ds(h * DH, DH)]).then_inc(w_loaded, 16)
                        sp.dma_start(wv[:], inp["L3_attn_Wkv"][:, ds(h * DH + H * DH, DH)]).then_inc(w_loaded, 16)

                @block.gpsimd
                def _(pool):
                    pool.memset(tri[:], 1.0).then_inc(const_set, 1)
                    pool.memset(v[:, :, 2 * DH:VW], 1.0).then_inc(const_set, 1)
                    pool.wait_ge(const_set, 2)
                    pool.affine_select(out=tri[:], in_=tri[:], compare_op=ALU.is_ge, fill=0.0, base=0,
                                       pattern=[[-1, P]], channel_multiplier=1).then_inc(const_set, 1)
                    pool.wait_ge(const_set, 3)
                    with pool.Fori(0, H) as h:
                        for t in range(NT):
                            pool.wait_ge(exped, h * G + g0(t + 1))
                            diag = p[:, t % 2, t * P:(t + 1) * P]
                            pool.tensor_tensor(diag, diag, tri[:], ALU.mult).then_inc(masked, 1)

                @block.tensor
                def _(pe):
                    with pe.Fori(0, H) as h:
                        pe.wait_ge(w_loaded, h * 80 + 80)
                        pe.wait_ge(exped, h * G)
                        pe.wait_ge(chunk_maxed, h * N_CH)
                        pe.wait_ge(pt_low, h * G)
                        pe.wait_ge(o_summed, h * NT)
                        for c in range(NCH):
                            pe.matmul(ps[:, c, :], wq[:].rearrange("p r d -> p (r d)"), m.xn[:, cs(c)],
                                      start=True, stop=True).then_inc(q_raw, 1)
                        for c in range(NCH):
                            pe.matmul(ps[:, 4 + c, :], wk[:].rearrange("p r d -> p (r d)"), m.xn[:, cs(c)],
                                      start=True, stop=True).then_inc(k_raw, 1)
                        for n in range(NT):
                            if n % 8 == 0:
                                pe.wait_ge(q_low, h * NCH + n // 8 + 1)
                            mm = pe.matmul(ps[:, n // 8, n % 8 * DH:(n % 8 + 1) * DH], m.xn[:, n * P:(n + 1) * P], wv[:],
                                           start=True, stop=True)
                            if n % 8 == 7:
                                mm.then_inc(v_raw, 1)
                        pe.wait_ge(v_raw, h * 2 + 2)
                        pe.sem_inc(w_used, 1)
                        pe.wait_ge(v_low, h * 2 + 2)
                        pe.wait_ge(k_lows, h * NCH + NCH)

                        def scores(t):
                            for c in reversed(range(NCH)):
                                k = t * NCH + NCH - 1 - c
                                if k >= RB:
                                    t1, c1 = divmod(k - RB, NCH)
                                    c1 = NCH - 1 - c1
                                    pe.wait_ge(chunk_maxed, h * N_CH + k - RB + 1)
                                    if c1 < groups(t1):
                                        pe.wait_ge(exped, h * G + g0(t1) + groups(t1) - c1)
                                b = bank(t, c)
                                pe.matmul(ps[:, b, :], qs[:, t * P:(t + 1) * P], kh[:, cs(c)], start=True, stop=False)
                                pe.matmul(ps[:, b, :], qs[:, t * P:(t + 1) * P], kl[:, cs(c)], start=False, stop=True)\
                                  .then_inc(scored, 1)

                        def turn(t, g):
                            n = g0(t) + g
                            if n >= 2:
                                pe.wait_ge(pt_low, h * G + n - 1)
                            if g == 0:
                                pe.wait_ge(masked, h * NT + t + 1)
                            for b in range(4 * g, min(4 * g + 4, t + 1)):
                                mm = pe.transpose(ps[:, 5 + n % 2, b % 4 * P:(b % 4 + 1) * P],
                                                  p[:, t % 2, b * P:(b + 1) * P], m.ident[:])
                            mm.then_inc(turned, 1)

                        def add_up(t, g):
                            n = g0(t) + g
                            pe.wait_ge(pt_low, h * G + n + 1)
                            if g == 0 and t:
                                pe.wait_ge(o_summed, h * NT + t)
                            for b in range(4 * g, min(4 * g + 4, t + 1)):
                                for part in (ph, pl):
                                    mm = pe.matmul(ps[:, 7, 0:VW], part[:, n % 2, b % 4 * P:(b % 4 + 1) * P], v[:, b, :],
                                                   start=(b == 0 and part is ph), stop=(b == t and part is pl))
                            mm.then_inc(summed, 1)

                        scores(0)
                        for t in range(NT):
                            if t + 1 < NT:
                                scores(t + 1)
                            turn(t, 0)
                            for g in range(1, groups(t)):
                                turn(t, g)
                                add_up(t, g - 1)
                            add_up(t, groups(t) - 1)

                @block.scalar
                def _(act):
                    with act.Fori(0, H) as h:
                        act.wait_ge(summed, h * G)
                        for c in range(NCH):
                            act.wait_ge(q_raw, h * NCH + c + 1)
                            act.activation(qs[:, cs(c)], ps[:, c, :], ACT.Copy).then_inc(q_high, 1)
                        for c in range(NCH):
                            act.wait_ge(k_raw, h * NCH + c + 1)
                            act.activation(kh[:, cs(c)], ps[:, 4 + c, :], ACT.Copy).then_inc(k_highs, 1)
                        for i in range(2):
                            act.wait_ge(v_raw, h * 2 + i + 1)
                            act.activation(v[:, 8 * i:8 * i + 8, 0:DH], ps[:, i, :].rearrange("p (n d) -> p n d", d=DH),
                                           ACT.Copy).then_inc(v_high, 1)
                        for t in range(NT):
                            if t >= 2:
                                act.wait_ge(turned, h * G + g0(t - 1))
                            act.wait_ge(biased, h * NT + t + 1)
                            for c in reversed(range(groups(t))):
                                w = min(CH, (t + 1) * P - c * CH)
                                act.activation(p[:, t % 2, c * CH:c * CH + w], ps[:, bank(t, c), 0:w], ACT.Exp,
                                               bias=bias[:, t % 2, 1:2], scale=SCALE).then_inc(exped, 1)
                            for g in range(groups(t)):
                                n = g0(t) + g
                                w = min(CH, (t + 1) * P - g * CH)
                                act.wait_ge(turned, h * G + n + 1)
                                if n >= 2:
                                    act.wait_ge(summed, h * G + n - 1)
                                act.activation(ph[:, n % 2, 0:w], ps[:, 5 + n % 2, 0:w], ACT.Copy).then_inc(pt_high, 1)
                            act.wait_ge(summed, h * G + g0(t + 1))
                            if t:
                                act.wait_ge(o_summed, h * NT + t)
                            act.activation(olow[:], ps[:, 7, DH:2 * DH], ACT.Copy).then_inc(o_lowed, 1)

                @block.vector
                def _(dve):
                    with dve.Fori(0, H) as h:
                        hi = slice(DH, P)
                        for c in range(NCH):
                            dve.wait_ge(q_high, h * NCH + c + 1)
                            dve.tensor_tensor(qs[hi, cs(c)], ps[hi, c, :], qs[hi, cs(c)], ALU.subtract).then_inc(q_low, 1)
                        for c in range(NCH):
                            dve.wait_ge(k_highs, h * NCH + c + 1)
                            dve.tensor_tensor(kl[:, cs(c)], ps[:, 4 + c, :], kh[:, cs(c)], ALU.subtract).then_inc(k_lows, 1)
                        for i in range(2):
                            dve.wait_ge(v_high, h * 2 + i + 1)
                            dve.tensor_tensor(v[:, 8 * i:8 * i + 8, DH:2 * DH], ps[:, i, :].rearrange("p (n d) -> p n d", d=DH),
                                              v[:, 8 * i:8 * i + 8, 0:DH], ALU.subtract).then_inc(v_low, 1)

                        def maxima(t):
                            for c in reversed(range(NCH)):
                                dve.wait_ge(scored, h * N_CH + t * NCH + NCH - c)
                                dve.tensor_reduce(mx[:, t % 2, c:c + 1], ps[:, bank(t, c), :], AX.X, ALU.max)\
                                   .then_inc(chunk_maxed, 1)
                            dve.wait_ge(chunk_maxed, h * N_CH + (t + 1) * NCH)
                            dve.tensor_reduce(bias[:, t % 2, 0:1], mx[:, t % 2, :], AX.X, ALU.max).then_inc(tile_maxed, 1)
                            dve.wait_ge(tile_maxed, h * NT + t + 1)
                            if t >= 2:
                                dve.wait_ge(exped, h * G + g0(t - 1))
                            dve.tensor_scalar(bias[:, t % 2, 1:2], bias[:, t % 2, 0:1], -SCALE, LIFT * 0.6931471805599453,
                                              ALU.mult, ALU.add).then_inc(biased, 1)

                        maxima(0)
                        for t in range(NT):
                            if t + 1 < NT:
                                maxima(t + 1)
                            for g in range(groups(t)):
                                n = g0(t) + g
                                w = min(CH, (t + 1) * P - g * CH)
                                dve.wait_ge(pt_high, h * G + n + 1)
                                dve.tensor_tensor(pl[:, n % 2, 0:w], ps[:, 5 + n % 2, 0:w], ph[:, n % 2, 0:w], ALU.subtract)\
                                   .then_inc(pt_low, 1)
                            dve.wait_ge(o_lowed, h * NT + t + 1)
                            dve.tensor_scalar(den[:, 0:1], ps[:, 7, 2 * DH:VW], EPS * 2.0 ** LIFT, None, ALU.add)\
                               .then_inc(den_set, 1)
                            if t:
                                dve.wait_ge(o_ready, h * NT + t)
                            dve.tensor_tensor(osum[:], ps[:, 7, 0:DH], olow[:], ALU.add).then_inc(o_summed, 1)
                            dve.wait_ge(den_set, h * NT + t + 1)
                            dve.reciprocal(den[:, 1:2], den[:, 0:1]).then_inc(den_inverted, 1)
                            dve.wait_ge(o_summed, h * NT + t + 1)
                            dve.wait_ge(den_inverted, h * NT + t + 1)
                            dve.tensor_scalar(o_all[:, t, ds(h * DH, DH)], osum[:], den[:, 1:2], None, ALU.mult)\
                               .then_inc(o_ready, 1)
        wo = own.enter_context(sbuf(nc, "w_o3", [P, H * DH // P, P]))
        oT = own.enter_context(sbuf(nc, "o_T", [P, 2, CH]))
        tps = own.enter_context(psum(nc, "o_turned", [P, 2, CH]))
        ops = own.enter_context(psum(nc, "o_proj", [P, NCH, CH]))
        KT = H * DH // P
        load_all(nc, [(wo[:], inp["L3_attn_Wo"].rearrange("(k p) n -> p k n", p=P))])
        with stage(nc, "turned", "copied", "projected", "added") as (block, turned, copied, projected, added):
            @block.tensor
            def _(pe):
                def project(i):
                    c, k = divmod(i, KT)
                    pe.wait_ge(copied, i + 1)
                    pe.matmul(ops[:, c, :], wo[:, k, :], oT[:, i % 2, :], start=(k == 0), stop=(k == KT - 1)).then_inc(projected, 1)

                for i in range(NCH * KT):
                    c, k = divmod(i, KT)
                    if i >= 2:
                        pe.wait_ge(copied, i - 1)
                    for n in range(4):
                        mm = pe.transpose(tps[:, i % 2, n * P:(n + 1) * P], o_all[:, 4 * c + n, k * P:(k + 1) * P], m.ident[:])
                    mm.then_inc(turned, 1)
                    if i:
                        project(i - 1)
                project(NCH * KT - 1)

            @block.scalar
            def _(act):
                for i in range(NCH * KT):
                    act.wait_ge(turned, i + 1)
                    if i >= 2:
                        act.wait_ge(projected, i - 1)
                    act.activation(oT[:, i % 2, :], tps[:, i % 2, :], ACT.Copy).then_inc(copied, 1)

            @block.vector
            def _(dve):
                for c in range(NCH):
                    dve.wait_ge(projected, (c + 1) * KT)
                    dve.scalar_tensor_tensor(out=m.x[:, cs(c)], in0=ops[:, c, :], scalar=m.col("L3_attn_bo"),
                                             in1=m.x[:, cs(c)], op0=ALU.add, op1=ALU.add).then_inc(added, 1)



def build(nc, inp, out):
    with ExitStack() as own:
        m = Named()
        alloc = lambda name, shape: own.enter_context(sbuf(nc, name, shape))
        constants(nc, m, inp, alloc)
        m.x = alloc("x_features", [P, TOK])
        m.xn = alloc("xn_features", [P, TOK])
        turn_in(nc, m, inp["L0_attn_x"])
        for attention, ffn in ((layer0_attention, layer0_experts), (layer1_attention, layer1_ffn),
                               (layer2_attention, layer2_ffn), (layer3_attention, layer3_experts)):
            layernorm(nc, m, m.x, m.xn, LN_EPS)
            attention(nc, m, inp)
            ffn(nc, m, inp)
        turn_out(nc, m, out)


_OUTS = [((1, 2048, 128), 'float32')]


def kernel(**inputs):
    import numpy as _np
    import concourse.bacc as _bacc
    from concourse import mybir as _mybir
    from concourse.bass_utils import run_bass_kernel_spmd as _run

    nc = _bacc.Bacc("TRN2", target_bir_lowering=False, num_devices=1)
    arrays, args = {}, {}
    for name in inputs:
        a = _np.ascontiguousarray(inputs[name])
        arrays[f"in_{name}_dram"] = a
        args[name] = nc.dram_tensor(f"in_{name}_dram", a.shape, _mybir.dt.from_np(a.dtype), kind="ExternalInput").ap()
    shape, dtype = _OUTS[0]
    out = nc.dram_tensor("out_0_dram", shape, _mybir.dt.from_np(_np.dtype(dtype)), kind="ExternalOutput").ap()
    build(nc, args, out)
    r = _run(nc, [arrays], core_ids=[0])
    return r.results[0]["out_0_dram"]
```

```python
from contextlib import ExitStack, contextmanager

import concourse.bass as bass
from concourse import mybir

F32 = mybir.dt.float32
ALU = mybir.AluOpType
ACT = mybir.ActivationFunctionType
AX = mybir.AxisListType
ds = bass.ds

P = 128
TOK = 2048
CH = 512
NCH = TOK // CH
NT = TOK // P
HEADS, HD = 16, 8
LN_EPS = 1e-5


class Named:
    pass


def sbuf(nc, name, shape):
    return nc.sbuf_tensor(f"{name}_{nc.next_id()}", shape, F32)


def psum(nc, name, shape):
    return nc.psum_tensor(f"{name}_{nc.next_id()}", shape, F32)


def cs(c):
    return slice(c * CH, (c + 1) * CH)


@contextmanager
def stage(nc, *signals):
    sems = [nc.alloc_semaphore(f"{name}_{nc.next_id()}") for name in signals]
    with nc.Block() as block:
        yield (block, *sems)
    nc.clear_and_free_semaphores(sems)
    nc.all_engine_barrier()


VECTORS = {
    "L0_attn_bq": 1, "L0_attn_bk": 1, "L0_attn_bv": 1, "L0_attn_bg": 1, "L0_attn_gn_scale": 1,
    "L0_attn_gn_bias": 1, "L0_attn_bo": 1, "L0_ffn_b1": 64, "L0_ffn_b2": 8,
    "L1_attn_ln1_scale": 1, "L1_attn_ln1_bias": 1, "L1_attn_bq": 1, "L1_attn_bo": 1,
    "L1_attn_ln2_scale": 1, "L1_attn_ln2_bias": 1, "L1_attn_b1": 4, "L1_attn_b2": 1,
    "L1_ffn_b1": 8, "L1_ffn_W1": 8, "L1_ffn_W2": 8, "L1_ffn_bout": 1,
    "L2_ffn_mu_r": 1, "L2_ffn_mu_k": 1, "L2_attn_gate_local_w": 1, "L2_attn_gate_remote_w": 1,
    "L3_attn_bo": 1, "L3_ffn_attn_nw": 1, "L3_ffn_attn_nb": 1, "L3_ffn_inter_b": 32, "L3_ffn_output_b": 8,
    "L3_ffn_res_inter_b": 4, "L3_ffn_res_output_b": 1,
    "L0_ffn_br1": 1, "L0_ffn_ln_scale": 1, "L0_ffn_ln_bias": 1, "L1_ffn_bin_": 1, "L1_ffn_b2": 1,
}
SHORT = {"L0_ffn_br1": 64, "L0_ffn_ln_scale": 64, "L0_ffn_ln_bias": 64, "L1_ffn_bin_": 64, "L1_ffn_b2": 64}


def row_of_vectors():
    at, n = {}, 0
    for name, rows in VECTORS.items():
        if n % P + rows > P:
            n = (n // P + 1) * P
        at[name] = n
        n += rows
    return at, -(-n // P)


def constants(nc, m, inp, alloc):
    at, tiles = row_of_vectors()
    m.at = at
    m.ident = alloc("ident", [P, P])
    m.mean_w = alloc("mean_w", [P, P])
    m.head_ones = alloc("head_ones", [P, P])
    m.pick = alloc("pick", [P, HD, P])
    m.hmod = alloc("hmod", [P, 4])
    m.eye8 = alloc("eye8", [P, HD])
    m.hdiv = alloc("hdiv", [P, 4])
    m.ones = alloc("ones", [P, P])
    m.cols = alloc("cols", [P, tiles * P])
    m.col = lambda name, i=0, n=P: m.cols[0:n, at[name] + i:at[name] + i + 1]
    with ExitStack() as own:
        rows = own.enter_context(sbuf(nc, "vector_rows", [P, tiles, P]))
        turned = own.enter_context(psum(nc, "vectors_turned", [P, tiles, CH]))
        with stage(nc, "rows_zeroed", "ones_set", "shaped", "rows_loaded", "vectors_turned", "cols_ready") as (
                block, rows_zeroed, ones_set, shaped, rows_loaded, vectors_turned, cols_ready):

            @block.gpsimd
            def _(pool):
                for t in (m.ident, m.head_ones, m.pick, m.ones):
                    pool.memset(t[:], 1.0).then_inc(ones_set, 1)
                pool.memset(m.mean_w[:], 1.0 / P).then_inc(ones_set, 1)
                pool.memset(m.hdiv[:], 1.0).then_inc(ones_set, 1)
                pool.wait_ge(ones_set, 6)
                pool.affine_select(out=m.ident[:], in_=m.ident[:], compare_op=ALU.is_equal, fill=0.0, base=0,
                                   pattern=[[-1, P]], channel_multiplier=1).then_inc(shaped, 1)
                pool.affine_select(out=m.pick[:].rearrange("p e (h d) -> p e h d", d=HD),
                                   in_=m.pick[:].rearrange("p e (h d) -> p e h d", d=HD),
                                   compare_op=ALU.is_equal, fill=0.0, base=0,
                                   pattern=[[-1, HD], [-HD, HEADS], [0, HD]], channel_multiplier=1).then_inc(shaped, 1)
                blocks = m.head_ones[:].rearrange("p (h d) -> p h d", d=HD)
                pool.affine_select(out=blocks, in_=blocks, compare_op=ALU.is_ge, fill=0.0, base=0,
                                   pattern=[[-HD, HEADS], [0, HD]], channel_multiplier=1).then_inc(shaped, 1)
                pool.wait_ge(shaped, 3)
                pool.affine_select(out=blocks, in_=blocks, compare_op=ALU.is_ge, fill=0.0, base=HD - 1,
                                   pattern=[[HD, HEADS], [0, HD]], channel_multiplier=-1).then_inc(shaped, 1)
                pool.affine_select(out=m.hdiv[:], in_=m.hdiv[:], compare_op=ALU.is_ge, fill=0.0, base=0,
                                   pattern=[[-32, 4]], channel_multiplier=1).then_inc(shaped, 1)
                pool.wait_ge(shaped, 5)
                pool.affine_select(out=m.hdiv[:], in_=m.hdiv[:], compare_op=ALU.is_ge, fill=0.0, base=31,
                                   pattern=[[32, 4]], channel_multiplier=-1).then_inc(shaped, 1)

            @block.sync
            def _(sp):
                sp.wait_ge(rows_zeroed, 1)
                n = 0
                for name, k in VECTORS.items():
                    tile, r = divmod(at[name], P)
                    src = inp[name]
                    if len(src.shape) == 2:
                        src = src.rearrange("a b -> (a b)")
                    w = SHORT.get(name, P)
                    sp.dma_start(rows[r:r + k, tile, 0:w], src.rearrange("(r c) -> r c", c=w)).then_inc(rows_loaded, 16)
                    n += 1
                m.n_vector_loads = n

            @block.vector
            def _(dve):
                dve.memset(rows[:], 0.0).then_inc(rows_zeroed, 1)
                for t in range(tiles):
                    dve.wait_ge(vectors_turned, t + 1)
                    dve.tensor_copy(m.cols[:, t * P:(t + 1) * P], turned[:, t, 0:P]).then_inc(cols_ready, 1)
                dve.wait_ge(shaped, 6)
                dve.tensor_reduce(m.hmod[:], m.head_ones[:].rearrange("p (g i d) -> p i g d", g=4, i=4)[:, :, :, 0],
                                  AX.X, ALU.max).then_inc(cols_ready, 1)
                dve.tensor_reduce(m.eye8[:], m.ident[:].rearrange("p (h e) -> p e h", e=HD),
                                  AX.X, ALU.max).then_inc(cols_ready, 1)

            @block.tensor
            def _(pe):
                pe.wait_ge(shaped, 6)
                pe.wait_ge(rows_loaded, 16 * m.n_vector_loads)
                for t in range(tiles):
                    pe.transpose(turned[:, t, 0:P], rows[:, t, :], m.ident[:]).then_inc(vectors_turned, 1)


def turn_in(nc, m, x_dram):
    with ExitStack() as own:
        xtm = own.enter_context(sbuf(nc, "x_token_major", [P, NT, P]))
        ps = own.enter_context(psum(nc, "x_turned", [P, NCH, CH]))
        with stage(nc, "x_loaded", "x_turned", "xT_ready") as (block, x_loaded, x_turned, xT_ready):
            @block.sync
            def _(sp):
                sp.dma_start(xtm[:], x_dram.rearrange("b (n p) f -> p (b n) f", p=P)).then_inc(x_loaded, 16)

            @block.tensor
            def _(pe):
                pe.wait_ge(x_loaded, 16)
                for n in range(NT):
                    c, k = divmod(n, CH // P)
                    pe.transpose(ps[:, c, k * P:(k + 1) * P], xtm[:, n, :], m.ident[:]).then_inc(x_turned, 1)

            @block.vector
            def _(dve):
                for c in range(NCH):
                    dve.wait_ge(x_turned, (c + 1) * (CH // P))
                    dve.tensor_copy(m.x[:, cs(c)], ps[:, c, :]).then_inc(xT_ready, 1)


def turn_out(nc, m, out_dram):
    with ExitStack() as own:
        xtm = own.enter_context(sbuf(nc, "y_token_major", [P, NT, P]))
        ps = own.enter_context(psum(nc, "y_turned", [P, NCH, CH]))
        with stage(nc, "y_turned", "y_copied", "y_stored") as (block, y_turned, y_copied, y_stored):
            @block.tensor
            def _(pe):
                for n in range(NT):
                    c, k = divmod(n, CH // P)
                    pe.transpose(ps[:, c, k * P:(k + 1) * P], m.x[:, n * P:(n + 1) * P], m.ident[:]).then_inc(y_turned, 1)

            @block.vector
            def _(dve):
                for c in range(NCH):
                    dve.wait_ge(y_turned, (c + 1) * (CH // P))
                    dve.tensor_copy(xtm[:, 4 * c:4 * c + 4, :], ps[:, c, :].rearrange("p (n f) -> p n f", f=P))\
                       .then_inc(y_copied, 1)

            @block.sync
            def _(sp):
                out = out_dram.rearrange("b (n p) f -> p (b n) f", p=P)
                for c in range(NCH):
                    sp.wait_ge(y_copied, c + 1)
                    sp.dma_start(out[:, 4 * c:4 * c + 4, :], xtm[:, 4 * c:4 * c + 4, :]).then_inc(y_stored, 16)
                sp.wait_ge(y_stored, 16 * NCH)


def layernorm(nc, m, src, dst, eps, width=P, scale=None, bias=None, after=None):
    w = slice(0, width)
    with ExitStack() as own:
        mean = own.enter_context(psum(nc, "ln_mean", [P, NCH, CH]))
        var = own.enter_context(psum(nc, "ln_var", [P, NCH, CH]))
        cen = own.enter_context(sbuf(nc, "ln_centered", [P, TOK]))
        work = own.enter_context(sbuf(nc, "ln_work", [P, TOK]))
        epst = own.enter_context(sbuf(nc, "ln_eps", [P, 1]))
        with stage(nc, "eps_set", "mean_ready", "centered", "squared", "var_ready", "std_ready", "inverted", "normed",
                   "scaled", "activated") as (
                block, eps_set, mean_ready, centered, squared, var_ready, std_ready, inverted, normed, scaled, activated):
            @block.tensor
            def _(pe):
                for c in range(NCH):
                    pe.matmul(mean[w, c, :], m.mean_w[w, w], src[w, cs(c)], start=True, stop=True).then_inc(mean_ready, 1)
                for c in range(NCH):
                    pe.wait_ge(squared, c + 1)
                    pe.matmul(var[w, c, :], m.mean_w[w, w], work[w, cs(c)], start=True, stop=True).then_inc(var_ready, 1)

            @block.scalar
            def _(act):
                act.wait_ge(eps_set, 1)
                for c in range(NCH):
                    act.wait_ge(centered, c + 1)
                    act.activation(work[w, cs(c)], cen[w, cs(c)], ACT.Square).then_inc(squared, 1)
                for c in range(NCH):
                    act.wait_ge(var_ready, c + 1)
                    act.activation(work[w, cs(c)], var[w, c, :], ACT.Sqrt, bias=epst[w, :], scale=float(P // width))\
                       .then_inc(std_ready, 1)
                if after is not None:
                    for c in range(NCH):
                        act.wait_ge(scaled, c + 1)
                        act.activation(dst[w, cs(c)], dst[w, cs(c)], after).then_inc(activated, 1)

            @block.vector
            def _(dve):
                dve.memset(epst[:], eps).then_inc(eps_set, 1)
                for c in range(NCH):
                    dve.wait_ge(mean_ready, c + 1)
                    dve.scalar_tensor_tensor(out=cen[w, cs(c)], in0=mean[w, c, :], scalar=-float(P // width),
                                             in1=src[w, cs(c)], op0=ALU.mult, op1=ALU.add).then_inc(centered, 1)
                for c in range(NCH):
                    dve.wait_ge(std_ready, c + 1)
                    dve.reciprocal(work[w, cs(c)], work[w, cs(c)]).then_inc(inverted, 1)
                    dve.wait_ge(inverted, c + 1)
                    dve.tensor_tensor(dst[w, cs(c)], cen[w, cs(c)], work[w, cs(c)], ALU.mult).then_inc(normed, 1)
                    if scale is not None:
                        dve.wait_ge(normed, c + 1)
                        dve.tensor_scalar(dst[w, cs(c)], dst[w, cs(c)], scale, bias, ALU.mult, ALU.add)\
                           .then_inc(scaled, 1)


def load_all(nc, loads):
    with stage(nc, "loaded") as (block, loaded):
        @block.sync
        def _(sp):
            for dst, src in loads[0::2]:
                sp.dma_start(dst, src).then_inc(loaded, 16)
            sp.wait_ge(loaded, 16 * len(loads))

        @block.scalar
        def _(act):
            for dst, src in loads[1::2]:
                act.dma_start(dst, src).then_inc(loaded, 16)



SEG = 32
NSEG = TOK // SEG


def l0_project(nc, m, inp, r):
    with ExitStack() as own:
        sb = lambda name, shape: own.enter_context(sbuf(nc, name, shape))
        wqkvg = sb("w_qkvg", [P, 4, P])
        wab = sb("w_ab", [P, 2, HEADS])
        wab_wide = sb("w_ab_wide", [P, 2, P])
        bab, bab_wide, bab_col = sb("b_ab", [1, 2, HEADS]), sb("b_ab_wide", [1, 2, P]), sb("b_ab_col", [P, 2])
        conv = sb("conv_w", [P, 3, 4])
        raw = sb("raw", [P, 2, 3 + TOK])
        load_all(nc, [(wqkvg[:, 0, :], inp["L0_attn_Wq"]), (wqkvg[:, 1, :], inp["L0_attn_Wk"]),
                      (wqkvg[:, 2, :], inp["L0_attn_Wv"]), (wqkvg[:, 3, :], inp["L0_attn_Wg"]),
                      (wab[:, 0, :], inp["L0_attn_Wa"]), (wab[:, 1, :], inp["L0_attn_Wb"]),
                      (bab[:, 0, :], inp["L0_attn_ba"].rearrange("(a h) -> a h", a=1)),
                      (bab[:, 1, :], inp["L0_attn_bb"].rearrange("(a h) -> a h", a=1)),
                      (conv[:, 0, :], inp["L0_attn_q_conv"]), (conv[:, 1, :], inp["L0_attn_k_conv"]),
                      (conv[:, 2, :], inp["L0_attn_v_conv"])])
        ps = own.enter_context(psum(nc, "proj", [P, 2, 4, CH]))
        tmp = sb("tmp", [P, TOK])
        sq = sb("sq", [P, TOK])
        for i, (dst, b) in enumerate(((r.q, "L0_attn_bq"), (r.k, "L0_attn_bk"), (r.bv, "L0_attn_bv"))):
            with stage(nc, "padded", "projected", "biased", "tap", "silued", "squared", "summed", "rooted", "shifted",
                       "inverted", "done") as (
                    block, padded, projected, biased, tap, silued, squared, summed, rooted, shifted, inverted, done):
                x = raw[:, i % 2, :]

                @block.tensor
                def _(pe):
                    for c in range(NCH):
                        pe.matmul(ps[:, 0, c, :], wqkvg[:, i, :], m.xn[:, cs(c)], start=True, stop=True)\
                          .then_inc(projected, 1)
                    if i < 2:
                        for c in range(NCH):
                            pe.wait_ge(squared, c + 1)
                            pe.matmul(ps[:, 1, c, :], m.head_ones[:], sq[:, cs(c)], start=True, stop=True)\
                              .then_inc(summed, 1)

                @block.vector
                def _(dve):
                    dve.memset(x[:, 0:3], 0.0).then_inc(padded, 1)
                    dve.wait_ge(padded, 1)
                    dve.wait_ge(biased, NCH)
                    dve.tensor_scalar(tmp[:], x[:, 0:TOK], conv[:, i, 0:1], None, ALU.mult).then_inc(tap, 1)
                    for j in range(1, 4):
                        dve.wait_ge(tap, j)
                        dve.scalar_tensor_tensor(out=tmp[:], in0=x[:, j:j + TOK], scalar=conv[:, i, j:j + 1], in1=tmp[:],
                                                 op0=ALU.mult, op1=ALU.add).then_inc(tap, 1)
                    if i < 2:
                        for c in range(NCH):
                            dve.wait_ge(rooted, c + 1)
                            dve.tensor_scalar(sq[:, cs(c)], sq[:, cs(c)], 1e-6, None, ALU.add).then_inc(shifted, 1)
                            dve.wait_ge(shifted, c + 1)
                            dve.reciprocal(sq[:, cs(c)], sq[:, cs(c)]).then_inc(inverted, 1)
                            dve.wait_ge(inverted, c + 1)
                            dve.tensor_tensor(dst[:, cs(c)], dst[:, cs(c)], sq[:, cs(c)], ALU.mult).then_inc(done, 1)

                @block.scalar
                def _(act):
                    for c in range(NCH):
                        act.wait_ge(projected, c + 1)
                        act.activation(x[:, 3 + c * CH:3 + (c + 1) * CH], ps[:, 0, c, :], ACT.Identity,
                                       bias=m.col(b)).then_inc(biased, 1)
                    act.wait_ge(tap, 4)
                    for c in range(NCH):
                        act.activation(dst[:, cs(c)], tmp[:, cs(c)], ACT.Silu).then_inc(silued, 1)
                    if i < 2:
                        for c in range(NCH):
                            act.wait_ge(silued, c + 1)
                            act.activation(sq[:, cs(c)], dst[:, cs(c)], ACT.Square).then_inc(squared, 1)
                        for c in range(NCH):
                            act.wait_ge(summed, c + 1)
                            act.activation(sq[:, cs(c)], ps[:, 1, c, :], ACT.Sqrt).then_inc(rooted, 1)
        with stage(nc, "widened", "bias_turned", "bias_ready", "a_logits", "b_logits", "g_logits", "a_ready", "b_ready", "g_ready", "used") as (
                block, widened, bias_turned, bias_ready, a_logits, b_logits, g_logits, a_ready, b_ready, g_ready, used):
            @block.tensor
            def _(pe):
                pe.wait_ge(widened, 4)
                for i in range(2):
                    mm = pe.matmul(ps[:, 0, 0, i:i + 1], bab_wide[:, i, :], m.ones[0:1, 0:1], start=True, stop=True)
                mm.then_inc(bias_turned, 1)
                pe.wait_ge(bias_ready, 1)
                for c in range(NCH):
                    pe.matmul(ps[:, 0, c, :], wab_wide[:, 0, :], m.xn[:, cs(c)], start=True, stop=True).then_inc(a_logits, 1)
                for c in range(NCH):
                    pe.matmul(ps[:, 1, c, :], wab_wide[:, 1, :], m.xn[:, cs(c)], start=True, stop=True).then_inc(b_logits, 1)
                for c in range(NCH):
                    pe.wait_ge(a_ready, c + 1)
                    pe.matmul(ps[:, 0, c, :], wqkvg[:, 3, :], m.xn[:, cs(c)], start=True, stop=True).then_inc(g_logits, 1)

            @block.scalar
            def _(act):
                for c in range(NCH):
                    act.wait_ge(a_logits, c + 1)
                    act.activation(r.a[:, cs(c)], ps[:, 0, c, :], ACT.Sigmoid, bias=bab_col[:, 0:1]).then_inc(a_ready, 1)
                for c in range(NCH):
                    act.wait_ge(b_logits, c + 1)
                    act.activation(tmp[:, cs(c)], ps[:, 1, c, :], ACT.Sigmoid, bias=bab_col[:, 1:2]).then_inc(b_ready, 1)
                for c in range(NCH):
                    act.wait_ge(g_logits, c + 1)
                    act.activation(r.gate[:, cs(c)], ps[:, 0, c, :], ACT.Silu, bias=m.col("L0_attn_bg")).then_inc(g_ready, 1)

            @block.vector
            def _(dve):
                for i in range(2):
                    dve.tensor_copy(wab_wide[:, i, :].rearrange("p (h d) -> p h d", d=HD),
                                    wab[:, i, :].unsqueeze(2).to_broadcast([P, HEADS, HD])).then_inc(widened, 1)
                    dve.tensor_copy(bab_wide[:, i, :].rearrange("p (h d) -> p h d", d=HD),
                                    bab[:, i, :].unsqueeze(2).to_broadcast([1, HEADS, HD])).then_inc(widened, 1)
                dve.wait_ge(bias_turned, 1)
                dve.tensor_copy(bab_col[:], ps[:, 0, 0, 0:2]).then_inc(bias_ready, 1)
                for c in range(NCH):
                    dve.wait_ge(b_ready, c + 1)
                    dve.tensor_tensor(r.bv[:, cs(c)], r.bv[:, cs(c)], tmp[:, cs(c)], ALU.mult).then_inc(used, 1)
                    dve.scalar_tensor_tensor(out=r.nab[:, cs(c)], in0=r.a[:, cs(c)], scalar=-1.0, in1=tmp[:, cs(c)],
                                             op0=ALU.mult, op1=ALU.mult).then_inc(used, 1)


def l0_scan(nc, m, r):
    kT = r.k[:].rearrange("p (j t) -> p t j", t=SEG)
    qT = r.q[:].rearrange("p (j t) -> p t j", t=SEG)
    aT = r.a[:].rearrange("p (j t) -> p t j", t=SEG)
    nabT = r.nab[:].rearrange("p (j t) -> p t j", t=SEG)
    bvT = r.bv[:].rearrange("p (j t) -> p t j", t=SEG)
    woT = r.wo[:].rearrange("p k (j t) -> p k t j", t=SEG)
    FULL = [P, 2, HD, NSEG]
    with ExitStack() as own:
        sb = lambda name, shape: own.enter_context(sbuf(nc, name, shape))
        Zk, Zq, aZ, outer = (sb(n, [P, 2, HD * NSEG]) for n in ("Z_k", "Z_q", "a_Z", "u_k"))
        u = sb("u", [P, 2, NSEG])
        kps = own.enter_context(psum(nc, "k_spread", [P, 2, CH]))
        qps = own.enter_context(psum(nc, "q_spread", [P, 2, CH]))
        Z = r.Z
        ejk = lambda t: t.rearrange("p k (e j) -> p k j e", e=HD)
        with stage(nc, "z_set", "k_spread", "q_spread", "zk_ready", "r_ready", "nabr_ready", "u_ready", "uk_ready",
                   "az_ready", "z_ready", "zq_ready", "wo_ready") as (
                block, z_set, k_spread, q_spread, zk_ready, r_ready, nabr_ready, u_ready, uk_ready, az_ready, z_ready,
                zq_ready, wo_ready):
            @block.tensor
            def _(pe):
                with pe.Fori(0, SEG // 2) as pair:
                    for par in range(2):
                        t = pair * 2 + par
                        pe.wait_ge(uk_ready, t)
                        for e in range(HD):
                            mm = pe.matmul(kps[:, par, e * NSEG:(e + 1) * NSEG], m.pick[:, e, :], kT[:, ds(t, 1), :],
                                           start=True, stop=True)
                        mm.then_inc(k_spread, 1)
                        pe.wait_ge(wo_ready, t)
                        for e in range(HD):
                            mm = pe.matmul(qps[:, par, e * NSEG:(e + 1) * NSEG], m.pick[:, e, :], qT[:, ds(t, 1), :],
                                           start=True, stop=True)
                        mm.then_inc(q_spread, 1)

            @block.gpsimd
            def _(pool):
                pool.wait_ge(z_set, 2)
                with pool.Fori(0, SEG) as t:
                    pool.wait_ge(z_ready, t)
                    pool.tensor_tensor(aZ[:].rearrange("p k (e j) -> p (k e) j", e=HD),
                                       Z[:].rearrange("p k (e j) -> p (k e) j", e=HD),
                                       aT[:, ds(t, 1), :].to_broadcast([P, 2 * HD, NSEG]), ALU.mult).then_inc(az_ready, 1)

            @block.vector
            def _(dve):
                dve.memset(Z[:, 0, :], 0.0).then_inc(z_set, 1)
                dve.tensor_copy(Z[:, 1, :].rearrange("p (e j) -> p e j", e=HD),
                                m.eye8[:].unsqueeze(2).to_broadcast([P, HD, NSEG])).then_inc(z_set, 1)
                dve.wait_ge(z_set, 2)
                with dve.Fori(0, SEG // 2) as pair:
                    for par in range(2):
                        t = pair * 2 + par
                        kb = kps[:, par, :].unsqueeze(1).to_broadcast([P, 2, HD * NSEG])
                        qb = qps[:, par, :].unsqueeze(1).to_broadcast([P, 2, HD * NSEG])
                        dve.wait_ge(k_spread, t + 1)
                        dve.wait_ge(z_ready, t)
                        dve.tensor_tensor(Zk[:], Z[:], kb, ALU.mult).then_inc(zk_ready, 1)
                        dve.wait_ge(zk_ready, t + 1)
                        dve.tensor_reduce(u[:], ejk(Zk[:]), AX.X, ALU.add).then_inc(r_ready, 1)
                        dve.wait_ge(r_ready, t + 1)
                        dve.tensor_tensor(u[:], u[:], nabT[:, ds(t, 1), :].to_broadcast([P, 2, NSEG]), ALU.mult)\
                           .then_inc(nabr_ready, 1)
                        dve.wait_ge(nabr_ready, t + 1)
                        dve.tensor_tensor(u[:, 0:1, :], u[:, 0:1, :], bvT[:, ds(t, 1), :], ALU.add).then_inc(u_ready, 1)
                        dve.wait_ge(u_ready, t + 1)
                        dve.tensor_tensor(outer[:].rearrange("p k (e j) -> p k e j", e=HD),
                                          kb.rearrange("p k (e j) -> p k e j", e=HD),
                                          u[:].unsqueeze(2).to_broadcast(FULL), ALU.mult).then_inc(uk_ready, 1)
                        dve.wait_ge(uk_ready, t + 1)
                        dve.wait_ge(az_ready, t + 1)
                        dve.tensor_tensor(Z[:], aZ[:], outer[:], ALU.add).then_inc(z_ready, 1)
                        dve.wait_ge(q_spread, t + 1)
                        dve.wait_ge(z_ready, t + 1)
                        dve.tensor_tensor(Zq[:], Z[:], qb, ALU.mult).then_inc(zq_ready, 1)
                        dve.wait_ge(zq_ready, t + 1)
                        dve.tensor_reduce(woT[:, :, ds(t, 1), :], ejk(Zq[:]).unsqueeze(2), AX.X, ALU.add)\
                           .then_inc(wo_ready, 1)


def l0_join(nc, m, r):
    with ExitStack() as own:
        sb = lambda name, shape: own.enter_context(sbuf(nc, name, shape))
        T = sb("T", [P, NSEG + 1, HD])
        Pb, Cb, Sb = (sb(n, [P, 2, P]) for n in ("P_blocks", "C_blocks", "S_blocks"))
        nxt = own.enter_context(psum(nc, "T_next", [P, 2, CH]))
        add = own.enter_context(psum(nc, "o_carried", [P, NCH, CH]))
        Zj = r.Z[:].rearrange("p k (e j) -> p k j e", e=HD)
        hb = m.head_ones[:].rearrange("p (h e) -> p h e", e=HD)
        WIDE = [P, HEADS, HD]
        with stage(nc, "t_zeroed", "p_blocks", "c_blocks", "s_blocks", "t_next", "t_ready", "carried", "o_ready") as (
                block, t_zeroed, p_blocks, c_blocks, s_blocks, t_next, t_ready, carried, o_ready):
            @block.gpsimd
            def _(pool):
                pool.memset(T[:, 0:1, :], 0.0).then_inc(t_zeroed, 1)
                pool.wait_ge(t_zeroed, 1)
                with pool.Fori(0, NSEG // 2) as pair:
                    for par in range(2):
                        j = pair * 2 + par
                        pool.wait_ge(t_ready, j)
                        pool.wait_ge(carried, j)
                        pool.tensor_tensor(Pb[:, par, :].rearrange("p (h e) -> p h e", e=HD),
                                           Zj[:, 1, ds(j, 1), :].to_broadcast(WIDE), hb, ALU.mult).then_inc(p_blocks, 1)
                        pool.tensor_tensor(Cb[:, par, :].rearrange("p (h e) -> p h e", e=HD),
                                           Zj[:, 0, ds(j, 1), :].to_broadcast(WIDE), hb, ALU.mult).then_inc(c_blocks, 1)
                        pool.tensor_tensor(Sb[:, par, :].rearrange("p (h e) -> p h e", e=HD),
                                           T[:, ds(j, 1), :].to_broadcast(WIDE), hb, ALU.mult).then_inc(s_blocks, 1)

            @block.tensor
            def _(pe):
                with pe.Fori(0, NSEG // 2) as pair:
                    for par in range(2):
                        j = pair * 2 + par
                        pe.wait_ge(c_blocks, j + 1)
                        pe.wait_ge(t_ready, j)
                        pe.matmul(nxt[:, par, 0:HD], Cb[:, par, :], m.eye8[:], start=True, stop=False)
                        pe.wait_ge(p_blocks, j + 1)
                        pe.matmul(nxt[:, par, 0:HD], Pb[:, par, :], T[:, ds(j, 1), :], start=False, stop=True)\
                          .then_inc(t_next, 1)
                        pe.wait_ge(s_blocks, j + 1)
                        pe.matmul(add[:].rearrange("p a (b t) -> p (a b) t", t=SEG)[:, ds(j, 1), :], Sb[:, par, :],
                                  r.wo[:, 1, ds(j * SEG, SEG)], start=True, stop=True).then_inc(carried, 1)

            @block.vector
            def _(dve):
                dve.wait_ge(t_zeroed, 1)
                with dve.Fori(0, NSEG // 2) as pair:
                    for par in range(2):
                        j = pair * 2 + par
                        dve.wait_ge(t_next, j + 1)
                        dve.tensor_copy(T[:, ds(j + 1, 1), :], nxt[:, par:par + 1, 0:HD]).then_inc(t_ready, 1)
                dve.wait_ge(carried, NSEG)
                for c in range(NCH):
                    dve.tensor_tensor(r.o[:, cs(c)], add[:, c, :], r.wo[:, 0, cs(c)], ALU.add).then_inc(o_ready, 1)


def l0_output(nc, m, inp, r):
    with ExitStack() as own:
        sb = lambda name, shape: own.enter_context(sbuf(nc, name, shape))
        wo = sb("w_o", [P, P])
        load_all(nc, [(wo[:], inp["L0_attn_Wo"])])
        st = sb("stats", [P, 8])
        sq = sb("o_squared", [P, TOK])
        ps = own.enter_context(psum(nc, "group_sums", [P, CH]))
        po = own.enter_context(psum(nc, "out_proj", [P, NCH, CH]))
        with stage(nc, "summed", "over_heads", "std_ready", "chain", "gated", "projected", "added") as (
                block, summed, over_heads, std_ready, chain, gated, projected, added):
            @block.scalar
            def _(act):
                act.activation(sq[:], r.o[:], ACT.Square, accum_out=st[:, 1:2]).then_inc(summed, 1)
                act.wait_ge(chain, 5)
                act.activation(st[:, 4:5], st[:, 4:5], ACT.Sqrt).then_inc(std_ready, 1)

            @block.tensor
            def _(pe):
                pe.wait_ge(summed, 2)
                pe.matmul(ps[:, 0:2], m.head_ones[:], st[:, 0:2], start=True, stop=True).then_inc(over_heads, 1)
                for c in range(NCH):
                    pe.wait_ge(gated, c + 1)
                    pe.matmul(po[:, c, :], wo[:], r.o[:, cs(c)], start=True, stop=True).then_inc(projected, 1)

            @block.vector
            def _(dve):
                n = [0]

                def link(ins):
                    n[0] += 1
                    ins.then_inc(chain, 1)
                    dve.wait_ge(chain, n[0])

                dve.tensor_reduce(st[:, 0:1], r.o[:], AX.X, ALU.add).then_inc(summed, 1)
                dve.wait_ge(over_heads, 1)
                link(dve.tensor_scalar(st[:, 2:4], ps[:, 0:2], 1.0 / (TOK * HD), None, ALU.mult))
                link(dve.tensor_tensor(st[:, 4:5], st[:, 2:3], st[:, 2:3], ALU.mult))
                link(dve.tensor_tensor(st[:, 4:5], st[:, 3:4], st[:, 4:5], ALU.subtract))
                link(dve.tensor_scalar(st[:, 4:5], st[:, 4:5], 1e-5, None, ALU.add))
                link(dve.tensor_scalar(st[:, 5:6], st[:, 2:3], -1.0, None, ALU.mult))
                dve.wait_ge(std_ready, 1)
                link(dve.reciprocal(st[:, 4:5], st[:, 4:5]))
                link(dve.tensor_tensor(st[:, 6:7], st[:, 4:5], m.col("L0_attn_gn_scale"), ALU.mult))
                link(dve.tensor_scalar(r.o[:], r.o[:], st[:, 5:6], st[:, 6:7], ALU.add, ALU.mult))
                for c in range(NCH):
                    dve.scalar_tensor_tensor(out=r.o[:, cs(c)], in0=r.o[:, cs(c)], scalar=m.col("L0_attn_gn_bias"),
                                             in1=r.gate[:, cs(c)], op0=ALU.add, op1=ALU.mult).then_inc(gated, 1)
                for c in range(NCH):
                    dve.wait_ge(projected, c + 1)
                    dve.scalar_tensor_tensor(out=m.x[:, cs(c)], in0=po[:, c, :], scalar=m.col("L0_attn_bo"),
                                             in1=m.x[:, cs(c)], op0=ALU.add, op1=ALU.add).then_inc(added, 1)


def layer0_attention(nc, m, inp):
    with ExitStack() as own:
        r = Named()
        r.q, r.k, r.bv, r.a, r.nab, r.gate, r.o = (own.enter_context(sbuf(nc, "r_" + name, [P, TOK]))
                                                   for name in ("q", "k", "bv", "a", "nab", "gate", "o"))
        r.Z = own.enter_context(sbuf(nc, "r_Z", [P, 2, HD * NSEG]))
        r.wo = own.enter_context(sbuf(nc, "r_wo", [P, 2, TOK]))
        l0_project(nc, m, inp, r)
        l0_scan(nc, m, r)
        l0_join(nc, m, r)
        l0_output(nc, m, inp, r)



EXPERTS = 8
FF = 512
FT = FF // P


def expert_weights(nc, m, h, width, w, bias, k, renormalize, wT, kept=None, post=None):
    SH = [P, NT, EXPERTS]
    SQ = [P, NT, EXPERTS, EXPERTS]
    with ExitStack() as own:
        sb = lambda name, shape: own.enter_context(sbuf(nc, name, shape))
        p, sel = sb("probs", SH), sb("selected", [P, 2, NT, EXPERTS])
        gt, eq = sb("greater", SQ), sb("equal", SQ)
        lower = sb("lower", [P, EXPERTS, EXPERTS])
        s = sb("s", [P, NT])
        selT = sb("selected_T", [EXPERTS, 3, TOK])
        logits = own.enter_context(psum(nc, "router_logits", [P, NT, EXPERTS]))
        turned = own.enter_context(psum(nc, "weights_turned", [P, NCH, CH]))
        with stage(nc, "lower_set", "lower_shaped", "logits_ready", "less_max", "exp_ready", "chain", "w_ready", "w_turned", "m_turned",
                   "w_copied", "m_copied") as (
                block, lower_set, lower_shaped, logits_ready, less_max, exp_ready, chain, w_ready, w_turned, m_turned,
                w_copied, m_copied):
            @block.gpsimd
            def _(pool):
                pool.memset(lower[:], 1.0).then_inc(lower_set, 1)
                pool.wait_ge(lower_set, 1)
                pool.affine_select(out=lower[:], in_=lower[:], compare_op=ALU.is_gt, fill=0.0, base=0,
                                   pattern=[[1, EXPERTS], [-1, EXPERTS]], channel_multiplier=0).then_inc(lower_shaped, 1)

            @block.tensor
            def _(pe):
                for n in range(NT):
                    mm = pe.matmul(logits[:, n, :], h[0:width, n * P:(n + 1) * P], w, start=True, stop=bias is None)
                    if bias is not None:
                        mm = pe.matmul(logits[:, n, :], m.ones[0:1, :], bias, start=False, stop=True)
                mm.then_inc(logits_ready, 1)
                pe.wait_ge(w_ready, 1)
                for n in range(NT):
                    c, k4 = divmod(n, CH // P)
                    mm = pe.transpose(turned[0:EXPERTS, c, k4 * P:(k4 + 1) * P], p[:, n, :], m.ident[:])
                mm.then_inc(w_turned, 1)
                if kept is not None:
                    pe.wait_ge(w_copied, 1)
                    for n in range(NT):
                        c, k4 = divmod(n, CH // P)
                        mm = pe.transpose(turned[0:EXPERTS, c, k4 * P:(k4 + 1) * P], sel[:, 0, n, :], m.ident[:])
                    mm.then_inc(m_turned, 1)

            @block.scalar
            def _(act):
                act.wait_ge(less_max, 1)
                act.activation(p[:], p[:], ACT.Exp).then_inc(exp_ready, 1)

            @block.vector
            def _(dve):
                n = [0]

                def link(ins):
                    n[0] += 1
                    ins.then_inc(chain, 1)
                    dve.wait_ge(chain, n[0])

                dve.wait_ge(logits_ready, 1)
                link(dve.tensor_reduce(s[:], logits[:], AX.X, ALU.max))
                dve.tensor_tensor(p[:], logits[:], s[:].unsqueeze(2).to_broadcast(SH), ALU.subtract).then_inc(less_max, 1)
                dve.wait_ge(exp_ready, 1)
                link(dve.tensor_reduce(s[:], p[:], AX.X, ALU.add))
                link(dve.reciprocal(s[:], s[:]))
                link(dve.tensor_tensor(p[:], p[:], s[:].unsqueeze(2).to_broadcast(SH), ALU.mult))
                pj, pe_ = p[:].unsqueeze(2).to_broadcast(SQ), p[:].unsqueeze(3).to_broadcast(SQ)
                link(dve.tensor_tensor(gt[:], pj, pe_, ALU.is_gt))
                link(dve.tensor_tensor(eq[:], pj, pe_, ALU.is_equal))
                dve.wait_ge(lower_shaped, 1)
                link(dve.tensor_tensor(eq[:], eq[:], lower[:].unsqueeze(1).to_broadcast(SQ), ALU.mult))
                link(dve.tensor_tensor(gt[:], gt[:], eq[:], ALU.add))
                link(dve.tensor_reduce(sel[:, 1], gt[:], AX.X, ALU.add))
                link(dve.tensor_scalar(sel[:, 0], sel[:, 1], float(k), None, ALU.is_lt))
                link(dve.tensor_tensor(p[:], p[:], sel[:, 0], ALU.mult))
                if renormalize:
                    link(dve.tensor_reduce(s[:], p[:], AX.X, ALU.add))
                    link(dve.reciprocal(s[:], s[:]))
                    link(dve.tensor_tensor(p[:], p[:], s[:].unsqueeze(2).to_broadcast(SH), ALU.mult))
                dve.tensor_copy(eq[:, 0, 0, 0:1], s[:, 0:1]).then_inc(w_ready, 1)
                dve.wait_ge(w_turned, 1)
                dve.tensor_copy(wT, turned[0:EXPERTS, :, :].rearrange("p a b -> p (a b)")).then_inc(w_copied, 1)
                if kept is not None:
                    dve.wait_ge(m_turned, 1)
                    link(dve.tensor_copy(selT[:, 0, :], turned[0:EXPERTS, :, :].rearrange("p a b -> p (a b)")))
                    link(dve.tensor_scalar(selT[:, 1, :], selT[:, 0, :], 0.0, None, ALU.mult))
                    link(dve.tensor_tensor_scan(selT[:, 2, :], selT[:, 0, :], selT[:, 1, :], 0.0, ALU.add, ALU.add))
                    link(dve.tensor_scalar(selT[:, 2, :], selT[:, 2, :], float(kept), None, ALU.is_le))
                    dve.wait_ge(w_copied, 1)
                    dve.tensor_tensor(wT, wT, selT[:, 2, :], ALU.mult).then_inc(m_copied, 1)


def expert_sum(nc, m, src, w1, w2, halves, b1, b2, wT):
    HT = halves * FT
    with ExitStack() as own:
        sb = lambda name, shape: own.enter_context(sbuf(nc, name, shape))
        wa = sb("w_up", [P, 2, halves * FF])
        wb = sb("w_down", [P, 2, FT, P])
        bcol = sb("up_bias", [P, HT])
        gel = sb("gelu_out", [P, 2, CH])
        hid = sb("hidden", [P, 2, FT, CH])
        wrow = sb("expert_row", [EXPERTS, 2, CH])
        wcol = sb("expert_weight", [P, 2, CH])
        part = sb("weighted", [P, 2, CH])
        ups = own.enter_context(psum(nc, "up", [P, 4, CH]))
        yps = own.enter_context(psum(nc, "down", [P, 2, CH]))
        mps = own.enter_context(psum(nc, "weight_spread", [P, 2, CH]))
        with stage(nc, "w_loaded0", "w_loaded1", "bias_ready", "up_ready", "activated", "hid_ready",
                   "row_ready", "spread", "wcol_ready", "down_ready", "y_weighted", "added") as (
                block, w_loaded0, w_loaded1, bias_ready, up_ready, activated, hid_ready,
                row_ready, spread, wcol_ready, down_ready, y_weighted, added):
            loaded = (w_loaded0, w_loaded1)
            w1v = w1.rearrange("e p n -> p e n")
            w2v = w2.rearrange("e (t p) n -> p e t n", p=P)
            UP = 4 // halves

            @block.sync
            def _(sp):
                for par in range(2):
                    sp.dma_start(wa[:, par, :], w1v[:, par, :]).then_inc(loaded[par], 16)
                    sp.dma_start(wb[:, par, :, :], w2v[:, par, :, :]).then_inc(loaded[par], 16)
                with sp.Fori(1, EXPERTS // 2) as pair:
                    for par in range(2):
                        sp.wait_ge(down_ready, (pair * 2 + par - 1) * NCH)
                        sp.dma_start(wa[:, par:par + 1, :], w1v[:, ds(pair * 2 + par, 1), :]).then_inc(loaded[par], 16)
                        sp.dma_start(wb[:, par:par + 1, :, :], w2v[:, ds(pair * 2 + par, 1), :, :]).then_inc(loaded[par], 16)

            @block.gpsimd
            def _(pool):
                with pool.Fori(0, EXPERTS) as e:
                    for c in range(NCH):
                        i = e * NCH + c
                        pool.wait_ge(y_weighted, i + 1)
                        pool.tensor_tensor(m.x[:, cs(c)], m.x[:, cs(c)], part[:, c % 2, :], ALU.add).then_inc(added, 1)

            @block.tensor
            def _(pe):
                with pe.Fori(0, EXPERTS // 2) as pair:
                    for par in range(2):
                        e = pair * 2 + par
                        pe.wait_ge(loaded[par], pair * 32 + 32)
                        for c in range(NCH):
                            i = e * NCH + c
                            for f in range(FT):
                                pe.wait_ge(hid_ready, i * FT + f + 1 - UP if c or f >= UP else e * NCH * FT)
                                for s in reversed(range(halves)):
                                    t = s * FT + f
                                    pe.matmul(ups[:, (f % UP) * halves + s, :], wa[:, par, t * P:(t + 1) * P],
                                              src[:, cs(c)], start=True, stop=True).then_inc(up_ready, 1)
                            pe.wait_ge(row_ready, i + 1)
                            if c >= 2:
                                pe.wait_ge(wcol_ready, i - 1)
                            else:
                                pe.wait_ge(wcol_ready, e * NCH)
                            pe.matmul(mps[:, c % 2, :], m.ones[0:EXPERTS, :], wrow[:, c % 2, :],
                                      start=True, stop=True).then_inc(spread, 1)
                            pe.wait_ge(y_weighted, i - 1 if c >= 2 else e * NCH)
                            for f in range(FT):
                                pe.wait_ge(hid_ready, i * FT + f + 1)
                                mm = pe.matmul(yps[:, c % 2, :], wb[:, par, f, :], hid[:, c % 2, f, :],
                                               start=(f == 0), stop=(f == FT - 1))
                            mm.then_inc(down_ready, 1)

            @block.scalar
            def _(act):
                with act.Fori(0, EXPERTS) as e:
                    act.wait_ge(bias_ready, e + 1)
                    for c in range(NCH):
                        i = e * NCH + c
                        for f in range(FT):
                            bias = bcol[:, (halves - 1) * FT + f:(halves - 1) * FT + f + 1]
                            act.wait_ge(up_ready, (i * FT + f) * halves + 1)
                            if halves == 1:
                                act.wait_ge(down_ready, i - 1 if c >= 2 else e * NCH)
                                act.activation(hid[:, c % 2, f, :], ups[:, f, :], ACT.Gelu_apprx_tanh, bias=bias)\
                                   .then_inc(hid_ready, 1)
                            else:
                                act.wait_ge(hid_ready, i * FT + f - 1 if c or f >= 2 else e * NCH * FT)
                                act.activation(gel[:, f % 2, :], ups[:, (f % UP) * halves + 1, :], ACT.Gelu_apprx_tanh,
                                               bias=bias).then_inc(activated, 1)
                        act.wait_ge(spread, i + 1)
                        act.wait_ge(y_weighted, i - 1 if c >= 2 else e * NCH)
                        act.activation(wcol[:, c % 2, :], mps[:, c % 2, :], ACT.Copy).then_inc(wcol_ready, 1)

            @block.vector
            def _(dve):
                with dve.Fori(0, EXPERTS) as e:
                    dve.wait_ge(hid_ready, e * NCH * FT)
                    dve.tensor_scalar(bcol[:], m.cols[:, ds(m.at[b1] + e * HT, HT)], 1.0, None, ALU.mult)\
                       .then_inc(bias_ready, 1)
                    for c in range(NCH):
                        i = e * NCH + c
                        dve.wait_ge(spread, i - 1 if c >= 2 else e * NCH)
                        dve.tensor_scalar(wrow[:, c % 2, :], wT[:, cs(c)], m.ident[0:EXPERTS, ds(e, 1)], None, ALU.mult)\
                           .then_inc(row_ready, 1)
                        if halves == 2:
                            dve.wait_ge(bias_ready, e + 1)
                            for f in range(FT):
                                dve.wait_ge(activated, i * FT + f + 1)
                                dve.wait_ge(up_ready, (i * FT + f) * halves + 2)
                                dve.wait_ge(down_ready, i - 1 if c >= 2 else e * NCH)
                                dve.scalar_tensor_tensor(out=hid[:, c % 2, f, :], in0=ups[:, (f % UP) * halves, :],
                                                         scalar=bcol[:, f:f + 1],
                                                         in1=gel[:, f % 2, :], op0=ALU.add, op1=ALU.mult)\
                                   .then_inc(hid_ready, 1)
                        dve.wait_ge(down_ready, i + 1)
                        dve.wait_ge(wcol_ready, i + 1)
                        dve.wait_ge(added, i - 1 if c >= 2 else e * NCH)
                        dve.scalar_tensor_tensor(out=part[:, c % 2, :], in0=yps[:, c % 2, :],
                                                 scalar=m.cols[:, ds(m.at[b2] + e, 1)], in1=wcol[:, c % 2, :],
                                                 op0=ALU.add, op1=ALU.mult).then_inc(y_weighted, 1)


def layer0_experts(nc, m, inp):
    with ExitStack() as own:
        sb = lambda name, shape: own.enter_context(sbuf(nc, name, shape))
        R = P // 2
        wr1, wr2, br2 = sb("w_r1", [P, R]), sb("w_r2", [R, EXPERTS]), sb("b_r2", [1, EXPERTS])
        h, wT = sb("router_hidden", [R, TOK]), sb("weights_T", [EXPERTS, TOK])
        load_all(nc, [(wr1[:], inp["L0_ffn_Wr1"]), (wr2[:], inp["L0_ffn_Wr2"]),
                      (br2[:], inp["L0_ffn_br2"].rearrange("(a e) -> a e", a=1))])
        with psum(nc, "router_up", [R, NCH, CH]) as ps, stage(nc, "up", "biased") as (block, up, biased):
            @block.tensor
            def _(pe):
                for c in range(NCH):
                    pe.matmul(ps[:, c, :], wr1[:], m.xn[:, cs(c)], start=True, stop=True).then_inc(up, 1)

            @block.scalar
            def _(act):
                for c in range(NCH):
                    act.wait_ge(up, c + 1)
                    act.activation(h[:, cs(c)], ps[:, c, :], ACT.Identity, bias=m.col("L0_ffn_br1", 0, R)).then_inc(biased, 1)
        layernorm(nc, m, h, h, 1e-6, width=R, scale=m.col("L0_ffn_ln_scale", 0, R), bias=m.col("L0_ffn_ln_bias", 0, R),
                  after=ACT.Gelu_apprx_tanh)
        expert_weights(nc, m, h, R, wr2[:], br2[:], 2, True, wT[:])
        expert_sum(nc, m, m.xn, inp["L0_ffn_W1"], inp["L0_ffn_W2"], 2, "L0_ffn_b1", "L0_ffn_b2", wT)



def layer3_experts(nc, m, inp):
    CAP = max(4, TOK // EXPERTS)
    with ExitStack() as own:
        sb = lambda name, shape: own.enter_context(sbuf(nc, name, shape))
        wg, coef_w = sb("w_gate", [P, EXPERTS]), sb("w_coef", [P, 2])
        w1, w2 = sb("w_res_up", [P, FF]), sb("w_res_down", [P, FT, P])
        y, wT = sb("attn_out", [P, TOK]), sb("weights_T3", [EXPERTS, TOK])
        dif = sb("coef_dif", [P, 2, P])
        cf = sb("coef", [P, 2, TOK])
        hid = sb("res_hidden", [P, 2, FT, CH])
        load_all(nc, [(wg[:], inp["L3_ffn_wg"]), (coef_w[:], inp["L3_ffn_res_coef"]), (w1[:], inp["L3_ffn_res_inter_w"]),
                      (w2[:], inp["L3_ffn_res_output_w"].rearrange("(t p) n -> p t n", p=P))])
        layernorm(nc, m, m.xn, y, 1e-12, scale=m.col("L3_ffn_attn_nw"), bias=m.col("L3_ffn_attn_nb"))
        expert_weights(nc, m, y, P, wg[:], None, 1, False, wT[:], kept=CAP)
        with psum(nc, "coef_logits", [P, 2, CH]) as cps, psum(nc, "res_up", [P, 4, CH]) as ups, \
                psum(nc, "res_down", [P, 2, CH]) as yps, \
                stage(nc, "dif_ready", "logits", "coef_ready", "wT_done", "up", "hidden", "down", "res_weighted", "summed") as (
                block, dif_ready, logits, coef_ready, wT_done, up, hidden, down, res_weighted, summed):
            @block.vector
            def _(dve):
                dve.tensor_scalar(dif[:, 0, 0:1], coef_w[:, 0:1], coef_w[:, 1:2], None, ALU.subtract).then_inc(dif_ready, 1)
                dve.wait_ge(dif_ready, 1)
                dve.tensor_copy(dif[:, 1, :], dif[:, 0, 0:1].to_broadcast([P, P])).then_inc(dif_ready, 1)
                for c in range(NCH):
                    dve.wait_ge(coef_ready, 2 * c + 2)
                    dve.tensor_tensor(wT[:, cs(c)], wT[:, cs(c)], cf[0:EXPERTS, 1, cs(c)], ALU.mult).then_inc(wT_done, 1)
                    dve.tensor_tensor(m.x[:, cs(c)], m.x[:, cs(c)], m.xn[:, cs(c)], ALU.add).then_inc(summed, 1)
                for c in range(NCH):
                    dve.wait_ge(down, c + 1)
                    dve.scalar_tensor_tensor(out=cf[:, 0, cs(c)], in0=yps[:, c % 2, :], scalar=m.col("L3_ffn_res_output_b"),
                                             in1=cf[:, 0, cs(c)], op0=ALU.add, op1=ALU.mult).then_inc(res_weighted, 1)
                    dve.wait_ge(res_weighted, c + 1)
                    dve.wait_ge(summed, NCH)
                    dve.tensor_tensor(m.x[:, cs(c)], m.x[:, cs(c)], cf[:, 0, cs(c)], ALU.add).then_inc(summed, 1)

            @block.tensor
            def _(pe):
                pe.wait_ge(dif_ready, 2)
                for c in range(NCH):
                    if c >= 2:
                        pe.wait_ge(coef_ready, 2 * (c - 1))
                    pe.matmul(cps[:, c % 2, :], dif[:, 1, :], y[:, cs(c)], start=True, stop=True).then_inc(logits, 1)
                for c in range(NCH):
                    for f in range(FT):
                        if c:
                            pe.wait_ge(hidden, (c - 1) * FT + f + 1)
                        pe.matmul(ups[:, f, :], w1[:, f * P:(f + 1) * P], y[:, cs(c)], start=True, stop=True).then_inc(up, 1)
                    if c >= 2:
                        pe.wait_ge(res_weighted, c - 1)
                    for f in range(FT):
                        pe.wait_ge(hidden, c * FT + f + 1)
                        mm = pe.matmul(yps[:, c % 2, :], w2[:, f, :], hid[:, c % 2, f, :], start=(f == 0), stop=(f == FT - 1))
                    mm.then_inc(down, 1)

            @block.scalar
            def _(act):
                for c in range(NCH):
                    act.wait_ge(logits, c + 1)
                    act.activation(cf[:, 0, cs(c)], cps[:, c % 2, :], ACT.Sigmoid).then_inc(coef_ready, 1)
                    act.activation(cf[:, 1, cs(c)], cps[:, c % 2, :], ACT.Sigmoid, scale=-1.0).then_inc(coef_ready, 1)
                for c in range(NCH):
                    if c >= 2:
                        act.wait_ge(down, c - 1)
                    for f in range(FT):
                        act.wait_ge(up, c * FT + f + 1)
                        act.activation(hid[:, c % 2, f, :], ups[:, f, :], ACT.Gelu_apprx_tanh,
                                       bias=m.col("L3_ffn_res_inter_b", f)).then_inc(hidden, 1)
        expert_sum(nc, m, y, inp["L3_ffn_inter_w"], inp["L3_ffn_output_w"], 1, "L3_ffn_inter_b", "L3_ffn_output_b", wT)



def hidden_mlp(nc, m, src, w1, w2, b1, b2, base):
    with ExitStack() as own:
        wa, wb = own.enter_context(sbuf(nc, "w_up", [P, FF])), own.enter_context(sbuf(nc, "w_down", [P, FT, P]))
        hid = own.enter_context(sbuf(nc, "mlp_hidden", [P, 2, FT, CH]))
        ups, yps = own.enter_context(psum(nc, "mlp_up", [P, 4, CH])), own.enter_context(psum(nc, "mlp_down", [P, 2, CH]))
        load_all(nc, [(wa[:], w1), (wb[:], w2.rearrange("(t p) n -> p t n", p=P))])
        with stage(nc, "up", "hidden", "down", "based", "added") as (block, up, hidden, down, based, added):
            @block.tensor
            def _(pe):
                for c in range(NCH):
                    for f in range(FT):
                        if c:
                            pe.wait_ge(hidden, (c - 1) * FT + f + 1)
                        pe.matmul(ups[:, f, :], wa[:, f * P:(f + 1) * P], src[:, cs(c)], start=True, stop=True).then_inc(up, 1)
                    if c >= 2:
                        pe.wait_ge(added, c - 1)
                    for f in range(FT):
                        pe.wait_ge(hidden, c * FT + f + 1)
                        mm = pe.matmul(yps[:, c % 2, :], wb[:, f, :], hid[:, c % 2, f, :], start=(f == 0), stop=(f == FT - 1))
                    mm.then_inc(down, 1)

            @block.scalar
            def _(act):
                for c in range(NCH):
                    if c >= 2:
                        act.wait_ge(down, c - 1)
                    for f in range(FT):
                        act.wait_ge(up, c * FT + f + 1)
                        act.activation(hid[:, c % 2, f, :], ups[:, f, :], ACT.Gelu_apprx_tanh, bias=m.col(b1, f))\
                           .then_inc(hidden, 1)

            @block.gpsimd
            def _(pool):
                for c in range(NCH):
                    pool.tensor_tensor(m.x[:, cs(c)], m.x[:, cs(c)], base[:, cs(c)], ALU.add).then_inc(based, 1)

            @block.vector
            def _(dve):
                for c in range(NCH):
                    dve.wait_ge(down, c + 1)
                    dve.wait_ge(based, c + 1)
                    dve.scalar_tensor_tensor(out=m.x[:, cs(c)], in0=yps[:, c % 2, :], scalar=m.col(b2),
                                             in1=m.x[:, cs(c)], op0=ALU.add, op1=ALU.add).then_inc(added, 1)


def layer1_attention(nc, m, inp):
    KEPS = 1e-3
    with ExitStack() as own:
        sb = lambda name, shape: own.enter_context(sbuf(nc, name, shape))
        y, q, xres = sb("l1_y", [P, TOK]), sb("phi_q", [P, TOK]), sb("x_res", [P, TOK])
        wq, wkv, wo, bkv = sb("w_q", [P, P]), sb("w_kv", [P, 2 * P]), sb("w_o", [P, P]), sb("b_kv", [1, 2 * P])
        load_all(nc, [(wq[:], inp["L1_attn_Wq"].rearrange("i h d -> i (h d)")),
                      (wkv[:, 0:P], inp["L1_attn_Wk"].rearrange("i h d -> i (h d)")),
                      (wkv[:, P:2 * P], inp["L1_attn_Wv"].rearrange("i h d -> i (h d)")),
                      (wo[:], inp["L1_attn_Wo"].rearrange("h d o -> (h d) o")),
                      (bkv[:, 0:P], inp["L1_attn_bk"].rearrange("(o h) d -> o (h d)", o=1)),
                      (bkv[:, P:2 * P], inp["L1_attn_bv"].rearrange("(o h) d -> o (h d)", o=1))])
        layernorm(nc, m, m.xn, y, 1e-6, scale=m.col("L1_attn_ln1_scale"), bias=m.col("L1_attn_ln1_bias"))
        kf, vo = sb("phi_k", [P, 2, P]), sb("v_and_one", [P, 2, P + 1])
        kvb, ksb = sb("kv_blocks", [P, P]), sb("ksum_blocks", [P, P])
        inv = sb("inverse_den", [P, 2, CH])
        with ExitStack() as inner:
            kvps = inner.enter_context(psum(nc, "k_v_tokens", [P, 2, CH]))
            kvsum = inner.enter_context(psum(nc, "kv_sum", [P, CH]))
            qps = inner.enter_context(psum(nc, "q_proj", [P, NCH, CH]))
            with stage(nc, "kv_tokens", "q_logits", "kv_raw", "k_ready", "v_ready", "kv_sum", "ones_set", "blocks", "q_ready",
                       "q_biased") as (
                    block, kv_tokens, q_logits, kv_raw, k_ready, v_ready, kv_sum, ones_set, blocks, q_ready, q_biased):
                @block.tensor
                def _(pe):
                    def sums(n):
                        pe.wait_ge(k_ready, n + 1)
                        pe.wait_ge(v_ready, n + 1)
                        pe.matmul(kvsum[:, 0:P + 1], kf[:, n % 2, :], vo[:, n % 2, :], start=(n == 0), stop=(n == NT - 1))\
                          .then_inc(kv_sum, 1)

                    for n in range(NT):
                        if n >= 2:
                            pe.wait_ge(k_ready, n - 1)
                            pe.wait_ge(v_ready, n - 1)
                        pe.matmul(kvps[:, n % 2, 0:2 * P], y[:, n * P:(n + 1) * P], wkv[:], start=True, stop=False)
                        pe.matmul(kvps[:, n % 2, 0:2 * P], m.ones[0:1, :], bkv[:], start=False, stop=True)\
                          .then_inc(kv_tokens, 1)
                        if n:
                            sums(n - 1)
                    sums(NT - 1)
                    for c in range(NCH):
                        pe.matmul(qps[:, c, :], wq[:], y[:, cs(c)], start=True, stop=True).then_inc(q_logits, 1)

                @block.scalar
                def _(act):
                    act.wait_ge(ones_set, 1)
                    for n in range(NT):
                        act.wait_ge(kv_tokens, n + 1)
                        if n >= 2:
                            act.wait_ge(kv_sum, n - 1)
                        act.activation(vo[:, n % 2, 0:P], kvps[:, n % 2, P:2 * P], ACT.Copy).then_inc(v_ready, 1)
                    for c in range(NCH):
                        act.wait_ge(q_logits, c + 1)
                        act.activation(q[:, cs(c)], qps[:, c, :], ACT.Relu, bias=m.col("L1_attn_bq")).then_inc(q_biased, 1)

                @block.vector
                def _(dve):
                    dve.memset(vo[:, :, P:P + 1], 1.0).then_inc(ones_set, 1)
                    for n in range(NT):
                        dve.wait_ge(v_ready, n + 1)
                        if n >= 2:
                            dve.wait_ge(kv_sum, n - 1)
                        dve.tensor_scalar(kf[:, n % 2, :], kvps[:, n % 2, 0:P], 0.0, KEPS, ALU.max, ALU.add).then_inc(k_ready, 1)
                    dve.wait_ge(kv_sum, NT)
                    dve.tensor_tensor(kvb[:], kvsum[:, 0:P], m.head_ones[:], ALU.mult).then_inc(blocks, 1)
                    dve.tensor_scalar(ksb[:], m.head_ones[:], kvsum[:, P:P + 1], None, ALU.mult).then_inc(blocks, 1)
                    for c in range(NCH):
                        dve.wait_ge(q_biased, c + 1)
                        dve.tensor_scalar(q[:, cs(c)], q[:, cs(c)], KEPS, None, ALU.add).then_inc(q_ready, 1)
        with ExitStack() as inner:
            num = inner.enter_context(psum(nc, "numerator", [P, 2, CH]))
            den = inner.enter_context(psum(nc, "denominator", [P, 2, CH]))
            ops = inner.enter_context(psum(nc, "attn_proj", [P, 2, CH]))
            with stage(nc, "num_ready", "den_ready", "inverted", "attn_ready", "projected", "res_ready", "res_biased") as (
                    block, num_ready, den_ready, inverted, attn_ready, projected, res_ready, res_biased):
                @block.tensor
                def _(pe):
                    def project(c):
                        pe.wait_ge(attn_ready, c + 1)
                        if c >= 2:
                            pe.wait_ge(res_ready, c - 1)
                        pe.matmul(ops[:, c % 2, :], wo[:], q[:, cs(c)], start=True, stop=True).then_inc(projected, 1)

                    for c in range(NCH):
                        if c >= 2:
                            pe.wait_ge(attn_ready, c - 1)
                        pe.matmul(den[:, c % 2, :], ksb[:], q[:, cs(c)], start=True, stop=True).then_inc(den_ready, 1)
                        pe.matmul(num[:, c % 2, :], kvb[:], q[:, cs(c)], start=True, stop=True).then_inc(num_ready, 1)
                        if c:
                            project(c - 1)
                    project(NCH - 1)

                @block.vector
                def _(dve):
                    def residual(c):
                        dve.wait_ge(projected, c + 1)
                        dve.scalar_tensor_tensor(out=xres[:, cs(c)], in0=ops[:, c % 2, :], scalar=m.col("L1_attn_bo"),
                                                 in1=m.xn[:, cs(c)], op0=ALU.add, op1=ALU.add).then_inc(res_ready, 1)

                    for c in range(NCH):
                        dve.wait_ge(den_ready, c + 1)
                        dve.reciprocal(inv[:, c % 2, :], den[:, c % 2, :]).then_inc(inverted, 1)
                        dve.wait_ge(inverted, c + 1)
                        dve.wait_ge(num_ready, c + 1)
                        dve.tensor_tensor(q[:, cs(c)], num[:, c % 2, :], inv[:, c % 2, :], ALU.mult).then_inc(attn_ready, 1)
                        if c:
                            residual(c - 1)
                    residual(NCH - 1)
        layernorm(nc, m, xres, y, 1e-6, scale=m.col("L1_attn_ln2_scale"), bias=m.col("L1_attn_ln2_bias"))
        hidden_mlp(nc, m, y, inp["L1_attn_W1"], inp["L1_attn_W2"], "L1_attn_b1", "L1_attn_b2", xres)


def layer1_ffn(nc, m, inp):
    U, INNER = 64, 16
    UT = U * INNER // P
    PER = P // INNER
    with ExitStack() as own:
        sb = lambda name, shape: own.enter_context(sbuf(nc, name, shape))
        win, wout = sb("w_in", [P, U]), sb("w_out", [U, P])
        unit_rows = sb("unit_rows", [U, UT, P])
        unit_cols = sb("unit_cols", [P, UT, U])
        s, hid, g = sb("units", [U, TOK]), sb("unit_hidden", [P, 2, CH]), sb("unit_out", [U, TOK])
        load_all(nc, [(win[:], inp["L1_ffn_Win"]), (wout[:], inp["L1_ffn_Wout"])])
        sps = own.enter_context(psum(nc, "units_in", [U, 2, CH]))
        hps = own.enter_context(psum(nc, "units_spread", [P, 2, CH]))
        gps = own.enter_context(psum(nc, "units_sum", [U, 2, CH]))
        ops = own.enter_context(psum(nc, "units_out", [P, 2, CH]))
        with stage(nc, "ones_set", "shaped", "scaled", "units_in", "units_ready", "spread", "hidden", "summed", "biased",
                   "out_ready", "added") as (
                block, ones_set, shaped, scaled, units_in, units_ready, spread, hidden, summed, biased, out_ready, added):
            @block.gpsimd
            def _(pool):
                pool.memset(unit_rows[:], 1.0).then_inc(ones_set, 1)
                pool.memset(unit_cols[:], 1.0).then_inc(ones_set, 1)
                pool.wait_ge(ones_set, 2)
                v = unit_rows[:].rearrange("m i (u h) -> m i u h", h=INNER)
                pool.affine_select(out=v, in_=v, compare_op=ALU.is_equal, fill=0.0, base=0,
                                   pattern=[[-PER, UT], [-1, PER], [0, INNER]], channel_multiplier=1).then_inc(shaped, 1)
                pool.affine_select(out=unit_cols[:], in_=unit_cols[:], compare_op=ALU.is_ge, fill=0.0, base=0,
                                   pattern=[[P, UT], [-INNER, U]], channel_multiplier=1).then_inc(shaped, 1)
                pool.wait_ge(shaped, 2)
                pool.affine_select(out=unit_cols[:], in_=unit_cols[:], compare_op=ALU.is_ge, fill=0.0, base=INNER - 1,
                                   pattern=[[-P, UT], [INNER, U]], channel_multiplier=-1).then_inc(shaped, 1)

            @block.tensor
            def _(pe):
                for c in range(NCH):
                    if c >= 2:
                        pe.wait_ge(units_ready, c - 1)
                    pe.matmul(sps[:, c % 2, :], win[:], m.xn[:, cs(c)], start=True, stop=True).then_inc(units_in, 1)
                pe.wait_ge(shaped, 3)
                pe.wait_ge(scaled, UT)

                def add_up(k):
                    c, i = divmod(k, UT)
                    pe.wait_ge(hidden, k + 1)
                    if i == 0 and c >= 2:
                        pe.wait_ge(biased, c - 1)
                    pe.matmul(gps[:, c % 2, :], unit_cols[:, i, :], hid[:, k % 2, :], start=(i == 0), stop=(i == UT - 1))\
                      .then_inc(summed, 1)

                for k in range(NCH * UT):
                    c, i = divmod(k, UT)
                    pe.wait_ge(units_ready, c + 1)
                    if k >= 2:
                        pe.wait_ge(hidden, k - 1)
                    pe.matmul(hps[:, k % 2, :], unit_rows[:, i, :], s[:, cs(c)], start=True, stop=True).then_inc(spread, 1)
                    if k:
                        add_up(k - 1)
                add_up(NCH * UT - 1)
                for c in range(NCH):
                    pe.wait_ge(biased, c + 1)
                    if c >= 2:
                        pe.wait_ge(added, c - 1)
                    pe.matmul(ops[:, c % 2, :], wout[:], g[:, cs(c)], start=True, stop=True).then_inc(out_ready, 1)

            @block.scalar
            def _(act):
                for k in range(NCH * UT):
                    c, i = divmod(k, UT)
                    act.wait_ge(spread, k + 1)
                    if k >= 2:
                        act.wait_ge(summed, k - 1)
                    act.activation(hid[:, k % 2, :], hps[:, k % 2, :], ACT.Relu, bias=m.col("L1_ffn_b1", i),
                                   scale=m.col("L1_ffn_W1", i)).then_inc(hidden, 1)

            @block.vector
            def _(dve):
                dve.wait_ge(shaped, 3)
                for i in range(UT):
                    dve.tensor_scalar(unit_cols[:, i, :], unit_cols[:, i, :], m.col("L1_ffn_W2", i), None, ALU.mult)\
                       .then_inc(scaled, 1)
                for c in range(NCH):
                    dve.wait_ge(units_in, c + 1)
                    dve.tensor_scalar(s[:, cs(c)], sps[:, c % 2, :], m.col("L1_ffn_bin_", 0, U), None, ALU.add)\
                       .then_inc(units_ready, 1)
                for c in range(NCH):
                    dve.wait_ge(summed, (c + 1) * UT)
                    dve.tensor_scalar(g[:, cs(c)], gps[:, c % 2, :], m.col("L1_ffn_b2", 0, U), None, ALU.add).then_inc(biased, 1)
                for c in range(NCH):
                    dve.wait_ge(out_ready, c + 1)
                    dve.scalar_tensor_tensor(out=m.x[:, cs(c)], in0=ops[:, c % 2, :], scalar=m.col("L1_ffn_bout"),
                                             in1=m.x[:, cs(c)], op0=ALU.add, op1=ALU.add).then_inc(added, 1)



def layer2_ffn(nc, m, inp):
    with ExitStack() as own:
        sb = lambda name, shape: own.enter_context(sbuf(nc, name, shape))
        w, wt = sb("w_rkv", [P, 3, P]), sb("w_rkv_T", [P, 3, P])
        om = sb("one_less_mu", [P, 2])
        prev = sb("x_before", [P, TOK])
        mix = sb("mixed", [P, 2, TOK])
        rr, kk = sb("r_gate", [P, TOK]), sb("k_act", [P, TOK])
        load_all(nc, [(w[:, 0, :], inp["L2_ffn_W_r"]), (w[:, 1, :], inp["L2_ffn_W_k"]), (w[:, 2, :], inp["L2_ffn_W_v"])])
        wps = own.enter_context(psum(nc, "w_turned", [P, CH]))
        ps = own.enter_context(psum(nc, "rk", [P, 4, CH]))
        vps = own.enter_context(psum(nc, "v", [P, 2, CH]))
        mus = ("L2_ffn_mu_r", "L2_ffn_mu_k")
        with stage(nc, "w_turned", "w_ready", "om_ready", "zeroed", "prev_ready", "first", "mixed", "r_logits", "k_logits",
                   "r_ready", "k_relu", "k_ready", "v_ready", "gated", "added") as (
                block, w_turned, w_ready, om_ready, zeroed, prev_ready, first, mixed, r_logits, k_logits,
                r_ready, k_relu, k_ready, v_ready, gated, added):
            @block.tensor
            def _(pe):
                for i in range(3):
                    pe.transpose(wps[:, i * P:(i + 1) * P], w[:, i, :], m.ident[:]).then_inc(w_turned, 1)
                pe.wait_ge(w_ready, 1)
                for c in range(NCH):
                    pe.wait_ge(mixed, 2 * c + 2)
                    if c >= 2:
                        pe.wait_ge(r_ready, c - 1)
                        pe.wait_ge(k_relu, c - 1)
                    pe.matmul(ps[:, c % 2, :], wt[:, 0, :], mix[:, 0, cs(c)], start=True, stop=True).then_inc(r_logits, 1)
                    pe.matmul(ps[:, 2 + c % 2, :], wt[:, 1, :], mix[:, 1, cs(c)], start=True, stop=True).then_inc(k_logits, 1)
                for c in range(NCH):
                    pe.wait_ge(k_ready, c + 1)
                    if c >= 2:
                        pe.wait_ge(gated, c - 1)
                    pe.matmul(vps[:, c % 2, :], wt[:, 2, :], kk[:, cs(c)], start=True, stop=True).then_inc(v_ready, 1)

            @block.scalar
            def _(act):
                for c in range(NCH):
                    act.wait_ge(r_logits, c + 1)
                    act.activation(rr[:, cs(c)], ps[:, c % 2, :], ACT.Sigmoid).then_inc(r_ready, 1)
                    act.wait_ge(k_logits, c + 1)
                    act.activation(kk[:, cs(c)], ps[:, 2 + c % 2, :], ACT.Relu).then_inc(k_relu, 1)
                    act.wait_ge(k_relu, c + 1)
                    act.activation(kk[:, cs(c)], kk[:, cs(c)], ACT.Square).then_inc(k_ready, 1)

            @block.gpsimd
            def _(pool):
                pool.memset(prev[:, 0:1], 0.0).then_inc(zeroed, 1)
                pool.tensor_copy(prev[:, 1:TOK], m.xn[:, 0:TOK - 1]).then_inc(prev_ready, 1)
                for c in range(NCH):
                    pool.wait_ge(gated, c + 1)
                    pool.tensor_tensor(m.x[:, cs(c)], m.x[:, cs(c)], rr[:, cs(c)], ALU.add).then_inc(added, 1)

            @block.vector
            def _(dve):
                dve.wait_ge(w_turned, 3)
                dve.tensor_copy(wt[:].rearrange("p i n -> p (i n)"), wps[:, 0:3 * P]).then_inc(w_ready, 1)
                for i in range(2):
                    dve.tensor_scalar(om[:, i:i + 1], m.col(mus[i]), -1.0, 1.0, ALU.mult, ALU.add).then_inc(om_ready, 1)
                dve.wait_ge(om_ready, 2)
                dve.wait_ge(zeroed, 1)
                dve.wait_ge(prev_ready, 1)
                for c in range(NCH):
                    for i in range(2):
                        dve.tensor_scalar(mix[:, i, cs(c)], prev[:, cs(c)], om[:, i:i + 1], None, ALU.mult).then_inc(first, 1)
                        dve.wait_ge(first, 2 * c + i + 1)
                        dve.scalar_tensor_tensor(out=mix[:, i, cs(c)], in0=m.xn[:, cs(c)], scalar=m.col(mus[i]),
                                                 in1=mix[:, i, cs(c)], op0=ALU.mult, op1=ALU.add).then_inc(mixed, 1)
                for c in range(NCH):
                    dve.wait_ge(v_ready, c + 1)
                    dve.wait_ge(r_ready, c + 1)
                    dve.tensor_tensor(rr[:, cs(c)], rr[:, cs(c)], vps[:, c % 2, :], ALU.mult).then_inc(gated, 1)



WIN = 32
LAT, LH = 64, 8
NEG = -1e30


def l2_window(nc, m, inp, r):
    STEPS = TOK // (2 * WIN)
    KW = 2 * WIN
    with ExitStack() as own:
        sb = lambda name, shape: own.enter_context(sbuf(nc, name, shape))
        xpad = sb("x_padded", [P, WIN + TOK])
        kg = sb("k_groups", [P, 4, WIN + TOK])
        mask = sb("window_mask", [P, KW])
        mask0 = sb("first_mask", [P, 2, KW])
        vmask = sb("v_mask", [P, 2, P])
        wv = sb("w_v", [P, P])
        qm = sb("q_masked", [P, 2, 2, 4, WIN])
        xw = sb("x_window", [P, 2, 2, 2, KW])
        x = sb("window_scores", [P, 2, 2 * 4, KW])
        st = sb("window_stats", [P, 2, 2, 8])
        pt = sb("window_pT", [P, 2, 4, P])
        vm = sb("v_masked", [P, 2, 2, 2, P])
        o = sb("window_o", [P, 2, 2, 4, WIN])
        load_all(nc, [(wv[:], inp["L2_attn_wv"])])
        vps = own.enter_context(psum(nc, "v_window", [P, 2, CH]))
        sps = own.enter_context(psum(nc, "window_qk", [P, 2, CH]))
        tps = own.enter_context(psum(nc, "window_turned", [P, 2, CH]))
        ops = own.enter_context(psum(nc, "window_out", [P, 2, CH]))
        with stage(nc, "padded", "k_cut", "masks_set", "vmask_set", "q_masked", "x_copied", "v_raw", "scored",
                      "v_masked", "shifted", "maxed", "less_max", "exped", "totaled", "inverted", "p_ready",
                      "turned", "pt_ready", "out_raw", "out_picked", "local_ready") as (
                block, padded, k_cut, masks_set, vmask_set, q_masked, x_copied, v_raw, scored, v_masked, shifted,
                maxed, less_max, exped, totaled, inverted, p_ready, turned, pt_ready, out_raw, out_picked,
                local_ready):

            def steps(eng, body):
                body(0, 0, True)
                body(1, 1, True)
                with eng.Fori(0, (STEPS - 4) // 2) as i:
                    body(i * 2 + 2, 0, False)
                    body(i * 2 + 3, 1, False)
                body(STEPS - 2, 0, False)
                body(STEPS - 1, 1, False)

            def at(t, s, off):
                return t[:, s * KW + off:s * KW + off + KW] if isinstance(s, int) else t[:, ds(s * KW + off, KW)]

            @block.gpsimd
            def _(pool):
                pool.memset(xpad[:, 0:WIN], 0.0).then_inc(padded, 1)
                pool.tensor_copy(xpad[:, WIN:], m.xn[:]).then_inc(padded, 1)
                pool.memset(kg[:, :, 0:WIN], 0.0).then_inc(padded, 1)
                pool.memset(mask[:], 0.0).then_inc(masks_set, 1)
                pool.wait_ge(masks_set, 1)
                for q in range(4):
                    part = mask[q * WIN:(q + 1) * WIN, :]
                    pool.affine_select(out=part, in_=part, compare_op=ALU.is_gt, fill=NEG, base=0,
                                       pattern=[[1, KW]], channel_multiplier=-1).then_inc(masks_set, 1)
                pool.wait_ge(masks_set, 5)
                for q in range(4):
                    part = mask[q * WIN:(q + 1) * WIN, :]
                    pool.affine_select(out=part, in_=part, compare_op=ALU.is_ge, fill=NEG, base=WIN,
                                       pattern=[[-1, KW]], channel_multiplier=1).then_inc(masks_set, 1)
                pool.wait_ge(masks_set, 9)
                for b in range(2):
                    pool.tensor_copy(mask0[:, b, :], mask[:]).then_inc(masks_set, 1)
                pool.wait_ge(masks_set, 11)
                pool.memset(mask0[:, 0, 0:WIN], NEG).then_inc(masks_set, 1)

                def body(s, par, first):
                    if not first:
                        pool.wait_ge(scored, s - 1)
                        pool.wait_ge(v_raw, s - 1)
                    if first and s == 0:
                        pool.wait_ge(padded, 3)
                    pool.tensor_tensor(qm[:, par], at(r.q, s, 0).rearrange("p (b i) -> p b i", b=2).unsqueeze(2)
                                       .to_broadcast([P, 2, 4, WIN]),
                                       m.hmod[:].unsqueeze(1).unsqueeze(3).to_broadcast([P, 2, 4, WIN]), ALU.mult)\
                        .then_inc(q_masked, 1)
                    for b in range(2):
                        win = at(xpad, s, b * WIN)
                        pool.tensor_copy(xw[:, par, b], win.unsqueeze(1).to_broadcast([P, 2, KW])).then_inc(x_copied, 1)

                steps(pool, body)

            @block.tensor
            def _(pe):
                pe.wait_ge(k_cut, 4)
                pe.wait_ge(padded, 3)

                def front(s, par, first):
                    pe.wait_ge(q_masked, s + 1)
                    pe.wait_ge(x_copied, s * 2 + 2)
                    if not first:
                        pe.wait_ge(shifted, s - 1)
                        pe.wait_ge(v_masked, (s - 1) * 2)
                    for b in range(2):
                        mm = pe.matmul(vps[:, par, b * P:(b + 1) * P], xw[:, par, b].rearrange("p a j -> p (a j)"), wv[:],
                                       start=True, stop=True)
                    mm.then_inc(v_raw, 1)
                    for b in range(2):
                        keys = kg[:, :, (s * 2 + b) * WIN:(s * 2 + b + 2) * WIN] if isinstance(s, int) \
                            else kg[:, :, ds(s * KW + b * WIN, KW)]
                        mm = pe.matmul(sps[:, par, b * 256:(b + 1) * 256], qm[:, par, b].rearrange("p a i -> p (a i)"), keys,
                                       start=True, stop=True)
                    mm.then_inc(scored, 1)

                def back(s, par, first):
                    pe.wait_ge(p_ready, s + 1)
                    if not first:
                        pe.wait_ge(pt_ready, s - 1)
                        pe.wait_ge(out_picked, s - 1)
                    for i in range(4):
                        mm = pe.transpose(tps[:, par, i * P:(i + 1) * P],
                                          x[:, par, 2 * i:2 * i + 2, :].rearrange("p g j -> p (g j)"), m.ident[:])
                    mm.then_inc(turned, 1)
                    pe.wait_ge(pt_ready, s + 1)
                    pe.wait_ge(v_masked, s * 2 + 2)
                    for b in range(2):
                        for i in range(2):
                            mm = pe.matmul(ops[:, par, b * P:(b + 1) * P], vm[:, par, b, i, :], pt[:, par, 2 * b + i, :],
                                           start=(i == 0), stop=(i == 1))
                    mm.then_inc(out_raw, 1)

                def body(s, par, first):
                    if not isinstance(s, int) or s + 1 < STEPS:
                        front(s + 1, 1 - par, first and s == 0)
                    back(s, par, first)

                front(0, 0, True)
                steps(pe, body)

            @block.scalar
            def _(act):
                def body(s, par, first):
                    act.wait_ge(less_max, s + 1)
                    act.activation(x[:, par], x[:, par], ACT.Exp).then_inc(exped, 1)
                    act.wait_ge(turned, s + 1)
                    if not first:
                        act.wait_ge(out_raw, s - 1)
                    act.activation(pt[:, par].rearrange("p a n -> p (a n)"), tps[:, par, :], ACT.Copy).then_inc(pt_ready, 1)

                steps(act, body)

            @block.vector
            def _(dve):
                for g in range(4):
                    dve.tensor_scalar(kg[:, g, WIN:], r.k[:], m.hdiv[:, g:g + 1], None, ALU.mult).then_inc(k_cut, 1)
                for i in range(2):
                    for pair in range(2):
                        g = 2 * pair + i
                        dve.tensor_scalar(vmask[i * 64:(i + 1) * 64, pair, :], m.ones[i * 64:(i + 1) * 64, :], 0.0, None,
                                          ALU.mult).then_inc(vmask_set, 1)
                        dve.wait_ge(vmask_set, 2 * (2 * i + pair) + 1)
                        dve.memset(vmask[i * 64:(i + 1) * 64, pair, 32 * g:32 * g + 32], 1.0).then_inc(vmask_set, 1)
                dve.wait_ge(vmask_set, 8)
                dve.wait_ge(masks_set, 12)
                G8 = [P, 8, KW]

                def front(s, par, first):
                    if not first:
                        dve.wait_ge(out_raw, s - 1)
                        dve.wait_ge(turned, s - 1)
                    dve.wait_ge(v_raw, s + 1)
                    for b in range(2):
                        dve.tensor_tensor(vm[:, par, b], vps[:, par, b * P:(b + 1) * P].unsqueeze(1).to_broadcast([P, 2, P]),
                                          vmask[:], ALU.mult).then_inc(v_masked, 1)
                    dve.wait_ge(scored, s + 1)
                    if first and s == 0:
                        mk = mask0[:].unsqueeze(2).to_broadcast([P, 2, 4, KW])
                        for b in range(2):
                            ins = dve.scalar_tensor_tensor(
                                out=x[:, par, 4 * b:4 * b + 4], in0=sps[:, par, b * 256:(b + 1) * 256].rearrange("p (g j) -> p g j", j=KW),
                                scalar=HD ** -0.5, in1=mk[:, b], op0=ALU.mult, op1=ALU.add)
                        ins.then_inc(shifted, 1)
                    else:
                        dve.scalar_tensor_tensor(out=x[:, par], in0=sps[:, par, :].rearrange("p (g j) -> p g j", j=KW),
                                                 scalar=HD ** -0.5, in1=mask[:].unsqueeze(1).to_broadcast(G8),
                                                 op0=ALU.mult, op1=ALU.add).then_inc(shifted, 1)
                    dve.wait_ge(shifted, s + 1)
                    dve.tensor_reduce(st[:, par, 0, :], x[:, par], AX.X, ALU.max).then_inc(maxed, 1)
                    dve.wait_ge(maxed, s + 1)
                    dve.tensor_tensor(x[:, par], x[:, par], st[:, par, 0, :].unsqueeze(2).to_broadcast(G8), ALU.subtract)\
                       .then_inc(less_max, 1)

                def middle(s, par):
                    dve.wait_ge(exped, s + 1)
                    dve.tensor_reduce(st[:, par, 1, :], x[:, par], AX.X, ALU.add).then_inc(totaled, 1)
                    dve.wait_ge(totaled, s + 1)
                    dve.reciprocal(st[:, par, 1, :], st[:, par, 1, :]).then_inc(inverted, 1)
                    dve.wait_ge(inverted, s + 1)
                    dve.tensor_tensor(x[:, par], x[:, par], st[:, par, 1, :].unsqueeze(2).to_broadcast(G8), ALU.mult)\
                       .then_inc(p_ready, 1)

                def back(s, par):
                    dve.wait_ge(out_raw, s + 1)
                    dve.tensor_tensor(o[:, par], ops[:, par, 0:2 * P].rearrange("p (b a i) -> p b a i", b=2, a=4),
                                      m.hmod[:].unsqueeze(1).unsqueeze(3).to_broadcast([P, 2, 4, WIN]), ALU.mult)\
                       .then_inc(out_picked, 1)
                    dve.wait_ge(out_picked, s + 1)
                    dve.tensor_reduce(at(r.local, s, 0).rearrange("p (b i) -> p b i", b=2),
                                      o[:, par].rearrange("p b a i -> p b i a"), AX.X, ALU.add).then_inc(local_ready, 1)

                def body(s, par, first):
                    middle(s, par)
                    if not isinstance(s, int) or s + 1 < STEPS:
                        front(s + 1, 1 - par, first and s == 0)
                    back(s, par)

                front(0, 0, True)
                steps(dve, body)


def l2_latent(nc, m, inp, r):
    NL = LAT
    W = LH * NL
    LD = 64
    with ExitStack() as own:
        sb = lambda name, shape: own.enter_context(sbuf(nc, name, shape))
        wg = sb("w_latent", [P, 3, LD])
        pool2 = sb("pooled", [P, 2, NL])
        gk = sb("latent_keys", [LD, LH, NL])
        gv = sb("latent_values", [P, 4, LD])
        lmask = sb("latent_mask", [P, NT, NL])
        gq = sb("latent_q", [LD, 2, P])
        x = sb("latent_scores", [P, 2, LH, NL])
        st = sb("latent_stats", [P, 2, 2, LH])
        pt = sb("latent_pT", [P, 2, 4, P])
        pm = sb("pooled_mean", [P, NL])
        load_all(nc, [(wg[:, 0, :], inp["L2_attn_wgq"]), (wg[:, 1, :], inp["L2_attn_wgk"]), (wg[:, 2, :], inp["L2_attn_wgv"])])
        cps = own.enter_context(psum(nc, "latent_const", [P, CH]))
        qps = own.enter_context(psum(nc, "latent_q_raw", [P, CH]))
        sps = own.enter_context(psum(nc, "latent_qk", [P, 2, CH]))
        tps = own.enter_context(psum(nc, "latent_turned", [P, 2, CH]))
        rps = own.enter_context(psum(nc, "latent_out", [LD, 2, CH]))
        with stage(nc, "mask_set", "pooled", "kv_raw", "blocks", "q_raw", "q_ready", "scored", "shifted", "maxed",
                      "less_max", "exped", "totaled", "inverted", "p_ready", "turned", "pt_ready", "out_raw",
                      "rem_ready") as (
                block, mask_set, pooled, kv_raw, blocks, q_raw, q_ready, scored, shifted, maxed, less_max, exped,
                totaled, inverted, p_ready, turned, pt_ready, out_raw, rem_ready):

            def steps(eng, body):
                body(0, 0, True)
                body(1, 1, True)
                with eng.Fori(0, (NT - 4) // 2) as i:
                    body(i * 2 + 2, 0, False)
                    body(i * 2 + 3, 1, False)
                body(NT - 2, 0, False)
                body(NT - 1, 1, False)

            def tile(t, n):
                return t[:, n * P:(n + 1) * P] if isinstance(n, int) else t[:, ds(n * P, P)]

            @block.gpsimd
            def _(pool):
                pool.memset(lmask[:], 0.0).then_inc(mask_set, 1)
                pool.wait_ge(mask_set, 1)
                for q in range(4):
                    part = lmask[q * 32:(q + 1) * 32]
                    pool.affine_select(out=part, in_=part, compare_op=ALU.is_ge, fill=NEG, base=q,
                                       pattern=[[4, NT], [-1, NL]], channel_multiplier=0).then_inc(mask_set, 1)

            @block.tensor
            def _(pe):
                pe.wait_ge(pooled, 3)
                pe.matmul(cps[0:LD, 0:NL], wg[:, 1, :], pm[:], start=True, stop=True)
                pe.matmul(cps[:, NL:NL + LD], pool2[:].rearrange("p a n -> p (a n)"), wg[:, 2, :], start=True, stop=True)\
                  .then_inc(kv_raw, 1)
                pe.wait_ge(blocks, 10)

                def front(n, par, first):
                    if not (isinstance(n, int) and n == 0):
                        pe.wait_ge(q_ready, n)
                    pe.matmul(qps[0:LD, 0:P], wg[:, 0, :], tile(m.xn, n), start=True, stop=True).then_inc(q_raw, 1)
                    pe.wait_ge(q_ready, n + 1)
                    if not first:
                        pe.wait_ge(shifted, n - 1)
                    pe.matmul(sps[:, par, :], gq[:, par, :], gk[:].rearrange("p h n -> p (h n)"), start=True, stop=True)\
                      .then_inc(scored, 1)

                def back(n, par, first):
                    pe.wait_ge(p_ready, n + 1)
                    if not first:
                        pe.wait_ge(pt_ready, n - 1)
                        pe.wait_ge(rem_ready, n - 1)
                    for i in range(4):
                        mm = pe.transpose(tps[:, par, i * P:(i + 1) * P],
                                          x[:, par, 2 * i:2 * i + 2, :].rearrange("p g j -> p (g j)"), m.ident[:])
                    mm.then_inc(turned, 1)
                    pe.wait_ge(pt_ready, n + 1)
                    for i in range(4):
                        mm = pe.matmul(rps[:, par, 0:P], gv[:, i, :], pt[:, par, i, :], start=(i == 0), stop=(i == 3))
                    mm.then_inc(out_raw, 1)

                def body(n, par, first):
                    if not isinstance(n, int) or n + 1 < NT:
                        front(n + 1, 1 - par, first and n == 0)
                    back(n, par, first)

                front(0, 0, True)
                steps(pe, body)

            @block.scalar
            def _(act):
                def copy_q(n, par, first):
                    act.wait_ge(q_raw, n + 1)
                    if not first:
                        act.wait_ge(scored, n - 1)
                    act.activation(gq[:, par, :], qps[0:LD, 0:P], ACT.Copy).then_inc(q_ready, 1)

                def body(n, par, first):
                    act.wait_ge(less_max, n + 1)
                    act.activation(x[:, par], x[:, par], ACT.Exp).then_inc(exped, 1)
                    if not isinstance(n, int) or n + 1 < NT:
                        copy_q(n + 1, 1 - par, first and n == 0)
                    act.wait_ge(turned, n + 1)
                    if not first:
                        act.wait_ge(out_raw, n - 1)
                    act.activation(pt[:, par].rearrange("p a n -> p (a n)"), tps[:, par, :], ACT.Copy).then_inc(pt_ready, 1)

                copy_q(0, 0, True)
                steps(act, body)

            @block.vector
            def _(dve):
                CHUNK = TOK // NL
                dve.tensor_reduce(pm[:], m.xn[:].rearrange("p (n c) -> p n c", c=CHUNK), AX.X, ALU.add).then_inc(pooled, 1)
                dve.wait_ge(pooled, 1)
                dve.tensor_scalar(pm[:], pm[:], 1.0 / CHUNK, None, ALU.mult).then_inc(pooled, 1)
                dve.wait_ge(pooled, 2)
                dve.tensor_copy(pool2[:], pm[:].unsqueeze(1).to_broadcast([P, 2, NL])).then_inc(pooled, 1)
                dve.wait_ge(kv_raw, 1)
                dve.tensor_tensor(gk[:], cps[0:LD, 0:NL].unsqueeze(1).to_broadcast([LD, LH, NL]),
                                  m.head_ones[0:LD, 0:LD].rearrange("p (h e) -> p h e", e=HD)[:, :, 0:1]
                                  .to_broadcast([LD, LH, NL]), ALU.mult).then_inc(blocks, 1)
                dve.tensor_scalar(gv[:], m.ones[:, 0:64].unsqueeze(1).to_broadcast([P, 4, LD]), 0.0, None, ALU.mult)\
                   .then_inc(blocks, 1)
                dve.wait_ge(blocks, 2)
                for i in range(4):
                    for half in range(2):
                        h = 2 * i + half
                        rows = slice(half * 64, half * 64 + 64)
                        dve.tensor_copy(gv[rows, i, HD * h:HD * h + HD], cps[rows, NL + HD * h:NL + HD * h + HD])\
                           .then_inc(blocks, 1)
                dve.wait_ge(mask_set, 5)
                G8 = [P, LH, NL]

                def front(n, par, first):
                    if not first:
                        dve.wait_ge(turned, n - 1)
                    mk = lmask[:, n:n + 1, :] if isinstance(n, int) else lmask[:, ds(n, 1), :]
                    dve.wait_ge(scored, n + 1)
                    dve.scalar_tensor_tensor(out=x[:, par], in0=sps[:, par, :].rearrange("p (g j) -> p g j", j=NL),
                                             scalar=HD ** -0.5, in1=mk.to_broadcast(G8),
                                             op0=ALU.mult, op1=ALU.add).then_inc(shifted, 1)
                    dve.wait_ge(shifted, n + 1)
                    dve.tensor_reduce(st[:, par, 0, :], x[:, par], AX.X, ALU.max).then_inc(maxed, 1)
                    dve.wait_ge(maxed, n + 1)
                    dve.tensor_tensor(x[:, par], x[:, par], st[:, par, 0, :].unsqueeze(2).to_broadcast(G8), ALU.subtract)\
                       .then_inc(less_max, 1)

                def middle(n, par):
                    dve.wait_ge(exped, n + 1)
                    dve.tensor_reduce(st[:, par, 1, :], x[:, par], AX.X, ALU.add).then_inc(totaled, 1)
                    dve.wait_ge(totaled, n + 1)
                    dve.reciprocal(st[:, par, 1, :], st[:, par, 1, :]).then_inc(inverted, 1)
                    dve.wait_ge(inverted, n + 1)
                    dve.tensor_tensor(x[:, par], x[:, par], st[:, par, 1, :].unsqueeze(2).to_broadcast(G8), ALU.mult)\
                       .then_inc(p_ready, 1)

                def body(n, par, first):
                    middle(n, par)
                    if not isinstance(n, int) or n + 1 < NT:
                        front(n + 1, 1 - par, first and n == 0)
                    dve.wait_ge(out_raw, n + 1)
                    dve.tensor_copy(tile(r.rem, n), rps[:, par, 0:P]).then_inc(rem_ready, 1)

                front(0, 0, True)
                steps(dve, body)


def layer2_attention(nc, m, inp):
    with ExitStack() as own:
        sb = lambda name, shape: own.enter_context(sbuf(nc, name, shape))
        r = Named()
        r.q, r.local, r.rem = sb("l2_q", [P, TOK]), sb("l2_local", [P, TOK]), sb("l2_rem", [64, TOK])
        w = sb("w_l2", [P, 3, P])
        wr = sb("w_r_out", [64, P])
        gate_w = sb("gate_blocks", [P, 2, P])
        load_all(nc, [(w[:, 0, :], inp["L2_attn_wq"]), (w[:, 1, :], inp["L2_attn_wk"]), (w[:, 2, :], inp["L2_attn_w_out"]),
                      (wr[:], inp["L2_attn_r_out_w"])])
        with ExitStack() as inner:
            r.k = inner.enter_context(sbuf(nc, "l2_k", [P, TOK]))
            with psum(nc, "qk_proj", [P, 2, NCH, CH]) as ps, stage(nc, "q_raw", "k_raw", "q_ready", "k_ready", "gates") as (
                    block, q_raw, k_raw, q_ready, k_ready, gates):
                @block.tensor
                def _(pe):
                    for c in range(NCH):
                        pe.matmul(ps[:, 0, c, :], w[:, 0, :], m.xn[:, cs(c)], start=True, stop=True).then_inc(q_raw, 1)
                        pe.matmul(ps[:, 1, c, :], w[:, 1, :], m.xn[:, cs(c)], start=True, stop=True).then_inc(k_raw, 1)

                @block.scalar
                def _(act):
                    for c in range(NCH):
                        act.wait_ge(q_raw, c + 1)
                        act.activation(r.q[:, cs(c)], ps[:, 0, c, :], ACT.Copy).then_inc(q_ready, 1)

                @block.vector
                def _(dve):
                    for i, name in enumerate(("L2_attn_gate_local_w", "L2_attn_gate_remote_w")):
                        dve.tensor_scalar(gate_w[:, i, :], m.head_ones[:], m.col(name), None, ALU.mult).then_inc(gates, 1)
                    for c in range(NCH):
                        dve.wait_ge(k_raw, c + 1)
                        dve.tensor_copy(r.k[:, cs(c)], ps[:, 1, c, :]).then_inc(k_ready, 1)
            l2_window(nc, m, inp, r)
        l2_latent(nc, m, inp, r)
        gate = sb("gates", [P, 2, 2, CH])
        gps = own.enter_context(psum(nc, "gate_logits", [P, 2, 2, CH]))
        rps = own.enter_context(psum(nc, "rem_proj", [P, 2, CH]))
        ops = own.enter_context(psum(nc, "l2_out", [P, 2, CH]))
        with stage(nc, "logits", "gated", "rem_raw", "local_scaled", "rem_scaled", "mixed", "projected", "added") as (
                block, logits, gated, rem_raw, local_scaled, rem_scaled, mixed, projected, added):
            @block.tensor
            def _(pe):
                def project(c):
                    pe.wait_ge(mixed, c + 1)
                    if c >= 2:
                        pe.wait_ge(added, c - 1)
                    pe.matmul(ops[:, c % 2, :], w[:, 2, :], r.local[:, cs(c)], start=True, stop=True).then_inc(projected, 1)

                for c in range(NCH):
                    if c >= 2:
                        pe.wait_ge(gated, 2 * c - 2)
                        pe.wait_ge(rem_scaled, c - 1)
                    for i in range(2):
                        pe.matmul(gps[:, i, c % 2, :], gate_w[:, i, :], r.q[:, cs(c)], start=True, stop=True).then_inc(logits, 1)
                    pe.matmul(rps[:, c % 2, :], wr[:], r.rem[:, cs(c)], start=True, stop=True).then_inc(rem_raw, 1)
                    if c:
                        project(c - 1)
                project(NCH - 1)

            @block.scalar
            def _(act):
                for c in range(NCH):
                    if c >= 2:
                        act.wait_ge(mixed, c - 1)
                    for i in range(2):
                        act.wait_ge(logits, 2 * c + i + 1)
                        act.activation(gate[:, i, c % 2, :], gps[:, i, c % 2, :], ACT.Sigmoid).then_inc(gated, 1)

            @block.vector
            def _(dve):
                def add(c):
                    dve.wait_ge(projected, c + 1)
                    dve.tensor_tensor(m.x[:, cs(c)], ops[:, c % 2, :], m.x[:, cs(c)], ALU.add).then_inc(added, 1)

                for c in range(NCH):
                    dve.wait_ge(gated, 2 * c + 1)
                    dve.tensor_tensor(r.local[:, cs(c)], r.local[:, cs(c)], gate[:, 0, c % 2, :], ALU.mult).then_inc(local_scaled, 1)
                    dve.wait_ge(gated, 2 * c + 2)
                    dve.wait_ge(rem_raw, c + 1)
                    dve.tensor_tensor(gate[:, 1, c % 2, :], rps[:, c % 2, :], gate[:, 1, c % 2, :], ALU.mult).then_inc(rem_scaled, 1)
                    dve.wait_ge(rem_scaled, c + 1)
                    dve.wait_ge(local_scaled, c + 1)
                    dve.tensor_tensor(r.local[:, cs(c)], r.local[:, cs(c)], gate[:, 1, c % 2, :], ALU.add).then_inc(mixed, 1)
                    if c:
                        add(c - 1)
                add(NCH - 1)



F16 = mybir.dt.float16


def weave(a, b, early=0.0):
    out, i = [], 0
    for j, y in enumerate(b):
        while i < len(a) and i * len(b) <= (j + early) * len(a):
            out.append(a[i])
            i += 1
        out.append(y)
    return out + a[i:]


def layer3_attention(nc, m, inp):
    H, DH = 16, 64
    SCALE, EPS = DH ** -0.5, 1e-8
    LIFT = 2.0 ** 14
    RB = 5
    VW = 2 * DH + 1
    groups = lambda t: t // 4 + 1
    g0 = lambda t: sum(groups(x) for x in range(t))
    G = g0(NT)
    width = lambda t, g: min(CH, (t + 1) * P - g * CH)
    hi = slice(DH, P)

    UNITS = [("q", c) for c in range(NCH)] + [("k", c) for c in range(NCH)] + [("v", i) for i in range(2)]
    unit_of_step = lambda t: t - 1 if 1 <= t <= len(UNITS) else None
    slots, slot_of = [], {}
    for t in range(NT):
        if unit_of_step(t) is not None:
            slot_of["unit", unit_of_step(t)] = len(slots)
            slots.append(("unit", unit_of_step(t)))
        if t == NT - 1:
            slots.append(None)
        for c in reversed(range(NCH)):
            slot_of[t + 1, c] = len(slots)
            slots.append((t + 1, c))
    assert len(slots) % RB == 0
    for c in range(NCH):
        slot_of[0, c] = slot_of[NT, c] - len(slots)
    bank = lambda *what: slot_of[what] % RB

    with ExitStack() as own:
        sb = lambda name, shape, dt=F32: own.enter_context(nc.sbuf_tensor(f"{name}_{nc.next_id()}", shape, dt))
        o_all = sb("o_all", [P, NT, H * DH])
        with ExitStack() as inner:
            sb = lambda name, shape, dt=F32: inner.enter_context(nc.sbuf_tensor(f"{name}_{nc.next_id()}", shape, dt))
            wq, wk, wv = sb("w_q2", [P, 2, DH]), sb("w_k2", [P, 2, DH]), sb("w_v", [P, DH])
            qs2, kh2, kl2 = (sb(n, [P, 2, TOK], F16) for n in ("q_pair", "k_high", "k_low"))
            v2 = sb("v_pair", [P, 2, NT, VW], F16)
            p = sb("p", [P, 2, TOK])
            ph, pl = sb("pT_high", [P, 4, CH], F16), sb("pT_low", [P, 4, CH], F16)
            tri = sb("past", [P, P])
            mx, bias = sb("chunk_max", [P, 2, NCH]), sb("exp_bias", [P, NT])
            raw = sb("o_raw", [P, 2, NT, VW])
            den = sb("den", [P, 2, 2, NT])
            ps = inner.enter_context(psum(nc, "scores", [P, 8, CH]))
            with stage(nc, "w_loaded", "const_set", "q_raw", "k_raw", "v_raw", "q_high", "q_low", "k_highs",
                       "k_lows", "v_high", "v_low", "scored", "chunk_maxed", "biased", "exped", "masked", "turned",
                       "pt_high", "pt_low", "summed", "o_out", "den_set", "den_inverted", "o_summed", "o_ready") as (
                    block, w_loaded, const_set, q_raw, k_raw, v_raw, q_high, q_low, k_highs, k_lows, v_high, v_low,
                    scored, chunk_maxed, biased, exped, masked, turned, pt_high, pt_low, summed, o_out, den_set,
                    den_inverted, o_summed, o_ready):

                def heads(eng, prologue, head):
                    prologue(lambda per_head, k, ahead=0: per_head * ahead + k - per_head)

                    def pair(i, last):
                        for par in range(2):
                            head(lambda per_head, k, ahead=0: i * (2 * per_head) + (par + ahead) * per_head + k,
                                 par, i * 2 + par, last and par == 1)

                    with eng.Fori(0, H // 2 - 1) as i:
                        pair(i, False)
                    pair(H // 2 - 1, True)

                @block.sync
                def _(sp):
                    def load(h):
                        for dst, src in ((wq, inp["L3_attn_Wq"]), (wk, inp["L3_attn_Wkv"])):
                            for r in range(2):
                                sp.dma_start(dst[:, r, :], src[:, ds(h * DH, DH)]).then_inc(w_loaded, 16)
                        sp.dma_start(wv[:], inp["L3_attn_Wkv"][:, ds(h * DH + H * DH, DH)]).then_inc(w_loaded, 16)

                    load(0)
                    with sp.Fori(1, H) as h:
                        sp.wait_ge(v_raw, h * 2)
                        load(h)

                @block.gpsimd
                def _(pool):
                    pool.memset(tri[:], 1.0).then_inc(const_set, 1)
                    pool.memset(v2[:, :, :, 2 * DH:VW], 1.0).then_inc(const_set, 1)
                    pool.wait_ge(const_set, 2)
                    pool.affine_select(out=tri[:], in_=tri[:], compare_op=ALU.is_ge, fill=0.0, base=0,
                                       pattern=[[-1, P]], channel_multiplier=1).then_inc(const_set, 1)
                    pool.wait_ge(const_set, 3)

                    def head(at, par, h, last):
                        for t in range(NT):
                            pool.wait_ge(exped, at(G, g0(t + 1)))
                            diag = p[:, t % 2, t * P:(t + 1) * P]
                            pool.tensor_tensor(diag, diag, tri[:], ALU.mult).then_inc(masked, 1)
                        pool.wait_ge(o_out, at(NT, NT))
                        part = lambda a: raw[:, par, :, a:a + DH]
                        pool.tensor_tensor(part(0), part(0), part(DH), ALU.add).then_inc(o_summed, 1)
                        pool.wait_ge(o_summed, at(1, 1))
                        pool.wait_ge(den_inverted, at(1, 1))
                        pool.tensor_tensor(o_all[:, :, ds(h * DH, DH)], part(0),
                                           den[:, par, 1, :].unsqueeze(2).to_broadcast([P, NT, DH]), ALU.mult)\
                            .then_inc(o_ready, 1)

                    heads(pool, lambda at: None, head)

                @block.tensor
                def _(pe):
                    def free(at, slot, last):
                        slot -= RB
                        while last and slot >= 0 and slots[slot][0] == "unit":
                            slot -= RB
                        ahead = 0
                        if slot < 0:
                            slot, ahead = slot + len(slots), -1
                        what = slots[slot]
                        if what is None:
                            return
                        if what[0] == "unit":
                            kind, k = UNITS[what[1]]
                            done, each = {"q": (q_low, NCH), "k": (k_lows, NCH), "v": (v_low, 2)}[kind]
                            pe.wait_ge(done, at(each, k + 1, ahead + 1))
                        else:
                            t, c = what
                            if t == NT:
                                t, ahead = 0, ahead + 1
                            pe.wait_ge(chunk_maxed, at(NT * NCH, t * NCH + NCH - c, ahead))
                            if c < groups(t):
                                pe.wait_ge(exped, at(G, g0(t) + groups(t) - c, ahead))

                    def project(at, u, b):
                        kind, c = UNITS[u]
                        if u == 0:
                            pe.wait_ge(w_loaded, at(80, 80, 1))
                        if kind == "v":
                            for n in range(8):
                                mm = pe.matmul(ps[:, b, n * DH:(n + 1) * DH], m.xn[:, (8 * c + n) * P:(8 * c + n + 1) * P],
                                               wv[:], start=True, stop=True)
                            mm.then_inc(v_raw, 1)
                        else:
                            w, done = (wq, q_raw) if kind == "q" else (wk, k_raw)
                            pe.matmul(ps[:, b, :], w[:].rearrange("p r d -> p (r d)"), m.xn[:, cs(c)],
                                      start=True, stop=True).then_inc(done, 1)

                    def scores(at, par, t, c):
                        b = bank(t, c)
                        if t == NT:
                            t, par = 0, 1 - par
                            if c == NCH - 1:
                                pe.wait_ge(q_low, at(NCH, NCH, 1))
                                pe.wait_ge(k_lows, at(NCH, NCH, 1))
                        q = qs2[:, par, t * P:(t + 1) * P]
                        pe.matmul(ps[:, b, :], q, kh2[:, par, cs(c)], start=True, stop=False)
                        pe.matmul(ps[:, b, :], q, kl2[:, par, cs(c)], start=False, stop=True).then_inc(scored, 1)

                    def turn(at, t, g):
                        n = g0(t) + g
                        if n >= 2:
                            pe.wait_ge(pt_low, at(G, n - 1))
                        if g == 0:
                            pe.wait_ge(masked, at(NT, t + 1))
                        for b in range(4 * g, min(4 * g + 4, t + 1)):
                            mm = pe.transpose(ps[:, 5 + n % 2, b % 4 * P:(b % 4 + 1) * P],
                                              p[:, t % 2, b * P:(b + 1) * P], m.ident[:])
                        mm.then_inc(turned, 1)

                    def add_up(at, par, t, g):
                        n = g0(t) + g
                        pe.wait_ge(pt_low, at(G, n + 1))
                        if g == 0:
                            if t:
                                pe.wait_ge(o_out, at(NT, t))
                            else:
                                pe.wait_ge(v_low, at(2, 2))
                        for b in range(4 * g, min(4 * g + 4, t + 1)):
                            for part in (ph, pl):
                                mm = pe.matmul(ps[:, 7, 0:VW], part[:, n % 4, b % 4 * P:(b % 4 + 1) * P], v2[:, par, b, :],
                                               start=(b == 0 and part is ph), stop=(b == t and part is pl))
                        mm.then_inc(summed, 1)

                    def products(t):
                        if t < 0:
                            return []
                        use = [("t", t, 0)]
                        for g in range(1, groups(t)):
                            use += [("t", t, g), ("a", t, g - 1)]
                        return use + [("a", t, groups(t) - 1)]

                    def head(at, par, h, last):
                        for t in range(NT):
                            u = unit_of_step(t)
                            fill = [] if last and t == NT - 1 else [("s", c) for c in reversed(range(NCH))]
                            if u is not None and not last:
                                fill = [("u", u)] + fill
                            work = weave(fill, products(t - 1), 0.5)
                            if t == NT - 1:
                                work += products(t)
                            for what in work:
                                if what[0] == "u":
                                    free(at, slot_of["unit", what[1]], last)
                                    project(at, what[1], bank("unit", what[1]))
                                elif what[0] == "s":
                                    free(at, slot_of[t + 1, what[1]], last)
                                    scores(at, par, t + 1, what[1])
                                elif what[0] == "t":
                                    turn(at, what[1], what[2])
                                else:
                                    add_up(at, par, what[1], what[2])

                    def prologue(at):
                        for u in range(len(UNITS)):
                            if u >= 8:
                                pe.wait_ge(q_low, u - 7)
                            project(at, u, u % 8)
                        pe.wait_ge(v_low, 2)
                        for c in reversed(range(NCH)):
                            scores(at, 1, NT, c)

                    heads(pe, prologue, head)

                @block.scalar
                def _(act):
                    def high(at, par, u, b):
                        kind, c = UNITS[u]
                        if kind == "q":
                            act.wait_ge(q_raw, at(NCH, c + 1, 1))
                            act.activation(qs2[:, par, cs(c)], ps[:, b, :], ACT.Copy, scale=SCALE).then_inc(q_high, 1)
                        elif kind == "k":
                            act.wait_ge(k_raw, at(NCH, c + 1, 1))
                            act.activation(kh2[:, par, cs(c)], ps[:, b, :], ACT.Copy).then_inc(k_highs, 1)
                        else:
                            act.wait_ge(v_raw, at(2, c + 1, 1))
                            act.activation(v2[:, par, 8 * c:8 * c + 8, 0:DH],
                                           ps[:, b, :].rearrange("p (n d) -> p n d", d=DH), ACT.Copy).then_inc(v_high, 1)

                    def exp(at, t, c):
                        if c == groups(t) - 1:
                            if t >= 2:
                                act.wait_ge(turned, at(G, g0(t - 1)))
                            act.wait_ge(biased, at(NT, t + 1))
                        w = width(t, c)
                        act.activation(p[:, t % 2, c * CH:c * CH + w], ps[:, bank(t, c), 0:w], ACT.Exp,
                                       bias=bias[:, t:t + 1]).then_inc(exped, 1)

                    def pt(at, t, g):
                        n, w = g0(t) + g, width(t, g)
                        act.wait_ge(turned, at(G, n + 1))
                        if n >= 4:
                            act.wait_ge(summed, at(G, n - 3))
                        act.activation(ph[:, n % 4, 0:w], ps[:, 5 + n % 2, 0:w], ACT.Copy, scale=LIFT).then_inc(pt_high, 1)

                    def out(at, par, t):
                        act.wait_ge(summed, at(G, g0(t + 1)))
                        act.activation(raw[:, par, t, :], ps[:, 7, 0:VW], ACT.Copy).then_inc(o_out, 1)

                    def head(at, par, h, last):
                        for t in range(NT):
                            if unit_of_step(t) is not None and not last:
                                high(at, 1 - par, unit_of_step(t), bank("unit", unit_of_step(t)))
                            exps = [("e", c) for c in reversed(range(groups(t)))]
                            pts = [("p", g) for g in range(groups(t - 1))] if t else []
                            for what in weave(exps, pts):
                                if what[0] == "e":
                                    exp(at, t, what[1])
                                else:
                                    pt(at, t - 1, what[1])
                            if t:
                                out(at, par, t - 1)
                        for g in range(groups(NT - 1)):
                            pt(at, NT - 1, g)
                        out(at, par, NT - 1)

                    def prologue(at):
                        for u in range(len(UNITS)):
                            high(at, 0, u, u % 8)

                    heads(act, prologue, head)

                @block.vector
                def _(dve):
                    def low(at, par, u, b):
                        kind, c = UNITS[u]
                        if kind == "q":
                            dve.wait_ge(q_high, at(NCH, c + 1, 1))
                            low_part = qs2[hi, par, cs(c)]
                            dve.scalar_tensor_tensor(out=low_part, in0=ps[hi, b, :], scalar=SCALE, in1=low_part,
                                                     op0=ALU.mult, op1=ALU.subtract).then_inc(q_low, 1)
                        elif kind == "k":
                            dve.wait_ge(k_highs, at(NCH, c + 1, 1))
                            dve.tensor_tensor(kl2[:, par, cs(c)], ps[:, b, :], kh2[:, par, cs(c)], ALU.subtract)\
                               .then_inc(k_lows, 1)
                        else:
                            dve.wait_ge(v_high, at(2, c + 1, 1))
                            dve.tensor_tensor(v2[:, par, 8 * c:8 * c + 8, DH:2 * DH],
                                              ps[:, b, :].rearrange("p (n d) -> p n d", d=DH),
                                              v2[:, par, 8 * c:8 * c + 8, 0:DH], ALU.subtract).then_inc(v_low, 1)

                    def chunk_max(at, t, c):
                        t, ahead, b = (0, 1, NT) if t == NT else (t, 0, t)
                        dve.wait_ge(scored, at(NT * NCH, t * NCH + NCH - c, ahead))
                        dve.tensor_reduce(mx[:, t % 2, c:c + 1], ps[:, bank(b, c), :], AX.X, ALU.max)\
                           .then_inc(chunk_maxed, 1)

                    def tile_max(at, t):
                        t, ahead = (0, 1) if t == NT else (t, 0)
                        dve.wait_ge(chunk_maxed, at(NT * NCH, (t + 1) * NCH, ahead))
                        dve.tensor_reduce(bias[:, t:t + 1], mx[:, t % 2, :], AX.X, ALU.max, negate=True)\
                           .then_inc(biased, 1)

                    def pt(at, t, g):
                        n, w = g0(t) + g, width(t, g)
                        dve.wait_ge(pt_high, at(G, n + 1))
                        dve.scalar_tensor_tensor(out=pl[:, n % 4, 0:w], in0=ps[:, 5 + n % 2, 0:w], scalar=LIFT,
                                                 in1=ph[:, n % 4, 0:w], op0=ALU.mult, op1=ALU.subtract).then_inc(pt_low, 1)

                    def head(at, par, h, last):
                        for t in range(NT):
                            if unit_of_step(t) is not None and not last:
                                low(at, 1 - par, unit_of_step(t), bank("unit", unit_of_step(t)))
                            ahead = [] if last and t == NT - 1 else [("m", c) for c in reversed(range(NCH))]
                            pts = [("p", g) for g in range(groups(t - 1))] if t else []
                            for what in weave(ahead, pts, -1):
                                if what[0] == "m":
                                    chunk_max(at, t + 1, what[1])
                                else:
                                    pt(at, t - 1, what[1])
                            if ahead:
                                tile_max(at, t + 1)
                        for g in range(groups(NT - 1)):
                            pt(at, NT - 1, g)
                        dve.wait_ge(o_out, at(NT, NT))
                        dve.tensor_scalar(den[:, par, 0, :], raw[:, par, :, 2 * DH], EPS * LIFT, None, ALU.add)\
                           .then_inc(den_set, 1)
                        dve.wait_ge(den_set, at(1, 1))
                        dve.reciprocal(den[:, par, 1, :], den[:, par, 0, :]).then_inc(den_inverted, 1)

                    def prologue(at):
                        for u in range(len(UNITS)):
                            low(at, 0, u, u % 8)
                        for c in reversed(range(NCH)):
                            chunk_max(at, NT, c)
                        tile_max(at, NT)

                    heads(dve, prologue, head)
        wo = own.enter_context(sbuf(nc, "w_o3", [P, H * DH // P, P]))
        oT = own.enter_context(sbuf(nc, "o_T", [P, 2, CH]))
        tps = own.enter_context(psum(nc, "o_turned", [P, 2, CH]))
        ops = own.enter_context(psum(nc, "o_proj", [P, NCH, CH]))
        KT = H * DH // P
        load_all(nc, [(wo[:], inp["L3_attn_Wo"].rearrange("(k p) n -> p k n", p=P))])
        with stage(nc, "turned", "copied", "projected", "added") as (block, turned, copied, projected, added):
            @block.tensor
            def _(pe):
                def project(i):
                    c, k = divmod(i, KT)
                    pe.wait_ge(copied, i + 1)
                    pe.matmul(ops[:, c, :], wo[:, k, :], oT[:, i % 2, :], start=(k == 0), stop=(k == KT - 1)).then_inc(projected, 1)

                for i in range(NCH * KT):
                    c, k = divmod(i, KT)
                    if i >= 2:
                        pe.wait_ge(copied, i - 1)
                    for n in range(4):
                        mm = pe.transpose(tps[:, i % 2, n * P:(n + 1) * P], o_all[:, 4 * c + n, k * P:(k + 1) * P], m.ident[:])
                    mm.then_inc(turned, 1)
                    if i:
                        project(i - 1)
                project(NCH * KT - 1)

            @block.scalar
            def _(act):
                for i in range(NCH * KT):
                    act.wait_ge(turned, i + 1)
                    if i >= 2:
                        act.wait_ge(projected, i - 1)
                    act.activation(oT[:, i % 2, :], tps[:, i % 2, :], ACT.Copy).then_inc(copied, 1)

            @block.vector
            def _(dve):
                for c in range(NCH):
                    dve.wait_ge(projected, (c + 1) * KT)
                    dve.scalar_tensor_tensor(out=m.x[:, cs(c)], in0=ops[:, c, :], scalar=m.col("L3_attn_bo"),
                                             in1=m.x[:, cs(c)], op0=ALU.add, op1=ALU.add).then_inc(added, 1)



def build(nc, inp, out):
    with ExitStack() as own:
        m = Named()
        alloc = lambda name, shape: own.enter_context(sbuf(nc, name, shape))
        constants(nc, m, inp, alloc)
        m.x = alloc("x_features", [P, TOK])
        m.xn = alloc("xn_features", [P, TOK])
        turn_in(nc, m, inp["L0_attn_x"])
        for attention, ffn in ((layer0_attention, layer0_experts), (layer1_attention, layer1_ffn),
                               (layer2_attention, layer2_ffn), (layer3_attention, layer3_experts)):
            layernorm(nc, m, m.x, m.xn, LN_EPS)
            attention(nc, m, inp)
            ffn(nc, m, inp)
        turn_out(nc, m, out)


_OUTS = [((1, 2048, 128), 'float32')]


def kernel(**inputs):
    import numpy as _np
    import concourse.bacc as _bacc
    from concourse import mybir as _mybir
    from concourse.bass_utils import run_bass_kernel_spmd as _run

    nc = _bacc.Bacc("TRN2", target_bir_lowering=False, num_devices=1)
    arrays, args = {}, {}
    for name in inputs:
        a = _np.ascontiguousarray(inputs[name])
        arrays[f"in_{name}_dram"] = a
        args[name] = nc.dram_tensor(f"in_{name}_dram", a.shape, _mybir.dt.from_np(a.dtype), kind="ExternalInput").ap()
    shape, dtype = _OUTS[0]
    out = nc.dram_tensor("out_0_dram", shape, _mybir.dt.from_np(_np.dtype(dtype)), kind="ExternalOutput").ap()
    build(nc, args, out)
    r = _run(nc, [arrays], core_ids=[0])
    return r.results[0]["out_0_dram"]
```

```python
from contextlib import ExitStack, contextmanager

import concourse.bass as bass
from concourse import mybir

F32 = mybir.dt.float32
ALU = mybir.AluOpType
ACT = mybir.ActivationFunctionType
AX = mybir.AxisListType
ds = bass.ds

P = 128
TOK = 2048
CH = 512
NCH = TOK // CH
NT = TOK // P
HEADS, HD = 16, 8
LN_EPS = 1e-5


class Named:
    pass


def sbuf(nc, name, shape):
    return nc.sbuf_tensor(f"{name}_{nc.next_id()}", shape, F32)


def psum(nc, name, shape):
    return nc.psum_tensor(f"{name}_{nc.next_id()}", shape, F32)


def cs(c):
    return slice(c * CH, (c + 1) * CH)


@contextmanager
def stage(nc, *signals):
    sems = [nc.alloc_semaphore(f"{name}_{nc.next_id()}") for name in signals]
    with nc.Block() as block:
        yield (block, *sems)
    nc.clear_and_free_semaphores(sems)
    nc.all_engine_barrier()


VECTORS = {
    "L0_attn_bq": 1, "L0_attn_bk": 1, "L0_attn_bv": 1, "L0_attn_bg": 1, "L0_attn_gn_scale": 1,
    "L0_attn_gn_bias": 1, "L0_attn_bo": 1, "L0_ffn_b1": 64, "L0_ffn_b2": 8,
    "L1_attn_ln1_scale": 1, "L1_attn_ln1_bias": 1, "L1_attn_bq": 1, "L1_attn_bo": 1,
    "L1_attn_ln2_scale": 1, "L1_attn_ln2_bias": 1, "L1_attn_b1": 4, "L1_attn_b2": 1,
    "L1_ffn_b1": 8, "L1_ffn_W1": 8, "L1_ffn_W2": 8, "L1_ffn_bout": 1,
    "L2_ffn_mu_r": 1, "L2_ffn_mu_k": 1, "L2_attn_gate_local_w": 1, "L2_attn_gate_remote_w": 1,
    "L3_attn_bo": 1, "L3_ffn_attn_nw": 1, "L3_ffn_attn_nb": 1, "L3_ffn_inter_b": 32, "L3_ffn_output_b": 8,
    "L3_ffn_res_inter_b": 4, "L3_ffn_res_output_b": 1,
    "L0_ffn_br1": 1, "L0_ffn_ln_scale": 1, "L0_ffn_ln_bias": 1, "L1_ffn_bin_": 1, "L1_ffn_b2": 1,
}
SHORT = {"L0_ffn_br1": 64, "L0_ffn_ln_scale": 64, "L0_ffn_ln_bias": 64, "L1_ffn_bin_": 64, "L1_ffn_b2": 64}


def row_of_vectors():
    at, n = {}, 0
    for name, rows in VECTORS.items():
        if n % P + rows > P:
            n = (n // P + 1) * P
        at[name] = n
        n += rows
    return at, -(-n // P)


def constants(nc, m, inp, alloc, x_dram):
    at, tiles = row_of_vectors()
    m.at = at
    m.ident = alloc("ident", [P, P])
    m.mean_w = alloc("mean_w", [P, P])
    m.head_ones = alloc("head_ones", [P, P])
    m.pick = alloc("pick", [P, HD, P])
    m.hmod = alloc("hmod", [P, 4])
    m.eye8 = alloc("eye8", [P, HD])
    m.hdiv = alloc("hdiv", [P, 4])
    m.ones = alloc("ones", [P, P])
    m.cols = alloc("cols", [P, tiles * P])
    m.col = lambda name, i=0, n=P: m.cols[0:n, at[name] + i:at[name] + i + 1]
    with ExitStack() as own:
        rows = own.enter_context(sbuf(nc, "vector_rows", [P, tiles, P]))
        turned = own.enter_context(psum(nc, "vectors_turned", [P, tiles, CH]))
        with stage(nc, "rows_zeroed", "ones_set", "shaped", "rows_loaded", "vectors_turned", "cols_ready",
                   "x_loaded") as (
                block, rows_zeroed, ones_set, shaped, rows_loaded, vectors_turned, cols_ready, x_loaded):

            @block.gpsimd
            def _(pool):
                for t in (m.ident, m.head_ones, m.pick, m.ones):
                    pool.memset(t[:], 1.0).then_inc(ones_set, 1)
                pool.memset(m.mean_w[:], 1.0 / P).then_inc(ones_set, 1)
                pool.memset(m.hdiv[:], 1.0).then_inc(ones_set, 1)
                pool.wait_ge(ones_set, 6)
                pool.affine_select(out=m.ident[:], in_=m.ident[:], compare_op=ALU.is_equal, fill=0.0, base=0,
                                   pattern=[[-1, P]], channel_multiplier=1).then_inc(shaped, 1)
                pool.affine_select(out=m.pick[:].rearrange("p e (h d) -> p e h d", d=HD),
                                   in_=m.pick[:].rearrange("p e (h d) -> p e h d", d=HD),
                                   compare_op=ALU.is_equal, fill=0.0, base=0,
                                   pattern=[[-1, HD], [-HD, HEADS], [0, HD]], channel_multiplier=1).then_inc(shaped, 1)
                blocks = m.head_ones[:].rearrange("p (h d) -> p h d", d=HD)
                pool.affine_select(out=blocks, in_=blocks, compare_op=ALU.is_ge, fill=0.0, base=0,
                                   pattern=[[-HD, HEADS], [0, HD]], channel_multiplier=1).then_inc(shaped, 1)
                pool.wait_ge(shaped, 3)
                pool.affine_select(out=blocks, in_=blocks, compare_op=ALU.is_ge, fill=0.0, base=HD - 1,
                                   pattern=[[HD, HEADS], [0, HD]], channel_multiplier=-1).then_inc(shaped, 1)
                pool.affine_select(out=m.hdiv[:], in_=m.hdiv[:], compare_op=ALU.is_ge, fill=0.0, base=0,
                                   pattern=[[-32, 4]], channel_multiplier=1).then_inc(shaped, 1)
                pool.wait_ge(shaped, 5)
                pool.affine_select(out=m.hdiv[:], in_=m.hdiv[:], compare_op=ALU.is_ge, fill=0.0, base=31,
                                   pattern=[[32, 4]], channel_multiplier=-1).then_inc(shaped, 1)

            def load(eng, names):
                for name in names:
                    tile, r = divmod(at[name], P)
                    src = inp[name]
                    if len(src.shape) == 2:
                        src = src.rearrange("a b -> (a b)")
                    w = SHORT.get(name, P)
                    eng.dma_start(rows[r:r + VECTORS[name], tile, 0:w], src.rearrange("(r c) -> r c", c=w))\
                       .then_inc(rows_loaded, 16)

            @block.sync
            def _(sp):
                sp.dma_start(m.xn[:].rearrange("p (n f) -> p n f", f=P), x_dram.rearrange("b (n p) f -> p (b n) f", p=P)).then_inc(x_loaded, 16)
                sp.wait_ge(rows_zeroed, 1)
                load(sp, list(VECTORS)[0::2])
                sp.wait_ge(x_loaded, 16)

            @block.scalar
            def _(act):
                act.wait_ge(rows_zeroed, 1)
                load(act, list(VECTORS)[1::2])

            @block.vector
            def _(dve):
                dve.memset(rows[:], 0.0).then_inc(rows_zeroed, 1)
                for t in range(tiles):
                    dve.wait_ge(vectors_turned, t + 1)
                    dve.tensor_copy(m.cols[:, t * P:(t + 1) * P], turned[:, t, 0:P]).then_inc(cols_ready, 1)
                dve.wait_ge(shaped, 6)
                dve.tensor_reduce(m.hmod[:], m.head_ones[:].rearrange("p (g i d) -> p i g d", g=4, i=4)[:, :, :, 0],
                                  AX.X, ALU.max).then_inc(cols_ready, 1)
                dve.tensor_reduce(m.eye8[:], m.ident[:].rearrange("p (h e) -> p e h", e=HD),
                                  AX.X, ALU.max).then_inc(cols_ready, 1)

            @block.tensor
            def _(pe):
                pe.wait_ge(shaped, 6)
                pe.wait_ge(rows_loaded, 16 * len(VECTORS))
                for t in range(tiles):
                    pe.transpose(turned[:, t, 0:P], rows[:, t, :], m.ident[:]).then_inc(vectors_turned, 1)


def turn_in(nc, m):
    with ExitStack() as own:
        ps = own.enter_context(psum(nc, "x_turned", [P, NCH, CH]))
        with stage(nc, "x_turned", "xT_ready") as (block, x_turned, xT_ready):
            @block.tensor
            def _(pe):
                for n in range(NT):
                    c, k = divmod(n, CH // P)
                    pe.transpose(ps[:, c, k * P:(k + 1) * P], m.xn[:, n * P:(n + 1) * P], m.ident[:]).then_inc(x_turned, 1)

            @block.vector
            def _(dve):
                for c in range(NCH):
                    dve.wait_ge(x_turned, (c + 1) * (CH // P))
                    dve.tensor_copy(m.x[:, cs(c)], ps[:, c, :]).then_inc(xT_ready, 1)


def turn_out(nc, m, out_dram):
    with ExitStack() as own:
        xtm = own.enter_context(sbuf(nc, "y_token_major", [P, NT, P]))
        ps = own.enter_context(psum(nc, "y_turned", [P, NCH, CH]))
        with stage(nc, "y_turned", "y_copied", "y_stored") as (block, y_turned, y_copied, y_stored):
            @block.tensor
            def _(pe):
                for n in range(NT):
                    c, k = divmod(n, CH // P)
                    pe.transpose(ps[:, c, k * P:(k + 1) * P], m.x[:, n * P:(n + 1) * P], m.ident[:]).then_inc(y_turned, 1)

            @block.vector
            def _(dve):
                for c in range(NCH):
                    dve.wait_ge(y_turned, (c + 1) * (CH // P))
                    dve.tensor_copy(xtm[:, 4 * c:4 * c + 4, :], ps[:, c, :].rearrange("p (n f) -> p n f", f=P))\
                       .then_inc(y_copied, 1)

            @block.sync
            def _(sp):
                out = out_dram.rearrange("b (n p) f -> p (b n) f", p=P)
                for c in range(NCH):
                    sp.wait_ge(y_copied, c + 1)
                    sp.dma_start(out[:, 4 * c:4 * c + 4, :], xtm[:, 4 * c:4 * c + 4, :]).then_inc(y_stored, 16)
                sp.wait_ge(y_stored, 16 * NCH)


def layernorm(nc, m, src, dst, eps, width=P, scale=None, bias=None, after=None, loads=()):
    w = slice(0, width)
    with ExitStack() as own:
        mean = own.enter_context(psum(nc, "ln_mean", [P, NCH, CH]))
        var = own.enter_context(psum(nc, "ln_var", [P, NCH, CH]))
        cen = own.enter_context(sbuf(nc, "ln_centered", [P, TOK]))
        work = own.enter_context(sbuf(nc, "ln_work", [P, TOK]))
        epst = own.enter_context(sbuf(nc, "ln_eps", [P, 1]))
        with stage(nc, "eps_set", "mean_ready", "centered", "squared", "var_ready", "logged", "inverted", "normed",
                   "scaled", "activated", "loaded") as (
                block, eps_set, mean_ready, centered, squared, var_ready, logged, inverted, normed, scaled, activated,
                loaded):
            @block.sync
            def _(sp):
                for tile, source in loads:
                    sp.dma_start(tile, source).then_inc(loaded, 16)
                if loads:
                    sp.wait_ge(loaded, 16 * len(loads))

            @block.tensor
            def _(pe):
                for c in range(NCH):
                    pe.matmul(mean[w, c, :], m.mean_w[w, w], src[w, cs(c)], start=True, stop=True).then_inc(mean_ready, 1)
                for c in range(NCH):
                    pe.wait_ge(squared, c + 1)
                    pe.matmul(var[w, c, :], m.mean_w[w, w], work[w, cs(c)], start=True, stop=True).then_inc(var_ready, 1)

            @block.scalar
            def _(act):
                act.wait_ge(eps_set, 1)
                for c in range(NCH):
                    act.wait_ge(centered, c + 1)
                    act.activation(work[w, cs(c)], cen[w, cs(c)], ACT.Square).then_inc(squared, 1)
                for c in range(NCH):
                    act.wait_ge(var_ready, c + 1)
                    act.activation(work[w, cs(c)], var[w, c, :], ACT.Ln, bias=epst[w, :], scale=float(P // width))\
                       .then_inc(logged, 1)
                for c in range(NCH):
                    act.wait_ge(logged, c + 1)
                    act.activation(work[w, cs(c)], work[w, cs(c)], ACT.Exp, scale=-0.5).then_inc(inverted, 1)
                if after is not None:
                    for c in range(NCH):
                        act.wait_ge(scaled, c + 1)
                        act.activation(dst[w, cs(c)], dst[w, cs(c)], after).then_inc(activated, 1)

            @block.vector
            def _(dve):
                dve.memset(epst[:], eps).then_inc(eps_set, 1)
                for c in range(NCH):
                    dve.wait_ge(mean_ready, c + 1)
                    dve.scalar_tensor_tensor(out=cen[w, cs(c)], in0=mean[w, c, :], scalar=-float(P // width),
                                             in1=src[w, cs(c)], op0=ALU.mult, op1=ALU.add).then_inc(centered, 1)
                for c in range(NCH):
                    dve.wait_ge(inverted, c + 1)
                    dve.tensor_tensor(dst[w, cs(c)], cen[w, cs(c)], work[w, cs(c)], ALU.mult).then_inc(normed, 1)
                    if scale is not None:
                        dve.wait_ge(normed, c + 1)
                        dve.tensor_scalar(dst[w, cs(c)], dst[w, cs(c)], scale, bias, ALU.mult, ALU.add)\
                           .then_inc(scaled, 1)


def load_all(nc, loads):
    with stage(nc, "loaded") as (block, loaded):
        @block.sync
        def _(sp):
            for dst, src in loads[0::2]:
                sp.dma_start(dst, src).then_inc(loaded, 16)
            sp.wait_ge(loaded, 16 * len(loads))

        @block.scalar
        def _(act):
            for dst, src in loads[1::2]:
                act.dma_start(dst, src).then_inc(loaded, 16)



SEG = 32
NSEG = TOK // SEG


def l0_weights(nc, own, inp):
    sb = lambda name, shape: own.enter_context(sbuf(nc, name, shape))
    w = Named()
    w.qkvg, w.ab, w.bab, w.conv = sb("w_qkvg", [P, 4, P]), sb("w_ab", [P, 2, HEADS]), sb("b_ab", [1, 2, HEADS]), \
        sb("conv_w", [P, 3, 4])
    return w, [(w.qkvg[:, 0, :], inp["L0_attn_Wq"]), (w.qkvg[:, 1, :], inp["L0_attn_Wk"]),
               (w.qkvg[:, 2, :], inp["L0_attn_Wv"]), (w.qkvg[:, 3, :], inp["L0_attn_Wg"]),
               (w.ab[:, 0, :], inp["L0_attn_Wa"]), (w.ab[:, 1, :], inp["L0_attn_Wb"]),
               (w.bab[:, 0, :], inp["L0_attn_ba"].rearrange("(a h) -> a h", a=1)),
               (w.bab[:, 1, :], inp["L0_attn_bb"].rearrange("(a h) -> a h", a=1)),
               (w.conv[:, 0, :], inp["L0_attn_q_conv"]), (w.conv[:, 1, :], inp["L0_attn_k_conv"]),
               (w.conv[:, 2, :], inp["L0_attn_v_conv"])]


def l0_project(nc, m, r, w):
    with ExitStack() as own:
        sb = lambda name, shape: own.enter_context(sbuf(nc, name, shape))
        wqkvg, wab, bab, conv = w.qkvg, w.ab, w.bab, w.conv
        wab_wide = sb("w_ab_wide", [P, 2, P])
        bab_wide, bab_col = sb("b_ab_wide", [1, 2, P]), sb("b_ab_col", [P, 2])
        raw = sb("raw", [P, 2, 3 + TOK])
        ps = own.enter_context(psum(nc, "proj", [P, 2, 4, CH]))
        tmp = sb("tmp", [P, TOK])
        sq = sb("sq", [P, 2, TOK])
        norm_eps = sb("norm_eps", [P, 1])
        QKV = ((r.q, "L0_attn_bq"), (r.k, "L0_attn_bk"), (r.bv, "L0_attn_bv"))
        with stage(nc, "padded", "projected", "biased", "tap", "silued", "squared", "summed", "rooted", "logged",
                   "inverted", "done") as (
                block, padded, projected, biased, tap, silued, squared, summed, rooted, logged, inverted, done):

            @block.tensor
            def _(pe):
                for i in range(3):
                    for c in range(NCH):
                        if i == 2:
                            pe.wait_ge(biased, c + 1)
                        pe.matmul(ps[:, i % 2, c, :], wqkvg[:, i, :], m.xn[:, cs(c)], start=True, stop=True)\
                          .then_inc(projected, 1)
                for i in range(2):
                    for c in range(NCH):
                        pe.wait_ge(biased, (i + 1) * NCH + c + 1)
                        pe.wait_ge(squared, i * NCH + c + 1)
                        pe.matmul(ps[:, 1 - i, c, :], m.head_ones[:], sq[:, i, cs(c)], start=True, stop=True)\
                          .then_inc(summed, 1)

            @block.vector
            def _(dve):
                dve.memset(norm_eps[:], 1e-6).then_inc(padded, 1)
                dve.memset(raw[:, :, 0:3], 0.0).then_inc(padded, 1)
                dve.wait_ge(padded, 2)
                for i in range(3):
                    for c in range(NCH):
                        x = lambda j: raw[:, i % 2, c * CH + j:c * CH + j + CH]
                        dve.wait_ge(biased, i * NCH + c + 1)
                        if i:
                            dve.wait_ge(silued, (i - 1) * NCH + c + 1)
                        dve.tensor_scalar(tmp[:, cs(c)], x(0), conv[:, i, 0:1], None, ALU.mult).then_inc(tap, 1)
                        for j in range(1, 4):
                            dve.wait_ge(tap, (i * NCH + c) * 4 + j)
                            dve.scalar_tensor_tensor(out=tmp[:, cs(c)], in0=x(j), scalar=conv[:, i, j:j + 1],
                                                     in1=tmp[:, cs(c)], op0=ALU.mult, op1=ALU.add).then_inc(tap, 1)
                for i in range(2):
                    for c in range(NCH):
                        dst = QKV[i][0][:, cs(c)]
                        dve.wait_ge(inverted, i * NCH + c + 1)
                        dve.tensor_tensor(dst, dst, sq[:, i, cs(c)], ALU.mult).then_inc(done, 1)

            @block.scalar
            def _(act):
                def add_bias(i):
                    for c in range(NCH):
                        act.wait_ge(projected, i * NCH + c + 1)
                        act.activation(raw[:, i % 2, 3 + c * CH:3 + (c + 1) * CH], ps[:, i % 2, c, :], ACT.Identity,
                                       bias=m.col(QKV[i][1])).then_inc(biased, 1)

                add_bias(0)
                add_bias(1)
                for i in range(3):
                    for c in range(NCH):
                        act.wait_ge(tap, (i * NCH + c + 1) * 4)
                        act.activation(QKV[i][0][:, cs(c)], tmp[:, cs(c)], ACT.Silu).then_inc(silued, 1)
                    if i == 0:
                        add_bias(2)
                    if i < 2:
                        for c in range(NCH):
                            act.wait_ge(silued, i * NCH + c + 1)
                            act.activation(sq[:, i, cs(c)], QKV[i][0][:, cs(c)], ACT.Square).then_inc(squared, 1)
                for i in range(2):
                    for c in range(NCH):
                        act.wait_ge(summed, i * NCH + c + 1)
                        act.activation(sq[:, i, cs(c)], ps[:, 1 - i, c, :], ACT.Sqrt).then_inc(rooted, 1)
                act.wait_ge(padded, 1)
                for i in range(2):
                    act.wait_ge(rooted, (i + 1) * NCH)
                    act.activation(sq[:, i, :], sq[:, i, :], ACT.Ln, bias=norm_eps[:]).then_inc(logged, 1)
                for i in range(2):
                    act.wait_ge(logged, i + 1)
                    for c in range(NCH):
                        act.activation(sq[:, i, cs(c)], sq[:, i, cs(c)], ACT.Exp, scale=-1.0).then_inc(inverted, 1)
        with stage(nc, "widened", "bias_turned", "bias_ready", "a_logits", "b_logits", "g_logits", "a_ready", "b_ready", "g_ready", "used") as (
                block, widened, bias_turned, bias_ready, a_logits, b_logits, g_logits, a_ready, b_ready, g_ready, used):
            @block.tensor
            def _(pe):
                pe.wait_ge(widened, 4)
                for i in range(2):
                    mm = pe.matmul(ps[:, 0, 0, i:i + 1], bab_wide[:, i, :], m.ones[0:1, 0:1], start=True, stop=True)
                mm.then_inc(bias_turned, 1)
                pe.wait_ge(bias_ready, 1)
                for c in range(NCH):
                    pe.matmul(ps[:, 0, c, :], wab_wide[:, 0, :], m.xn[:, cs(c)], start=True, stop=True).then_inc(a_logits, 1)
                for c in range(NCH):
                    pe.matmul(ps[:, 1, c, :], wab_wide[:, 1, :], m.xn[:, cs(c)], start=True, stop=True).then_inc(b_logits, 1)
                for c in range(NCH):
                    pe.wait_ge(a_ready, c + 1)
                    pe.matmul(ps[:, 0, c, :], wqkvg[:, 3, :], m.xn[:, cs(c)], start=True, stop=True).then_inc(g_logits, 1)

            @block.scalar
            def _(act):
                for c in range(NCH):
                    act.wait_ge(a_logits, c + 1)
                    act.activation(r.a[:, cs(c)], ps[:, 0, c, :], ACT.Sigmoid, bias=bab_col[:, 0:1]).then_inc(a_ready, 1)
                for c in range(NCH):
                    act.wait_ge(b_logits, c + 1)
                    act.activation(tmp[:, cs(c)], ps[:, 1, c, :], ACT.Sigmoid, bias=bab_col[:, 1:2]).then_inc(b_ready, 1)
                for c in range(NCH):
                    act.wait_ge(g_logits, c + 1)
                    act.activation(r.gate[:, cs(c)], ps[:, 0, c, :], ACT.Silu, bias=m.col("L0_attn_bg")).then_inc(g_ready, 1)

            @block.vector
            def _(dve):
                for i in range(2):
                    dve.tensor_copy(wab_wide[:, i, :].rearrange("p (h d) -> p h d", d=HD),
                                    wab[:, i, :].unsqueeze(2).to_broadcast([P, HEADS, HD])).then_inc(widened, 1)
                    dve.tensor_copy(bab_wide[:, i, :].rearrange("p (h d) -> p h d", d=HD),
                                    bab[:, i, :].unsqueeze(2).to_broadcast([1, HEADS, HD])).then_inc(widened, 1)
                dve.wait_ge(bias_turned, 1)
                dve.tensor_copy(bab_col[:], ps[:, 0, 0, 0:2]).then_inc(bias_ready, 1)
                for c in range(NCH):
                    dve.wait_ge(b_ready, c + 1)
                    dve.tensor_tensor(r.bv[:, cs(c)], r.bv[:, cs(c)], tmp[:, cs(c)], ALU.mult).then_inc(used, 1)
                    dve.scalar_tensor_tensor(out=r.nab[:, cs(c)], in0=r.a[:, cs(c)], scalar=-1.0, in1=tmp[:, cs(c)],
                                             op0=ALU.mult, op1=ALU.mult).then_inc(used, 1)


def l0_join(nc, m, r):
    GJ = 8
    NG = NSEG // GJ
    with ExitStack() as own:
        sb = lambda name, shape: own.enter_context(sbuf(nc, name, shape))
        T = sb("T", [P, NSEG + 1, HD])
        Pb, Cb, Sb = sb("P_blocks", [P, NSEG, P]), sb("C_blocks", [P, 3, GJ, P]), sb("S_blocks", [P, 2, GJ, P])
        nxt = own.enter_context(psum(nc, "T_next", [P, 2, CH]))
        add = own.enter_context(psum(nc, "o_carried", [P, NCH, CH]))
        Zj = r.Z[:].rearrange("p k (e j) -> p k j e", e=HD)
        WIDE = [P, GJ, HEADS, HD]
        hb = m.head_ones[:].rearrange("p (h e) -> p h e", e=HD).unsqueeze(1).to_broadcast(WIDE)
        blocks = lambda x: x.rearrange("p j (h e) -> p j h e", e=HD)
        wide = lambda x: x.unsqueeze(2).to_broadcast(WIDE)
        js = lambda g: slice(g * GJ, (g + 1) * GJ)
        with stage(nc, "t_zeroed", "p_blocks", "c_blocks", "s_blocks", "t_next", "t_ready", "carried", "o_ready") as (
                block, t_zeroed, p_blocks, c_blocks, s_blocks, t_next, t_ready, carried, o_ready):
            @block.gpsimd
            def _(pool):
                pool.memset(T[:, 0:1, :], 0.0).then_inc(t_zeroed, 1)
                pool.wait_ge(t_zeroed, 1)

                def c_group(g):
                    if g >= 3:
                        pool.wait_ge(t_next, (g - 2) * GJ)
                    pool.tensor_tensor(blocks(Cb[:, g % 3, :, :]), wide(Zj[:, 0, js(g), :]), hb, ALU.mult)\
                        .then_inc(c_blocks, 1)

                c_group(0)
                c_group(1)
                for g in range(NG):
                    if g + 2 < NG:
                        c_group(g + 2)
                    pool.wait_ge(t_ready, min((g + 1) * GJ, NSEG) - 1)
                    if g >= 2:
                        pool.wait_ge(carried, (g - 1) * GJ)
                    pool.tensor_tensor(blocks(Sb[:, g % 2, :, :]), wide(T[:, js(g), :]), hb, ALU.mult)\
                        .then_inc(s_blocks, 1)

            @block.tensor
            def _(pe):
                def carry(j):
                    g = j // GJ
                    if j % GJ == 0:
                        pe.wait_ge(s_blocks, g + 1)
                    pe.matmul(add[:].rearrange("p a (b t) -> p (a b) t", t=SEG)[:, j, :], Sb[:, g % 2, j % GJ, :],
                              r.wo[:, 1, j * SEG:(j + 1) * SEG], start=True, stop=True).then_inc(carried, 1)

                for j in range(NSEG):
                    g = j // GJ
                    if j % GJ == 0:
                        pe.wait_ge(c_blocks, g + 1)
                        pe.wait_ge(p_blocks, g + 1)
                    if j >= 2:
                        pe.wait_ge(t_ready, j - 1)
                    pe.matmul(nxt[:, j % 2, 0:HD], Cb[:, g % 3, j % GJ, :], m.eye8[:], start=True, stop=False)
                    if j:
                        pe.wait_ge(t_ready, j)
                    else:
                        pe.wait_ge(t_zeroed, 1)
                    pe.matmul(nxt[:, j % 2, 0:HD], Pb[:, j, :], T[:, j, :], start=False, stop=True).then_inc(t_next, 1)
                    if g >= 2:
                        carry(j - 2 * GJ)
                for j in range(NSEG - 2 * GJ, NSEG):
                    carry(j)

            @block.vector
            def _(dve):
                def p_group(g):
                    dve.tensor_tensor(blocks(Pb[:, js(g), :]), wide(Zj[:, 1, js(g), :]), hb, ALU.mult).then_inc(p_blocks, 1)

                p_group(0)
                p_group(1)
                dve.wait_ge(t_zeroed, 1)
                for j in range(NSEG):
                    if j % GJ == GJ // 2 and j // GJ + 2 < NG:
                        p_group(j // GJ + 2)
                    dve.wait_ge(t_next, j + 1)
                    dve.tensor_copy(T[:, j + 1, :], nxt[:, j % 2, 0:HD]).then_inc(t_ready, 1)
                for c in range(NCH):
                    dve.wait_ge(carried, (c + 1) * NSEG // NCH)
                    dve.tensor_tensor(r.o[:, cs(c)], add[:, c, :], r.wo[:, 0, cs(c)], ALU.add).then_inc(o_ready, 1)


def l0_output(nc, m, inp, r):
    with ExitStack() as own:
        sb = lambda name, shape: own.enter_context(sbuf(nc, name, shape))
        wo = sb("w_o", [P, P])
        load_all(nc, [(wo[:], inp["L0_attn_Wo"])])
        st = sb("stats", [P, 8])
        sq = sb("o_squared", [P, TOK])
        ps = own.enter_context(psum(nc, "group_sums", [P, CH]))
        po = own.enter_context(psum(nc, "out_proj", [P, NCH, CH]))
        with stage(nc, "summed", "over_heads", "std_ready", "chain", "gated", "projected", "added") as (
                block, summed, over_heads, std_ready, chain, gated, projected, added):
            @block.scalar
            def _(act):
                act.activation(sq[:], r.o[:], ACT.Square, accum_out=st[:, 1:2]).then_inc(summed, 1)
                act.wait_ge(chain, 5)
                act.activation(st[:, 4:5], st[:, 4:5], ACT.Sqrt).then_inc(std_ready, 1)

            @block.tensor
            def _(pe):
                pe.wait_ge(summed, 2)
                pe.matmul(ps[:, 0:2], m.head_ones[:], st[:, 0:2], start=True, stop=True).then_inc(over_heads, 1)
                for c in range(NCH):
                    pe.wait_ge(gated, c + 1)
                    pe.matmul(po[:, c, :], wo[:], r.o[:, cs(c)], start=True, stop=True).then_inc(projected, 1)

            @block.vector
            def _(dve):
                n = [0]

                def link(ins):
                    n[0] += 1
                    ins.then_inc(chain, 1)
                    dve.wait_ge(chain, n[0])

                dve.tensor_reduce(st[:, 0:1], r.o[:], AX.X, ALU.add).then_inc(summed, 1)
                dve.wait_ge(over_heads, 1)
                link(dve.tensor_scalar(st[:, 2:4], ps[:, 0:2], 1.0 / (TOK * HD), None, ALU.mult))
                link(dve.tensor_tensor(st[:, 4:5], st[:, 2:3], st[:, 2:3], ALU.mult))
                link(dve.tensor_tensor(st[:, 4:5], st[:, 3:4], st[:, 4:5], ALU.subtract))
                link(dve.tensor_scalar(st[:, 4:5], st[:, 4:5], 1e-5, None, ALU.add))
                link(dve.tensor_scalar(st[:, 5:6], st[:, 2:3], -1.0, None, ALU.mult))
                dve.wait_ge(std_ready, 1)
                link(dve.reciprocal(st[:, 4:5], st[:, 4:5]))
                link(dve.tensor_tensor(st[:, 6:7], st[:, 4:5], m.col("L0_attn_gn_scale"), ALU.mult))
                link(dve.tensor_scalar(r.o[:], r.o[:], st[:, 5:6], st[:, 6:7], ALU.add, ALU.mult))
                for c in range(NCH):
                    dve.scalar_tensor_tensor(out=r.o[:, cs(c)], in0=r.o[:, cs(c)], scalar=m.col("L0_attn_gn_bias"),
                                             in1=r.gate[:, cs(c)], op0=ALU.add, op1=ALU.mult).then_inc(gated, 1)
                for c in range(NCH):
                    dve.wait_ge(projected, c + 1)
                    dve.scalar_tensor_tensor(out=m.x[:, cs(c)], in0=po[:, c, :], scalar=m.col("L0_attn_bo"),
                                             in1=m.x[:, cs(c)], op0=ALU.add, op1=ALU.add).then_inc(added, 1)



EXPERTS = 8
FF = 512
FT = FF // P


def expert_weights(nc, m, h, width, w, bias, k, renormalize, wT, kept=None, post=None):
    SH = [P, NT, EXPERTS]
    SQ = [P, NT, EXPERTS, EXPERTS]
    with ExitStack() as own:
        sb = lambda name, shape: own.enter_context(sbuf(nc, name, shape))
        p, sel = sb("probs", SH), sb("selected", [P, 2, NT, EXPERTS])
        gt, eq = sb("greater", SQ), sb("equal", SQ)
        lower = sb("lower", [P, EXPERTS, EXPERTS])
        s = sb("s", [P, NT])
        selT = sb("selected_T", [EXPERTS, 3, TOK])
        logits = own.enter_context(psum(nc, "router_logits", [P, NT, EXPERTS]))
        turned = own.enter_context(psum(nc, "weights_turned", [P, NCH, CH]))
        with stage(nc, "lower_set", "lower_shaped", "logits_ready", "less_max", "exp_ready", "chain", "w_ready", "w_turned", "m_turned",
                   "w_copied", "m_copied") as (
                block, lower_set, lower_shaped, logits_ready, less_max, exp_ready, chain, w_ready, w_turned, m_turned,
                w_copied, m_copied):
            @block.gpsimd
            def _(pool):
                pool.memset(lower[:], 1.0).then_inc(lower_set, 1)
                pool.wait_ge(lower_set, 1)
                pool.affine_select(out=lower[:], in_=lower[:], compare_op=ALU.is_gt, fill=0.0, base=0,
                                   pattern=[[1, EXPERTS], [-1, EXPERTS]], channel_multiplier=0).then_inc(lower_shaped, 1)

            @block.tensor
            def _(pe):
                for n in range(NT):
                    mm = pe.matmul(logits[:, n, :], h[0:width, n * P:(n + 1) * P], w, start=True, stop=bias is None)
                    if bias is not None:
                        mm = pe.matmul(logits[:, n, :], m.ones[0:1, :], bias, start=False, stop=True)
                mm.then_inc(logits_ready, 1)
                pe.wait_ge(w_ready, 1)
                for n in range(NT):
                    c, k4 = divmod(n, CH // P)
                    mm = pe.transpose(turned[0:EXPERTS, c, k4 * P:(k4 + 1) * P], p[:, n, :], m.ident[:])
                mm.then_inc(w_turned, 1)
                if kept is not None:
                    pe.wait_ge(w_copied, 1)
                    for n in range(NT):
                        c, k4 = divmod(n, CH // P)
                        mm = pe.transpose(turned[0:EXPERTS, c, k4 * P:(k4 + 1) * P], sel[:, 0, n, :], m.ident[:])
                    mm.then_inc(m_turned, 1)

            @block.scalar
            def _(act):
                act.wait_ge(less_max, 1)
                act.activation(p[:], p[:], ACT.Exp).then_inc(exp_ready, 1)

            @block.vector
            def _(dve):
                n = [0]

                def link(ins):
                    n[0] += 1
                    ins.then_inc(chain, 1)
                    dve.wait_ge(chain, n[0])

                dve.wait_ge(logits_ready, 1)
                link(dve.tensor_reduce(s[:], logits[:], AX.X, ALU.max))
                dve.tensor_tensor(p[:], logits[:], s[:].unsqueeze(2).to_broadcast(SH), ALU.subtract).then_inc(less_max, 1)
                dve.wait_ge(exp_ready, 1)
                link(dve.tensor_reduce(s[:], p[:], AX.X, ALU.add))
                link(dve.reciprocal(s[:], s[:]))
                link(dve.tensor_tensor(p[:], p[:], s[:].unsqueeze(2).to_broadcast(SH), ALU.mult))
                pj, pe_ = p[:].unsqueeze(2).to_broadcast(SQ), p[:].unsqueeze(3).to_broadcast(SQ)
                link(dve.tensor_tensor(gt[:], pj, pe_, ALU.is_gt))
                link(dve.tensor_tensor(eq[:], pj, pe_, ALU.is_equal))
                dve.wait_ge(lower_shaped, 1)
                link(dve.tensor_tensor(eq[:], eq[:], lower[:].unsqueeze(1).to_broadcast(SQ), ALU.mult))
                link(dve.tensor_tensor(gt[:], gt[:], eq[:], ALU.add))
                link(dve.tensor_reduce(sel[:, 1], gt[:], AX.X, ALU.add))
                link(dve.tensor_scalar(sel[:, 0], sel[:, 1], float(k), None, ALU.is_lt))
                link(dve.tensor_tensor(p[:], p[:], sel[:, 0], ALU.mult))
                if renormalize:
                    link(dve.tensor_reduce(s[:], p[:], AX.X, ALU.add))
                    link(dve.reciprocal(s[:], s[:]))
                    link(dve.tensor_tensor(p[:], p[:], s[:].unsqueeze(2).to_broadcast(SH), ALU.mult))
                dve.tensor_copy(eq[:, 0, 0, 0:1], s[:, 0:1]).then_inc(w_ready, 1)
                dve.wait_ge(w_turned, 1)
                dve.tensor_copy(wT, turned[0:EXPERTS, :, :].rearrange("p a b -> p (a b)")).then_inc(w_copied, 1)
                if kept is not None:
                    dve.wait_ge(m_turned, 1)
                    link(dve.tensor_copy(selT[:, 0, :], turned[0:EXPERTS, :, :].rearrange("p a b -> p (a b)")))
                    link(dve.tensor_scalar(selT[:, 1, :], selT[:, 0, :], 0.0, None, ALU.mult))
                    link(dve.tensor_tensor_scan(selT[:, 2, :], selT[:, 0, :], selT[:, 1, :], 0.0, ALU.add, ALU.add))
                    link(dve.tensor_scalar(selT[:, 2, :], selT[:, 2, :], float(kept), None, ALU.is_le))
                    dve.wait_ge(w_copied, 1)
                    dve.tensor_tensor(wT, wT, selT[:, 2, :], ALU.mult).then_inc(m_copied, 1)


def expert_sum(nc, m, src, w1, w2, halves, b1, b2, wT, scan=None):
    HT = halves * FT
    with ExitStack() as own:
        sb = lambda name, shape: own.enter_context(sbuf(nc, name, shape))
        wa = sb("w_up", [P, 2, halves * FF])
        wb = sb("w_down", [P, 2, FT, P])
        bcol = sb("up_bias", [P, HT])
        gel = sb("gelu_out", [P, 2, CH]) if halves == 2 else None
        hid = sb("hidden", [P, 2, FT, CH])
        wrow = sb("expert_row", [EXPERTS, 2, CH])
        wcol = sb("expert_weight", [P, 2, CH])
        part = sb("weighted", [P, 2, CH])
        ups = own.enter_context(psum(nc, "up", [P, 4, CH]))
        yps = own.enter_context(psum(nc, "down", [P, 2, CH]))
        mps = own.enter_context(psum(nc, "weight_spread", [P, CH]))
        with stage(nc, "w_loaded0", "w_loaded1", "bias_ready", "up_ready", "activated", "hid_ready",
                   "row_ready", "spread", "wcol_ready", "down_ready", "y_weighted", "added",
                   "z_set", "kq_spread", "kq_ready", "zk_ready", "r_ready", "nabr_ready", "u_ready", "uk_ready",
                   "az_ready", "z_ready", "zq_ready", "wo_ready") as (
                block, w_loaded0, w_loaded1, bias_ready, up_ready, activated, hid_ready,
                row_ready, spread, wcol_ready, down_ready, y_weighted, added,
                z_set, kq_spread, kq_ready, zk_ready, r_ready, nabr_ready, u_ready, uk_ready,
                az_ready, z_ready, zq_ready, wo_ready):
            loaded = (w_loaded0, w_loaded1)
            w1v = w1.rearrange("e p n -> p e n")
            w2v = w2.rearrange("e (t p) n -> p e t n", p=P)
            UP = 4 // halves

            def experts(eng, one):
                one(0, 0, False)
                with eng.Fori(0, EXPERTS // 2 - 1) as pair:
                    for par in (1, 0):
                        one(pair * 2 + 2 - par, par, False)
                one(EXPERTS - 1, 1, True)

            @block.sync
            def _(sp):
                for par in range(2):
                    sp.dma_start(wa[:, par, :], w1v[:, par, :]).then_inc(loaded[par], 16)
                    sp.dma_start(wb[:, par, :, :], w2v[:, par, :, :]).then_inc(loaded[par], 16)
                with sp.Fori(1, EXPERTS // 2) as pair:
                    for par in range(2):
                        sp.wait_ge(down_ready, (pair * 2 + par - 1) * NCH)
                        sp.dma_start(wa[:, par:par + 1, :], w1v[:, ds(pair * 2 + par, 1), :]).then_inc(loaded[par], 16)
                        sp.dma_start(wb[:, par:par + 1, :, :], w2v[:, ds(pair * 2 + par, 1), :, :]).then_inc(loaded[par], 16)

            @block.gpsimd
            def _(pool):
                if scan:
                    pool.wait_ge(z_set, 2)

                def one(e, par, last):
                    for c in range(NCH):
                        i = e * NCH + c
                        if scan:
                            pool.wait_ge(z_ready, i)
                            pool.tensor_tensor(scan.aZ[:].rearrange("p k (e j) -> p (k e) j", e=HD),
                                               scan.Z[:].rearrange("p k (e j) -> p (k e) j", e=HD),
                                               scan.aT[:, ds(i, 1), :].to_broadcast([P, 2 * HD, NSEG]), ALU.mult)\
                                .then_inc(az_ready, 1)
                        pool.wait_ge(y_weighted, i + 1)
                        pool.tensor_tensor(m.x[:, cs(c)], m.x[:, cs(c)], part[:, c % 2, :], ALU.add).then_inc(added, 1)

                experts(pool, one)

            @block.tensor
            def _(pe):
                def spread_kq(batch, part):
                    if not (isinstance(batch, int) and batch == 0 and part == 0):
                        pe.wait_ge(kq_ready, batch * 4 + part)
                    src_t = (scan.kT, scan.qT)[part // 2]
                    for k in range(4):
                        mm = pe.matmul(scan.ps[:, k * P:(k + 1) * P], m.pick[:, part % 2 * 4 + k, :],
                                       src_t[:, ds(batch * 2, 2), :], start=True, stop=True)
                    mm.then_inc(kq_spread, 1)

                if scan:
                    for part in range(4):
                        spread_kq(0, part)

                def one(e, par, last):
                    pe.wait_ge(loaded[par], (e - par) * 16 + 32)
                    for c in range(NCH):
                        i = e * NCH + c
                        for f in range(FT):
                            pe.wait_ge(hid_ready, i * FT + f + 1 - UP if c or f >= UP else e * NCH * FT)
                            for s in reversed(range(halves)):
                                t = s * FT + f
                                pe.matmul(ups[:, (f % UP) * halves + s, :], wa[:, par, t * P:(t + 1) * P],
                                          src[:, cs(c)], start=True, stop=True).then_inc(up_ready, 1)
                        pe.wait_ge(row_ready, i + 1)
                        pe.wait_ge(wcol_ready, i)
                        pe.matmul(mps[:], m.ones[0:EXPERTS, :], wrow[:, c % 2, :],
                                  start=True, stop=True).then_inc(spread, 1)
                        ahead = scan and not (last and c >= 2)
                        if ahead:
                            spread_kq(e * 2 + c // 2 + 1, c % 2 * 2)
                        pe.wait_ge(y_weighted, i - 1 if c >= 2 else e * NCH)
                        for f in range(FT):
                            pe.wait_ge(hid_ready, i * FT + f + 1)
                            mm = pe.matmul(yps[:, c % 2, :], wb[:, par, f, :], hid[:, c % 2, f, :],
                                           start=(f == 0), stop=(f == FT - 1))
                        mm.then_inc(down_ready, 1)
                        if ahead:
                            spread_kq(e * 2 + c // 2 + 1, c % 2 * 2 + 1)

                experts(pe, one)

            @block.scalar
            def _(act):
                def copy_kq(batch, half, part):
                    act.wait_ge(kq_spread, batch * 4 + part + 1)
                    k = part % 2 * 4
                    act.activation(scan.kq[:, half, part // 2, k:k + 4, :, :].rearrange("p e t j -> p (e t j)"), scan.ps[:],
                                   ACT.Copy).then_inc(kq_ready, 1)

                if scan:
                    for part in range(4):
                        copy_kq(0, 0, part)

                def one(e, par, last):
                    act.wait_ge(bias_ready, e + 1)
                    for c in range(NCH):
                        i = e * NCH + c
                        for f in range(FT):
                            bias = bcol[:, (halves - 1) * FT + f:(halves - 1) * FT + f + 1]
                            act.wait_ge(up_ready, (i * FT + f) * halves + 1)
                            if halves == 1:
                                act.wait_ge(down_ready, i - 1 if c >= 2 else e * NCH)
                                act.activation(hid[:, c % 2, f, :], ups[:, f, :], ACT.Gelu_apprx_tanh, bias=bias)\
                                   .then_inc(hid_ready, 1)
                            else:
                                act.wait_ge(hid_ready, i * FT + f - 1 if c or f >= 2 else e * NCH * FT)
                                act.activation(gel[:, f % 2, :], ups[:, (f % UP) * halves + 1, :], ACT.Gelu_apprx_tanh,
                                               bias=bias).then_inc(activated, 1)
                        act.wait_ge(spread, i + 1)
                        act.wait_ge(y_weighted, i - 1 if c >= 2 else e * NCH)
                        act.activation(wcol[:, c % 2, :], mps[:], ACT.Copy).then_inc(wcol_ready, 1)
                        if scan and not (last and c >= 2):
                            act.wait_ge(wo_ready, e * NCH + c // 2 * 2)
                            for part in range(2):
                                copy_kq(e * 2 + c // 2 + 1, 1 - c // 2, c % 2 * 2 + part)

                experts(act, one)

            @block.vector
            def _(dve):
                def row(i, e, c):
                    dve.wait_ge(spread, i - 1 if c >= 2 else e * NCH)
                    dve.tensor_scalar(wrow[:, c % 2, :], wT[:, cs(c)], m.ident[0:EXPERTS, ds(e, 1)], None, ALU.mult)\
                       .then_inc(row_ready, 1)

                def hidden(i, e, c, f):
                    if halves == 1:
                        return
                    dve.wait_ge(activated, i * FT + f + 1)
                    dve.wait_ge(up_ready, (i * FT + f) * halves + 2)
                    dve.wait_ge(down_ready, i - 1 if c >= 2 else e * NCH)
                    dve.scalar_tensor_tensor(out=hid[:, c % 2, f, :], in0=ups[:, (f % UP) * halves, :],
                                             scalar=bcol[:, f:f + 1],
                                             in1=gel[:, f % 2, :], op0=ALU.add, op1=ALU.mult)\
                       .then_inc(hid_ready, 1)

                def weigh(i, e, c):
                    dve.wait_ge(down_ready, i + 1)
                    dve.wait_ge(wcol_ready, i + 1)
                    dve.wait_ge(added, i - 1 if c >= 2 else e * NCH)
                    dve.scalar_tensor_tensor(out=part[:, c % 2, :], in0=yps[:, c % 2, :],
                                             scalar=m.cols[:, ds(m.at[b2] + e, 1)], in1=wcol[:, c % 2, :],
                                             op0=ALU.add, op1=ALU.mult).then_inc(y_weighted, 1)

                def biases(e):
                    dve.wait_ge(hid_ready, e * NCH * FT)
                    dve.tensor_scalar(bcol[:], m.cols[:, ds(m.at[b1] + e * HT, HT)], 1.0, None, ALU.mult)\
                       .then_inc(bias_ready, 1)

                if not scan:
                    def plain(e, par, last):
                        biases(e)
                        dve.wait_ge(bias_ready, e + 1)
                        for c in range(NCH):
                            i = e * NCH + c
                            row(i, e, c)
                            for f in range(FT):
                                hidden(i, e, c, f)
                            weigh(i, e, c)

                    experts(dve, plain)
                    return

                Z, Zk, Zq, aZ, u, outer = scan.Z, scan.Zk, scan.Zq, scan.aZ, scan.u, scan.outer
                FULL = [P, 2, HD, NSEG]
                kej = lambda x: x[:].rearrange("p k (e j) -> p k e j", e=HD)
                ejk = lambda x: x[:].rearrange("p k (e j) -> p k j e", e=HD)
                dve.memset(Z[:, 0, :], 0.0).then_inc(z_set, 1)
                dve.tensor_copy(Z[:, 1, :].rearrange("p (e j) -> p e j", e=HD),
                                m.eye8[:].unsqueeze(2).to_broadcast([P, HD, NSEG])).then_inc(z_set, 1)
                dve.wait_ge(z_set, 2)

                def one(e, par, last):
                    biases(e)
                    dve.wait_ge(bias_ready, e + 1)
                    for c in range(NCH):
                        i = t = e * NCH + c
                        kb, qb = (scan.kq[:, c // 2, a, :, c % 2, :].unsqueeze(1).to_broadcast(FULL) for a in range(2))
                        row(i, e, c)
                        if c % 2 == 0:
                            dve.wait_ge(kq_ready, (e * 2 + c // 2) * 4 + 4)
                        dve.wait_ge(z_ready, t)
                        dve.tensor_tensor(kej(Zk), kej(Z), kb, ALU.mult).then_inc(zk_ready, 1)
                        hidden(i, e, c, 0)
                        dve.wait_ge(zk_ready, t + 1)
                        dve.tensor_reduce(u[:], ejk(Zk), AX.X, ALU.add).then_inc(r_ready, 1)
                        dve.wait_ge(r_ready, t + 1)
                        dve.tensor_tensor(u[:], u[:], scan.nabT[:, ds(t, 1), :].to_broadcast([P, 2, NSEG]), ALU.mult)\
                           .then_inc(nabr_ready, 1)
                        hidden(i, e, c, 1)
                        dve.wait_ge(nabr_ready, t + 1)
                        dve.tensor_tensor(u[:, 0:1, :], u[:, 0:1, :], scan.bvT[:, ds(t, 1), :], ALU.add).then_inc(u_ready, 1)
                        dve.wait_ge(u_ready, t + 1)
                        dve.tensor_tensor(kej(outer), kb, u[:].unsqueeze(2).to_broadcast(FULL), ALU.mult)\
                           .then_inc(uk_ready, 1)
                        hidden(i, e, c, 2)
                        dve.wait_ge(uk_ready, t + 1)
                        dve.wait_ge(az_ready, t + 1)
                        dve.tensor_tensor(Z[:], aZ[:], outer[:], ALU.add).then_inc(z_ready, 1)
                        dve.wait_ge(z_ready, t + 1)
                        dve.tensor_tensor(kej(Zq), kej(Z), qb, ALU.mult).then_inc(zq_ready, 1)
                        hidden(i, e, c, 3)
                        dve.wait_ge(zq_ready, t + 1)
                        dve.tensor_reduce(scan.woT[:, :, ds(t, 1), :], ejk(Zq).unsqueeze(2), AX.X, ALU.add)\
                           .then_inc(wo_ready, 1)
                        weigh(i, e, c)

                experts(dve, one)


def layer0_router(nc, m, inp, wT, loads):
    with ExitStack() as own:
        sb = lambda name, shape: own.enter_context(sbuf(nc, name, shape))
        R = P // 2
        wr1, wr2, br2 = sb("w_r1", [P, R]), sb("w_r2", [R, EXPERTS]), sb("b_r2", [1, EXPERTS])
        h = sb("router_hidden", [R, TOK])
        load_all(nc, [(wr1[:], inp["L0_ffn_Wr1"]), (wr2[:], inp["L0_ffn_Wr2"]),
                      (br2[:], inp["L0_ffn_br2"].rearrange("(a e) -> a e", a=1))])
        with psum(nc, "router_up", [R, NCH, CH]) as ps, stage(nc, "up", "biased") as (block, up, biased):
            @block.tensor
            def _(pe):
                for c in range(NCH):
                    pe.matmul(ps[:, c, :], wr1[:], m.xn[:, cs(c)], start=True, stop=True).then_inc(up, 1)

            @block.scalar
            def _(act):
                for c in range(NCH):
                    act.wait_ge(up, c + 1)
                    act.activation(h[:, cs(c)], ps[:, c, :], ACT.Identity, bias=m.col("L0_ffn_br1", 0, R)).then_inc(biased, 1)
        layernorm(nc, m, h, h, 1e-6, width=R, scale=m.col("L0_ffn_ln_scale", 0, R), bias=m.col("L0_ffn_ln_bias", 0, R),
                  after=ACT.Gelu_apprx_tanh, loads=loads)
        expert_weights(nc, m, h, R, wr2[:], br2[:], 2, True, wT)


def layer0(nc, m, inp):
    with ExitStack() as own:
        sb = lambda name, shape: own.enter_context(sbuf(nc, name, shape))
        r = Named()
        r.bv, r.a, r.nab, r.gate = (sb("r_" + name, [P, TOK]) for name in ("bv", "a", "nab", "gate"))
        r.Z, r.wo = sb("r_Z", [P, 2, HD * NSEG]), sb("r_wo", [P, 2, TOK])
        with ExitStack() as inner:
            sb = lambda name, shape: inner.enter_context(sbuf(nc, name, shape))
            wT = sb("weights_T", [EXPERTS, TOK])
            w, loads = l0_weights(nc, inner, inp)
            layer0_router(nc, m, inp, wT[:], loads)
            r.q, r.k = sb("r_q", [P, TOK]), sb("r_k", [P, TOK])
            l0_project(nc, m, r, w)
            scan = Named()
            scan.kT, scan.qT, scan.aT, scan.nabT, scan.bvT = (
                x[:].rearrange("p (j t) -> p t j", t=SEG) for x in (r.k, r.q, r.a, r.nab, r.bv))
            scan.woT = r.wo[:].rearrange("p k (j t) -> p k t j", t=SEG)
            scan.Z = r.Z
            scan.Zk, scan.Zq, scan.aZ, scan.outer = (sb(n, [P, 2, HD * NSEG]) for n in ("Z_k", "Z_q", "a_Z", "u_k"))
            scan.u = sb("u", [P, 2, NSEG])
            scan.kq = sb("kq_spread", [P, 2, 2, HD, 2, NSEG])
            scan.ps = inner.enter_context(psum(nc, "kq_raw", [P, CH]))
            expert_sum(nc, m, m.xn, inp["L0_ffn_W1"], inp["L0_ffn_W2"], 2, "L0_ffn_b1", "L0_ffn_b2", wT, scan)
        r.o = own.enter_context(sbuf(nc, "r_o", [P, TOK]))
        l0_join(nc, m, r)
        l0_output(nc, m, inp, r)



def layer3_experts(nc, m, inp):
    CAP = max(4, TOK // EXPERTS)
    with ExitStack() as own:
        sb = lambda name, shape: own.enter_context(sbuf(nc, name, shape))
        wg, coef_w = sb("w_gate", [P, EXPERTS]), sb("w_coef", [P, 2])
        w1, w2 = sb("w_res_up", [P, FF]), sb("w_res_down", [P, FT, P])
        y, wT = sb("attn_out", [P, TOK]), sb("weights_T3", [EXPERTS, TOK])
        dif = sb("coef_dif", [P, 2, P])
        cf = sb("coef", [P, 2, TOK])
        hid = sb("res_hidden", [P, 2, FT, CH])
        layernorm(nc, m, m.xn, y, 1e-12, scale=m.col("L3_ffn_attn_nw"), bias=m.col("L3_ffn_attn_nb"),
                  loads=[(wg[:], inp["L3_ffn_wg"]), (coef_w[:], inp["L3_ffn_res_coef"]), (w1[:], inp["L3_ffn_res_inter_w"]),
                         (w2[:], inp["L3_ffn_res_output_w"].rearrange("(t p) n -> p t n", p=P))])
        expert_weights(nc, m, y, P, wg[:], None, 1, False, wT[:], kept=CAP)
        with psum(nc, "coef_logits", [P, 2, CH]) as cps, psum(nc, "res_up", [P, 4, CH]) as ups, \
                psum(nc, "res_down", [P, 2, CH]) as yps, \
                stage(nc, "dif_ready", "logits", "coef_ready", "wT_done", "up", "hidden", "down", "res_weighted", "summed") as (
                block, dif_ready, logits, coef_ready, wT_done, up, hidden, down, res_weighted, summed):
            @block.vector
            def _(dve):
                dve.tensor_scalar(dif[:, 0, 0:1], coef_w[:, 0:1], coef_w[:, 1:2], None, ALU.subtract).then_inc(dif_ready, 1)
                dve.wait_ge(dif_ready, 1)
                dve.tensor_copy(dif[:, 1, :], dif[:, 0, 0:1].to_broadcast([P, P])).then_inc(dif_ready, 1)
                for c in range(NCH):
                    dve.wait_ge(coef_ready, 2 * c + 2)
                    dve.tensor_tensor(wT[:, cs(c)], wT[:, cs(c)], cf[0:EXPERTS, 1, cs(c)], ALU.mult).then_inc(wT_done, 1)
                    dve.tensor_tensor(m.x[:, cs(c)], m.x[:, cs(c)], m.xn[:, cs(c)], ALU.add).then_inc(summed, 1)
                for c in range(NCH):
                    dve.wait_ge(down, c + 1)
                    dve.scalar_tensor_tensor(out=cf[:, 0, cs(c)], in0=yps[:, c % 2, :], scalar=m.col("L3_ffn_res_output_b"),
                                             in1=cf[:, 0, cs(c)], op0=ALU.add, op1=ALU.mult).then_inc(res_weighted, 1)
                    dve.wait_ge(res_weighted, c + 1)
                    dve.wait_ge(summed, NCH)
                    dve.tensor_tensor(m.x[:, cs(c)], m.x[:, cs(c)], cf[:, 0, cs(c)], ALU.add).then_inc(summed, 1)

            @block.tensor
            def _(pe):
                pe.wait_ge(dif_ready, 2)
                for c in range(NCH):
                    if c >= 2:
                        pe.wait_ge(coef_ready, 2 * (c - 1))
                    pe.matmul(cps[:, c % 2, :], dif[:, 1, :], y[:, cs(c)], start=True, stop=True).then_inc(logits, 1)
                for c in range(NCH):
                    for f in range(FT):
                        if c:
                            pe.wait_ge(hidden, (c - 1) * FT + f + 1)
                        pe.matmul(ups[:, f, :], w1[:, f * P:(f + 1) * P], y[:, cs(c)], start=True, stop=True).then_inc(up, 1)
                    if c >= 2:
                        pe.wait_ge(res_weighted, c - 1)
                    for f in range(FT):
                        pe.wait_ge(hidden, c * FT + f + 1)
                        mm = pe.matmul(yps[:, c % 2, :], w2[:, f, :], hid[:, c % 2, f, :], start=(f == 0), stop=(f == FT - 1))
                    mm.then_inc(down, 1)

            @block.scalar
            def _(act):
                for c in range(NCH):
                    act.wait_ge(logits, c + 1)
                    act.activation(cf[:, 0, cs(c)], cps[:, c % 2, :], ACT.Sigmoid).then_inc(coef_ready, 1)
                    act.activation(cf[:, 1, cs(c)], cps[:, c % 2, :], ACT.Sigmoid, scale=-1.0).then_inc(coef_ready, 1)
                for c in range(NCH):
                    if c >= 2:
                        act.wait_ge(down, c - 1)
                    for f in range(FT):
                        act.wait_ge(up, c * FT + f + 1)
                        act.activation(hid[:, c % 2, f, :], ups[:, f, :], ACT.Gelu_apprx_tanh,
                                       bias=m.col("L3_ffn_res_inter_b", f)).then_inc(hidden, 1)
        expert_sum(nc, m, y, inp["L3_ffn_inter_w"], inp["L3_ffn_output_w"], 1, "L3_ffn_inter_b", "L3_ffn_output_b", wT)



def hidden_mlp(nc, m, src, wa, wb, b1, b2, base):
    with ExitStack() as own:
        hid = own.enter_context(sbuf(nc, "mlp_hidden", [P, 2, FT, CH]))
        ups, yps = own.enter_context(psum(nc, "mlp_up", [P, 4, CH])), own.enter_context(psum(nc, "mlp_down", [P, 2, CH]))
        with stage(nc, "up", "hidden", "down", "based", "added") as (block, up, hidden, down, based, added):
            @block.tensor
            def _(pe):
                for c in range(NCH):
                    for f in range(FT):
                        if c:
                            pe.wait_ge(hidden, (c - 1) * FT + f + 1)
                        pe.matmul(ups[:, f, :], wa[:, f * P:(f + 1) * P], src[:, cs(c)], start=True, stop=True).then_inc(up, 1)
                    if c >= 2:
                        pe.wait_ge(added, c - 1)
                    for f in range(FT):
                        pe.wait_ge(hidden, c * FT + f + 1)
                        mm = pe.matmul(yps[:, c % 2, :], wb[:, f, :], hid[:, c % 2, f, :], start=(f == 0), stop=(f == FT - 1))
                    mm.then_inc(down, 1)

            @block.scalar
            def _(act):
                for c in range(NCH):
                    if c >= 2:
                        act.wait_ge(down, c - 1)
                    for f in range(FT):
                        act.wait_ge(up, c * FT + f + 1)
                        act.activation(hid[:, c % 2, f, :], ups[:, f, :], ACT.Gelu_apprx_tanh, bias=m.col(b1, f))\
                           .then_inc(hidden, 1)

            @block.gpsimd
            def _(pool):
                for c in range(NCH):
                    pool.tensor_tensor(m.x[:, cs(c)], m.x[:, cs(c)], base[:, cs(c)], ALU.add).then_inc(based, 1)

            @block.vector
            def _(dve):
                for c in range(NCH):
                    dve.wait_ge(down, c + 1)
                    dve.wait_ge(based, c + 1)
                    dve.scalar_tensor_tensor(out=m.x[:, cs(c)], in0=yps[:, c % 2, :], scalar=m.col(b2),
                                             in1=m.x[:, cs(c)], op0=ALU.add, op1=ALU.add).then_inc(added, 1)


def layer1_attention(nc, m, inp):
    KEPS = 1e-3
    with ExitStack() as own:
        sb = lambda name, shape: own.enter_context(sbuf(nc, name, shape))
        y, q, xres = sb("l1_y", [P, TOK]), sb("phi_q", [P, TOK]), sb("x_res", [P, TOK])
        wq, wkv, wo, bkv = sb("w_q", [P, P]), sb("w_kv", [P, 2 * P]), sb("w_o", [P, P]), sb("b_kv", [1, 2 * P])
        loads = [(wq[:], inp["L1_attn_Wq"].rearrange("i h d -> i (h d)")),
                      (wkv[:, 0:P], inp["L1_attn_Wk"].rearrange("i h d -> i (h d)")),
                      (wkv[:, P:2 * P], inp["L1_attn_Wv"].rearrange("i h d -> i (h d)")),
                      (wo[:], inp["L1_attn_Wo"].rearrange("h d o -> (h d) o")),
                      (bkv[:, 0:P], inp["L1_attn_bk"].rearrange("(o h) d -> o (h d)", o=1)),
                      (bkv[:, P:2 * P], inp["L1_attn_bv"].rearrange("(o h) d -> o (h d)", o=1))]
        layernorm(nc, m, m.xn, y, 1e-6, scale=m.col("L1_attn_ln1_scale"), bias=m.col("L1_attn_ln1_bias"), loads=loads)
        kf, vo = sb("phi_k", [P, 4, P]), sb("v_and_one", [P, 4, P + 1])
        kvbias = sb("kv_bias", [P, 2 * P])
        kvb, ksb = sb("kv_blocks", [P, P]), sb("ksum_blocks", [P, P])
        inv = sb("inverse_den", [P, NCH, CH])
        with ExitStack() as inner:
            kvps = inner.enter_context(psum(nc, "k_v_tokens", [P, 3, CH]))
            kvsum = inner.enter_context(psum(nc, "kv_sum", [P, CH]))
            qps = inner.enter_context(psum(nc, "q_proj", [P, NCH, CH]))
            with stage(nc, "kv_tokens", "q_logits", "kv_raw", "k_ready", "v_ready", "kv_sum", "ones_set", "blocks", "q_ready",
                       "q_biased", "bias_spread", "bias_ready", "k_biased") as (
                    block, kv_tokens, q_logits, kv_raw, k_ready, v_ready, kv_sum, ones_set, blocks, q_ready, q_biased,
                    bias_spread, bias_ready, k_biased):
                @block.tensor
                def _(pe):
                    def sums(n):
                        pe.wait_ge(k_ready, n + 1)
                        pe.wait_ge(v_ready, n + 1)
                        pe.matmul(kvsum[:, 0:P + 1], kf[:, n % 4, :], vo[:, n % 4, :], start=(n == 0), stop=(n == NT - 1))\
                          .then_inc(kv_sum, 1)

                    pe.matmul(qps[:, 0, 0:2 * P], m.ones[0:1, :], bkv[:], start=True, stop=True).then_inc(bias_spread, 1)
                    for n in range(NT):
                        if n >= 3:
                            pe.wait_ge(k_ready, n - 2)
                            pe.wait_ge(v_ready, n - 2)
                        pe.matmul(kvps[:, n % 3, 0:2 * P], y[:, n * P:(n + 1) * P], wkv[:], start=True, stop=True)\
                          .then_inc(kv_tokens, 1)
                        if n >= 2:
                            sums(n - 2)
                    sums(NT - 2)
                    sums(NT - 1)
                    pe.wait_ge(bias_ready, 1)
                    for c in range(NCH):
                        pe.matmul(qps[:, c, :], wq[:], y[:, cs(c)], start=True, stop=True).then_inc(q_logits, 1)

                @block.scalar
                def _(act):
                    for c in range(NCH):
                        act.wait_ge(q_logits, c + 1)
                        act.activation(q[:, cs(c)], qps[:, c, :], ACT.Relu, bias=m.col("L1_attn_bq")).then_inc(q_biased, 1)

                @block.vector
                def _(dve):
                    dve.memset(vo[:, :, P:P + 1], 1.0).then_inc(ones_set, 1)
                    dve.wait_ge(bias_spread, 1)
                    dve.tensor_copy(kvbias[:], qps[:, 0, 0:2 * P]).then_inc(bias_ready, 1)
                    dve.wait_ge(bias_ready, 1)
                    dve.wait_ge(ones_set, 1)
                    for n in range(NT):
                        dve.wait_ge(kv_tokens, n + 1)
                        if n >= 4:
                            dve.wait_ge(kv_sum, n - 3)
                        dve.tensor_tensor(kf[:, n % 4, :], kvps[:, n % 3, 0:P], kvbias[:, 0:P], ALU.add).then_inc(k_biased, 1)
                        dve.tensor_tensor(vo[:, n % 4, 0:P], kvps[:, n % 3, P:2 * P], kvbias[:, P:2 * P], ALU.add)\
                           .then_inc(v_ready, 1)
                        dve.wait_ge(k_biased, n + 1)
                        dve.tensor_scalar(kf[:, n % 4, :], kf[:, n % 4, :], 0.0, KEPS, ALU.max, ALU.add).then_inc(k_ready, 1)
                    dve.wait_ge(kv_sum, NT)
                    dve.tensor_tensor(kvb[:], kvsum[:, 0:P], m.head_ones[:], ALU.mult).then_inc(blocks, 1)
                    dve.tensor_scalar(ksb[:], m.head_ones[:], kvsum[:, P:P + 1], None, ALU.mult).then_inc(blocks, 1)
                    for c in range(NCH):
                        dve.wait_ge(q_biased, c + 1)
                        dve.tensor_scalar(q[:, cs(c)], q[:, cs(c)], KEPS, None, ALU.add).then_inc(q_ready, 1)
        with ExitStack() as inner:
            num = inner.enter_context(psum(nc, "numerator", [P, 2, CH]))
            den = inner.enter_context(psum(nc, "denominator", [P, 2, CH]))
            ops = inner.enter_context(psum(nc, "attn_proj", [P, 2, CH]))
            with stage(nc, "num_ready", "den_ready", "logged", "inverted", "attn_ready", "projected", "res_ready", "res_biased") as (
                    block, num_ready, den_ready, logged, inverted, attn_ready, projected, res_ready, res_biased):
                @block.tensor
                def _(pe):
                    def project(c):
                        pe.wait_ge(attn_ready, c + 1)
                        if c >= 2:
                            pe.wait_ge(res_ready, c - 1)
                        pe.matmul(ops[:, c % 2, :], wo[:], q[:, cs(c)], start=True, stop=True).then_inc(projected, 1)

                    for c in range(NCH):
                        if c >= 2:
                            pe.wait_ge(attn_ready, c - 1)
                        pe.matmul(den[:, c % 2, :], ksb[:], q[:, cs(c)], start=True, stop=True).then_inc(den_ready, 1)
                        pe.matmul(num[:, c % 2, :], kvb[:], q[:, cs(c)], start=True, stop=True).then_inc(num_ready, 1)
                        if c:
                            project(c - 1)
                    project(NCH - 1)

                @block.scalar
                def _(act):
                    for c in range(NCH):
                        act.wait_ge(den_ready, c + 1)
                        act.activation(inv[:, c, :], den[:, c % 2, :], ACT.Ln).then_inc(logged, 1)
                        if c % 2:
                            for k in (c - 1, c):
                                act.wait_ge(logged, k + 1)
                                act.activation(inv[:, k, :], inv[:, k, :], ACT.Exp, scale=-1.0).then_inc(inverted, 1)

                @block.vector
                def _(dve):
                    def residual(c):
                        dve.wait_ge(projected, c + 1)
                        dve.scalar_tensor_tensor(out=xres[:, cs(c)], in0=ops[:, c % 2, :], scalar=m.col("L1_attn_bo"),
                                                 in1=m.xn[:, cs(c)], op0=ALU.add, op1=ALU.add).then_inc(res_ready, 1)

                    for c in range(NCH):
                        dve.wait_ge(inverted, c + 1)
                        dve.wait_ge(num_ready, c + 1)
                        dve.tensor_tensor(q[:, cs(c)], num[:, c % 2, :], inv[:, c, :], ALU.mult).then_inc(attn_ready, 1)
                        if c:
                            residual(c - 1)
                    residual(NCH - 1)
        wa, wb = sb("w_up", [P, FF]), sb("w_down", [P, FT, P])
        layernorm(nc, m, xres, y, 1e-6, scale=m.col("L1_attn_ln2_scale"), bias=m.col("L1_attn_ln2_bias"),
                  loads=[(wa[:], inp["L1_attn_W1"]), (wb[:], inp["L1_attn_W2"].rearrange("(t p) n -> p t n", p=P))])
        hidden_mlp(nc, m, y, wa, wb, "L1_attn_b1", "L1_attn_b2", xres)


def layer1_ffn(nc, m, inp):
    U, INNER = 64, 16
    UT = U * INNER // P
    PER = P // INNER
    with ExitStack() as own:
        sb = lambda name, shape: own.enter_context(sbuf(nc, name, shape))
        win, wout = sb("w_in", [P, U]), sb("w_out", [U, P])
        unit_rows = sb("unit_rows", [U, UT, P])
        unit_cols = sb("unit_cols", [P, UT, U])
        s, hid, g = sb("units", [U, TOK]), sb("unit_hidden", [P, 2, CH]), sb("unit_out", [U, TOK])
        load_all(nc, [(win[:], inp["L1_ffn_Win"]), (wout[:], inp["L1_ffn_Wout"])])
        sps = own.enter_context(psum(nc, "units_in", [U, 2, CH]))
        hps = own.enter_context(psum(nc, "units_spread", [P, 2, CH]))
        gps = own.enter_context(psum(nc, "units_sum", [U, 2, CH]))
        ops = own.enter_context(psum(nc, "units_out", [P, 2, CH]))
        with stage(nc, "ones_set", "shaped", "scaled", "units_in", "units_ready", "spread", "hidden", "summed", "biased",
                   "out_ready", "added") as (
                block, ones_set, shaped, scaled, units_in, units_ready, spread, hidden, summed, biased, out_ready, added):
            @block.gpsimd
            def _(pool):
                pool.memset(unit_rows[:], 1.0).then_inc(ones_set, 1)
                pool.memset(unit_cols[:], 1.0).then_inc(ones_set, 1)
                pool.wait_ge(ones_set, 2)
                v = unit_rows[:].rearrange("m i (u h) -> m i u h", h=INNER)
                pool.affine_select(out=v, in_=v, compare_op=ALU.is_equal, fill=0.0, base=0,
                                   pattern=[[-PER, UT], [-1, PER], [0, INNER]], channel_multiplier=1).then_inc(shaped, 1)
                pool.affine_select(out=unit_cols[:], in_=unit_cols[:], compare_op=ALU.is_ge, fill=0.0, base=0,
                                   pattern=[[P, UT], [-INNER, U]], channel_multiplier=1).then_inc(shaped, 1)
                pool.wait_ge(shaped, 2)
                pool.affine_select(out=unit_cols[:], in_=unit_cols[:], compare_op=ALU.is_ge, fill=0.0, base=INNER - 1,
                                   pattern=[[-P, UT], [INNER, U]], channel_multiplier=-1).then_inc(shaped, 1)

            @block.tensor
            def _(pe):
                for c in range(NCH):
                    if c >= 2:
                        pe.wait_ge(units_ready, c - 1)
                    pe.matmul(sps[:, c % 2, :], win[:], m.xn[:, cs(c)], start=True, stop=True).then_inc(units_in, 1)
                pe.wait_ge(shaped, 3)
                pe.wait_ge(scaled, UT)

                def add_up(k):
                    c, i = divmod(k, UT)
                    pe.wait_ge(hidden, k + 1)
                    if i == 0 and c >= 2:
                        pe.wait_ge(biased, c - 1)
                    pe.matmul(gps[:, c % 2, :], unit_cols[:, i, :], hid[:, k % 2, :], start=(i == 0), stop=(i == UT - 1))\
                      .then_inc(summed, 1)

                for k in range(NCH * UT):
                    c, i = divmod(k, UT)
                    pe.wait_ge(units_ready, c + 1)
                    if k >= 2:
                        pe.wait_ge(hidden, k - 1)
                    pe.matmul(hps[:, k % 2, :], unit_rows[:, i, :], s[:, cs(c)], start=True, stop=True).then_inc(spread, 1)
                    if k:
                        add_up(k - 1)
                add_up(NCH * UT - 1)
                for c in range(NCH):
                    pe.wait_ge(biased, c + 1)
                    if c >= 2:
                        pe.wait_ge(added, c - 1)
                    pe.matmul(ops[:, c % 2, :], wout[:], g[:, cs(c)], start=True, stop=True).then_inc(out_ready, 1)

            @block.scalar
            def _(act):
                for k in range(NCH * UT):
                    c, i = divmod(k, UT)
                    act.wait_ge(spread, k + 1)
                    if k >= 2:
                        act.wait_ge(summed, k - 1)
                    act.activation(hid[:, k % 2, :], hps[:, k % 2, :], ACT.Relu, bias=m.col("L1_ffn_b1", i),
                                   scale=m.col("L1_ffn_W1", i)).then_inc(hidden, 1)

            @block.vector
            def _(dve):
                dve.wait_ge(shaped, 3)
                for i in range(UT):
                    dve.tensor_scalar(unit_cols[:, i, :], unit_cols[:, i, :], m.col("L1_ffn_W2", i), None, ALU.mult)\
                       .then_inc(scaled, 1)
                for c in range(NCH):
                    dve.wait_ge(units_in, c + 1)
                    dve.tensor_scalar(s[:, cs(c)], sps[:, c % 2, :], m.col("L1_ffn_bin_", 0, U), None, ALU.add)\
                       .then_inc(units_ready, 1)
                for c in range(NCH):
                    dve.wait_ge(summed, (c + 1) * UT)
                    dve.tensor_scalar(g[:, cs(c)], gps[:, c % 2, :], m.col("L1_ffn_b2", 0, U), None, ALU.add).then_inc(biased, 1)
                for c in range(NCH):
                    dve.wait_ge(out_ready, c + 1)
                    dve.scalar_tensor_tensor(out=m.x[:, cs(c)], in0=ops[:, c % 2, :], scalar=m.col("L1_ffn_bout"),
                                             in1=m.x[:, cs(c)], op0=ALU.add, op1=ALU.add).then_inc(added, 1)



def layer2_ffn(nc, m, inp):
    with ExitStack() as own:
        sb = lambda name, shape: own.enter_context(sbuf(nc, name, shape))
        w, wt = sb("w_rkv", [P, 3, P]), sb("w_rkv_T", [P, 3, P])
        om = sb("one_less_mu", [P, 2])
        prev = sb("x_before", [P, TOK])
        mix = sb("mixed", [P, 2, TOK])
        rr, kk = sb("r_gate", [P, TOK]), sb("k_act", [P, TOK])
        load_all(nc, [(w[:, 0, :], inp["L2_ffn_W_r"]), (w[:, 1, :], inp["L2_ffn_W_k"]), (w[:, 2, :], inp["L2_ffn_W_v"])])
        wps = own.enter_context(psum(nc, "w_turned", [P, CH]))
        ps = own.enter_context(psum(nc, "rk", [P, 4, CH]))
        vps = own.enter_context(psum(nc, "v", [P, 2, CH]))
        mus = ("L2_ffn_mu_r", "L2_ffn_mu_k")
        with stage(nc, "w_turned", "w_ready", "om_ready", "zeroed", "prev_ready", "first", "mixed", "r_logits", "k_logits",
                   "r_ready", "k_relu", "k_ready", "v_ready", "gated", "added") as (
                block, w_turned, w_ready, om_ready, zeroed, prev_ready, first, mixed, r_logits, k_logits,
                r_ready, k_relu, k_ready, v_ready, gated, added):
            @block.tensor
            def _(pe):
                for i in range(3):
                    pe.transpose(wps[:, i * P:(i + 1) * P], w[:, i, :], m.ident[:]).then_inc(w_turned, 1)
                pe.wait_ge(w_ready, 1)
                for c in range(NCH):
                    pe.wait_ge(mixed, 2 * c + 2)
                    if c >= 2:
                        pe.wait_ge(r_ready, c - 1)
                        pe.wait_ge(k_relu, c - 1)
                    pe.matmul(ps[:, c % 2, :], wt[:, 0, :], mix[:, 0, cs(c)], start=True, stop=True).then_inc(r_logits, 1)
                    pe.matmul(ps[:, 2 + c % 2, :], wt[:, 1, :], mix[:, 1, cs(c)], start=True, stop=True).then_inc(k_logits, 1)
                for c in range(NCH):
                    pe.wait_ge(k_ready, c + 1)
                    if c >= 2:
                        pe.wait_ge(gated, c - 1)
                    pe.matmul(vps[:, c % 2, :], wt[:, 2, :], kk[:, cs(c)], start=True, stop=True).then_inc(v_ready, 1)

            @block.scalar
            def _(act):
                for c in range(NCH):
                    act.wait_ge(r_logits, c + 1)
                    act.activation(rr[:, cs(c)], ps[:, c % 2, :], ACT.Sigmoid).then_inc(r_ready, 1)
                    act.wait_ge(k_logits, c + 1)
                    act.activation(kk[:, cs(c)], ps[:, 2 + c % 2, :], ACT.Relu).then_inc(k_relu, 1)
                    act.wait_ge(k_relu, c + 1)
                    act.activation(kk[:, cs(c)], kk[:, cs(c)], ACT.Square).then_inc(k_ready, 1)

            @block.gpsimd
            def _(pool):
                pool.memset(prev[:, 0:1], 0.0).then_inc(zeroed, 1)
                pool.tensor_copy(prev[:, 1:TOK], m.xn[:, 0:TOK - 1]).then_inc(prev_ready, 1)
                for c in range(NCH):
                    pool.wait_ge(gated, c + 1)
                    pool.tensor_tensor(m.x[:, cs(c)], m.x[:, cs(c)], rr[:, cs(c)], ALU.add).then_inc(added, 1)

            @block.vector
            def _(dve):
                dve.wait_ge(w_turned, 3)
                dve.tensor_copy(wt[:].rearrange("p i n -> p (i n)"), wps[:, 0:3 * P]).then_inc(w_ready, 1)
                for i in range(2):
                    dve.tensor_scalar(om[:, i:i + 1], m.col(mus[i]), -1.0, 1.0, ALU.mult, ALU.add).then_inc(om_ready, 1)
                dve.wait_ge(om_ready, 2)
                dve.wait_ge(zeroed, 1)
                dve.wait_ge(prev_ready, 1)
                for c in range(NCH):
                    for i in range(2):
                        dve.tensor_scalar(mix[:, i, cs(c)], prev[:, cs(c)], om[:, i:i + 1], None, ALU.mult).then_inc(first, 1)
                        dve.wait_ge(first, 2 * c + i + 1)
                        dve.scalar_tensor_tensor(out=mix[:, i, cs(c)], in0=m.xn[:, cs(c)], scalar=m.col(mus[i]),
                                                 in1=mix[:, i, cs(c)], op0=ALU.mult, op1=ALU.add).then_inc(mixed, 1)
                for c in range(NCH):
                    dve.wait_ge(v_ready, c + 1)
                    dve.wait_ge(r_ready, c + 1)
                    dve.tensor_tensor(rr[:, cs(c)], rr[:, cs(c)], vps[:, c % 2, :], ALU.mult).then_inc(gated, 1)



WIN = 32
LAT, LH = 64, 8
NEG = -1e30


def l2_window(nc, m, inp, r):
    STEPS = TOK // (2 * WIN)
    KW = 2 * WIN
    with ExitStack() as own:
        sb = lambda name, shape: own.enter_context(sbuf(nc, name, shape))
        xpad = sb("x_padded", [P, WIN + TOK])
        kg = sb("k_groups", [P, 4, WIN + TOK])
        mask = sb("window_mask", [P, KW])
        mask0 = sb("first_mask", [P, 2, KW])
        vmask = sb("v_mask", [P, 2, P])
        wv = sb("w_v", [P, P])
        qm = sb("q_masked", [P, 2, 2, 4, WIN])
        xw = sb("x_window", [P, 2, 2, 2, KW])
        x = sb("window_scores", [P, 4, 2 * 4, KW])
        st = sb("window_stats", [P, 4, 2, 8])
        pt = sb("window_pT", [P, 2, 4, P])
        vm = sb("v_masked", [P, 4, 2, 2, P])
        o = sb("window_o", [P, 2, 2, 4, WIN])
        load_all(nc, [(wv[:], inp["L2_attn_wv"])])
        vps = own.enter_context(psum(nc, "v_window", [P, 2, CH]))
        sps = own.enter_context(psum(nc, "window_qk", [P, 2, CH]))
        tps = own.enter_context(psum(nc, "window_turned", [P, 2, CH]))
        ops = own.enter_context(psum(nc, "window_out", [P, 2, CH]))
        with stage(nc, "padded", "k_cut", "masks_set", "vmask_set", "q_masked", "x_copied", "v_raw", "scored",
                      "v_masked", "shifted", "maxed", "less_max", "exped", "totaled", "inverted", "p_ready",
                      "turned", "pt_ready", "out_raw", "out_picked", "local_ready") as (
                block, padded, k_cut, masks_set, vmask_set, q_masked, x_copied, v_raw, scored, v_masked, shifted,
                maxed, less_max, exped, totaled, inverted, p_ready, turned, pt_ready, out_raw, out_picked,
                local_ready):

            def steps(eng, body):
                for s in range(4):
                    body(s, s)
                with eng.Fori(1, STEPS // 4 - 1) as i:
                    for k in range(4):
                        body(i * 4 + k, k)
                for k in range(4):
                    body(STEPS - 4 + k, k)

            def before(s, n):
                return isinstance(s, int) and s < n

            def at(t, s, off):
                return t[:, s * KW + off:s * KW + off + KW] if isinstance(s, int) else t[:, ds(s * KW + off, KW)]

            G8 = [P, 8, KW]

            @block.gpsimd
            def _(pool):
                pool.memset(xpad[:, 0:WIN], 0.0).then_inc(padded, 1)
                pool.tensor_copy(xpad[:, WIN:], m.xn[:]).then_inc(padded, 1)
                pool.memset(kg[:, :, 0:WIN], 0.0).then_inc(padded, 1)
                pool.memset(mask[:], 0.0).then_inc(masks_set, 1)
                pool.wait_ge(masks_set, 1)
                for q in range(4):
                    part = mask[q * WIN:(q + 1) * WIN, :]
                    pool.affine_select(out=part, in_=part, compare_op=ALU.is_gt, fill=NEG, base=0,
                                       pattern=[[1, KW]], channel_multiplier=-1).then_inc(masks_set, 1)
                pool.wait_ge(masks_set, 5)
                for q in range(4):
                    part = mask[q * WIN:(q + 1) * WIN, :]
                    pool.affine_select(out=part, in_=part, compare_op=ALU.is_ge, fill=NEG, base=WIN,
                                       pattern=[[-1, KW]], channel_multiplier=1).then_inc(masks_set, 1)
                pool.wait_ge(masks_set, 9)
                for b in range(2):
                    pool.tensor_copy(mask0[:, b, :], mask[:]).then_inc(masks_set, 1)
                pool.wait_ge(masks_set, 11)
                pool.memset(mask0[:, 0, 0:WIN], NEG).then_inc(masks_set, 1)

                def prepare(s, par):
                    if not before(s, 2):
                        pool.wait_ge(scored, s - 1)
                        pool.wait_ge(v_raw, s - 1)
                    if before(s, 1):
                        pool.wait_ge(padded, 3)
                    pool.tensor_tensor(qm[:, par], at(r.q, s, 0).rearrange("p (b i) -> p b i", b=2).unsqueeze(2)
                                       .to_broadcast([P, 2, 4, WIN]),
                                       m.hmod[:].unsqueeze(1).unsqueeze(3).to_broadcast([P, 2, 4, WIN]), ALU.mult)\
                        .then_inc(q_masked, 1)
                    for b in range(2):
                        win = at(xpad, s, b * WIN)
                        pool.tensor_copy(xw[:, par, b], win.unsqueeze(1).to_broadcast([P, 2, KW])).then_inc(x_copied, 1)

                def body(s, k):
                    pool.wait_ge(maxed, s + 1)
                    pool.tensor_tensor(x[:, k], x[:, k], st[:, k, 0, :].unsqueeze(2).to_broadcast(G8), ALU.subtract)\
                        .then_inc(less_max, 1)
                    if not isinstance(s, int) or s + 2 < STEPS:
                        prepare(s + 2, k % 2)

                prepare(0, 0)
                prepare(1, 1)
                steps(pool, body)

            @block.tensor
            def _(pe):
                pe.wait_ge(k_cut, 4)
                pe.wait_ge(padded, 3)

                def front(s, par):
                    pe.wait_ge(q_masked, s + 1)
                    pe.wait_ge(x_copied, s * 2 + 2)
                    if not before(s, 2):
                        pe.wait_ge(shifted, s - 1)
                        pe.wait_ge(v_masked, (s - 1) * 2)
                    for b in range(2):
                        mm = pe.matmul(vps[:, par, b * P:(b + 1) * P], xw[:, par, b].rearrange("p a j -> p (a j)"), wv[:],
                                       start=True, stop=True)
                    mm.then_inc(v_raw, 1)
                    for b in range(2):
                        keys = kg[:, :, (s * 2 + b) * WIN:(s * 2 + b + 2) * WIN] if isinstance(s, int) \
                            else kg[:, :, ds(s * KW + b * WIN, KW)]
                        mm = pe.matmul(sps[:, par, b * 256:(b + 1) * 256], qm[:, par, b].rearrange("p a i -> p (a i)"), keys,
                                       start=True, stop=True)
                    mm.then_inc(scored, 1)

                def back(s, k):
                    par = k % 2
                    pe.wait_ge(p_ready, s + 1)
                    if not before(s, 2):
                        pe.wait_ge(pt_ready, s - 1)
                        pe.wait_ge(out_picked, s - 1)
                    for i in range(4):
                        mm = pe.transpose(tps[:, par, i * P:(i + 1) * P],
                                          x[:, k, 2 * i:2 * i + 2, :].rearrange("p g j -> p (g j)"), m.ident[:])
                    mm.then_inc(turned, 1)
                    pe.wait_ge(pt_ready, s + 1)
                    pe.wait_ge(v_masked, s * 2 + 2)
                    for b in range(2):
                        for i in range(2):
                            mm = pe.matmul(ops[:, par, b * P:(b + 1) * P], vm[:, k, b, i, :], pt[:, par, 2 * b + i, :],
                                           start=(i == 0), stop=(i == 1))
                    mm.then_inc(out_raw, 1)

                def body(s, k):
                    if not isinstance(s, int) or s + 2 < STEPS:
                        front(s + 2, k % 2)
                    back(s, k)

                front(0, 0)
                front(1, 1)
                steps(pe, body)

            @block.scalar
            def _(act):
                def exp(s, k):
                    act.wait_ge(less_max, s + 1)
                    act.activation(x[:, k], x[:, k], ACT.Exp).then_inc(exped, 1)

                exp(0, 0)

                def body(s, k):
                    par = k % 2
                    if not isinstance(s, int) or s + 1 < STEPS:
                        exp(s + 1, (k + 1) % 4)
                    act.wait_ge(turned, s + 1)
                    if not before(s, 2):
                        act.wait_ge(out_raw, s - 1)
                    act.activation(pt[:, par].rearrange("p a n -> p (a n)"), tps[:, par, :], ACT.Copy).then_inc(pt_ready, 1)

                steps(act, body)

            @block.vector
            def _(dve):
                for g in range(4):
                    dve.tensor_scalar(kg[:, g, WIN:], r.k[:], m.hdiv[:, g:g + 1], None, ALU.mult).then_inc(k_cut, 1)
                for i in range(2):
                    for pair in range(2):
                        g = 2 * pair + i
                        dve.tensor_scalar(vmask[i * 64:(i + 1) * 64, pair, :], m.ones[i * 64:(i + 1) * 64, :], 0.0, None,
                                          ALU.mult).then_inc(vmask_set, 1)
                        dve.wait_ge(vmask_set, 2 * (2 * i + pair) + 1)
                        dve.memset(vmask[i * 64:(i + 1) * 64, pair, 32 * g:32 * g + 32], 1.0).then_inc(vmask_set, 1)
                dve.wait_ge(vmask_set, 8)
                dve.wait_ge(masks_set, 12)

                def front(s, k):
                    par = k % 2
                    if not before(s, 4):
                        dve.wait_ge(out_raw, s - 3)
                        dve.wait_ge(turned, s - 3)
                    dve.wait_ge(v_raw, s + 1)
                    for b in range(2):
                        dve.tensor_tensor(vm[:, k, b], vps[:, par, b * P:(b + 1) * P].unsqueeze(1).to_broadcast([P, 2, P]),
                                          vmask[:], ALU.mult).then_inc(v_masked, 1)
                    dve.wait_ge(scored, s + 1)
                    if before(s, 1):
                        mk = mask0[:].unsqueeze(2).to_broadcast([P, 2, 4, KW])
                        for b in range(2):
                            ins = dve.scalar_tensor_tensor(
                                out=x[:, k, 4 * b:4 * b + 4], in0=sps[:, par, b * 256:(b + 1) * 256].rearrange("p (g j) -> p g j", j=KW),
                                scalar=HD ** -0.5, in1=mk[:, b], op0=ALU.mult, op1=ALU.add)
                        ins.then_inc(shifted, 1)
                    else:
                        dve.scalar_tensor_tensor(out=x[:, k], in0=sps[:, par, :].rearrange("p (g j) -> p g j", j=KW),
                                                 scalar=HD ** -0.5, in1=mask[:].unsqueeze(1).to_broadcast(G8),
                                                 op0=ALU.mult, op1=ALU.add).then_inc(shifted, 1)
                    dve.wait_ge(shifted, s + 1)
                    dve.tensor_reduce(st[:, k, 0, :], x[:, k], AX.X, ALU.max).then_inc(maxed, 1)

                def middle(s, k):
                    dve.wait_ge(exped, s + 1)
                    dve.tensor_reduce(st[:, k, 1, :], x[:, k], AX.X, ALU.add).then_inc(totaled, 1)
                    dve.wait_ge(totaled, s + 1)
                    dve.reciprocal(st[:, k, 1, :], st[:, k, 1, :]).then_inc(inverted, 1)
                    dve.wait_ge(inverted, s + 1)
                    dve.tensor_tensor(x[:, k], x[:, k], st[:, k, 1, :].unsqueeze(2).to_broadcast(G8), ALU.mult)\
                       .then_inc(p_ready, 1)

                def back(s, par):
                    dve.wait_ge(out_raw, s + 1)
                    dve.tensor_tensor(o[:, par], ops[:, par, 0:2 * P].rearrange("p (b a i) -> p b a i", b=2, a=4),
                                      m.hmod[:].unsqueeze(1).unsqueeze(3).to_broadcast([P, 2, 4, WIN]), ALU.mult)\
                       .then_inc(out_picked, 1)
                    dve.wait_ge(out_picked, s + 1)
                    dve.tensor_reduce(at(r.local, s, 0).rearrange("p (b i) -> p b i", b=2),
                                      o[:, par].rearrange("p b a i -> p b i a"), AX.X, ALU.add).then_inc(local_ready, 1)

                def body(s, k):
                    middle(s, k)
                    if not isinstance(s, int) or s + 2 < STEPS:
                        front(s + 2, (k + 2) % 4)
                    if not before(s, 1):
                        back(s - 1, (k - 1) % 2)

                front(0, 0)
                front(1, 1)
                steps(dve, body)
                back(STEPS - 1, 1)


def l2_latent(nc, m, inp, r):
    NL = LAT
    W = LH * NL
    LD = 64
    with ExitStack() as own:
        sb = lambda name, shape: own.enter_context(sbuf(nc, name, shape))
        wg = sb("w_latent", [P, 3, LD])
        pool2 = sb("pooled", [P, 2, NL])
        gk = sb("latent_keys", [LD, LH, NL])
        gv = sb("latent_values", [P, 4, LD])
        lmask = sb("latent_mask", [P, NT, NL])
        gq = sb("latent_q", [LD, 2, P])
        x = sb("latent_scores", [P, 4, LH, NL])
        st = sb("latent_stats", [P, 4, 2, LH])
        pt = sb("latent_pT", [P, 2, 4, P])
        pm = sb("pooled_mean", [P, NL])
        load_all(nc, [(wg[:, 0, :], inp["L2_attn_wgq"]), (wg[:, 1, :], inp["L2_attn_wgk"]), (wg[:, 2, :], inp["L2_attn_wgv"])])
        cps = own.enter_context(psum(nc, "latent_const", [P, CH]))
        qps = own.enter_context(psum(nc, "latent_q_raw", [P, CH]))
        sps = own.enter_context(psum(nc, "latent_qk", [P, 2, CH]))
        tps = own.enter_context(psum(nc, "latent_turned", [P, 2, CH]))
        rps = own.enter_context(psum(nc, "latent_out", [LD, 2, CH]))
        with stage(nc, "mask_set", "pooled", "kv_raw", "blocks", "q_raw", "q_ready", "scored", "shifted", "maxed",
                      "less_max", "exped", "totaled", "inverted", "p_ready", "turned", "pt_ready", "out_raw",
                      "rem_ready") as (
                block, mask_set, pooled, kv_raw, blocks, q_raw, q_ready, scored, shifted, maxed, less_max, exped,
                totaled, inverted, p_ready, turned, pt_ready, out_raw, rem_ready):

            def steps(eng, body):
                for n in range(4):
                    body(n, n)
                with eng.Fori(1, NT // 4 - 1) as i:
                    for k in range(4):
                        body(i * 4 + k, k)
                for k in range(4):
                    body(NT - 4 + k, k)

            G8 = [P, LH, NL]

            def before(n, k):
                return isinstance(n, int) and n < k

            def ahead(n, k=2):
                return not isinstance(n, int) or n + k < NT

            def tile(t, n):
                return t[:, n * P:(n + 1) * P] if isinstance(n, int) else t[:, ds(n * P, P)]

            @block.gpsimd
            def _(pool):
                pool.memset(lmask[:], 0.0).then_inc(mask_set, 1)
                pool.wait_ge(mask_set, 1)
                for q in range(4):
                    part = lmask[q * 32:(q + 1) * 32]
                    pool.affine_select(out=part, in_=part, compare_op=ALU.is_ge, fill=NEG, base=q,
                                       pattern=[[4, NT], [-1, NL]], channel_multiplier=0).then_inc(mask_set, 1)

                def body(n, k):
                    pool.wait_ge(maxed, n + 1)
                    pool.tensor_tensor(x[:, k], x[:, k], st[:, k, 0, :].unsqueeze(2).to_broadcast(G8), ALU.subtract)\
                        .then_inc(less_max, 1)

                steps(pool, body)

            @block.tensor
            def _(pe):
                pe.wait_ge(pooled, 3)
                pe.matmul(cps[0:LD, 0:NL], wg[:, 1, :], pm[:], start=True, stop=True)
                pe.matmul(cps[:, NL:NL + LD], pool2[:].rearrange("p a n -> p (a n)"), wg[:, 2, :], start=True, stop=True)\
                  .then_inc(kv_raw, 1)
                pe.wait_ge(blocks, 10)

                def project(n):
                    if not before(n, 1):
                        pe.wait_ge(q_ready, n)
                    pe.matmul(qps[0:LD, 0:P], wg[:, 0, :], tile(m.xn, n), start=True, stop=True).then_inc(q_raw, 1)

                def score(n, par):
                    pe.wait_ge(q_ready, n + 1)
                    if not before(n, 2):
                        pe.wait_ge(shifted, n - 1)
                    pe.matmul(sps[:, par, :], gq[:, par, :], gk[:].rearrange("p h n -> p (h n)"), start=True, stop=True)\
                      .then_inc(scored, 1)

                def body(n, k):
                    par = k % 2
                    if ahead(n):
                        score(n + 2, par)
                    if ahead(n, 3):
                        project(n + 3)
                    pe.wait_ge(p_ready, n + 1)
                    if not before(n, 2):
                        pe.wait_ge(pt_ready, n - 1)
                        pe.wait_ge(rem_ready, n - 1)
                    for i in range(4):
                        mm = pe.transpose(tps[:, par, i * P:(i + 1) * P],
                                          x[:, k, 2 * i:2 * i + 2, :].rearrange("p g j -> p (g j)"), m.ident[:])
                    mm.then_inc(turned, 1)
                    pe.wait_ge(pt_ready, n + 1)
                    for i in range(4):
                        mm = pe.matmul(rps[:, par, 0:P], gv[:, i, :], pt[:, par, i, :], start=(i == 0), stop=(i == 3))
                    mm.then_inc(out_raw, 1)

                project(0)
                for n in range(2):
                    project(n + 1)
                    score(n, n)
                steps(pe, body)

            @block.scalar
            def _(act):
                def copy_q(n, par):
                    act.wait_ge(q_raw, n + 1)
                    if not before(n, 2):
                        act.wait_ge(scored, n - 1)
                    act.activation(gq[:, par, :], qps[0:LD, 0:P], ACT.Copy).then_inc(q_ready, 1)

                def exp(n, k):
                    act.wait_ge(less_max, n + 1)
                    act.activation(x[:, k], x[:, k], ACT.Exp).then_inc(exped, 1)

                def body(n, k):
                    par = k % 2
                    if ahead(n, 1):
                        exp(n + 1, (k + 1) % 4)
                    if ahead(n, 3):
                        copy_q(n + 3, 1 - par)
                    act.wait_ge(turned, n + 1)
                    if not before(n, 2):
                        act.wait_ge(out_raw, n - 1)
                    act.activation(pt[:, par].rearrange("p a n -> p (a n)"), tps[:, par, :], ACT.Copy).then_inc(pt_ready, 1)

                copy_q(0, 0)
                copy_q(1, 1)
                copy_q(2, 0)
                exp(0, 0)
                steps(act, body)

            @block.vector
            def _(dve):
                CHUNK = TOK // NL
                dve.tensor_reduce(pm[:], m.xn[:].rearrange("p (n c) -> p n c", c=CHUNK), AX.X, ALU.add).then_inc(pooled, 1)
                dve.wait_ge(pooled, 1)
                dve.tensor_scalar(pm[:], pm[:], 1.0 / CHUNK, None, ALU.mult).then_inc(pooled, 1)
                dve.wait_ge(pooled, 2)
                dve.tensor_copy(pool2[:], pm[:].unsqueeze(1).to_broadcast([P, 2, NL])).then_inc(pooled, 1)
                dve.wait_ge(kv_raw, 1)
                dve.tensor_tensor(gk[:], cps[0:LD, 0:NL].unsqueeze(1).to_broadcast([LD, LH, NL]),
                                  m.head_ones[0:LD, 0:LD].rearrange("p (h e) -> p h e", e=HD)[:, :, 0:1]
                                  .to_broadcast([LD, LH, NL]), ALU.mult).then_inc(blocks, 1)
                dve.tensor_scalar(gv[:], m.ones[:, 0:64].unsqueeze(1).to_broadcast([P, 4, LD]), 0.0, None, ALU.mult)\
                   .then_inc(blocks, 1)
                dve.wait_ge(blocks, 2)
                for i in range(4):
                    for half in range(2):
                        h = 2 * i + half
                        rows = slice(half * 64, half * 64 + 64)
                        dve.tensor_copy(gv[rows, i, HD * h:HD * h + HD], cps[rows, NL + HD * h:NL + HD * h + HD])\
                           .then_inc(blocks, 1)
                dve.wait_ge(mask_set, 5)

                def front(n, k):
                    par = k % 2
                    if not before(n, 4):
                        dve.wait_ge(turned, n - 3)
                    mk = lmask[:, n:n + 1, :] if isinstance(n, int) else lmask[:, ds(n, 1), :]
                    dve.wait_ge(scored, n + 1)
                    dve.scalar_tensor_tensor(out=x[:, k], in0=sps[:, par, :].rearrange("p (g j) -> p g j", j=NL),
                                             scalar=HD ** -0.5, in1=mk.to_broadcast(G8),
                                             op0=ALU.mult, op1=ALU.add).then_inc(shifted, 1)
                    dve.wait_ge(shifted, n + 1)
                    dve.tensor_reduce(st[:, k, 0, :], x[:, k], AX.X, ALU.max).then_inc(maxed, 1)

                def middle(n, k):
                    dve.wait_ge(exped, n + 1)
                    dve.tensor_reduce(st[:, k, 1, :], x[:, k], AX.X, ALU.add).then_inc(totaled, 1)
                    dve.wait_ge(totaled, n + 1)
                    dve.reciprocal(st[:, k, 1, :], st[:, k, 1, :]).then_inc(inverted, 1)
                    dve.wait_ge(inverted, n + 1)
                    dve.tensor_tensor(x[:, k], x[:, k], st[:, k, 1, :].unsqueeze(2).to_broadcast(G8), ALU.mult)\
                       .then_inc(p_ready, 1)

                def back(n, par):
                    dve.wait_ge(out_raw, n + 1)
                    dve.tensor_copy(tile(r.rem, n), rps[:, par, 0:P]).then_inc(rem_ready, 1)

                def body(n, k):
                    middle(n, k)
                    if ahead(n):
                        front(n + 2, (k + 2) % 4)
                    if not before(n, 1):
                        back(n - 1, (k - 1) % 2)

                front(0, 0)
                front(1, 1)
                steps(dve, body)
                back(NT - 1, 1)


def layer2_attention(nc, m, inp):
    with ExitStack() as own:
        sb = lambda name, shape: own.enter_context(sbuf(nc, name, shape))
        r = Named()
        r.q, r.local, r.rem = sb("l2_q", [P, TOK]), sb("l2_local", [P, TOK]), sb("l2_rem", [64, TOK])
        w = sb("w_l2", [P, 3, P])
        wr = sb("w_r_out", [64, P])
        gate_w = sb("gate_blocks", [P, 2, P])
        load_all(nc, [(w[:, 0, :], inp["L2_attn_wq"]), (w[:, 1, :], inp["L2_attn_wk"]), (w[:, 2, :], inp["L2_attn_w_out"]),
                      (wr[:], inp["L2_attn_r_out_w"])])
        with ExitStack() as inner:
            r.k = inner.enter_context(sbuf(nc, "l2_k", [P, TOK]))
            with psum(nc, "qk_proj", [P, 2, NCH, CH]) as ps, stage(nc, "q_raw", "k_raw", "q_ready", "k_ready", "gates") as (
                    block, q_raw, k_raw, q_ready, k_ready, gates):
                @block.tensor
                def _(pe):
                    for c in range(NCH):
                        pe.matmul(ps[:, 0, c, :], w[:, 0, :], m.xn[:, cs(c)], start=True, stop=True).then_inc(q_raw, 1)
                        pe.matmul(ps[:, 1, c, :], w[:, 1, :], m.xn[:, cs(c)], start=True, stop=True).then_inc(k_raw, 1)

                @block.scalar
                def _(act):
                    for c in range(NCH):
                        act.wait_ge(q_raw, c + 1)
                        act.activation(r.q[:, cs(c)], ps[:, 0, c, :], ACT.Copy).then_inc(q_ready, 1)

                @block.vector
                def _(dve):
                    for i, name in enumerate(("L2_attn_gate_local_w", "L2_attn_gate_remote_w")):
                        dve.tensor_scalar(gate_w[:, i, :], m.head_ones[:], m.col(name), None, ALU.mult).then_inc(gates, 1)
                    for c in range(NCH):
                        dve.wait_ge(k_raw, c + 1)
                        dve.tensor_copy(r.k[:, cs(c)], ps[:, 1, c, :]).then_inc(k_ready, 1)
            l2_window(nc, m, inp, r)
        l2_latent(nc, m, inp, r)
        gate = sb("gates", [P, 2, 2, CH])
        gps = own.enter_context(psum(nc, "gate_logits", [P, 2, 2, CH]))
        rps = own.enter_context(psum(nc, "rem_proj", [P, 2, CH]))
        ops = own.enter_context(psum(nc, "l2_out", [P, 2, CH]))
        with stage(nc, "logits", "gated", "rem_raw", "local_scaled", "rem_scaled", "mixed", "projected", "added") as (
                block, logits, gated, rem_raw, local_scaled, rem_scaled, mixed, projected, added):
            @block.tensor
            def _(pe):
                def project(c):
                    pe.wait_ge(mixed, c + 1)
                    if c >= 2:
                        pe.wait_ge(added, c - 1)
                    pe.matmul(ops[:, c % 2, :], w[:, 2, :], r.local[:, cs(c)], start=True, stop=True).then_inc(projected, 1)

                for c in range(NCH):
                    if c >= 2:
                        pe.wait_ge(gated, 2 * c - 2)
                        pe.wait_ge(rem_scaled, c - 1)
                    for i in range(2):
                        pe.matmul(gps[:, i, c % 2, :], gate_w[:, i, :], r.q[:, cs(c)], start=True, stop=True).then_inc(logits, 1)
                    pe.matmul(rps[:, c % 2, :], wr[:], r.rem[:, cs(c)], start=True, stop=True).then_inc(rem_raw, 1)
                    if c:
                        project(c - 1)
                project(NCH - 1)

            @block.scalar
            def _(act):
                for c in range(NCH):
                    if c >= 2:
                        act.wait_ge(mixed, c - 1)
                    for i in range(2):
                        act.wait_ge(logits, 2 * c + i + 1)
                        act.activation(gate[:, i, c % 2, :], gps[:, i, c % 2, :], ACT.Sigmoid).then_inc(gated, 1)

            @block.vector
            def _(dve):
                def add(c):
                    dve.wait_ge(projected, c + 1)
                    dve.tensor_tensor(m.x[:, cs(c)], ops[:, c % 2, :], m.x[:, cs(c)], ALU.add).then_inc(added, 1)

                for c in range(NCH):
                    dve.wait_ge(gated, 2 * c + 1)
                    dve.tensor_tensor(r.local[:, cs(c)], r.local[:, cs(c)], gate[:, 0, c % 2, :], ALU.mult).then_inc(local_scaled, 1)
                    dve.wait_ge(gated, 2 * c + 2)
                    dve.wait_ge(rem_raw, c + 1)
                    dve.tensor_tensor(gate[:, 1, c % 2, :], rps[:, c % 2, :], gate[:, 1, c % 2, :], ALU.mult).then_inc(rem_scaled, 1)
                    dve.wait_ge(rem_scaled, c + 1)
                    dve.wait_ge(local_scaled, c + 1)
                    dve.tensor_tensor(r.local[:, cs(c)], r.local[:, cs(c)], gate[:, 1, c % 2, :], ALU.add).then_inc(mixed, 1)
                    if c:
                        add(c - 1)
                add(NCH - 1)



F16 = mybir.dt.float16


def weave(a, b, early=0.0):
    out, i = [], 0
    for j, y in enumerate(b):
        while i < len(a) and i * len(b) <= (j + early) * len(a):
            out.append(a[i])
            i += 1
        out.append(y)
    return out + a[i:]


def layer3_attention(nc, m, inp):
    H, DH = 16, 64
    SCALE, EPS = DH ** -0.5, 1e-8
    LIFT = 2.0 ** 14
    RB = 5
    VW = 2 * DH + 1
    groups = lambda t: t // 4 + 1
    g0 = lambda t: sum(groups(x) for x in range(t))
    G = g0(NT)
    width = lambda t, g: min(CH, (t + 1) * P - g * CH)
    hi = slice(DH, P)

    UNITS = [("q", c) for c in range(NCH)] + [("k", c) for c in range(NCH)] + [("v", i) for i in range(2)]
    unit_of_step = lambda t: t - 1 if 1 <= t <= len(UNITS) else None
    slots, slot_of = [], {}
    for t in range(NT):
        if unit_of_step(t) is not None:
            slot_of["unit", unit_of_step(t)] = len(slots)
            slots.append(("unit", unit_of_step(t)))
        if t == NT - 1:
            slots.append(None)
        for c in reversed(range(NCH)):
            slot_of[t + 1, c] = len(slots)
            slots.append((t + 1, c))
    assert len(slots) % RB == 0
    for c in range(NCH):
        slot_of[0, c] = slot_of[NT, c] - len(slots)
    bank = lambda *what: slot_of[what] % RB

    with ExitStack() as own:
        sb = lambda name, shape, dt=F32: own.enter_context(nc.sbuf_tensor(f"{name}_{nc.next_id()}", shape, dt))
        o_all = sb("o_all", [P, NT, H * DH])
        with ExitStack() as inner:
            sb = lambda name, shape, dt=F32: inner.enter_context(nc.sbuf_tensor(f"{name}_{nc.next_id()}", shape, dt))
            wq, wk, wv = sb("w_q2", [P, 2, DH]), sb("w_k2", [P, 2, DH]), sb("w_v", [P, DH])
            qs2, kh2, kl2 = (sb(n, [P, 2, TOK], F16) for n in ("q_pair", "k_high", "k_low"))
            v2 = sb("v_pair", [P, 2, NT, VW], F16)
            p = sb("p", [P, 2, TOK])
            ph, pl = sb("pT_high", [P, 4, CH], F16), sb("pT_low", [P, 4, CH], F16)
            tri = sb("past", [P, P])
            mx, bias = sb("chunk_max", [P, 2, NCH]), sb("exp_bias", [P, NT])
            raw = sb("o_raw", [P, 2, NT, VW])
            den = sb("den", [P, 2, 2, NT])
            ps = inner.enter_context(psum(nc, "scores", [P, 8, CH]))
            with stage(nc, "w_loaded", "const_set", "q_raw", "k_raw", "v_raw", "q_high", "q_low", "k_highs",
                       "k_lows", "v_high", "v_low", "scored", "chunk_maxed", "biased", "exped", "masked", "turned",
                       "pt_high", "pt_low", "summed", "o_out", "den_set", "den_inverted", "o_summed", "o_ready") as (
                    block, w_loaded, const_set, q_raw, k_raw, v_raw, q_high, q_low, k_highs, k_lows, v_high, v_low,
                    scored, chunk_maxed, biased, exped, masked, turned, pt_high, pt_low, summed, o_out, den_set,
                    den_inverted, o_summed, o_ready):

                def heads(eng, prologue, head):
                    prologue(lambda per_head, k, ahead=0: per_head * ahead + k - per_head)

                    def pair(i, last):
                        for par in range(2):
                            head(lambda per_head, k, ahead=0: i * (2 * per_head) + (par + ahead) * per_head + k,
                                 par, i * 2 + par, last and par == 1)

                    with eng.Fori(0, H // 2 - 1) as i:
                        pair(i, False)
                    pair(H // 2 - 1, True)

                @block.sync
                def _(sp):
                    def load(h):
                        for dst, src in ((wq, inp["L3_attn_Wq"]), (wk, inp["L3_attn_Wkv"])):
                            for r in range(2):
                                sp.dma_start(dst[:, r, :], src[:, ds(h * DH, DH)]).then_inc(w_loaded, 16)
                        sp.dma_start(wv[:], inp["L3_attn_Wkv"][:, ds(h * DH + H * DH, DH)]).then_inc(w_loaded, 16)

                    load(0)
                    with sp.Fori(1, H) as h:
                        sp.wait_ge(v_raw, h * 2)
                        load(h)

                @block.gpsimd
                def _(pool):
                    pool.memset(tri[:], 1.0).then_inc(const_set, 1)
                    pool.memset(v2[:, :, :, 2 * DH:VW], 1.0).then_inc(const_set, 1)
                    pool.wait_ge(const_set, 2)
                    pool.affine_select(out=tri[:], in_=tri[:], compare_op=ALU.is_ge, fill=0.0, base=0,
                                       pattern=[[-1, P]], channel_multiplier=1).then_inc(const_set, 1)
                    pool.wait_ge(const_set, 3)

                    def head(at, par, h, last):
                        for t in range(NT):
                            pool.wait_ge(exped, at(G, g0(t + 1)))
                            diag = p[:, t % 2, t * P:(t + 1) * P]
                            pool.tensor_tensor(diag, diag, tri[:], ALU.mult).then_inc(masked, 1)
                        pool.wait_ge(o_out, at(NT, NT))
                        part = lambda a: raw[:, par, :, a:a + DH]
                        pool.tensor_tensor(part(0), part(0), part(DH), ALU.add).then_inc(o_summed, 1)
                        pool.wait_ge(o_summed, at(1, 1))
                        pool.wait_ge(den_inverted, at(1, 1))
                        pool.tensor_tensor(o_all[:, :, ds(h * DH, DH)], part(0),
                                           den[:, par, 1, :].unsqueeze(2).to_broadcast([P, NT, DH]), ALU.mult)\
                            .then_inc(o_ready, 1)

                    heads(pool, lambda at: None, head)

                @block.tensor
                def _(pe):
                    def free(at, slot, last):
                        slot -= RB
                        while last and slot >= 0 and slots[slot][0] == "unit":
                            slot -= RB
                        ahead = 0
                        if slot < 0:
                            slot, ahead = slot + len(slots), -1
                        what = slots[slot]
                        if what is None:
                            return
                        if what[0] == "unit":
                            kind, k = UNITS[what[1]]
                            done, each = {"q": (q_low, NCH), "k": (k_lows, NCH), "v": (v_low, 2)}[kind]
                            pe.wait_ge(done, at(each, k + 1, ahead + 1))
                        else:
                            t, c = what
                            if t == NT:
                                t, ahead = 0, ahead + 1
                            pe.wait_ge(chunk_maxed, at(NT * NCH, t * NCH + NCH - c, ahead))
                            if c < groups(t):
                                pe.wait_ge(exped, at(G, g0(t) + groups(t) - c, ahead))

                    def project(at, u, b):
                        kind, c = UNITS[u]
                        if u == 0:
                            pe.wait_ge(w_loaded, at(80, 80, 1))
                        if kind == "v":
                            for n in range(8):
                                mm = pe.matmul(ps[:, b, n * DH:(n + 1) * DH], m.xn[:, (8 * c + n) * P:(8 * c + n + 1) * P],
                                               wv[:], start=True, stop=True)
                            mm.then_inc(v_raw, 1)
                        else:
                            w, done = (wq, q_raw) if kind == "q" else (wk, k_raw)
                            pe.matmul(ps[:, b, :], w[:].rearrange("p r d -> p (r d)"), m.xn[:, cs(c)],
                                      start=True, stop=True).then_inc(done, 1)

                    def scores(at, par, t, c):
                        b = bank(t, c)
                        if t == NT:
                            t, par = 0, 1 - par
                            if c == NCH - 1:
                                pe.wait_ge(q_low, at(NCH, NCH, 1))
                                pe.wait_ge(k_lows, at(NCH, NCH, 1))
                        q = qs2[:, par, t * P:(t + 1) * P]
                        pe.matmul(ps[:, b, :], q, kh2[:, par, cs(c)], start=True, stop=False)
                        pe.matmul(ps[:, b, :], q, kl2[:, par, cs(c)], start=False, stop=True).then_inc(scored, 1)

                    def turn(at, t, g):
                        n = g0(t) + g
                        if n >= 2:
                            pe.wait_ge(pt_low, at(G, n - 1))
                        if g == 0:
                            pe.wait_ge(masked, at(NT, t + 1))
                        for b in range(4 * g, min(4 * g + 4, t + 1)):
                            mm = pe.transpose(ps[:, 5 + n % 2, b % 4 * P:(b % 4 + 1) * P],
                                              p[:, t % 2, b * P:(b + 1) * P], m.ident[:])
                        mm.then_inc(turned, 1)

                    def add_up(at, par, t, g):
                        n = g0(t) + g
                        pe.wait_ge(pt_low, at(G, n + 1))
                        if g == 0:
                            if t:
                                pe.wait_ge(o_out, at(NT, t))
                            else:
                                pe.wait_ge(v_low, at(2, 2))
                        for b in range(4 * g, min(4 * g + 4, t + 1)):
                            for part in (ph, pl):
                                mm = pe.matmul(ps[:, 7, 0:VW], part[:, n % 4, b % 4 * P:(b % 4 + 1) * P], v2[:, par, b, :],
                                               start=(b == 0 and part is ph), stop=(b == t and part is pl))
                        mm.then_inc(summed, 1)

                    def products(t):
                        if t < 0:
                            return []
                        use = [("t", t, 0)]
                        for g in range(1, groups(t)):
                            use += [("t", t, g), ("a", t, g - 1)]
                        return use + [("a", t, groups(t) - 1)]

                    def head(at, par, h, last):
                        for t in range(NT):
                            u = unit_of_step(t)
                            fill = [] if last and t == NT - 1 else [("s", c) for c in reversed(range(NCH))]
                            if u is not None and not last:
                                fill = [("u", u)] + fill
                            work = weave(fill, products(t - 1), 0.5)
                            if t == NT - 1:
                                work += products(t)
                            for what in work:
                                if what[0] == "u":
                                    free(at, slot_of["unit", what[1]], last)
                                    project(at, what[1], bank("unit", what[1]))
                                elif what[0] == "s":
                                    free(at, slot_of[t + 1, what[1]], last)
                                    scores(at, par, t + 1, what[1])
                                elif what[0] == "t":
                                    turn(at, what[1], what[2])
                                else:
                                    add_up(at, par, what[1], what[2])

                    def prologue(at):
                        for u in range(len(UNITS)):
                            if u >= 8:
                                pe.wait_ge(q_low, u - 7)
                            project(at, u, u % 8)
                        pe.wait_ge(v_low, 2)
                        for c in reversed(range(NCH)):
                            scores(at, 1, NT, c)

                    heads(pe, prologue, head)

                @block.scalar
                def _(act):
                    def high(at, par, u, b):
                        kind, c = UNITS[u]
                        if kind == "q":
                            act.wait_ge(q_raw, at(NCH, c + 1, 1))
                            act.activation(qs2[:, par, cs(c)], ps[:, b, :], ACT.Copy, scale=SCALE).then_inc(q_high, 1)
                        elif kind == "k":
                            act.wait_ge(k_raw, at(NCH, c + 1, 1))
                            act.activation(kh2[:, par, cs(c)], ps[:, b, :], ACT.Copy).then_inc(k_highs, 1)
                        else:
                            act.wait_ge(v_raw, at(2, c + 1, 1))
                            act.activation(v2[:, par, 8 * c:8 * c + 8, 0:DH],
                                           ps[:, b, :].rearrange("p (n d) -> p n d", d=DH), ACT.Copy).then_inc(v_high, 1)

                    def exp(at, t, c):
                        if c == groups(t) - 1:
                            if t >= 2:
                                act.wait_ge(turned, at(G, g0(t - 1)))
                            act.wait_ge(biased, at(NT, t + 1))
                        w = width(t, c)
                        act.activation(p[:, t % 2, c * CH:c * CH + w], ps[:, bank(t, c), 0:w], ACT.Exp,
                                       bias=bias[:, t:t + 1]).then_inc(exped, 1)

                    def pt(at, t, g):
                        n, w = g0(t) + g, width(t, g)
                        act.wait_ge(turned, at(G, n + 1))
                        if n >= 4:
                            act.wait_ge(summed, at(G, n - 3))
                        act.activation(ph[:, n % 4, 0:w], ps[:, 5 + n % 2, 0:w], ACT.Copy, scale=LIFT).then_inc(pt_high, 1)

                    def out(at, par, t):
                        act.wait_ge(summed, at(G, g0(t + 1)))
                        act.activation(raw[:, par, t, :], ps[:, 7, 0:VW], ACT.Copy).then_inc(o_out, 1)

                    def head(at, par, h, last):
                        for t in range(NT):
                            unit = [("u", unit_of_step(t))] if unit_of_step(t) is not None and not last else []
                            exps = [("e", c) for c in reversed(range(groups(t)))]
                            pts = [("p", g) for g in range(groups(t - 1))] if t else []
                            work = weave(exps, pts)
                            for what in unit + work:
                                if what[0] == "u":
                                    high(at, 1 - par, what[1], bank("unit", what[1]))
                                elif what[0] == "e":
                                    exp(at, t, what[1])
                                else:
                                    pt(at, t - 1, what[1])
                            if t:
                                out(at, par, t - 1)
                        for g in range(groups(NT - 1)):
                            pt(at, NT - 1, g)
                        out(at, par, NT - 1)

                    def prologue(at):
                        for u in range(len(UNITS)):
                            high(at, 0, u, u % 8)

                    heads(act, prologue, head)

                @block.vector
                def _(dve):
                    def low(at, par, u, b):
                        kind, c = UNITS[u]
                        if kind == "q":
                            dve.wait_ge(q_high, at(NCH, c + 1, 1))
                            low_part = qs2[hi, par, cs(c)]
                            dve.scalar_tensor_tensor(out=low_part, in0=ps[hi, b, :], scalar=SCALE, in1=low_part,
                                                     op0=ALU.mult, op1=ALU.subtract).then_inc(q_low, 1)
                        elif kind == "k":
                            dve.wait_ge(k_highs, at(NCH, c + 1, 1))
                            dve.tensor_tensor(kl2[:, par, cs(c)], ps[:, b, :], kh2[:, par, cs(c)], ALU.subtract)\
                               .then_inc(k_lows, 1)
                        else:
                            dve.wait_ge(v_high, at(2, c + 1, 1))
                            dve.tensor_tensor(v2[:, par, 8 * c:8 * c + 8, DH:2 * DH],
                                              ps[:, b, :].rearrange("p (n d) -> p n d", d=DH),
                                              v2[:, par, 8 * c:8 * c + 8, 0:DH], ALU.subtract).then_inc(v_low, 1)

                    def chunk_max(at, t, c):
                        t, ahead, b = (0, 1, NT) if t == NT else (t, 0, t)
                        dve.wait_ge(scored, at(NT * NCH, t * NCH + NCH - c, ahead))
                        dve.tensor_reduce(mx[:, t % 2, c:c + 1], ps[:, bank(b, c), :], AX.X, ALU.max)\
                           .then_inc(chunk_maxed, 1)

                    def tile_max(at, t):
                        t, ahead = (0, 1) if t == NT else (t, 0)
                        dve.wait_ge(chunk_maxed, at(NT * NCH, (t + 1) * NCH, ahead))
                        dve.tensor_reduce(bias[:, t:t + 1], mx[:, t % 2, :], AX.X, ALU.max, negate=True)\
                           .then_inc(biased, 1)

                    def pt(at, t, g):
                        n, w = g0(t) + g, width(t, g)
                        dve.wait_ge(pt_high, at(G, n + 1))
                        dve.scalar_tensor_tensor(out=pl[:, n % 4, 0:w], in0=ps[:, 5 + n % 2, 0:w], scalar=LIFT,
                                                 in1=ph[:, n % 4, 0:w], op0=ALU.mult, op1=ALU.subtract).then_inc(pt_low, 1)

                    def head(at, par, h, last):
                        for t in range(NT):
                            unit = [("u", unit_of_step(t))] if unit_of_step(t) is not None and not last else []
                            ahead = [] if last and t == NT - 1 else [("m", c) for c in reversed(range(NCH))]
                            pts = [("p", g) for g in range(groups(t - 1))] if t else []
                            work = weave(ahead, pts, -1)
                            for what in unit + work:
                                if what[0] == "u":
                                    low(at, 1 - par, what[1], bank("unit", what[1]))
                                elif what[0] == "m":
                                    chunk_max(at, t + 1, what[1])
                                else:
                                    pt(at, t - 1, what[1])
                            if ahead:
                                tile_max(at, t + 1)
                        for g in range(groups(NT - 1)):
                            pt(at, NT - 1, g)
                        dve.wait_ge(o_out, at(NT, NT))
                        dve.tensor_scalar(den[:, par, 0, :], raw[:, par, :, 2 * DH], EPS * LIFT, None, ALU.add)\
                           .then_inc(den_set, 1)
                        dve.wait_ge(den_set, at(1, 1))
                        dve.reciprocal(den[:, par, 1, :], den[:, par, 0, :]).then_inc(den_inverted, 1)

                    def prologue(at):
                        for u in range(len(UNITS)):
                            low(at, 0, u, u % 8)
                        for c in reversed(range(NCH)):
                            chunk_max(at, NT, c)
                        tile_max(at, NT)

                    heads(dve, prologue, head)
        wo = own.enter_context(sbuf(nc, "w_o3", [P, H * DH // P, P]))
        oT = own.enter_context(sbuf(nc, "o_T", [P, 2, CH]))
        tps = own.enter_context(psum(nc, "o_turned", [P, 2, CH]))
        ops = own.enter_context(psum(nc, "o_proj", [P, NCH, CH]))
        KT = H * DH // P
        load_all(nc, [(wo[:], inp["L3_attn_Wo"].rearrange("(k p) n -> p k n", p=P))])
        with stage(nc, "turned", "copied", "projected", "added") as (block, turned, copied, projected, added):
            @block.tensor
            def _(pe):
                def project(i):
                    c, k = divmod(i, KT)
                    pe.wait_ge(copied, i + 1)
                    pe.matmul(ops[:, c, :], wo[:, k, :], oT[:, i % 2, :], start=(k == 0), stop=(k == KT - 1)).then_inc(projected, 1)

                for i in range(NCH * KT):
                    c, k = divmod(i, KT)
                    if i >= 2:
                        pe.wait_ge(copied, i - 1)
                    for n in range(4):
                        mm = pe.transpose(tps[:, i % 2, n * P:(n + 1) * P], o_all[:, 4 * c + n, k * P:(k + 1) * P], m.ident[:])
                    mm.then_inc(turned, 1)
                    if i:
                        project(i - 1)
                project(NCH * KT - 1)

            @block.scalar
            def _(act):
                for i in range(NCH * KT):
                    act.wait_ge(turned, i + 1)
                    if i >= 2:
                        act.wait_ge(projected, i - 1)
                    act.activation(oT[:, i % 2, :], tps[:, i % 2, :], ACT.Copy).then_inc(copied, 1)

            @block.vector
            def _(dve):
                for c in range(NCH):
                    dve.wait_ge(projected, (c + 1) * KT)
                    dve.scalar_tensor_tensor(out=m.x[:, cs(c)], in0=ops[:, c, :], scalar=m.col("L3_attn_bo"),
                                             in1=m.x[:, cs(c)], op0=ALU.add, op1=ALU.add).then_inc(added, 1)



def build(nc, inp, out):
    with ExitStack() as own:
        m = Named()
        alloc = lambda name, shape: own.enter_context(sbuf(nc, name, shape))
        m.x = alloc("x_features", [P, TOK])
        m.xn = alloc("xn_features", [P, TOK])
        constants(nc, m, inp, alloc, inp["L0_attn_x"])
        turn_in(nc, m)
        for branches in ((layer0,), (layer1_attention, layer1_ffn), (layer2_attention, layer2_ffn),
                         (layer3_attention, layer3_experts)):
            layernorm(nc, m, m.x, m.xn, LN_EPS)
            for branch in branches:
                branch(nc, m, inp)
        turn_out(nc, m, out)


_OUTS = [((1, 2048, 128), 'float32')]


def kernel(**inputs):
    import numpy as _np
    import concourse.bacc as _bacc
    from concourse import mybir as _mybir
    from concourse.bass_utils import run_bass_kernel_spmd as _run

    nc = _bacc.Bacc("TRN2", target_bir_lowering=False, num_devices=1)
    arrays, args = {}, {}
    for name in inputs:
        a = _np.ascontiguousarray(inputs[name])
        arrays[f"in_{name}_dram"] = a
        args[name] = nc.dram_tensor(f"in_{name}_dram", a.shape, _mybir.dt.from_np(a.dtype), kind="ExternalInput").ap()
    shape, dtype = _OUTS[0]
    out = nc.dram_tensor("out_0_dram", shape, _mybir.dt.from_np(_np.dtype(dtype)), kind="ExternalOutput").ap()
    build(nc, args, out)
    r = _run(nc, [arrays], core_ids=[0])
    return r.results[0]["out_0_dram"]
```
